# Optimizing a Trainium2 kernel written in Bass

```python
import numpy as np
import jax
import jax.numpy as jnp

def _softmax(x, axis=-1):
    return jax.nn.softmax(x, axis=axis)

def _gelu(x):
    return jax.nn.gelu(x, approximate=True)

def _silu(x):
    return jax.nn.silu(x)

def _sigmoid(x):
    return jax.nn.sigmoid(x)

def _layernorm(x, axis=-1, eps=1e-05):
    m = jnp.mean(x, axis=axis, keepdims=True)
    v = jnp.var(x, axis=axis, keepdims=True)
    return (x - m) / jnp.sqrt(v + eps)

def _scatter_add(tgt, idx, src, axis=0):
    return tgt.at[idx].add(src)

def _segment_sum(src, seg, n):
    return jax.ops.segment_sum(src, seg, n)
kernel_name = 'mk_gps_d2_gnn_r32_3458bd'

def setup_inputs(seed: int=0):
    np.random.seed(seed)
    _w = jnp.asarray

    def _rec_inputs():
        import jax
        import jax.numpy as jnp
        _gk = jax.random.key(seed)
        x = -0.0003713 + 1 * jax.random.normal(jax.random.fold_in(_gk, 1), (3125, 256), jnp.float32)
        src = jax.random.randint(jax.random.fold_in(_gk, 2), (50000,), 0, 3125, jnp.int32)
        dst = jax.random.randint(jax.random.fold_in(_gk, 3), (50000,), 0, 3125, jnp.int32)
        _o = jnp.argsort(dst, stable=True)
        src = src[_o]
        dst = dst[_o]
        edge_attr_3 = -1.09012e-05 + 0.99985 * jax.random.normal(jax.random.fold_in(_gk, 11), (50000, 3), jnp.float32)
        edge_type_3 = jax.random.randint(jax.random.fold_in(_gk, 14), (50000,), 0, 3, jnp.int32)
        return (x, src, dst, edge_attr_3, edge_type_3)
    x, src, dst, edge_attr_3, edge_type_3 = _rec_inputs()

    def _L0_gnn_setup():
        import jax, jax.numpy as jnp
        import numpy as np
        N = 50000
        E = 12500
        IN = 256
        H = 8
        D = 32
        EF = 3
        key = jax.random.key(seed)
        ks = jax.random.split(key, 8)
        x = jax.random.normal(ks[0], (N, IN), dtype=jnp.float32)
        edge_index = jax.random.randint(ks[1], (2, E), 0, N, dtype=jnp.int64)
        edge_attr = jax.random.normal(ks[2], (E, EF), dtype=jnp.float32)
        W = jax.random.normal(ks[3], (H * D, IN), dtype=jnp.float32) * np.float32(np.sqrt(2.0 / (IN + H * D)))
        a_src = jax.random.normal(ks[4], (H, D), dtype=jnp.float32) * np.float32(np.sqrt(2.0 / (H + D)))
        a_dst = jax.random.normal(ks[5], (H, D), dtype=jnp.float32) * np.float32(np.sqrt(2.0 / (H + D)))
        edge_W = jax.random.normal(ks[6], (H * D, EF), dtype=jnp.float32) * np.float32(np.sqrt(2.0 / (EF + H * D)))
        edge_b = jnp.zeros((H * D,), dtype=jnp.float32)
        bias = jnp.zeros((H * D,), dtype=jnp.float32)
        return {'x': x, 'W': W, 'a_src': a_src, 'a_dst': a_dst, 'edge_W': edge_W, 'edge_b': edge_b, 'bias': bias, 'edge_attr': edge_attr, 'edge_index': edge_index}
    _L0_gnn_all = _L0_gnn_setup()
    _L0_gnn_in = {k: v for k, v in _L0_gnn_all.items() if k in ('W', 'a_src', 'a_dst', 'edge_W', 'edge_b', 'bias')}
    del _L0_gnn_all

    def _L0_mix_setup():
        import jax, jax.numpy as jnp
        import numpy as np
        C_CURV = 1.0
        MIN_NORM = 1e-15
        BALL_EPS = 1e-05
        ATT_EPS = 1e-15
        DIM = 32

        def _norm(x):
            return jnp.clip(jnp.linalg.norm(x, axis=-1, keepdims=True), MIN_NORM)

        def proj(x, c):
            maxnorm = (1.0 - BALL_EPS) / jnp.sqrt(c)
            n = _norm(x)
            return jnp.where(n > maxnorm, x / n * maxnorm, x)

        def expmap0(u, c):
            sc = jnp.sqrt(c)
            n = _norm(u)
            return jnp.tanh(sc * n) * u / (sc * n)

        def logmap0(p, c):
            sc = jnp.sqrt(c)
            n = _norm(p)
            return jnp.arctanh(jnp.clip(sc * n, -1.0 + 1e-07, 1.0 - 1e-07)) * p / (sc * n)

        def mobius_add(x, y, c):
            x2 = jnp.sum(x * x, -1, keepdims=True)
            y2 = jnp.sum(y * y, -1, keepdims=True)
            xy = jnp.sum(x * y, -1, keepdims=True)
            num = (1 + 2 * c * xy + c * y2) * x + (1 - c * x2) * y
            den = 1 + 2 * c * xy + c * c * x2 * y2
            return num / jnp.clip(den, MIN_NORM)

        def conv1d(x, w, pad, groups=1):
            return jax.lax.conv_general_dilated(x, w, (1,), [(pad, pad)], dimension_numbers=('NCH', 'OIH', 'NCH'), feature_group_count=groups)

        def batchnorm(x, gamma, beta):
            mean = jnp.mean(x, axis=(0, 2), keepdims=True)
            var = jnp.var(x, axis=(0, 2), keepdims=True)
            xn = (x - mean) * jax.lax.rsqrt(var + 1e-05)
            return gamma[None, :, None] * xn + beta[None, :, None]

        def _reference_tuple_inner(x, w_qkv, bn_gamma, bn_beta, w_dw, w_pw, w_res, b_res):
            c = C_CURV
            h = logmap0(proj(x, c), c)
            h = jnp.transpose(h, (1, 2, 0))
            h = conv1d(h, w_qkv, pad=2)
            h = batchnorm(h, bn_gamma, bn_beta)
            h = jax.nn.relu(jnp.transpose(h, (2, 0, 1)))
            qkv = proj(expmap0(h, c), c)
            t = jnp.transpose(logmap0(proj(qkv, c), c), (1, 2, 0))
            s = conv1d(t, w_dw, pad=2, groups=t.shape[1])
            s = conv1d(s, w_pw, pad=0, groups=t.shape[1] // DIM)
            cat = jnp.concatenate([t, s], axis=1)
            ai = proj(expmap0(jnp.transpose(cat, (2, 0, 1)), c), c)
            t2 = logmap0(proj(ai, c), c)
            L, N, C2 = t2.shape
            g = C2 // (3 * DIM)
            qkv3 = jnp.transpose(t2, (1, 2, 0)).reshape(N, g, 3 * DIM, L)
            q, k, v = jnp.split(qkv3, 3, axis=2)
            q = jax.nn.relu(q)
            k = jax.nn.relu(k)
            vk = jnp.einsum('ngdl,ngel->ngde', v, k)
            out = jnp.einsum('ngde,ngdl->ngdl', vk, q)
            out = out / (jnp.sum(v, -1, keepdims=True) + ATT_EPS)
            out = jnp.transpose(out.reshape(N, g * DIM, L), (2, 0, 1))
            fx_h = proj(expmap0(out, c), c)
            ft = jnp.transpose(logmap0(proj(fx_h, c), c), (1, 2, 0))
            ft = conv1d(ft, w_res, pad=0) + b_res[None, :, None]
            fx = proj(expmap0(jnp.transpose(ft, (2, 0, 1)), c), c)
            residual = mobius_add(fx, x, c)
            return (fx, residual)
        key = jax.random.key(seed)
        ks = jax.random.split(key, 6)
        L, N, C, TD = (64, 16, 256, 256)
        x = jax.random.normal(ks[0], (L, N, C), jnp.float32) * 0.05
        w_qkv = jax.random.normal(ks[1], (3 * TD, C, 5), jnp.float32) / np.sqrt(C * 5)
        bn_gamma = jnp.ones((3 * TD,), jnp.float32)
        bn_beta = jnp.zeros((3 * TD,), jnp.float32)
        w_dw = jax.random.normal(ks[2], (3 * TD, 1, 5), jnp.float32) / np.sqrt(5.0)
        w_pw = jax.random.normal(ks[3], (3 * TD, DIM, 1), jnp.float32) / np.sqrt(DIM)
        w_res = jax.random.normal(ks[4], (C, 2 * TD, 1), jnp.float32) / np.sqrt(2 * TD)
        b_res = jnp.zeros((C,), jnp.float32)
        return {'x': x, 'w_qkv': w_qkv, 'bn_gamma': bn_gamma, 'bn_beta': bn_beta, 'w_dw': w_dw, 'w_pw': w_pw, 'w_res': w_res, 'b_res': b_res}
    _L0_mix_all = _L0_mix_setup()
    _L0_mix_in = {k: v for k, v in _L0_mix_all.items() if k in ('w_qkv', 'bn_gamma', 'bn_beta', 'w_dw', 'w_pw', 'w_res', 'b_res')}
    del _L0_mix_all

    def _L0_ffn_setup():
        import jax, jax.numpy as jnp
        import numpy as np
        E, D, H, TOP_K = (6, 256, 256, 2)
        ROUTER_H = D // 2
        key = jax.random.key(seed)
        ks = jax.random.split(key, 12)
        s = 1.0 / np.sqrt(D)
        sh = 1.0 / np.sqrt(H)
        sr = 1.0 / np.sqrt(ROUTER_H)
        return {'features': jax.random.normal(ks[0], (8, 128, D), dtype=jnp.float32), 'router_w1': jax.random.uniform(ks[1], (D, ROUTER_H), jnp.float32, -s, s), 'router_b1': jnp.zeros((ROUTER_H,), jnp.float32), 'router_w2': jax.random.uniform(ks[2], (ROUTER_H, E), jnp.float32, -sr, sr), 'router_b2': jnp.zeros((E,), jnp.float32), 'expert_w1': jax.random.uniform(ks[3], (E, D, H), jnp.float32, -s, s), 'expert_b1': jnp.zeros((E, H), jnp.float32), 'expert_w2': jax.random.uniform(ks[4], (E, H, H), jnp.float32, -sh, sh), 'expert_b2': jnp.zeros((E, H), jnp.float32), 'expert_w3': jax.random.uniform(ks[5], (E, H, D), jnp.float32, -sh, sh), 'expert_b3': jnp.zeros((E, D), jnp.float32)}
    _L0_ffn_all = _L0_ffn_setup()
    _L0_ffn_in = {k: v for k, v in _L0_ffn_all.items() if k in ('router_w1', 'router_b1', 'router_w2', 'router_b2', 'expert_w1', 'expert_b1', 'expert_w2', 'expert_b2', 'expert_w3', 'expert_b3')}
    del _L0_ffn_all

    def _L1_gnn_setup():
        import jax, jax.numpy as jnp
        import numpy as np
        H = 4
        DH = 64
        HID = 256
        EPS = 1e-05
        N_NODES = 625
        N_EDGES = 10000
        N_LAYERS = 3

        def _layer_norm(x, g, b):
            mu = jnp.mean(x, axis=-1, keepdims=True)
            var = jnp.mean((x - mu) ** 2, axis=-1, keepdims=True)
            return (x - mu) * jax.lax.rsqrt(var + EPS) * g + b

        def _message_passing(h, src, tgt, et, Wq, bq, Wk, bk, Wv, bv, Ee, Wo, bo, n_nodes):
            Q = (h @ Wq.T + bq).reshape(-1, H, DH)
            K = (h @ Wk.T + bk).reshape(-1, H, DH)
            V = (h @ Wv.T + bv).reshape(-1, H, DH)
            scores = jnp.einsum('ehd,egd->ehg', Q[src], K[tgt]) / jnp.sqrt(jnp.float32(DH))
            attn = jax.nn.softmax(scores, axis=-1)
            msg = jnp.einsum('ehg,egd->ehd', attn, V[tgt]).reshape(-1, HID)
            msg = msg + Ee[et]
            proj = msg @ Wo.T + bo
            return jax.ops.segment_sum(proj, src, num_segments=n_nodes)
        key = jax.random.key(seed)
        ks = jax.random.split(key, 16)

        def w(k, shape, s=0.05):
            return jax.random.normal(k, shape, jnp.float32) * s
        return {'x': jax.random.normal(ks[0], (N_NODES, HID), jnp.float32), 'edges': jax.random.randint(ks[1], (N_EDGES, 2), 0, N_NODES), 'edge_types': jax.random.randint(ks[2], (N_EDGES,), 0, 3), 'Win': w(ks[3], (HID, HID)), 'b_in': jnp.zeros((HID,), jnp.float32), 'Wq': w(ks[4], (N_LAYERS, HID, HID)), 'bq': jnp.zeros((N_LAYERS, HID), jnp.float32), 'Wk': w(ks[5], (N_LAYERS, HID, HID)), 'bk': jnp.zeros((N_LAYERS, HID), jnp.float32), 'Wv': w(ks[6], (N_LAYERS, HID, HID)), 'bv': jnp.zeros((N_LAYERS, HID), jnp.float32), 'Eemb': w(ks[7], (N_LAYERS, 3, HID)), 'Wo': w(ks[8], (N_LAYERS, HID, HID)), 'bo': jnp.zeros((N_LAYERS, HID), jnp.float32), 'ln_g': jnp.ones((N_LAYERS, HID), jnp.float32), 'ln_b': jnp.zeros((N_LAYERS, HID), jnp.float32), 'W1': w(ks[9], (HID, HID)), 'b1': jnp.zeros((HID,), jnp.float32), 'W2': w(ks[10], (HID, HID)), 'b2': jnp.zeros((HID,), jnp.float32)}
    _L1_gnn_all = _L1_gnn_setup()
    _L1_gnn_in = {k: v for k, v in _L1_gnn_all.items() if k in ('Win', 'b_in', 'Wq', 'bq', 'Wk', 'bk', 'Wv', 'bv', 'Eemb', 'Wo', 'bo', 'ln_g', 'ln_b', 'W1', 'b1', 'W2', 'b2')}
    del _L1_gnn_all

    def _L1_mix_setup():
        import math
        import jax, jax.numpy as jnp
        import numpy as np
        EPS_DIV = 1e-07
        EPS_NORM = 1e-12

        def _l2_normalize(x, axis):
            n = jnp.sqrt(jnp.sum(x * x, axis=axis, keepdims=True))
            return x / jnp.maximum(n, EPS_NORM)
        key = jax.random.key(seed)
        ks = jax.random.split(key, 5)
        b, N, C = (8, 128, 256)
        x = jax.random.normal(ks[0], (b, N, C), dtype=jnp.float32)
        W_qkv = jax.random.normal(ks[1], (C, 3 * C), dtype=jnp.float32) * (1.0 / math.sqrt(C))
        b_qkv = jax.random.normal(ks[2], (3 * C,), dtype=jnp.float32) * 0.02
        W_out = jax.random.normal(ks[3], (C, C), dtype=jnp.float32) * (1.0 / math.sqrt(C))
        b_out = jax.random.normal(ks[4], (C,), dtype=jnp.float32) * 0.02
        return {'x': x, 'W_qkv': W_qkv, 'b_qkv': b_qkv, 'W_out': W_out, 'b_out': b_out}
    _L1_mix_all = _L1_mix_setup()
    _L1_mix_in = {k: v for k, v in _L1_mix_all.items() if k in ('W_qkv', 'b_qkv', 'W_out', 'b_out')}
    del _L1_mix_all

    def _L1_ffn_setup():
        import math
        import jax, jax.numpy as jnp
        import numpy as np
        CAPACITY_FACTOR = 1.25
        TOP_K = 2
        LN_EPS = 1e-05

        def _layer_norm(x, gamma, beta):
            mu = jnp.mean(x, axis=-1, keepdims=True)
            var = jnp.var(x, axis=-1, keepdims=True)
            return (x - mu) * jax.lax.rsqrt(var + LN_EPS) * gamma + beta
        key = jax.random.key(seed)
        ks = jax.random.split(key, 4)
        B, S, D, F, E = (8, 128, 256, 512, 8)
        x = jax.random.normal(ks[0], (B, S, D), dtype=jnp.float32)
        Wr = jax.random.normal(ks[1], (D, E), dtype=jnp.float32) / np.sqrt(D)
        br = jnp.zeros((E,), jnp.float32)
        W1 = jax.random.normal(ks[2], (E, D, F), dtype=jnp.float32) / np.sqrt(D)
        b1 = jnp.zeros((E, F), jnp.float32)
        W2 = jax.random.normal(ks[3], (E, F, D), dtype=jnp.float32) / np.sqrt(F)
        b2 = jnp.zeros((E, D), jnp.float32)
        gamma = jnp.ones((D,), jnp.float32)
        beta = jnp.zeros((D,), jnp.float32)
        return {'x': x, 'Wr': Wr, 'br': br, 'W1': W1, 'b1': b1, 'W2': W2, 'b2': b2, 'gamma': gamma, 'beta': beta}
    _L1_ffn_all = _L1_ffn_setup()
    _L1_ffn_in = {k: v for k, v in _L1_ffn_all.items() if k in ('Wr', 'br', 'W1', 'b1', 'W2', 'b2', 'gamma', 'beta')}
    del _L1_ffn_all
    return {'x': x, 'src': src, 'dst': dst, 'edge_attr_3': edge_attr_3, 'edge_type_3': edge_type_3, 'L0_gnn_W': _L0_gnn_in['W'], 'L0_gnn_a_src': _L0_gnn_in['a_src'], 'L0_gnn_a_dst': _L0_gnn_in['a_dst'], 'L0_gnn_edge_W': _L0_gnn_in['edge_W'], 'L0_gnn_edge_b': _L0_gnn_in['edge_b'], 'L0_gnn_bias': _L0_gnn_in['bias'], 'L0_mix_w_qkv': _L0_mix_in['w_qkv'], 'L0_mix_bn_gamma': _L0_mix_in['bn_gamma'], 'L0_mix_bn_beta': _L0_mix_in['bn_beta'], 'L0_mix_w_dw': _L0_mix_in['w_dw'], 'L0_mix_w_pw': _L0_mix_in['w_pw'], 'L0_mix_w_res': _L0_mix_in['w_res'], 'L0_mix_b_res': _L0_mix_in['b_res'], 'L0_ffn_router_w1': _L0_ffn_in['router_w1'], 'L0_ffn_router_b1': _L0_ffn_in['router_b1'], 'L0_ffn_router_w2': _L0_ffn_in['router_w2'], 'L0_ffn_router_b2': _L0_ffn_in['router_b2'], 'L0_ffn_expert_w1': _L0_ffn_in['expert_w1'], 'L0_ffn_expert_b1': _L0_ffn_in['expert_b1'], 'L0_ffn_expert_w2': _L0_ffn_in['expert_w2'], 'L0_ffn_expert_b2': _L0_ffn_in['expert_b2'], 'L0_ffn_expert_w3': _L0_ffn_in['expert_w3'], 'L0_ffn_expert_b3': _L0_ffn_in['expert_b3'], 'L1_gnn_Win': _L1_gnn_in['Win'], 'L1_gnn_b_in': _L1_gnn_in['b_in'], 'L1_gnn_Wq': _L1_gnn_in['Wq'], 'L1_gnn_bq': _L1_gnn_in['bq'], 'L1_gnn_Wk': _L1_gnn_in['Wk'], 'L1_gnn_bk': _L1_gnn_in['bk'], 'L1_gnn_Wv': _L1_gnn_in['Wv'], 'L1_gnn_bv': _L1_gnn_in['bv'], 'L1_gnn_Eemb': _L1_gnn_in['Eemb'], 'L1_gnn_Wo': _L1_gnn_in['Wo'], 'L1_gnn_bo': _L1_gnn_in['bo'], 'L1_gnn_ln_g': _L1_gnn_in['ln_g'], 'L1_gnn_ln_b': _L1_gnn_in['ln_b'], 'L1_gnn_W1': _L1_gnn_in['W1'], 'L1_gnn_b1': _L1_gnn_in['b1'], 'L1_gnn_W2': _L1_gnn_in['W2'], 'L1_gnn_b2': _L1_gnn_in['b2'], 'L1_mix_W_qkv': _L1_mix_in['W_qkv'], 'L1_mix_b_qkv': _L1_mix_in['b_qkv'], 'L1_mix_W_out': _L1_mix_in['W_out'], 'L1_mix_b_out': _L1_mix_in['b_out'], 'L1_ffn_Wr': _L1_ffn_in['Wr'], 'L1_ffn_br': _L1_ffn_in['br'], 'L1_ffn_W1': _L1_ffn_in['W1'], 'L1_ffn_b1': _L1_ffn_in['b1'], 'L1_ffn_W2': _L1_ffn_in['W2'], 'L1_ffn_b2': _L1_ffn_in['b2'], 'L1_ffn_gamma': _L1_ffn_in['gamma'], 'L1_ffn_beta': _L1_ffn_in['beta']}

def reference(x, src, dst, edge_attr_3, edge_type_3, L0_gnn_W, L0_gnn_a_src, L0_gnn_a_dst, L0_gnn_edge_W, L0_gnn_edge_b, L0_gnn_bias, L0_mix_w_qkv, L0_mix_bn_gamma, L0_mix_bn_beta, L0_mix_w_dw, L0_mix_w_pw, L0_mix_w_res, L0_mix_b_res, L0_ffn_router_w1, L0_ffn_router_b1, L0_ffn_router_w2, L0_ffn_router_b2, L0_ffn_expert_w1, L0_ffn_expert_b1, L0_ffn_expert_w2, L0_ffn_expert_b2, L0_ffn_expert_w3, L0_ffn_expert_b3, L1_gnn_Win, L1_gnn_b_in, L1_gnn_Wq, L1_gnn_bq, L1_gnn_Wk, L1_gnn_bk, L1_gnn_Wv, L1_gnn_bv, L1_gnn_Eemb, L1_gnn_Wo, L1_gnn_bo, L1_gnn_ln_g, L1_gnn_ln_b, L1_gnn_W1, L1_gnn_b1, L1_gnn_W2, L1_gnn_b2, L1_mix_W_qkv, L1_mix_b_qkv, L1_mix_W_out, L1_mix_b_out, L1_ffn_Wr, L1_ffn_br, L1_ffn_W1, L1_ffn_b1, L1_ffn_W2, L1_ffn_b2, L1_ffn_gamma, L1_ffn_beta):
    import jax
    import jax.numpy as jnp

    def _L0_gnn_ref(x, W, a_src, a_dst, edge_W, edge_b, bias, edge_attr, edge_index):
        import jax, jax.numpy as jnp
        import numpy as np
        N = 50000
        E = 12500
        IN = 256
        H = 8
        D = 32
        EF = 3
        n = x.shape[0]
        h = (x @ W.T).reshape(n, H, D)
        src, dst = (edge_index[0], edge_index[1])
        h_src = h[src]
        h_dst = h[dst]
        alpha = jnp.einsum('ehd,hd->eh', h_src, a_src) + jnp.einsum('ehd,hd->eh', h_dst, a_dst)
        enc = jax.nn.relu(edge_attr @ edge_W.T + edge_b).reshape(-1, H, D)
        alpha = alpha + jnp.sum(enc * h_dst, axis=-1)
        alpha = jnp.where(alpha >= 0, alpha, 0.2 * alpha)
        amax = jax.ops.segment_max(alpha, dst, num_segments=n)
        ex = jnp.exp(alpha - amax[dst])
        denom = jax.ops.segment_sum(ex, dst, num_segments=n)
        attn = ex / jnp.maximum(denom[dst], 1e-10)
        out = jax.ops.segment_sum(h_src * attn[..., None], dst, num_segments=n)
        return out.reshape(n, H * D) + bias

    def _L0_mix_ref(x, w_qkv, bn_gamma, bn_beta, w_dw, w_pw, w_res, b_res):
        import jax, jax.numpy as jnp
        import numpy as np
        C_CURV = 1.0
        MIN_NORM = 1e-15
        BALL_EPS = 1e-05
        ATT_EPS = 1e-15
        DIM = 32

        def _norm(x):
            return jnp.clip(jnp.linalg.norm(x, axis=-1, keepdims=True), MIN_NORM)

        def proj(x, c):
            maxnorm = (1.0 - BALL_EPS) / jnp.sqrt(c)
            n = _norm(x)
            return jnp.where(n > maxnorm, x / n * maxnorm, x)

        def expmap0(u, c):
            sc = jnp.sqrt(c)
            n = _norm(u)
            return jnp.tanh(sc * n) * u / (sc * n)

        def logmap0(p, c):
            sc = jnp.sqrt(c)
            n = _norm(p)
            return jnp.arctanh(jnp.clip(sc * n, -1.0 + 1e-07, 1.0 - 1e-07)) * p / (sc * n)

        def mobius_add(x, y, c):
            x2 = jnp.sum(x * x, -1, keepdims=True)
            y2 = jnp.sum(y * y, -1, keepdims=True)
            xy = jnp.sum(x * y, -1, keepdims=True)
            num = (1 + 2 * c * xy + c * y2) * x + (1 - c * x2) * y
            den = 1 + 2 * c * xy + c * c * x2 * y2
            return num / jnp.clip(den, MIN_NORM)

        def conv1d(x, w, pad, groups=1):
            return jax.lax.conv_general_dilated(x, w, (1,), [(pad, pad)], dimension_numbers=('NCH', 'OIH', 'NCH'), feature_group_count=groups)

        def batchnorm(x, gamma, beta):
            mean = jnp.mean(x, axis=(0, 2), keepdims=True)
            var = jnp.var(x, axis=(0, 2), keepdims=True)
            xn = (x - mean) * jax.lax.rsqrt(var + 1e-05)
            return gamma[None, :, None] * xn + beta[None, :, None]

        def _reference_tuple_inner(x, w_qkv, bn_gamma, bn_beta, w_dw, w_pw, w_res, b_res):
            c = C_CURV
            h = logmap0(proj(x, c), c)
            h = jnp.transpose(h, (1, 2, 0))
            h = conv1d(h, w_qkv, pad=2)
            h = batchnorm(h, bn_gamma, bn_beta)
            h = jax.nn.relu(jnp.transpose(h, (2, 0, 1)))
            qkv = proj(expmap0(h, c), c)
            t = jnp.transpose(logmap0(proj(qkv, c), c), (1, 2, 0))
            s = conv1d(t, w_dw, pad=2, groups=t.shape[1])
            s = conv1d(s, w_pw, pad=0, groups=t.shape[1] // DIM)
            cat = jnp.concatenate([t, s], axis=1)
            ai = proj(expmap0(jnp.transpose(cat, (2, 0, 1)), c), c)
            t2 = logmap0(proj(ai, c), c)
            L, N, C2 = t2.shape
            g = C2 // (3 * DIM)
            qkv3 = jnp.transpose(t2, (1, 2, 0)).reshape(N, g, 3 * DIM, L)
            q, k, v = jnp.split(qkv3, 3, axis=2)
            q = jax.nn.relu(q)
            k = jax.nn.relu(k)
            vk = jnp.einsum('ngdl,ngel->ngde', v, k)
            out = jnp.einsum('ngde,ngdl->ngdl', vk, q)
            out = out / (jnp.sum(v, -1, keepdims=True) + ATT_EPS)
            out = jnp.transpose(out.reshape(N, g * DIM, L), (2, 0, 1))
            fx_h = proj(expmap0(out, c), c)
            ft = jnp.transpose(logmap0(proj(fx_h, c), c), (1, 2, 0))
            ft = conv1d(ft, w_res, pad=0) + b_res[None, :, None]
            fx = proj(expmap0(jnp.transpose(ft, (2, 0, 1)), c), c)
            residual = mobius_add(fx, x, c)
            return (fx, residual)
        return _reference_tuple_inner(x, w_qkv, bn_gamma, bn_beta, w_dw, w_pw, w_res, b_res)[0]

    def _L0_ffn_ref(features, router_w1, router_b1, router_w2, router_b2, expert_w1, expert_b1, expert_w2, expert_b2, expert_w3, expert_b3):
        import jax, jax.numpy as jnp
        import numpy as np
        E, D, H, TOP_K = (6, 256, 256, 2)
        ROUTER_H = D // 2
        rh = jax.nn.relu(features @ router_w1 + router_b1)
        expert_logits = jax.nn.softmax(rh @ router_w2 + router_b2, axis=-1)
        top_w, top_i = jax.lax.top_k(expert_logits, TOP_K)
        routing_weights = jax.nn.softmax(top_w, axis=-1)
        h1 = jax.nn.relu(jnp.einsum('bsd,edh->bseh', features, expert_w1) + expert_b1)
        h2 = jax.nn.relu(jnp.einsum('bseh,ehf->bsef', h1, expert_w2) + expert_b2)
        expert_out = jnp.einsum('bsef,efo->bseo', h2, expert_w3) + expert_b3
        sel = jnp.take_along_axis(expert_out, top_i[:, :, :, None], axis=2)
        combined = jnp.sum(sel * routing_weights[..., None], axis=2)
        return combined

    def _L1_gnn_ref(x, edges, edge_types, Win, b_in, Wq, bq, Wk, bk, Wv, bv, Eemb, Wo, bo, ln_g, ln_b, W1, b1, W2, b2):
        import jax, jax.numpy as jnp
        import numpy as np
        H = 4
        DH = 64
        HID = 256
        EPS = 1e-05
        N_NODES = 625
        N_EDGES = 10000
        N_LAYERS = 3

        def _layer_norm(x, g, b):
            mu = jnp.mean(x, axis=-1, keepdims=True)
            var = jnp.mean((x - mu) ** 2, axis=-1, keepdims=True)
            return (x - mu) * jax.lax.rsqrt(var + EPS) * g + b

        def _message_passing(h, src, tgt, et, Wq, bq, Wk, bk, Wv, bv, Ee, Wo, bo, n_nodes):
            Q = (h @ Wq.T + bq).reshape(-1, H, DH)
            K = (h @ Wk.T + bk).reshape(-1, H, DH)
            V = (h @ Wv.T + bv).reshape(-1, H, DH)
            scores = jnp.einsum('ehd,egd->ehg', Q[src], K[tgt]) / jnp.sqrt(jnp.float32(DH))
            attn = jax.nn.softmax(scores, axis=-1)
            msg = jnp.einsum('ehg,egd->ehd', attn, V[tgt]).reshape(-1, HID)
            msg = msg + Ee[et]
            proj = msg @ Wo.T + bo
            return jax.ops.segment_sum(proj, src, num_segments=n_nodes)
        n_nodes = x.shape[0]
        src, tgt = (edges[:, 0], edges[:, 1])
        hidden = x @ Win.T + b_in
        for l in range(N_LAYERS):
            m = _message_passing(hidden, src, tgt, edge_types, Wq[l], bq[l], Wk[l], bk[l], Wv[l], bv[l], Eemb[l], Wo[l], bo[l], n_nodes)
            hidden = jax.nn.relu(_layer_norm(hidden + m, ln_g[l], ln_b[l]))
        adjustment = jax.nn.relu(hidden @ W1.T + b1) @ W2.T + b2
        return x + adjustment

    def _L1_mix_ref(x, W_qkv, b_qkv, W_out, b_out):
        import math
        import jax, jax.numpy as jnp
        import numpy as np
        EPS_DIV = 1e-07
        EPS_NORM = 1e-12

        def _l2_normalize(x, axis):
            n = jnp.sqrt(jnp.sum(x * x, axis=axis, keepdims=True))
            return x / jnp.maximum(n, EPS_NORM)
        b, N, C = x.shape
        qkv = x @ W_qkv + b_qkv
        q, k, v = jnp.split(qkv, 3, axis=2)
        q = q - jnp.mean(q, axis=2, keepdims=True)
        k = k - jnp.mean(k, axis=2, keepdims=True)
        q2 = q * q
        k2 = k * k
        q2s = jnp.sum(q2, axis=2, keepdims=True)
        k2s = jnp.sum(k2, axis=2, keepdims=True)
        k2 = _l2_normalize(k2 / (k2s + EPS_DIV), axis=-2)
        q2 = _l2_normalize(q2 / (q2s + EPS_DIV), axis=-1)
        kv = jnp.einsum('bnc,bnd->bcd', k2, v)
        t2 = jnp.einsum('bnc,bcd->bnd', q2, kv) / math.sqrt(N)
        attn = v + t2
        return attn @ W_out + b_out

    def _L1_ffn_ref(x, Wr, br, W1, b1, W2, b2, gamma, beta):
        import math
        import jax, jax.numpy as jnp
        import numpy as np
        CAPACITY_FACTOR = 1.25
        TOP_K = 2
        LN_EPS = 1e-05

        def _layer_norm(x, gamma, beta):
            mu = jnp.mean(x, axis=-1, keepdims=True)
            var = jnp.var(x, axis=-1, keepdims=True)
            return (x - mu) * jax.lax.rsqrt(var + LN_EPS) * gamma + beta
        B, S, D = x.shape
        E = Wr.shape[1]
        N = B * S
        K = TOP_K
        logits = jnp.mean(x, axis=1) @ Wr + br
        routing_weights = jax.nn.softmax(logits, axis=-1)
        capacity = float(math.ceil(N * CAPACITY_FACTOR / E))
        expected_loads = routing_weights.sum(axis=0) * (N / B)
        scale = jnp.where(expected_loads > capacity, capacity / expected_loads, 1.0)
        routing_weights = jax.nn.softmax(routing_weights * scale, axis=-1)
        rw_tok = jnp.broadcast_to(routing_weights[:, None, :], (B, S, E)).reshape(N, E)
        top_w, top_i = jax.lax.top_k(rw_tok, K)
        top_w = jax.nn.softmax(top_w, axis=-1)
        xf = x.reshape(N, D)
        h = jax.nn.gelu(jnp.einsum('nd,edf->enf', xf, W1) + b1[:, None, :], approximate=False)
        y = jnp.einsum('enf,efd->end', h, W2) + b2[:, None, :]
        w_dense = jnp.zeros((N, E), x.dtype).at[jnp.arange(N)[:, None], top_i].add(top_w)
        out = jnp.einsum('ne,end->nd', w_dense, y).reshape(B, S, D)
        out = _layer_norm(out + x, gamma, beta)
        return out
    edge_index = jnp.stack([src, dst])
    edge_index_t = jnp.stack([src, dst], axis=1)
    xn = _layernorm(x, axis=-1)
    x = x + _L0_gnn_ref(xn, L0_gnn_W, L0_gnn_a_src, L0_gnn_a_dst, L0_gnn_edge_W, L0_gnn_edge_b, L0_gnn_bias, edge_attr_3, edge_index) + _L0_mix_ref(xn[None], L0_mix_w_qkv, L0_mix_bn_gamma, L0_mix_bn_beta, L0_mix_w_dw, L0_mix_w_pw, L0_mix_w_res, L0_mix_b_res)[0]
    x = x + _L0_ffn_ref(_layernorm(x, axis=-1)[None], L0_ffn_router_w1, L0_ffn_router_b1, L0_ffn_router_w2, L0_ffn_router_b2, L0_ffn_expert_w1, L0_ffn_expert_b1, L0_ffn_expert_w2, L0_ffn_expert_b2, L0_ffn_expert_w3, L0_ffn_expert_b3)[0]
    xn = _layernorm(x, axis=-1)
    x = x + _L1_gnn_ref(xn, edge_index_t, edge_type_3, L1_gnn_Win, L1_gnn_b_in, L1_gnn_Wq, L1_gnn_bq, L1_gnn_Wk, L1_gnn_bk, L1_gnn_Wv, L1_gnn_bv, L1_gnn_Eemb, L1_gnn_Wo, L1_gnn_bo, L1_gnn_ln_g, L1_gnn_ln_b, L1_gnn_W1, L1_gnn_b1, L1_gnn_W2, L1_gnn_b2) + _L1_mix_ref(xn[None], L1_mix_W_qkv, L1_mix_b_qkv, L1_mix_W_out, L1_mix_b_out)[0]
    x = x + _L1_ffn_ref(_layernorm(x, axis=-1)[None], L1_ffn_Wr, L1_ffn_br, L1_ffn_W1, L1_ffn_b1, L1_ffn_W2, L1_ffn_b2, L1_ffn_gamma, L1_ffn_beta)[0]
    return x

_drawn_inputs = setup_inputs


def setup_inputs(seed=0):
    import zlib

    import numpy as np

    out = dict(_drawn_inputs(seed))
    spreads = {'L0_gnn_edge_b': (0.0, 0.1),
     'L0_gnn_bias': (0.0, 0.1),
     'L0_mix_bn_gamma': (1.0, 0.6),
     'L0_mix_bn_beta': (0.0, 0.403),
     'L0_mix_b_res': (0.0, 0.1),
     'L0_ffn_router_b1': (0.0, 0.1),
     'L0_ffn_router_b2': (0.0, 0.1),
     'L0_ffn_expert_b1': (0.0, 0.573),
     'L0_ffn_expert_b2': (0.0, 0.1),
     'L0_ffn_expert_b3': (0.0, 0.1),
     'L1_gnn_b_in': (0.0, 0.431),
     'L1_gnn_bq': (0.0, 0.8),
     'L1_gnn_bk': (0.0, 0.8),
     'L1_gnn_bv': (0.0, 0.287),
     'L1_gnn_bo': (0.0, 0.1),
     'L1_gnn_ln_g': (1.0, 0.2),
     'L1_gnn_ln_b': (0.0, 0.317),
     'L1_gnn_b1': (0.0, 0.377),
     'L1_gnn_b2': (0.0, 0.1),
     'L1_ffn_br': (0.0, 2.0),
     'L1_ffn_b1': (0.0, 0.643),
     'L1_ffn_b2': (0.0, 0.466),
     'L1_ffn_gamma': (1.0, 0.2),
     'L1_ffn_beta': (0.0, 0.295)}
    factors = {'L0_mix_w_dw': 4.495, 'L0_mix_w_pw': 4.084, 'L1_mix_b_out': 7.507, 'L1_gnn_Eemb': 3.588}
    for name, (base, spread) in spreads.items():
        noise = np.random.default_rng([zlib.crc32(name.encode()), seed]).standard_normal(out[name].shape)
        drawn = base * np.exp(spread * noise) if base else spread * noise
        out[name] = jnp.asarray(drawn.astype(out[name].dtype))
    for name, factor in factors.items():
        out[name] = (out[name] * factor).astype(out[name].dtype)
    return out
```

```python
import math
from contextlib import ExitStack

import numpy as np

import concourse.bass as bass
from concourse import mybir

F32 = mybir.dt.float32
BF16 = mybir.dt.bfloat16
I32 = mybir.dt.int32
ALU = mybir.AluOpType
ACT = mybir.ActivationFunctionType
AX = mybir.AxisListType.X
ds = bass.ds

P = 128
NODES = 3125
D = 256
KD = D // P
NT = 26
NPAD = NT * P
PAIRS = NT // 2
PW = 2 * P
FULL = NODES // P
REST = NODES - FULL * P
EDGES = 50000
ET = 392
U = 4
TURNS = ET // U
LASTP = EDGES // ET
LASTN = EDGES - LASTP * ET
H0, D0 = 8, 32
ROW0 = D + 2 * H0
ACC0 = H0 * (D0 + 1)
HG, DG = 4, 64
ROW1 = D + 4
TROWS = NPAD + P
NTAB = 4
LAYERS = 3
QKV = 3 * D
GRP, GD = 16, 32
EXPERTS0 = 6
EXPERTS1, F1, KF = 8, 512, 4
LOWEST = -3.0e38
EPS = 1e-5
BALL = float(np.float32(1.0 - 1e-5))
ATANH_BALL = 0.5 * math.log((1.0 + BALL) / (1.0 - BALL))
MIN_NORM = 1e-15
ATT_EPS = 1e-15


class Room:

    def __init__(self, nc, name):
        self.nc, self.name, self.ctx, self.taken = nc, name, ExitStack(), []

    def __enter__(self):
        return self

    def __exit__(self, *a):
        self.nc.clear_and_free_semaphores(self.taken)
        self.nc.all_engine_barrier()
        return self.ctx.__exit__(*a)

    def sbuf(self, name, shape, dt=F32):
        return self.ctx.enter_context(self.nc.sbuf_tensor(f"{self.name}_{name}", shape, dt))

    def psum(self, name, shape, dt=F32):
        return self.ctx.enter_context(self.nc.psum_tensor(f"{self.name}_{name}", shape, dt))

    def sem(self, name):
        self.taken.append(self.nc.alloc_semaphore(f"{self.name}_{name}"))
        return self.taken[-1]

    def sems(self, name, n):
        return [self.sem(f"{name}{i}") for i in range(n)]


class Chain:

    def __init__(self, eng, sems, turn):
        self.eng, self.sems, self.turn, self.n = eng, sems, turn, 0

    def __call__(self, ins):
        ins.then_inc(self.sems[self.n], 1)
        self.eng.wait_ge(self.sems[self.n], self.turn)
        self.n += 1


def credit(nc, sems, n=1):
    with nc.Block() as block:

        @block.sync
        def _(sp):
            for s in sems:
                sp.sem_inc(s, n)


def hold(eng, sem, value, passed):
    eng.wait_ge(sem, value)
    eng.sem_inc(passed)


def over(ap, axis, shape):
    return ap.unsqueeze(axis).to_broadcast(shape)


def weights(w):
    return w.rearrange("(k p) n -> p k n", p=P)


def to_all(v, n):
    return v.rearrange("(a n) -> a n", a=1).to_broadcast([P, n])


def rows(t, i, width=PW):
    return t[ds(i * width, width), :].rearrange("(t p) c -> p t c", p=P)


def load_inputs(nc, g, a):
    with Room(nc, "load") as r:
        idx1 = [r.sbuf(f"idx{i}", [P, ET], I32) for i in range(3)]
        tf = r.sbuf("typef", [P, ET])
        pi = r.sbuf("pidx", [P, 1], I32)
        pads, loaded = r.sem("pads_ready"), r.sem("loaded")
        steps, made, pool = r.sem("steps"), r.sem("made"), r.sem("pool")
        with nc.Block() as block:

            @block.vector
            def _(dve):
                dve.memset(g.x[:, FULL:NT, :], 0.0).then_inc(pads, 1)
                for i in range(2):
                    dve.memset(idx1[i][96:P, :], NPAD - 1).then_inc(pads, 1)
                dve.memset(idx1[2][96:P, :], 0).then_inc(pads, 1)
                dve.memset(g.ones[:, :], 1.0)
                dve.memset(g.valid[:, 0:FULL], 1.0)
                dve.memset(g.valid[:, FULL:NT], 0.0).then_inc(steps, 1)
                dve.wait_ge(steps, 1)
                dve.memset(g.valid[0:REST, FULL:FULL + 1], 1.0).then_inc(steps, 1)
                dve.wait_ge(loaded, 16 * 10)
                for i in range(2):
                    dve.tensor_copy(g.idx[:, :, i], idx1[i][:, :])
                dve.tensor_copy(tf[:, :], idx1[2][:, :]).then_inc(steps, 1)
                dve.wait_ge(steps, 3)
                for j in range(3):
                    dve.tensor_scalar(g.kinds[:, :, j], tf[:, :], float(j), None, ALU.is_equal)
                dve.memset(g.kinds[:, :, 3], 1.0).then_inc(steps, 1)
                dve.wait_ge(made, 4)
                dve.tensor_copy(g.identb[:, :], g.ident[:, :])
                dve.tensor_copy(g.spill[:, :], pi[:, :])
                dve.wait_ge(steps, 4)

            @block.gpsimd
            def _(pool_):
                pool_.memset(g.ident[:, :], 0.0).then_inc(pool, 1)
                pool_.memset(g.lower[:, :], 1.0).then_inc(pool, 1)
                pool_.wait_ge(pool, 2)
                pool_.affine_select(out=g.ident[:, :], in_=g.ident[:, :], compare_op=ALU.not_equal, fill=1.0,
                                    base=0, pattern=[[-1, P]], channel_multiplier=1).then_inc(made, 1)
                pool_.affine_select(out=g.lower[:, :], in_=g.lower[:, :], compare_op=ALU.is_gt, fill=0.0,
                                    base=0, pattern=[[-1, P]], channel_multiplier=1).then_inc(made, 1)
                pool_.iota(pi[:, :], pattern=[[0, 1]], base=NPAD, channel_multiplier=1).then_inc(made, 1)
                pool_.memset(g.picks[:, :, :], 0.0).then_inc(pool, 1)
                pool_.wait_ge(pool, 3)
                pool_.affine_select(out=g.picks[:, :, :], in_=g.picks[:, :, :], compare_op=ALU.not_equal, fill=1.0,
                                    base=0, pattern=[[-1, H0], [0, P]], channel_multiplier=1).then_inc(made, 1)

            @block.sync
            def _(sp):
                sp.dma_start(g.bn_scale[:, :], to_all(a["gamma"], QKV)).then_inc(loaded, 16)
                sp.dma_start(g.bn_beta[:, :], to_all(a["beta"], QKV)).then_inc(loaded, 16)
                sp.wait_ge(pads, 4)
                sp.dma_start(g.x[:, 0:FULL, :], a["x"][0:FULL * P, :].rearrange("(t p) c -> p t c", p=P)).then_inc(loaded, 16)
                for i, v in enumerate((a["src"], a["dst"], a["kind"])):
                    sp.dma_start(idx1[i][0:LASTP, :], v[0:LASTP * ET].rearrange("(p j) -> p j", j=ET)).then_inc(loaded, 16)
                    sp.dma_start(idx1[i][LASTP:P, 0:LASTN], v[LASTP * ET:EDGES].rearrange("(p j) -> p j", p=1)).then_inc(loaded, 16)
                sp.dma_start(g.x[0:REST, FULL, :], a["x"][FULL * P:NODES, :]).then_inc(loaded, 16)
                sp.wait_ge(loaded, 16 * 10)


def normalize(nc, g, name, squares=None):
    with Room(nc, name) as r:
        sq = r.sbuf("sq", [P, NT, D])
        st = r.sbuf("st", [P, 4, NT])
        step = r.sem("step")
        centred, squared, var, std = r.sem("centred"), r.sem("squared"), r.sem("var_ready"), r.sem("std_ready")
        with nc.Block() as block:

            @block.vector
            def _(dve):
                dve.tensor_reduce(st[:, 0, :], g.x[:, :, :], AX, ALU.add).then_inc(step, 1)
                dve.wait_ge(step, 1)
                dve.tensor_scalar(st[:, 1, :], st[:, 0, :], -1.0 / D, None, ALU.mult).then_inc(step, 1)
                dve.wait_ge(step, 2)
                dve.tensor_tensor(g.u[:, :, :], g.x[:, :, :], over(st[:, 1, :], 2, [P, NT, D]), ALU.add).then_inc(centred, 1)
                dve.wait_ge(squared, 1)
                dve.tensor_reduce(st[:, 0, :], sq[:, :, :], AX, ALU.add).then_inc(step, 1)
                dve.wait_ge(step, 3)
                dve.tensor_scalar(st[:, 2, :], st[:, 0, :], 1.0 / D, EPS, ALU.mult, ALU.add).then_inc(var, 1)
                dve.wait_ge(var, 1)
                dve.wait_ge(std, 1)
                dve.reciprocal(st[:, 2, :], st[:, 3, :]).then_inc(step, 1)
                dve.wait_ge(step, 4)
                dve.tensor_tensor(g.u[:, :, :], g.u[:, :, :], over(st[:, 2, :], 2, [P, NT, D]), ALU.mult).then_inc(step, 1)
                if squares is not None:
                    dve.tensor_tensor(st[:, 3, :], st[:, 2, :], st[:, 2, :], ALU.mult).then_inc(step, 1)
                    dve.wait_ge(step, 6)
                    dve.tensor_tensor(squares, st[:, 3, :], st[:, 0, :], ALU.mult).then_inc(step, 1)

            @block.scalar
            def _(act):
                act.wait_ge(centred, 1)
                act.activation(sq[:, :, :], g.u[:, :, :], ACT.Square).then_inc(squared, 1)
                act.wait_ge(var, 1)
                act.activation(st[:, 3, :], st[:, 2, :], ACT.Sqrt).then_inc(std, 1)


def log_scale(nc, g):
    SMALL = 0.25
    with Room(nc, "logs") as r:
        w = r.sbuf("w", [P, 10, NT])
        n, nn, z, poly, one_m, q, ln, rn, mask, tmp = (w[:, i, :] for i in range(10))
        step, rooted, ratio, logged, asked = r.sem("step"), r.sem("norm_ready"), r.sem("ratio_ready"), r.sem("log_ready"), r.sem("asked")
        with nc.Block() as block:

            @block.vector
            def _(dve):
                count = [0]

                def link(ins):
                    count[0] += 1
                    ins.then_inc(step, 1)
                    dve.wait_ge(step, count[0])

                dve.wait_ge(rooted, 1)
                link(dve.tensor_scalar(n, n, MIN_NORM, None, ALU.max))
                link(dve.tensor_scalar(nn, n, BALL, None, ALU.min))
                link(dve.tensor_scalar(one_m, nn, -1.0, 1.0, ALU.mult, ALU.add))
                link(dve.reciprocal(q, one_m))
                link(dve.tensor_scalar(tmp, nn, 1.0, None, ALU.add))
                dve.tensor_tensor(q, tmp, q, ALU.mult).then_inc(ratio, 1)
                link(dve.tensor_tensor(z, nn, nn, ALU.mult))
                link(dve.tensor_scalar(poly, z, 1.0 / 13, 1.0 / 11, ALU.mult, ALU.add))
                for c in (9, 7, 5, 3, 1):
                    link(dve.tensor_tensor(poly, poly, z, ALU.mult))
                    link(dve.tensor_scalar(poly, poly, 1.0 / c, None, ALU.add))
                link(dve.reciprocal(rn, n))
                dve.wait_ge(logged, 1)
                link(dve.scalar_tensor_tensor(out=ln, in0=ln, scalar=0.5, in1=rn, op0=ALU.mult, op1=ALU.mult))
                link(dve.tensor_scalar(mask, n, SMALL, None, ALU.is_lt))
                link(dve.tensor_tensor(tmp, poly, ln, ALU.subtract))
                link(dve.tensor_tensor(tmp, tmp, mask, ALU.mult))
                link(dve.tensor_tensor(g.g0[:, :], tmp, ln, ALU.add))

            @block.scalar
            def _(act):
                act.activation(n, g.g0[:, :], ACT.Sqrt).then_inc(rooted, 1)
                act.wait_ge(ratio, 1)
                act.activation(ln, q, ACT.Ln).then_inc(logged, 1)


def node_rows(nc, g, a):
    with Room(nc, "rows") as r:
        wnat = r.sbuf("wnat", [P, KD, D])
        ablk = r.sbuf("ablk", [P, KD, 2 * H0])
        wall = r.sbuf("wall", [P, KD, ROW0])
        un = r.sbuf("un", [P, 2, D])
        uts = r.sbuf("uts", [P, KD, PW])
        gs = r.sbuf("gs", [P, 2])
        ho = r.sbuf("ho", [P, 2, ROW0])
        pt = r.psum("pt", [P, KD, PW])
        ph = [r.psum(f"ph{i}", [P, 512]) for i in range(2)]
        pu = r.psum("pu", [P, 512])
        pa = r.psum("pa", [P, 512])
        loaded, folded, wready = r.sem("loaded"), r.sem("folded"), r.sem("wall_ready")
        copied, turned, ut_kept, uts_ready = r.sem("pair_copied"), r.sem("pair_turned"), r.sem("ut_kept"), r.sem("uts_ready")
        summed, added, projected = r.sem("summed"), r.sem("sum_added"), r.sem("projected")
        ho_ready, stored, ho_sent, passed = r.sem("ho_ready"), r.sem("stored"), r.sem("ho_sent"), r.sem("passed")
        credit(nc, [copied, turned, ut_kept, uts_ready, summed, added, projected, ho_ready, ho_sent])
        with nc.Block() as block:

            @block.sync
            def _(sp):
                sp.dma_start(wnat[:, :, :], weights(a["gW"])).then_inc(loaded, 16)
                sp.dma_start(ablk[:, :, :], weights(a["ablk"])).then_inc(loaded, 16)
                sp.dma_start(wall[:, :, 0:D], weights(a["gWT"])).then_inc(loaded, 16)
                with sp.Fori(0, PAIRS) as i:
                    hold(sp, ho_ready, i + 2, passed)
                    sp.dma_start(rows(g.table0, i), ho[:, :, :]).then_inc(stored, 16)
                    hold(sp, stored, i * 16 + 16, ho_sent)

            @block.tensor
            def _(pe):
                pe.wait_ge(loaded, 48)
                for c in range(KD):
                    for k in range(KD):
                        mm = pe.matmul(pa[:, c * 16:c * 16 + 16], wnat[:, k, c * P:(c + 1) * P], ablk[:, k, :],
                                       start=(k == 0), stop=(k == KD - 1))
                mm.then_inc(folded, 1)
                pe.wait_ge(wready, 1)
                with pe.Fori(0, PAIRS) as i:
                    before, now = i + 1, i + 2
                    pe.wait_ge(copied, now)
                    pe.wait_ge(uts_ready, before)
                    for t in range(2):
                        for k in range(KD):
                            mm = pe.transpose(pt[:, k, t * P:(t + 1) * P], un[:, t, k * P:(k + 1) * P], g.ident[:, :])
                    mm.then_inc(turned, 1)
                    pe.wait_ge(added, before)
                    for k in range(KD):
                        for t in range(2):
                            mm = pe.matmul(pu[:, k:k + 1], un[:, t, k * P:(k + 1) * P], gs[:, t:t + 1],
                                           start=(t == 0), stop=(t == 1))
                    mm.then_inc(summed, 1)
                    pe.wait_ge(uts_ready, now)
                    pe.wait_ge(ho_ready, before)
                    for t in range(2):
                        for k in range(KD):
                            mm = pe.matmul(ph[t][:, 0:ROW0], uts[:, k, t * P:(t + 1) * P], wall[:, k, :],
                                           start=(k == 0), stop=(k == KD - 1))
                    mm.then_inc(projected, 1)

            @block.scalar
            def _(act):
                with act.Fori(0, PAIRS) as i:
                    before, now = i + 1, i + 2
                    act.wait_ge(summed, before)
                    act.activation(un[:, :, :], g.u[:, ds(i * 2, 2), :], ACT.Copy)
                    act.activation(gs[:, :], g.g0[:, ds(i * 2, 2)], ACT.Copy).then_inc(copied, 1)
                    act.wait_ge(uts_ready, now)
                    act.activation(g.ut[:, :, ds(i * PW, PW)], uts[:, :, :], ACT.Copy).then_inc(ut_kept, 1)

            @block.vector
            def _(dve):
                dve.memset(g.usum[:, :], 0.0)
                dve.wait_ge(folded, 1)
                dve.tensor_copy(wall[:, :, D:ROW0], pa[:, 0:KD * 16].rearrange("p (k n) -> p k n", k=KD)).then_inc(wready, 1)
                dve.wait_ge(wready, 1)
                with dve.Fori(0, PAIRS) as i:
                    before, now = i + 1, i + 2
                    dve.wait_ge(turned, now)
                    dve.wait_ge(projected, before)
                    dve.wait_ge(ut_kept, before)
                    dve.tensor_copy(uts[:, :, :], pt[:, :, :]).then_inc(uts_ready, 1)
                    dve.wait_ge(summed, now)
                    dve.tensor_tensor(g.usum[:, :], g.usum[:, :], pu[:, 0:KD], ALU.add).then_inc(added, 1)
                    dve.wait_ge(projected, now)
                    dve.wait_ge(ho_sent, before)
                    dve.tensor_copy(ho[:, 0, :], ph[0][:, 0:ROW0])
                    dve.tensor_copy(ho[:, 1, :], ph[1][:, 0:ROW0]).then_inc(ho_ready, 1)


HALF = QKV // 2
KQ = QKV // P


def mix_stats(nc, g, a):
    with Room(nc, "ms") as r:
        w = r.sbuf("w", [P, KD, QKV])
        umean = r.sbuf("umean", [P, KD, P])
        mean = r.sbuf("mean", [P, QKV])
        uts = r.sbuf("uts", [P, KD, PW])
        hc = r.sbuf("hc", [P, 2, QKV])
        sq = r.sbuf("sq", [P, 2, QKV])
        ssum = r.sbuf("ssum", [P, QKV])
        ph = [r.psum(f"ph{i}", [P, 512]) for i in range(4)]
        ps = [r.psum(f"ps{i}", [P, 512]) for i in range(2)]
        loaded, step, msent, mready = r.sem("loaded"), r.sem("step"), r.sem("mean_sent"), r.sem("mean_ready")
        um, std, var = r.sem("umean_ready"), r.sem("std_ready"), r.sem("var_ready")
        copied, projected, hc_ready, squared = r.sem("copied"), r.sem("projected"), r.sem("hc_ready"), r.sem("squared")
        summed, added, stored, hc_sent, passed = r.sem("summed"), r.sem("added"), r.sem("stored"), r.sem("hc_sent"), r.sem("passed")
        credit(nc, [copied, projected, hc_ready, squared, summed, added, hc_sent])
        with nc.Block() as block:

            @block.sync
            def _(sp):
                sp.dma_start(w[:, :, :], weights(a["wqkv"])).then_inc(loaded, 16)
                with sp.Fori(0, PAIRS) as i:
                    hold(sp, hc_ready, i + 2, passed)
                    sp.dma_start(rows(g.hc, i), hc[:, :, :]).then_inc(stored, 16)
                    hold(sp, stored, i * 16 + 16, hc_sent)

            @block.scalar
            def _(act):
                with act.Fori(0, PAIRS) as i:
                    before, now = i + 1, i + 2
                    act.wait_ge(projected, before)
                    act.activation(uts[:, :, :], g.ut[:, :, ds(i * PW, PW)], ACT.Copy).then_inc(copied, 1)
                    act.wait_ge(hc_ready, now)
                    act.wait_ge(summed, before)
                    act.activation(sq[:, 0, :], hc[:, 0, :], ACT.Square, scale=g.valid[:, ds(i * 2, 1)])
                    act.activation(sq[:, 1, :], hc[:, 1, :], ACT.Square, scale=g.valid[:, ds(i * 2 + 1, 1)]).then_inc(squared, 1)
                act.wait_ge(var, 1)
                act.activation(ssum[:, :], ssum[:, :], ACT.Sqrt).then_inc(std, 1)

            @block.tensor
            def _(pe):
                pe.wait_ge(loaded, 16)
                pe.wait_ge(um, 1)
                for h in range(2):
                    for k in range(KD):
                        mm = pe.matmul(ps[h][:, 0:HALF], umean[:, k, :], w[:, k, h * HALF:(h + 1) * HALF],
                                       start=(k == 0), stop=(k == KD - 1))
                mm.then_inc(msent, 1)
                pe.wait_ge(mready, 1)
                with pe.Fori(0, PAIRS) as i:
                    before, now = i + 1, i + 2
                    pe.wait_ge(copied, now)
                    pe.wait_ge(hc_ready, before)
                    for t in range(2):
                        for h in range(2):
                            for k in range(KD):
                                mm = pe.matmul(ph[2 * t + h][:, 0:HALF], uts[:, k, t * P:(t + 1) * P],
                                               w[:, k, h * HALF:(h + 1) * HALF], start=(k == 0), stop=(k == KD - 1))
                    mm.then_inc(projected, 1)
                    pe.wait_ge(squared, now)
                    pe.wait_ge(added, before)
                    for h in range(2):
                        for t in range(2):
                            mm = pe.matmul(ps[h][:, 0:HALF], g.ones[:, :], sq[:, t, h * HALF:(h + 1) * HALF],
                                           start=(t == 0), stop=(t == 1))
                    mm.then_inc(summed, 1)

            @block.vector
            def _(dve):
                dve.tensor_scalar(umean[:, :, :], over(g.usum[:, :], 2, [P, KD, P]), 1.0 / NODES, None, ALU.mult).then_inc(um, 1)
                dve.memset(ssum[:, :], 0.0)
                dve.wait_ge(msent, 1)
                for h in range(2):
                    ins = dve.tensor_copy(mean[:, h * HALF:(h + 1) * HALF], ps[h][:, 0:HALF])
                ins.then_inc(mready, 1)
                dve.wait_ge(mready, 1)
                with dve.Fori(0, PAIRS) as i:
                    before, now = i + 1, i + 2
                    dve.wait_ge(projected, now)
                    dve.wait_ge(hc_sent, before)
                    dve.wait_ge(squared, before)
                    for t in range(2):
                        for h in range(2):
                            c = slice(h * HALF, (h + 1) * HALF)
                            ins = dve.scalar_tensor_tensor(out=hc[:, t, c], in0=ph[2 * t + h][:, 0:HALF],
                                                           scalar=g.g0[:, ds(i * 2 + t, 1)], in1=mean[:, c],
                                                           op0=ALU.mult, op1=ALU.subtract)
                    ins.then_inc(hc_ready, 1)
                    dve.wait_ge(summed, now)
                    for h in range(2):
                        c = slice(h * HALF, (h + 1) * HALF)
                        ins = dve.tensor_tensor(ssum[:, c], ssum[:, c], ps[h][:, 0:HALF], ALU.add)
                    ins.then_inc(added, 1)
                hold(dve, added, PAIRS + 1, passed)
                dve.tensor_scalar(ssum[:, :], ssum[:, :], 1.0 / NODES, EPS, ALU.mult, ALU.add).then_inc(var, 1)
                dve.wait_ge(std, 1)
                dve.reciprocal(ssum[:, :], ssum[:, :]).then_inc(step, 1)
                dve.wait_ge(step, 1)
                dve.tensor_tensor(g.bn_scale[:, :], g.bn_scale[:, :], ssum[:, :], ALU.mult).then_inc(step, 1)


def mix(nc, g, a):
    with Room(nc, "mx") as r:
        bd = r.sbuf("bd", [P, KQ, P])
        wdw = r.sbuf("wdw", [P, KQ])
        wres = r.sbuf("wres", [P, 4, D])
        bres = r.sbuf("bres", [P, D])
        rr = r.sbuf("r", [P, 2, QKV])
        rt = r.sbuf("rt", [P, KQ, PW])
        s = r.sbuf("s", [P, 2, QKV])
        junk = r.sbuf("junk", [P, 2, QKV])
        sm = r.sbuf("sm", [P, 12, 2])
        ks = r.sbuf("ks", [P, 2, GRP])
        v = r.sbuf("v", [P, 2, GRP, GD])
        ve = r.sbuf("ve", [P, 2, GRP, GD])
        o = r.sbuf("o", [P, 2, GRP, GD])
        ot = r.sbuf("ot", [P, 4, PW])
        ft = r.sbuf("ft", [P, 2, D])
        prt = [r.psum(f"prt{i}", [P, 2, PW]) for i in range(3)]
        pss = [[r.psum(f"ps{t}{h}", [P, 512]) for h in range(2)] for t in range(2)]
        pf = r.psum("pf", [P, 2, D])
        nr, ns, c1, nc_, kap, no, c2, nf, th, tmp, tmp2, ncat = (sm[:, j, :] for j in range(12))
        loaded, scaled = r.sem("loaded"), r.sem("scaled")
        ld, r_ready, turned, rt_ready, mixed = r.sem("ld"), r.sem("r_ready"), r.sem("turned"), r.sem("rt_ready"), r.sem("mixed")
        s_ready, sqd, rooted, so_ready, norm_o, o_ready = r.sem("s_ready"), r.sem("sums_ready"), r.sem("roots_ready"), r.sem("cat_ready"), r.sem("o_norm_ready"), r.sem("o_ready")
        oturned, ot_ready, fin, ft_ready, tanhed, asked, passed = r.sem("o_turned"), r.sem("ot_ready"), r.sem("final"), r.sem("ft_ready"), r.sem("tanh_ready"), r.sem("root_asked"), r.sem("passed")
        cat_rooted, o_rooted, f_rooted, o_asked, xdone = r.sem("cat_rooted"), r.sem("o_rooted"), r.sem("f_rooted"), r.sem("o_asked"), r.sem("x_done")
        chain = r.sems("step", 40)
        credit(nc, [r_ready, turned, rt_ready, mixed, s_ready, sqd, so_ready, norm_o, o_ready, oturned, ot_ready,
                    fin, ft_ready, tanhed, asked, cat_rooted, o_rooted, f_rooted, o_asked, xdone])
        with nc.Block() as block:

            @block.sync
            def _(sp):
                sp.dma_start(bd[:, :, :], weights(a["pw"])).then_inc(loaded, 16)
                sp.dma_start(wdw[:, :], a["wdw"]).then_inc(loaded, 16)
                sp.dma_start(wres[:, :, :], weights(a["wres"])).then_inc(loaded, 16)
                sp.dma_start(bres[:, :], to_all(a["bres"], D)).then_inc(loaded, 16)
                with sp.Fori(0, PAIRS) as i:
                    hold(sp, xdone, i + 1, passed)
                    sp.dma_start(rr[:, :, :], rows(g.hc, i)).then_inc(ld, 16)

            @block.tensor
            def _(pe):
                pe.wait_ge(scaled, 1)
                with pe.Fori(0, PAIRS) as i:
                    before, now = i + 1, i + 2
                    pe.wait_ge(r_ready, now)
                    for k in range(KQ):
                        for t in range(2):
                            mm = pe.transpose(prt[k // 2][:, k % 2, t * P:(t + 1) * P], rr[:, t, k * P:(k + 1) * P], g.ident[:, :])
                    mm.then_inc(turned, 1)
                    pe.wait_ge(rt_ready, now)
                    for t in range(2):
                        for k in range(KQ):
                            mm = pe.matmul(pss[t][k // 4][:, (k % 4) * P:(k % 4 + 1) * P], rt[:, k, t * P:(t + 1) * P], bd[:, k, :],
                                           start=True, stop=True)
                    mm.then_inc(mixed, 1)
                    pe.wait_ge(o_ready, now)
                    for k in range(4):
                        for t in range(2):
                            mm = pe.transpose(prt[k // 2][:, k % 2, t * P:(t + 1) * P],
                                              o[:, t, 4 * k:4 * k + 4, :].rearrange("p a b -> p (a b)"), g.ident[:, :])
                    mm.then_inc(oturned, 1)
                    pe.wait_ge(ot_ready, now)
                    for t in range(2):
                        for k in range(4):
                            mm = pe.matmul(pf[:, t, :], ot[:, k, t * P:(t + 1) * P], wres[:, k, :], start=(k == 0), stop=(k == 3))
                    mm.then_inc(fin, 1)

            @block.scalar
            def _(act):
                with act.Fori(0, PAIRS) as i:
                    before, now = i + 1, i + 2
                    act.wait_ge(turned, now)
                    for j in range(3):
                        ins = act.activation(rt[:, 2 * j:2 * j + 2, :], prt[j][:, :, :], ACT.Copy)
                    ins.then_inc(rt_ready, 1)
                    for t in range(2):
                        act.activation(junk[:, t, :], rr[:, t, :], ACT.Square, accum_out=nr[:, t:t + 1])
                    act.wait_ge(mixed, now)
                    for t in range(2):
                        act.activation(s[:, t, 0:512], pss[t][0][:, :], ACT.Copy)
                        ins = act.activation(s[:, t, 512:QKV], pss[t][1][:, 0:QKV - 512], ACT.Copy)
                    ins.then_inc(s_ready, 1)
                    act.wait_ge(s_ready, now)
                    for t in range(2):
                        ins = act.activation(junk[:, t, :], s[:, t, :], ACT.Square, accum_out=ns[:, t:t + 1])
                    ins.then_inc(sqd, 1)
                    act.wait_ge(asked, now)
                    act.activation(nr, nr, ACT.Sqrt)
                    act.activation(ncat, ncat, ACT.Sqrt).then_inc(cat_rooted, 1)
                    act.wait_ge(so_ready, now)
                    for t in range(2):
                        ins = act.activation(junk[:, t, 0:512], o[:, t, :, :].rearrange("p a b -> p (a b)"), ACT.Square,
                                             accum_out=no[:, t:t + 1])
                    ins.then_inc(norm_o, 1)
                    act.wait_ge(norm_o, now)
                    act.activation(no, no, ACT.Sqrt).then_inc(o_rooted, 1)
                    act.wait_ge(oturned, now)
                    for j in range(2):
                        ins = act.activation(ot[:, 2 * j:2 * j + 2, :], prt[j][:, :, :], ACT.Copy)
                    ins.then_inc(ot_ready, 1)
                    act.wait_ge(ft_ready, now)
                    for t in range(2):
                        ins = act.activation(junk[:, t, 0:D], ft[:, t, :], ACT.Square, accum_out=nf[:, t:t + 1])
                    ins.then_inc(o_asked, 1)
                    act.wait_ge(o_asked, now)
                    act.activation(nf, nf, ACT.Sqrt).then_inc(f_rooted, 1)
                    act.wait_ge(f_rooted, now)
                    act.activation(th, nf, ACT.Tanh).then_inc(tanhed, 1)

            @block.vector
            def _(dve):
                dve.wait_ge(loaded, 64)
                dve.tensor_tensor(bd[:, :, :], bd[:, :, :], over(wdw[:, :], 2, [P, KQ, P]), ALU.mult).then_inc(scaled, 1)
                with dve.Fori(0, PAIRS) as i:
                    before, now = i + 1, i + 2
                    link = Chain(dve, chain, i + 1)
                    dve.wait_ge(ld, i * 16 + 16)
                    link(dve.tensor_tensor(rr[:, :, :], rr[:, :, :], over(g.bn_scale[:, :], 1, [P, 2, QKV]), ALU.mult))
                    link(dve.tensor_tensor(rr[:, :, :], rr[:, :, :], over(g.bn_beta[:, :], 1, [P, 2, QKV]), ALU.add))
                    dve.tensor_scalar(rr[:, :, :], rr[:, :, :], 0.0, None, ALU.max).then_inc(r_ready, 1)
                    dve.wait_ge(sqd, now)
                    dve.tensor_tensor(ncat, nr, ns, ALU.add).then_inc(asked, 1)
                    dve.wait_ge(cat_rooted, now)
                    link(dve.tensor_scalar(tmp, nr, MIN_NORM, None, ALU.max))
                    link(dve.reciprocal(tmp, tmp))
                    link(dve.scalar_tensor_tensor(out=c1, in0=nr, scalar=ATANH_BALL, in1=tmp, op0=ALU.min, op1=ALU.mult))
                    link(dve.tensor_tensor(nc_, c1, ncat, ALU.mult))
                    link(dve.tensor_scalar(tmp, nc_, MIN_NORM, None, ALU.max))
                    link(dve.reciprocal(tmp, tmp))
                    link(dve.scalar_tensor_tensor(out=tmp, in0=nc_, scalar=ATANH_BALL, in1=tmp, op0=ALU.min, op1=ALU.mult))
                    link(dve.tensor_tensor(kap, tmp, c1, ALU.mult))
                    parts = []
                    for t in range(2):
                        parts.append((t, 0, rr[:, t, :].rearrange("p (a b) -> p a b", b=3 * GD)))
                        parts.append((t, GRP // 2, s[:, t, :].rearrange("p (a b) -> p a b", b=3 * GD)))
                    for t in range(2):
                        ins = dve.tensor_scalar(parts[2 * t + 1][2][:, :, 0:2 * GD], parts[2 * t + 1][2][:, :, 0:2 * GD], 0.0, None, ALU.max)
                    link(ins)
                    for t, at, part in parts:
                        dve.tensor_reduce(ks[:, t, at:at + 8], part[:, :, GD:2 * GD], AX, ALU.add)
                        ins = dve.tensor_scalar(v[:, t, at:at + 8, :], part[:, :, 2 * GD:3 * GD], kap[:, t:t + 1], None, ALU.mult)
                    link(ins)
                    link(dve.tensor_scalar(ve[:, :, :, :], v[:, :, :, :], ATT_EPS, None, ALU.add))
                    link(dve.reciprocal(ve[:, :, :, :], ve[:, :, :, :]))
                    link(dve.tensor_tensor(v[:, :, :, :], v[:, :, :, :], ve[:, :, :, :], ALU.mult))
                    for t, at, part in parts:
                        ins = dve.tensor_tensor(o[:, t, at:at + 8, :], part[:, :, 0:GD], over(ks[:, t, at:at + 8], 2, [P, 8, GD]), ALU.mult)
                    link(ins)
                    for t in range(2):
                        ins = dve.scalar_tensor_tensor(out=o[:, t, :, :], in0=v[:, t, :, :], scalar=kap[:, t:t + 1], in1=o[:, t, :, :],
                                                       op0=ALU.mult, op1=ALU.mult)
                    link(ins)
                    for t in range(2):
                        ins = dve.tensor_scalar(o[:, t, :, :], o[:, t, :, :], kap[:, t:t + 1], None, ALU.mult)
                    link(ins)
                    dve.sem_inc(o_ready)
                    dve.sem_inc(so_ready)
                    dve.wait_ge(o_rooted, now)
                    link(dve.tensor_scalar(tmp, no, MIN_NORM, None, ALU.max))
                    link(dve.reciprocal(tmp, tmp))
                    link(dve.scalar_tensor_tensor(out=c2, in0=no, scalar=ATANH_BALL, in1=tmp, op0=ALU.min, op1=ALU.mult))
                    dve.wait_ge(fin, now)
                    for t in range(2):
                        ins = dve.scalar_tensor_tensor(out=ft[:, t, :], in0=pf[:, t, :], scalar=c2[:, t:t + 1], in1=bres[:, :],
                                                       op0=ALU.mult, op1=ALU.add)
                    ins.then_inc(ft_ready, 1)
                    dve.wait_ge(tanhed, now)
                    link(dve.tensor_scalar(tmp, nf, MIN_NORM, None, ALU.max))
                    link(dve.reciprocal(tmp, tmp))
                    link(dve.scalar_tensor_tensor(out=tmp2, in0=th, scalar=BALL, in1=tmp, op0=ALU.min, op1=ALU.mult))
                    for t in range(2):
                        ins = dve.scalar_tensor_tensor(out=g.x[:, ds(i * 2 + t, 1), :].rearrange("p a b -> p (a b)"), in0=ft[:, t, :], scalar=tmp2[:, t:t + 1],
                                                       in1=g.x[:, ds(i * 2 + t, 1), :].rearrange("p a b -> p (a b)"), op0=ALU.mult, op1=ALU.add)
                    ins.then_inc(xdone, 1)
def spill_duplicates(nc, g):
    with Room(nc, "dup") as r:
        key = r.sbuf("key", [P, U, 2])
        same = r.sbuf("same", [P, 2, U, P])
        junk = r.sbuf("junk", [P, 2, U, P])
        rank = r.sbuf("rank", [P, U, 2])
        ranks = r.sbuf("ranks", [P, ET, 2])
        keys = r.sbuf("keys", [P, ET, 2])
        pk = [r.psum(f"pk{j}", [P, U, P]) for j in range(2)]
        keyed, spread, matched, counted, kept, step = (r.sem(n) for n in ("keyed", "spread", "matched", "counted", "kept", "step"))
        credit(nc, [keyed, spread, matched, counted, kept])
        with nc.Block() as block:

            @block.tensor
            def _(pe):
                with pe.Fori(0, TURNS) as i:
                    pe.wait_ge(keyed, i + 2)
                    for j in range(2):
                        for b in range(U):
                            mm = pe.transpose(pk[j][:, b, :], key[:, b, j:j + 1].to_broadcast([P, P]), g.ident[:, :])
                    mm.then_inc(spread, 1)

            @block.vector
            def _(dve):
                with dve.Fori(0, TURNS) as i:
                    now = i + 2
                    dve.wait_ge(kept, i + 1)
                    dve.tensor_copy(key[:, :, :], g.idx[:, ds(i * U, U), 0:2]).then_inc(keyed, 1)
                    dve.wait_ge(spread, now)
                    for j in range(2):
                        ins = dve.tensor_tensor(same[:, j, :, :], pk[j][:, :, :], key[:, :, j:j + 1].to_broadcast([P, U, P]), ALU.is_equal)
                    ins.then_inc(matched, 1)
                    dve.wait_ge(matched, now)
                    for j in range(2):
                        for b in range(U):
                            ins = dve.tensor_tensor_reduce(junk[:, j, b, :], same[:, j, b, :], g.lower[:, :], 1.0, 0.0, ALU.mult, ALU.add,
                                                           rank[:, b, j:j + 1])
                    ins.then_inc(counted, 1)
                    dve.wait_ge(counted, now)
                    dve.tensor_copy(ranks[:, ds(i * U, U), :], rank[:, :, :]).then_inc(kept, 1)
                dve.tensor_copy(keys[:, :, :], g.idx[:, :, 0:2]).then_inc(step, 1)
                dve.wait_ge(kept, TURNS + 1)
                dve.tensor_scalar(ranks[:, :, :], ranks[:, :, :], 1.0, None, ALU.min).then_inc(step, 1)
                dve.wait_ge(step, 2)

                dve.tensor_scalar(g.rowf[:, :, :], keys[:, :, :], -1.0, g.spill[:, :], ALU.mult, ALU.add).then_inc(step, 1)
                dve.wait_ge(step, 3)
                dve.tensor_tensor(g.rowf[:, :, :], g.rowf[:, :, :], ranks[:, :, :], ALU.mult).then_inc(step, 1)
                dve.wait_ge(step, 4)
                dve.tensor_tensor(g.rowf[:, :, :], g.rowf[:, :, :], keys[:, :, :], ALU.add).then_inc(step, 1)
                dve.wait_ge(step, 5)
                dve.tensor_copy(g.idx[:, :, 2:4], g.rowf[:, :, :]).then_inc(step, 1)


class Edge:

    def __init__(self, r, marks, dmas):
        self.marks = {m: r.sem(m) for m in marks}
        self.dmas = {d: r.sems(d, U) for d in dmas}

    def credit(self, nc):
        credit(nc, list(self.marks.values()), U)

    def done(self, eng, name, t, lag=0, passed=None):
        eng.wait_ge(self.marks[name], t + (1 + U - lag))
        if passed is not None:
            eng.sem_inc(passed)


def steps_of(eng, body, tiles, first, last, turn0=None):
    lead = -(-first // U) * U
    for t in range(-first, lead):
        body(t, t // U, t % U)
    end = (tiles - lead) // U * U
    tail = -(-max(first, last) // U) * U
    with eng.Fori(lead // U, (tiles - tail) // U) as i:
        for b in range(U):
            body(i * U + b, i, b)
    for t in range(tiles - tail, tiles + last):
        body(t, t // U, t % U)


def exists(t, k, tiles=ET):
    return not isinstance(t, int) or 0 <= t + k < tiles


def attend0(nc, g, a):
    A = H0 * (D0 + 1)
    with Room(nc, "ga") as r:
        ixa = r.sbuf("ixa", [P, U, 4], I32)
        ixb = r.sbuf("ixb", [P, U, 4], I32)
        attr = r.sbuf("attr", [4, U, P])
        ew = r.sbuf("ew", [4, D])
        srow = r.sbuf("srow", [P, U, ROW0])
        drow = r.sbuf("drow", [P, U, ROW0])
        old = r.sbuf("old", [P, U, A + H0])
        new = r.sbuf("new", [P, U, A + H0])
        key = r.sbuf("key", [P, U, 1])
        same = r.sbuf("same", [P, U, P])
        pen = r.sbuf("pen", [P, U, P], BF16)
        we = r.sbuf("we", [P, U, D])
        z = r.sbuf("z", [P, U, H0])
        alpha = r.sbuf("alpha", [P, U, H0])
        at = r.sbuf("at", [P, U, P])
        mloc = r.sbuf("mloc", [P, U, H0])
        diff = r.sbuf("diff", [P, U, 2, H0])
        prod = r.sbuf("prod", [P, U, H0, D0 + 1])
        fade = r.sbuf("fade", [P, U, H0])
        blank = r.sbuf("blank", [P, A + H0])
        pkey = [r.psum(f"pkey{j}", [P, P]) for j in range(2)]
        penc = [r.psum(f"penc{j}", [P, D]) for j in range(2)]
        pat = r.psum("pat", [H0, P])
        pm = [r.psum(f"pm{j}", [P, 4, P]) for j in range(2)]
        psum = r.psum("psum", [P, A])
        e = Edge(r, ["keyed", "spread", "matched", "encoded", "weighed", "z1", "z2", "z3", "scored", "penned", "turned", "at_ready",
                     "masked", "mloc", "mnew", "differed", "exped", "faded", "multiplied", "summed", "old_faded", "new_ready"],
                 ["ixa", "ixb", "attr", "srow", "drow", "old", "new"])
        ready, blanked, inited, loaded, ones_set = r.sem("ready"), r.sem("blanked"), r.sem("inited"), r.sem("loaded"), r.sem("ones_set")
        passed, passed_sp = r.sem("passed"), r.sem("passed_sp")
        e.credit(nc)
        with nc.Block() as block:

            @block.vector
            def _(dve):
                dve.memset(blank[:, 0:A], 0.0)
                dve.memset(blank[:, A:A + H0], LOWEST).then_inc(blanked, 1)
                dve.memset(attr[:, :, :], 1.0)
                dve.memset(at[:, :, :], 0.0).then_inc(ones_set, 1)

            @block.sync
            def _(sp):
                sp.dma_start(ew[0:3, :], a["eWT"]).then_inc(loaded, 16)
                sp.dma_start(ew[3:4, :], a["eb"].rearrange("(a n) -> a n", a=1)).then_inc(loaded, 16)
                sp.wait_ge(blanked, 1)
                for t in g.tabs0:
                    sp.dma_start(t.rearrange("(t p) c -> p t c", p=P), over(blank[:, 0:A + H0], 1, [P, TROWS // P, A + H0])).then_inc(inited, 16)
                sp.wait_ge(inited, 16 * NTAB)
                sp.wait_ge(loaded, 32)
        with nc.Block() as block:

            @block.sync
            def _(sp):
                def step(t, i, b):
                    if exists(t, 3):
                        c = (b + 3) % U
                        if not (isinstance(t, int) and t < 1):
                            j = i if b == 0 else i + 1
                            hold(sp, e.dmas["old"][c], j * 16, passed_sp)
                            e.done(sp, "keyed", t, 1, passed_sp)
                            e.done(sp, "encoded", t, 1, passed_sp)
                        sp.dma_start(ixa[:, c, :], g.idx[:, t + 3, :] if isinstance(t, int) else g.idx[:, ds(t + 3, 1), :].rearrange("p a b -> p (a b)")).then_inc(e.dmas["ixa"][c], 16)
                        sp.dma_start(attr[0:3, c, :], a["ea"][:, t + 3, :] if isinstance(t, int) else a["ea"][:, ds(t + 3, 1), :].rearrange("p a b -> p (a b)")).then_inc(e.dmas["attr"][c], 16)
                    if exists(t, 0):
                        if not (isinstance(t, int) and t < U):
                            hold(sp, e.dmas["new"][b], i * 16, passed_sp)
                        sp.dma_start(ixb[:, b, :], g.idx[:, t, :] if isinstance(t, int) else g.idx[:, ds(t, 1), :].rearrange("p a b -> p (a b)")).then_inc(e.dmas["ixb"][b], 16)

                steps_of(sp, step, ET, 3, 0)

            @block.gpsimd
            def _(pool):
                def step(t, i, b):
                    if exists(t, -2):
                        c = (b - 2) % U
                        j = i + 1 if b >= 2 else i
                        pool.wait_ge(e.dmas["ixb"][c], j * 16)
                        e.done(pool, "new_ready", t, 2)
                        pool.sem_inc(passed)
                        pool.indirect_dma_start(out=g.tabs0[c][:, :], out_offset=bass.IndirectOffsetOnAxis(ap=ixb[:, c, 3:4], axis=0),
                                                in_=new[:, c, :], in_offset=None).then_inc(e.dmas["new"][c], 16)
                    if exists(t, 1):
                        c = (b + 1) % U
                        j = i + 1 if b == U - 1 else i
                        if not (isinstance(t, int) and t + 1 < U):
                            pool.wait_ge(e.dmas["new"][c], j * 16)
                            e.done(pool, "old_faded", t + 1, U)
                        pool.wait_ge(e.dmas["ixa"][c], (j + 1) * 16)
                        pool.sem_inc(passed)
                        pool.indirect_dma_start(out=old[:, c, :], out_offset=None, in_=g.tabs0[c][:, :],
                                                in_offset=bass.IndirectOffsetOnAxis(ap=ixa[:, c, 1:2], axis=0)).then_inc(e.dmas["old"][c], 16)
                    if exists(t, 2):
                        c = (b + 2) % U
                        j = i + 2 if b >= 2 else i + 1
                        pool.wait_ge(e.dmas["ixa"][c], j * 16)
                        if not (isinstance(t, int) and t + 2 < U):
                            e.done(pool, "multiplied", t + 2, U)
                            e.done(pool, "z2", t + 2, U)
                        pool.sem_inc(passed)
                        pool.indirect_dma_start(out=drow[:, c, :], out_offset=None, in_=g.table0[:, :],
                                                in_offset=bass.IndirectOffsetOnAxis(ap=ixa[:, c, 1:2], axis=0)).then_inc(e.dmas["drow"][c], 16)
                        pool.indirect_dma_start(out=srow[:, c, :], out_offset=None, in_=g.table0[:, :],
                                                in_offset=bass.IndirectOffsetOnAxis(ap=ixa[:, c, 0:1], axis=0)).then_inc(e.dmas["srow"][c], 16)

                steps_of(pool, step, ET, 2, 2)
                for c in range(U):
                    hold(pool, e.dmas["new"][c], 16 * TURNS, passed)

            @block.tensor
            def _(pe):
                def turn_alpha(t, b):
                    e.done(pe, "scored", t)
                    e.done(pe, "at_ready", t, 1)
                    pe.transpose(pat[:, :], alpha[:, b, :], g.ident[:, :]).then_inc(e.marks["turned"], 1)

                def encode(t, i, b):
                    e.done(pe, "keyed", t)
                    e.done(pe, "matched", t, 2)
                    pe.transpose(pkey[b % 2][:, :], key[:, b, :].to_broadcast([P, P]), g.ident[:, :]).then_inc(e.marks["spread"], 1)
                    pe.wait_ge(e.dmas["attr"][b], i * 16 + 16)
                    e.done(pe, "weighed", t, 2)
                    pe.matmul(penc[b % 2][:, :], attr[:, b, :], ew[:, :], start=True, stop=True).then_inc(e.marks["encoded"], 1)

                def mask(t, b):
                    e.done(pe, "at_ready", t)
                    e.done(pe, "penned", t)
                    e.done(pe, "mloc", t, 1)
                    for j in range(2):
                        for h in range(4):
                            pe.matmul(pm[j][:, h, :], g.picks[:, 4 * j + h, :], at[:, b, :], start=(h == 0), stop=False)
                        mm = pe.matmul(pm[j][:, :, :], g.identb[:, :], over(pen[:, b, :], 1, [P, 4, P]), start=False, stop=True)
                    mm.then_inc(e.marks["masked"], 1)

                def total(t, b):
                    e.done(pe, "multiplied", t)
                    e.done(pe, "new_ready", t, 1)
                    pe.matmul(psum[:, :], same[:, b, :], prod[:, b, :, :].rearrange("p a b -> p (a b)"), start=True, stop=True).then_inc(e.marks["summed"], 1)

                def step(t, i, b):
                    if exists(t, 1):
                        turn_alpha(t + 1, (b + 1) % U)
                    if exists(t, 2):
                        encode(t + 2, i + 1 if b >= 2 else i, (b + 2) % U)
                    if exists(t, 1):
                        mask(t + 1, (b + 1) % U)
                    if exists(t, 0):
                        total(t, b)

                encode(0, 0, 0)
                steps_of(pe, lambda t, i, b: step(t, i, b) if not (isinstance(t, int) and t < -1) else None, ET, 1, 0)

            @block.scalar
            def _(act):
                def step(t, i, b):
                    if exists(t, 1):
                        c = (b + 1) % U
                        e.done(act, "turned", t + 1)
                        act.activation(at[0:H0, c, :], pat[:, :], ACT.Copy).then_inc(e.marks["at_ready"], 1)
                    if exists(t, 0):
                        e.done(act, "differed", t)
                        e.done(act, "summed", t, U)
                        act.activation(prod[:, b, :, D0], diff[:, b, 0, :], ACT.Exp).then_inc(e.marks["exped"], 1)
                        act.activation(fade[:, b, :], diff[:, b, 1, :], ACT.Exp).then_inc(e.marks["faded"], 1)

                steps_of(act, step, ET, 1, 0)

            @block.vector
            def _(dve):
                m = e.marks

                def make_key(t, i, b):
                    dve.wait_ge(e.dmas["ixa"][b], i * 16 + 16)
                    e.done(dve, "spread", t, U)
                    dve.tensor_copy(key[:, b, :], ixa[:, b, 1:2]).then_inc(m["keyed"], 1)

                def score(t, i, b):
                    e.done(dve, "encoded", t)
                    dve.wait_ge(e.dmas["drow"][b], i * 16 + 16)
                    dve.scalar_tensor_tensor(out=we[:, b, :], in0=penc[b % 2][:, :], scalar=0.0, in1=drow[:, b, 0:D], op0=ALU.max,
                                             op1=ALU.mult).then_inc(m["weighed"], 1)
                    e.done(dve, "spread", t)
                    e.done(dve, "summed", t, U)
                    dve.tensor_scalar(same[:, b, :], pkey[b % 2][:, :], key[:, b, :], None, ALU.is_equal).then_inc(m["matched"], 1)
                    e.done(dve, "weighed", t)
                    dve.tensor_reduce(z[:, b, :], we[:, b, :].rearrange("p (h d) -> p h d", h=H0), AX, ALU.add).then_inc(m["z1"], 1)
                    e.done(dve, "matched", t)
                    dve.tensor_scalar(pen[:, b, :], same[:, b, :], -LOWEST, LOWEST, ALU.mult, ALU.add).then_inc(m["penned"], 1)
                    e.done(dve, "z1", t)
                    dve.tensor_tensor(z[:, b, :], z[:, b, :], drow[:, b, D + H0:ROW0], ALU.add).then_inc(m["z2"], 1)
                    e.done(dve, "z2", t)
                    dve.wait_ge(e.dmas["srow"][b], i * 16 + 16)
                    dve.tensor_tensor(z[:, b, :], z[:, b, :], srow[:, b, D:D + H0], ALU.add).then_inc(m["z3"], 1)
                    e.done(dve, "z3", t)
                    dve.scalar_tensor_tensor(out=alpha[:, b, :], in0=z[:, b, :], scalar=0.2, in1=z[:, b, :], op0=ALU.mult,
                                             op1=ALU.max).then_inc(m["scored"], 1)

                def maximum(t, i, b):
                    e.done(dve, "masked", t)
                    dve.tensor_reduce(mloc[:, b, 0:4], pm[0][:, :, :], AX, ALU.max)
                    dve.tensor_reduce(mloc[:, b, 4:8], pm[1][:, :, :], AX, ALU.max).then_inc(m["mloc"], 1)
                    e.done(dve, "mloc", t)
                    dve.wait_ge(e.dmas["old"][b], i * 16 + 16)
                    if not (isinstance(t, int) and t < U):
                        dve.wait_ge(e.dmas["new"][b], i * 16)
                    dve.tensor_tensor(new[:, b, A:A + H0], mloc[:, b, :], old[:, b, A:A + H0], ALU.max).then_inc(m["mnew"], 1)
                    e.done(dve, "mnew", t)
                    dve.tensor_tensor(diff[:, b, 0, :], alpha[:, b, :], new[:, b, A:A + H0], ALU.subtract)
                    dve.tensor_tensor(diff[:, b, 1, :], old[:, b, A:A + H0], new[:, b, A:A + H0], ALU.subtract).then_inc(m["differed"], 1)

                def update(t, b):
                    e.done(dve, "old_faded", t)
                    e.done(dve, "summed", t)
                    dve.tensor_tensor(new[:, b, 0:A], old[:, b, 0:A], psum[:, :], ALU.add).then_inc(m["new_ready"], 1)

                def multiply(t, b):
                    e.done(dve, "faded", t)
                    o = old[:, b, 0:A].rearrange("p (h d) -> p h d", h=H0)
                    dve.tensor_tensor(prod[:, b, :, 0:D0], srow[:, b, 0:D].rearrange("p (h d) -> p h d", h=H0),
                                      prod[:, b, :, D0:D0 + 1].to_broadcast([P, H0, D0]), ALU.mult).then_inc(m["multiplied"], 1)
                    dve.tensor_tensor(o, o, over(fade[:, b, :], 2, [P, H0, D0 + 1]), ALU.mult).then_inc(m["old_faded"], 1)

                def step(t, i, b):
                    if exists(t, 2):
                        make_key(t + 2, i + 1 if b >= 2 else i, (b + 2) % U)
                    if exists(t, 1):
                        score(t + 1, i + 1 if b == U - 1 else i, (b + 1) % U)
                    if exists(t, 0):
                        maximum(t, i, b)
                    if exists(t, -1):
                        update(t - 1, (b - 1) % U)
                    if exists(t, 0):
                        multiply(t, b)

                steps_of(dve, step, ET, 2, 1)


def merge0(nc, g, a):
    A = H0 * (D0 + 1)
    with Room(nc, "m0") as r:
        tb = r.sbuf("tb", [P, NTAB, 2, A + H0])
        mx = r.sbuf("mx", [P, 2, 2, H0])
        top = r.sbuf("top", [P, 2, H0])
        diff = r.sbuf("diff", [P, NTAB, 2, H0])
        fade = r.sbuf("fade", [P, NTAB, 2, H0])
        rden = r.sbuf("rden", [P, 2, H0])
        res = r.sbuf("res", [P, 2, D])
        bias = r.sbuf("bias", [P, D])
        loaded, ld, differed, exped, xdone, passed = (r.sem(n) for n in ("loaded", "ld", "differed", "exped", "x_done", "passed"))
        chain = r.sems("step", 16)
        credit(nc, [differed, exped, xdone])
        with nc.Block() as block:

            @block.sync
            def _(sp):
                sp.dma_start(bias[:, :], to_all(a["gbias"], D)).then_inc(loaded, 16)
                with sp.Fori(0, PAIRS) as i:
                    hold(sp, xdone, i + 1, passed)
                    for k in range(NTAB):
                        sp.dma_start(tb[:, k, :, :], rows(g.tabs0[k], i)).then_inc(ld, 16)

            @block.scalar
            def _(act):
                with act.Fori(0, PAIRS) as i:
                    act.wait_ge(differed, i + 2)
                    act.activation(fade[:, :, :, :], diff[:, :, :, :], ACT.Exp).then_inc(exped, 1)

            @block.vector
            def _(dve):
                dve.wait_ge(loaded, 16)
                with dve.Fori(0, PAIRS) as i:
                    now = i + 2
                    link = Chain(dve, chain, i + 1)
                    dve.wait_ge(ld, i * (16 * NTAB) + 16 * NTAB)
                    link(dve.tensor_tensor(mx[:, :, :, :], tb[:, 0:2, :, A:A + H0], tb[:, 2:4, :, A:A + H0], ALU.max))
                    link(dve.tensor_tensor(top[:, :, :], mx[:, 0, :, :], mx[:, 1, :, :], ALU.max))
                    dve.tensor_tensor(diff[:, :, :, :], tb[:, :, :, A:A + H0], over(top[:, :, :], 1, [P, NTAB, 2, H0]), ALU.subtract).then_inc(differed, 1)
                    dve.wait_ge(exped, now)
                    for k in range(NTAB):
                        v = tb[:, k, :, 0:A].rearrange("p t (h d) -> p t h d", h=H0)
                        ins = dve.tensor_tensor(v, v, over(fade[:, k, :, :], 3, [P, 2, H0, D0 + 1]), ALU.mult)
                    link(ins)
                    link(dve.tensor_tensor(tb[:, 0:2, :, 0:A], tb[:, 0:2, :, 0:A], tb[:, 2:4, :, 0:A], ALU.add))
                    link(dve.tensor_tensor(tb[:, 0, :, 0:A], tb[:, 0, :, 0:A], tb[:, 1, :, 0:A], ALU.add))
                    v = tb[:, 0, :, 0:A].rearrange("p t (h d) -> p t h d", h=H0)
                    link(dve.tensor_scalar(rden[:, :, :], v[:, :, :, D0], 1e-10, None, ALU.max))
                    link(dve.reciprocal(rden[:, :, :], rden[:, :, :]))
                    link(dve.tensor_tensor(res[:, :, :].rearrange("p t (h d) -> p t h d", h=H0), v[:, :, :, 0:D0],
                                           over(rden[:, :, :], 3, [P, 2, H0, D0]), ALU.mult))
                    link(dve.tensor_tensor(res[:, :, :], res[:, :, :], over(bias[:, :], 1, [P, 2, D]), ALU.add))
                    dve.tensor_tensor(g.x[:, ds(i * 2, 2), :], g.x[:, ds(i * 2, 2), :], res[:, :, :], ALU.add).then_inc(xdone, 1)


def turn_pair(pe, g, pt, un):
    for t in range(2):
        for k in range(KD):
            mm = pe.transpose(pt[:, k, t * P:(t + 1) * P], un[:, t, k * P:(k + 1) * P], g.ident[:, :])
    return mm


def pick_two(dve, link, p, w, n, m, wait_exp):
    s = w.scratch
    shape = [P, m, n]
    m1, m2, i1, i2, gap = (s.small[:, j, :] for j in range(5))
    link(dve.tensor_reduce(m1, p, AX, ALU.max))
    link(dve.tensor_tensor(s.eq, p, over(m1, 2, shape), ALU.is_equal))
    link(dve.scalar_tensor_tensor(out=s.cand, in0=s.eq, scalar=-float(n), in1=s.order_n, op0=ALU.mult, op1=ALU.add))
    link(dve.tensor_reduce(i1, s.cand, AX, ALU.min))
    link(dve.tensor_tensor(s.sel1, s.order, over(i1, 2, shape), ALU.is_equal))
    link(dve.scalar_tensor_tensor(out=s.rest, in0=s.sel1, scalar=-4.0, in1=p, op0=ALU.mult, op1=ALU.add))
    link(dve.tensor_reduce(m2, s.rest, AX, ALU.max))
    link(dve.tensor_tensor(s.eq, s.rest, over(m2, 2, shape), ALU.is_equal))
    link(dve.scalar_tensor_tensor(out=s.cand, in0=s.eq, scalar=-float(n), in1=s.order_n, op0=ALU.mult, op1=ALU.add))
    link(dve.tensor_reduce(i2, s.cand, AX, ALU.min))
    link(dve.tensor_tensor(s.sel2, s.order, over(i2, 2, shape), ALU.is_equal))
    wait_exp(dve.tensor_tensor(gap, m2, m1, ALU.subtract))
    w1, w2 = s.small[:, 5, :], s.small[:, 6, :]
    link(dve.tensor_scalar(w1, s.small[:, 7, :], 1.0, None, ALU.add))
    link(dve.reciprocal(w1, w1))
    link(dve.tensor_tensor(w2, s.small[:, 7, :], w1, ALU.mult))
    link(dve.tensor_tensor(s.eq, s.sel1, over(w1, 2, shape), ALU.mult))
    link(dve.tensor_tensor(s.cand, s.sel2, over(w2, 2, shape), ALU.mult))
    return dve.tensor_tensor(w.w, s.eq, s.cand, ALU.add)


class Picks:

    def __init__(self, r, n, m):
        self.w = r.sbuf("pick_w", [P, m, n])[:, :, :]
        self.scratch = self
        self.eq, self.cand, self.sel1, self.sel2, self.rest, self.order, self.order_n = (
            r.sbuf(f"pick_{name}", [P, m, n])[:, :, :] for name in ("eq", "cand", "sel1", "sel2", "rest", "order", "order_n"))
        self.small = r.sbuf("pick_small", [P, 8, m])
        self.n, self.m = n, m

    def order_of(self, dve):
        for j in range(self.n):
            dve.memset(self.order[:, :, j], float(j))
            ins = dve.memset(self.order_n[:, :, j], float(j + self.n))
        return ins


def experts0(nc, g, a):
    E = EXPERTS0
    with Room(nc, "ex") as r:
        rw1 = r.sbuf("rw1", [P, KD, P])
        rw2 = r.sbuf("rw2", [P, E])
        rb1 = r.sbuf("rb1", [P, 1])
        rb2 = r.sbuf("rb2", [P, E])
        w1, w2, w3 = (r.sbuf(f"w{j}", [P, E * KD, D]) for j in (1, 2, 3))
        b1, b2 = (r.sbuf(f"b{j}", [P, E * KD]) for j in (1, 2))
        b3 = r.sbuf("b3", [E, D])
        un = r.sbuf("un", [P, 2, D])
        xt = r.sbuf("xt", [P, KD, PW])
        rh = r.sbuf("rh", [P, PW])
        lg = r.sbuf("lg", [P, 2, E])
        ex = r.sbuf("exl", [P, 2, E])
        tot = r.sbuf("tot", [P, 2, 2])
        wt = r.sbuf("wt", [E, PW])
        h1 = r.sbuf("h1", [P, 2, KD, PW])
        h2 = r.sbuf("h2", [P, 2, KD, PW])
        acc = r.sbuf("acc", [P, 2, D])
        picks = Picks(r, E, 2)
        pt = r.psum("pt", [P, KD, PW])
        pr = r.psum("pr", [P, 512])
        p1, p2, p3 = ([r.psum(f"p{j}{s}", [P, KD, PW]) for s in range(2)] for j in (1, 2, 3))
        loaded, passed = r.sem("loaded"), r.sem("passed")
        m = {n: r.sem(n) for n in ("copied", "turned", "xt_ready", "routed1", "rh_ready", "logits", "centred", "exped", "gapped",
                                   "gap_exped", "picked", "w_turned", "wt_ready", "biased", "acc_ready", "xdone")}
        x = {n: r.sem(n) for n in ("l1", "h1_ready", "l2", "h2_ready", "l3", "combined")}
        chain = r.sems("step", 32)
        credit(nc, list(m.values()))
        credit(nc, list(x.values()), 2)
        with nc.Block() as block:

            @block.sync
            def _(sp):
                for dst, src in ((rw1[:, :, :], weights(a["rw1"])), (rw2[:, :], a["rw2"]), (rb1[:, :], a["rb1"]), (rb2[:, :], to_all(a["rb2"], E)),
                                 (w1[:, :, :], weights(a["ew1"])), (w2[:, :, :], weights(a["ew2"])), (w3[:, :, :], weights(a["ew3"])),
                                 (b1[:, :], a["eb1"]), (b2[:, :], a["eb2"]), (b3[:, :], a["eb3"])):
                    sp.dma_start(dst, src).then_inc(loaded, 16)
                sp.wait_ge(loaded, 160)

            @block.tensor
            def _(pe):
                pe.wait_ge(loaded, 160)
                with pe.Fori(0, PAIRS) as i:
                    before, now = i + 1, i + 2

                    def layer(s, e, p, w, src, need, out, free):
                        n = i * E + e
                        if need is not None:
                            pe.wait_ge(x[need], n + 3)
                        pe.wait_ge(x[free], n + 1)
                        for c in range(KD):
                            for k in range(KD):
                                mm = pe.matmul(p[:, c, :], w[:, e * KD + k, c * P:(c + 1) * P], src[:, k, :], start=(k == 0), stop=(k == KD - 1))
                        mm.then_inc(x[out], 1)

                    def last(e):
                        n = i * E + e
                        pe.wait_ge(x["h2_ready"], n + 3)
                        pe.wait_ge(x["combined"], n + 1)
                        for t in range(2):
                            for k in range(KD):
                                mm = pe.matmul(p3[e % 2][:, t, :], h2[:, e % 2, k, t * P:(t + 1) * P], w3[:, e * KD + k, :],
                                               start=(k == 0), stop=(k == KD - 1))
                        mm.then_inc(x["l3"], 1)

                    pe.wait_ge(m["copied"], now)
                    pe.wait_ge(m["wt_ready"], before)
                    turn_pair(pe, g, pt, un).then_inc(m["turned"], 1)
                    pe.wait_ge(m["xt_ready"], now)
                    pe.wait_ge(m["acc_ready"], before)
                    for k in range(KD):
                        mm = pe.matmul(pr[:, 0:PW], rw1[:, k, :], xt[:, k, :], start=(k == 0), stop=(k == KD - 1))
                    mm.then_inc(m["routed1"], 1)
                    for s in range(E + 2):
                        if s < E:
                            layer(s, s, p1[s % 2], w1, xt, None, "l1", "h1_ready")
                        if s == 0:
                            pe.wait_ge(m["rh_ready"], now)
                            for t in range(2):
                                mm = pe.matmul(pr[:, t * E:(t + 1) * E], rh[:, t * P:(t + 1) * P], rw2[:, :], start=True, stop=True)
                            mm.then_inc(m["logits"], 1)
                        if 0 <= s - 1 < E:
                            layer(s, s - 1, p2[(s - 1) % 2], w2, h1[:, (s - 1) % 2, :, :], "h1_ready", "l2", "h2_ready")
                        if s == 2:
                            pe.wait_ge(m["picked"], now)
                            for t in range(2):
                                mm = pe.transpose(pt[0:E, 0, t * P:(t + 1) * P], picks.w[:, t, :], g.ident[:, :])
                            mm.then_inc(m["w_turned"], 1)
                            pe.wait_ge(m["wt_ready"], now)
                            for t in range(2):
                                mm = pe.matmul(pr[:, t * D:(t + 1) * D], wt[:, t * P:(t + 1) * P], b3[:, :], start=True, stop=True)
                            mm.then_inc(m["biased"], 1)
                        if 0 <= s - 2 < E:
                            last(s - 2)

            @block.scalar
            def _(act):
                act.wait_ge(loaded, 160)
                with act.Fori(0, PAIRS) as i:
                    before, now = i + 1, i + 2

                    def relu(e, h, p, b, need, out, free, lag):
                        n = i * E + e
                        act.wait_ge(x[need], n + 3)
                        act.wait_ge(x[free], n + lag)
                        for c in range(KD):
                            ins = act.activation(h[:, e % 2, c, :], p[e % 2][:, c, :], ACT.Relu, bias=b[:, e * KD + c:e * KD + c + 1])
                        ins.then_inc(x[out], 1)

                    act.wait_ge(m["turned"], before)
                    act.activation(un[:, :, :], g.u[:, ds(i * 2, 2), :], ACT.Copy).then_inc(m["copied"], 1)
                    act.wait_ge(m["routed1"], now)
                    act.activation(rh[:, :], pr[:, 0:PW], ACT.Relu, bias=rb1[:, :]).then_inc(m["rh_ready"], 1)
                    for s in range(E + 1):
                        if s < E:
                            relu(s, h1, p1, b1, "l1", "h1_ready", "l2", 1)
                        if s == 0:
                            act.wait_ge(m["centred"], now)
                            act.activation(ex[:, :, :], lg[:, :, :], ACT.Exp).then_inc(m["exped"], 1)
                        if 0 <= s - 1 < E:
                            relu(s - 1, h2, p2, b2, "l2", "h2_ready", "l3", 1)
                        if s == 1:
                            act.wait_ge(m["gapped"], now)
                            act.activation(picks.small[:, 7, :], picks.small[:, 4, :], ACT.Exp).then_inc(m["gap_exped"], 1)
                            act.wait_ge(m["w_turned"], now)
                            act.activation(wt[:, :], pt[0:E, 0, :], ACT.Copy).then_inc(m["wt_ready"], 1)

            @block.vector
            def _(dve):
                dve.wait_ge(loaded, 160)
                picks.order_of(dve)
                with dve.Fori(0, PAIRS) as i:
                    before, now = i + 1, i + 2
                    link = Chain(dve, chain, i + 1)
                    dve.wait_ge(m["turned"], now)
                    dve.wait_ge(x["l1"], i * E + 2)
                    dve.tensor_copy(xt[:, :, :], pt[:, :, :]).then_inc(m["xt_ready"], 1)
                    dve.wait_ge(m["logits"], now)
                    link(dve.tensor_tensor(lg[:, :, :], pr[:, 0:2 * E].rearrange("p (t e) -> p t e", t=2), over(rb2[:, :], 1, [P, 2, E]), ALU.add))
                    link(dve.tensor_reduce(tot[:, 0, :], lg[:, :, :], AX, ALU.max))
                    dve.tensor_tensor(lg[:, :, :], lg[:, :, :], over(tot[:, 0, :], 2, [P, 2, E]), ALU.subtract).then_inc(m["centred"], 1)
                    dve.wait_ge(m["exped"], now)
                    link(dve.tensor_reduce(tot[:, 1, :], ex[:, :, :], AX, ALU.add))
                    link(dve.reciprocal(tot[:, 1, :], tot[:, 1, :]))
                    link(dve.tensor_tensor(ex[:, :, :], ex[:, :, :], over(tot[:, 1, :], 2, [P, 2, E]), ALU.mult))

                    def wait_exp(ins):
                        ins.then_inc(m["gapped"], 1)
                        dve.wait_ge(m["gap_exped"], now)

                    pick_two(dve, link, ex[:, :, :], picks, E, 2, wait_exp).then_inc(m["picked"], 1)
                    dve.wait_ge(m["biased"], now)
                    dve.tensor_tensor(acc[:, :, :], g.x[:, ds(i * 2, 2), :], pr[:, :].rearrange("p (t d) -> p t d", t=2), ALU.add).then_inc(m["acc_ready"], 1)
                    dve.wait_ge(m["acc_ready"], now)
                    for e in range(E):
                        n = i * E + e
                        dve.wait_ge(x["l3"], n + 3)
                        for t in range(2):
                            dst = acc[:, t, :] if e < E - 1 else g.x[:, ds(i * 2 + t, 1), :].rearrange("p a b -> p (a b)")
                            ins = dve.scalar_tensor_tensor(out=dst, in0=p3[e % 2][:, t, :], scalar=picks.w[:, t, e:e + 1], in1=acc[:, t, :],
                                                           op0=ALU.mult, op1=ALU.add)
                        ins.then_inc(x["combined"], 1)
                        dve.wait_ge(x["combined"], n + 3)


def enter1(nc, g, a):
    with Room(nc, "en") as r:
        w = r.sbuf("w", [P, KD, D])
        bias = r.sbuf("bias", [P, D])
        un = r.sbuf("un", [P, 2, D])
        xt = r.sbuf("xt", [P, KD, PW])
        pt = r.psum("pt", [P, KD, PW])
        po = r.psum("po", [P, 2, D])
        loaded = r.sem("loaded")
        m = {n: r.sem(n) for n in ("copied", "turned", "xt_ready", "projected", "kept")}
        credit(nc, list(m.values()))
        with nc.Block() as block:

            @block.sync
            def _(sp):
                sp.dma_start(w[:, :, :], weights(a["winT"])).then_inc(loaded, 16)
                sp.dma_start(bias[:, :], to_all(a["b_in"], D)).then_inc(loaded, 16)
                sp.wait_ge(loaded, 32)

            @block.scalar
            def _(act):
                with act.Fori(0, PAIRS) as i:
                    act.wait_ge(m["turned"], i + 1)
                    act.activation(un[:, :, :], g.u[:, ds(i * 2, 2), :], ACT.Copy).then_inc(m["copied"], 1)

            @block.tensor
            def _(pe):
                pe.wait_ge(loaded, 32)
                with pe.Fori(0, PAIRS) as i:
                    pe.wait_ge(m["copied"], i + 2)
                    pe.wait_ge(m["xt_ready"], i + 1)
                    turn_pair(pe, g, pt, un).then_inc(m["turned"], 1)
                    pe.wait_ge(m["xt_ready"], i + 2)
                    pe.wait_ge(m["kept"], i + 1)
                    for t in range(2):
                        for k in range(KD):
                            mm = pe.matmul(po[:, t, :], xt[:, k, t * P:(t + 1) * P], w[:, k, :], start=(k == 0), stop=(k == KD - 1))
                    mm.then_inc(m["projected"], 1)

            @block.vector
            def _(dve):
                dve.wait_ge(loaded, 32)
                with dve.Fori(0, PAIRS) as i:
                    dve.wait_ge(m["turned"], i + 2)
                    dve.wait_ge(m["projected"], i + 1)
                    dve.tensor_copy(xt[:, :, :], pt[:, :, :]).then_inc(m["xt_ready"], 1)
                    dve.wait_ge(m["projected"], i + 2)
                    dve.tensor_tensor(g.hid[:, ds(i * 2, 2), :], po[:, :, :], over(bias[:, :], 1, [P, 2, D]), ALU.add).then_inc(m["kept"], 1)


def project1(nc, g, a, l):
    with Room(nc, "pj") as r:
        wq, wk, wv = (r.sbuf(f"w{n}", [P, KD, D]) for n in "qkv")
        bias = r.sbuf("bias", [P, 3, D])
        un = r.sbuf("un", [P, 2, D])
        xt = r.sbuf("xt", [P, KD, PW])
        qo = r.sbuf("qo", [P, 2, D])
        kvo = r.sbuf("kvo", [P, 2, 2 * D])
        blank = r.sbuf("blank", [P, ROW1])
        pt = r.psum("pt", [P, KD, PW])
        pq = r.psum("pq", [P, 2, D])
        pkv = [r.psum(f"pkv{t}", [P, 2 * D]) for t in range(2)]
        loaded, blanked, inited, stored, passed = (r.sem(n) for n in ("loaded", "blanked", "inited", "stored", "passed"))
        m = {n: r.sem(n) for n in ("copied", "turned", "xt_ready", "projected", "rows_ready", "sent")}
        credit(nc, list(m.values()))
        with nc.Block() as block:

            @block.sync
            def _(sp):
                for dst, w in ((wq, a["wqT"]), (wk, a["wkT"]), (wv, a["wvT"])):
                    sp.dma_start(dst[:, :, :], weights(w[ds(l * D, D), :])).then_inc(loaded, 16)
                for j, b in enumerate((a["bq"], a["bk"], a["bv"])):
                    sp.dma_start(bias[:, j, :], b[ds(l, 1), :].to_broadcast([P, D])).then_inc(loaded, 16)
                sp.wait_ge(blanked, 1)
                for t in g.tabs1:
                    sp.dma_start(t.rearrange("(t p) c -> p t c", p=P), over(blank[:, :], 1, [P, TROWS // P, ROW1])).then_inc(inited, 16)
                with sp.Fori(0, PAIRS) as i:
                    hold(sp, m["rows_ready"], i + 2, passed)
                    sp.dma_start(rows(g.qrows, i), qo[:, :, :]).then_inc(stored, 16)
                    sp.dma_start(rows(g.kvrows, i), kvo[:, :, :]).then_inc(stored, 16)
                    hold(sp, stored, i * 32 + 32, m["sent"])
                sp.wait_ge(inited, 16 * NTAB)

            @block.scalar
            def _(act):
                with act.Fori(0, PAIRS) as i:
                    act.wait_ge(m["turned"], i + 1)
                    act.activation(un[:, :, :], g.hid[:, ds(i * 2, 2), :], ACT.Copy).then_inc(m["copied"], 1)

            @block.tensor
            def _(pe):
                pe.wait_ge(loaded, 96)
                with pe.Fori(0, PAIRS) as i:
                    pe.wait_ge(m["copied"], i + 2)
                    pe.wait_ge(m["xt_ready"], i + 1)
                    turn_pair(pe, g, pt, un).then_inc(m["turned"], 1)
                    pe.wait_ge(m["xt_ready"], i + 2)
                    pe.wait_ge(m["rows_ready"], i + 1)
                    for dst, w in (([pq[:, t, :] for t in range(2)], wq), ([pkv[t][:, 0:D] for t in range(2)], wk),
                                   ([pkv[t][:, D:2 * D] for t in range(2)], wv)):
                        for t in range(2):
                            for k in range(KD):
                                mm = pe.matmul(dst[t], xt[:, k, t * P:(t + 1) * P], w[:, k, :], start=(k == 0), stop=(k == KD - 1))
                    mm.then_inc(m["projected"], 1)

            @block.vector
            def _(dve):
                dve.memset(blank[:, :], 0.0).then_inc(blanked, 1)
                dve.wait_ge(loaded, 96)
                with dve.Fori(0, PAIRS) as i:
                    dve.wait_ge(m["turned"], i + 2)
                    dve.wait_ge(m["projected"], i + 1)
                    dve.tensor_copy(xt[:, :, :], pt[:, :, :]).then_inc(m["xt_ready"], 1)
                    dve.wait_ge(m["projected"], i + 2)
                    dve.wait_ge(m["sent"], i + 1)
                    dve.tensor_tensor(qo[:, :, :], pq[:, :, :], over(bias[:, 0, :], 1, [P, 2, D]), ALU.add)
                    for t in range(2):
                        ins = dve.tensor_tensor(kvo[:, t, :], pkv[t][:, :], bias[:, 1:3, :].rearrange("p a b -> p (a b)"), ALU.add)
                    ins.then_inc(m["rows_ready"], 1)


DVE_HEADS = 1


def attend1(nc, g):
    AH = HG - DVE_HEADS
    with Room(nc, "at") as r:
        ixa = r.sbuf("ixa", [P, U, 4], I32)
        ixb = r.sbuf("ixb", [P, U, 4], I32)
        q = r.sbuf("q", [P, U, D])
        kv = r.sbuf("kv", [P, U, 2 * D])
        key = r.sbuf("key", [P, U, 1])
        same = r.sbuf("same", [P, U, P])
        qk = r.sbuf("qk", [P, 2, HG, HG, DG])
        sc = r.sbuf("sc", [P, U, HG, HG])
        mx = r.sbuf("mx", [P, U, HG])
        ex = r.sbuf("exl", [P, U, HG, HG])
        den = r.sbuf("den", [P, U, HG])
        att = r.sbuf("att", [P, U, HG, HG])
        wv = r.sbuf("wv", [P, U, HG, D])
        new = r.sbuf("new", [P, U, ROW1])
        pkey = [r.psum(f"pkey{j}", [P, P]) for j in range(2)]
        pm = [r.psum(f"pm{j}", [P, ROW1]) for j in range(2)]
        e = Edge(r, ["keyed", "spread", "matched", "paired", "scored", "topped", "centred", "exped", "summed", "inverted", "attended",
                     "weighted_a", "weighted_v", "totalled", "new_ready"], ["ixa", "ixb", "q", "kv", "new"])
        passed, passed_sp = r.sem("passed"), r.sem("passed_sp")
        e.credit(nc)
        with nc.Block() as block:

            @block.sync
            def _(sp):
                def step(t, i, b):
                    if exists(t, 3):
                        c = (b + 3) % U
                        if not (isinstance(t, int) and t < 1):
                            j = i if b == 0 else i + 1
                            hold(sp, e.dmas["q"][c], j * 16, passed_sp)
                            hold(sp, e.dmas["kv"][c], j * 16, passed_sp)
                            e.done(sp, "keyed", t, 1, passed_sp)
                        sp.dma_start(ixa[:, c, :], tile_of(g.idx, t + 3)).then_inc(e.dmas["ixa"][c], 16)
                    if exists(t, 0):
                        if not (isinstance(t, int) and t < U):
                            hold(sp, e.dmas["new"][b], i * 16, passed_sp)
                        sp.dma_start(ixb[:, b, :], tile_of(g.idx, t)).then_inc(e.dmas["ixb"][b], 16)

                steps_of(sp, step, ET, 3, 0)

            @block.gpsimd
            def _(pool):
                def step(t, i, b):
                    if exists(t, -2):
                        c = (b - 2) % U
                        j = i + 1 if b >= 2 else i
                        pool.wait_ge(e.dmas["ixb"][c], j * 16)
                        if not (isinstance(t, int) and t - 2 < U):
                            pool.wait_ge(e.dmas["new"][c], (j - 1) * 16)
                        e.done(pool, "new_ready", t, 2)
                        pool.sem_inc(passed)
                        pool.indirect_dma_start(out=g.tabs1[c][:, :], out_offset=bass.IndirectOffsetOnAxis(ap=ixb[:, c, 2:3], axis=0),
                                                in_=new[:, c, :], in_offset=None, compute_op=ALU.add).then_inc(e.dmas["new"][c], 16)
                    if exists(t, 2):
                        c = (b + 2) % U
                        j = i + 2 if b >= 2 else i + 1
                        pool.wait_ge(e.dmas["ixa"][c], j * 16)
                        if not (isinstance(t, int) and t + 2 < U):
                            e.done(pool, "weighted_a", t + 2, U)
                            e.done(pool, "weighted_v", t + 2, U)
                            e.done(pool, "paired", t + 2, U)
                        pool.sem_inc(passed)
                        pool.indirect_dma_start(out=q[:, c, :], out_offset=None, in_=g.qrows[:, :],
                                                in_offset=bass.IndirectOffsetOnAxis(ap=ixa[:, c, 0:1], axis=0)).then_inc(e.dmas["q"][c], 16)
                        pool.indirect_dma_start(out=kv[:, c, :], out_offset=None, in_=g.kvrows[:, :],
                                                in_offset=bass.IndirectOffsetOnAxis(ap=ixa[:, c, 1:2], axis=0)).then_inc(e.dmas["kv"][c], 16)

                steps_of(pool, step, ET, 2, 2)
                for c in range(U):
                    hold(pool, e.dmas["new"][c], 16 * TURNS, passed)

            @block.tensor
            def _(pe):
                def spread(t, b):
                    e.done(pe, "keyed", t)
                    e.done(pe, "matched", t, 2)
                    pe.transpose(pkey[b % 2][:, :], key[:, b, :].to_broadcast([P, P]), g.ident[:, :]).then_inc(e.marks["spread"], 1)

                def total(t, b):
                    e.done(pe, "weighted_a", t)
                    e.done(pe, "weighted_v", t)
                    e.done(pe, "new_ready", t, 2)
                    p = pm[b % 2]
                    pe.matmul(p[:, D:ROW1], same[:, b, :], tile_of(g.kinds, t), start=True, stop=True)
                    for h in range(HG):
                        mm = pe.matmul(p[:, 0:D], same[:, b, :], wv[:, b, h, :], start=(h == 0), stop=(h == HG - 1))
                    mm.then_inc(e.marks["totalled"], 1)

                def step(t, i, b):
                    if exists(t, 2):
                        spread(t + 2, (b + 2) % U)
                    if exists(t, 0):
                        total(t, b)

                steps_of(pe, step, ET, 2, 0)

            @block.scalar
            def _(act):
                def step(t, i, b):
                    if exists(t, 0):
                        e.done(act, "attended", t)
                        e.done(act, "totalled", t, U)
                        for h in range(AH):
                            for s in range(HG):
                                ins = act.activation(wv[:, b, h, s * DG:(s + 1) * DG], kv[:, b, D + h * DG:D + (h + 1) * DG], ACT.Copy,
                                                     scale=att[:, b, s, h:h + 1])
                        ins.then_inc(e.marks["weighted_a"], 1)
                    if exists(t, 1):
                        e.done(act, "centred", t + 1)
                        act.activation(ex[:, (b + 1) % U, :, :], sc[:, (b + 1) % U, :, :], ACT.Exp, scale=DG ** -0.5).then_inc(e.marks["exped"], 1)

                steps_of(act, step, ET, 1, 0)

            @block.vector
            def _(dve):
                m = e.marks

                def make_key(t, i, b):
                    dve.wait_ge(e.dmas["ixa"][b], i * 16 + 16)
                    e.done(dve, "spread", t, U)
                    dve.tensor_copy(key[:, b, :], ixa[:, b, 0:1]).then_inc(m["keyed"], 1)

                def attention(t, b):
                    e.done(dve, "exped", t)
                    dve.tensor_reduce(den[:, b, :], ex[:, b, :, :], AX, ALU.add).then_inc(m["summed"], 1)
                    e.done(dve, "summed", t)
                    dve.reciprocal(den[:, b, :], den[:, b, :]).then_inc(m["inverted"], 1)
                    e.done(dve, "inverted", t)
                    dve.tensor_tensor(att[:, b, :, :], ex[:, b, :, :], over(den[:, b, :], 2, [P, HG, HG]), ALU.mult).then_inc(m["attended"], 1)
                    e.done(dve, "attended", t)
                    e.done(dve, "totalled", t, U)
                    for h in range(AH, HG):
                        ins = dve.tensor_tensor(wv[:, b, h, :].rearrange("p (s d) -> p s d", s=HG),
                                                over(kv[:, b, D + h * DG:D + (h + 1) * DG], 1, [P, HG, DG]),
                                                att[:, b, :, h:h + 1].to_broadcast([P, HG, DG]), ALU.mult)
                    ins.then_inc(m["weighted_v"], 1)

                def score(t, i, b):
                    dve.wait_ge(e.dmas["q"][b], i * 16 + 16)
                    dve.wait_ge(e.dmas["kv"][b], i * 16 + 16)
                    e.done(dve, "scored", t, 2)
                    qs = q[:, b, :].rearrange("p (h d) -> p h d", h=HG)
                    ks = kv[:, b, 0:D].rearrange("p (h d) -> p h d", h=HG)
                    dve.tensor_tensor(qk[:, b % 2, :, :, :], over(qs, 2, [P, HG, HG, DG]), over(ks, 1, [P, HG, HG, DG]), ALU.mult).then_inc(m["paired"], 1)
                    e.done(dve, "spread", t)
                    e.done(dve, "totalled", t, U)
                    dve.tensor_scalar(same[:, b, :], pkey[b % 2][:, :], key[:, b, :], None, ALU.is_equal).then_inc(m["matched"], 1)
                    e.done(dve, "paired", t)
                    dve.tensor_reduce(sc[:, b, :, :], qk[:, b % 2, :, :, :], AX, ALU.add).then_inc(m["scored"], 1)
                    e.done(dve, "scored", t)
                    dve.tensor_reduce(mx[:, b, :], sc[:, b, :, :], AX, ALU.max).then_inc(m["topped"], 1)
                    e.done(dve, "topped", t)
                    dve.tensor_tensor(sc[:, b, :, :], sc[:, b, :, :], over(mx[:, b, :], 2, [P, HG, HG]), ALU.subtract).then_inc(m["centred"], 1)

                def keep(t, i, b):
                    e.done(dve, "totalled", t)
                    if not (isinstance(t, int) and t < U):
                        dve.wait_ge(e.dmas["new"][b], i * 16)
                    dve.tensor_copy(new[:, b, :], pm[b % 2][:, :]).then_inc(m["new_ready"], 1)

                def step(t, i, b):
                    if exists(t, 0):
                        attention(t, b)
                    if exists(t, 2):
                        make_key(t + 2, i + 1 if b >= 2 else i, (b + 2) % U)
                    if exists(t, 1):
                        score(t + 1, i + 1 if b == U - 1 else i, (b + 1) % U)
                    if exists(t, -1):
                        keep(t - 1, i if b else i - 1, (b - 1) % U)

                steps_of(dve, step, ET, 2, 1)


def tile_of(buf, t):
    return buf[:, t, :] if isinstance(t, int) else buf[:, ds(t, 1), :].rearrange("p a b -> p (a b)")


def ln_pair(dve, link, z, stat, junk, ask, got):
    s, v = stat[:, 0, :], stat[:, 1, :]
    link(dve.tensor_reduce(s, z, AX, ALU.add))
    link(dve.tensor_scalar(s, s, -1.0 / D, None, ALU.mult))
    link(dve.tensor_tensor(z, z, over(s, 2, [P, 2, D]), ALU.add))
    for t in range(2):
        ins = dve.tensor_tensor_reduce(junk[:, t, :], z[:, t, :], z[:, t, :], 1.0, 0.0, ALU.mult, ALU.add, stat[:, 1, t:t + 1])
    link(ins)
    ask(dve.tensor_scalar(v, v, 1.0 / D, EPS, ALU.mult, ALU.add))
    got()
    link(dve.reciprocal(s, stat[:, 2, :]))
    link(dve.tensor_tensor(z, z, over(s, 2, [P, 2, D]), ALU.mult))


def update1(nc, g, a, l):
    with Room(nc, "up") as r:
        wo = r.sbuf("wo", [P, KD, D])
        em = r.sbuf("em", [P, KD, 3])
        te = r.sbuf("te", [4, D])
        gain, shift = r.sbuf("gain", [P, D]), r.sbuf("shift", [P, D])
        tb = r.sbuf("tb", [P, NTAB, 2, ROW1])
        st = r.sbuf("st", [P, KD, PW])
        ct = r.sbuf("ct", [4, PW])
        z = r.sbuf("z", [P, 2, D])
        junk = r.sbuf("junk", [P, 2, D])
        stat = r.sbuf("stat", [P, 3, 2])
        pt = r.psum("pt", [P, KD, PW])
        pc = r.psum("pc", [4, PW])
        po = r.psum("po", [P, 2, D])
        pe_ = r.psum("pe", [3, D])
        loaded, embedded, te_ready, ld, passed = (r.sem(n) for n in ("loaded", "embedded", "te_ready", "ld", "passed"))
        m = {n: r.sem(n) for n in ("added", "turned", "st_ready", "projected", "var_ready", "std_ready", "kept")}
        chain = r.sems("step", 16)
        credit(nc, list(m.values()))
        with nc.Block() as block:

            @block.sync
            def _(sp):
                sp.dma_start(wo[:, :, :], weights(a["woT"][ds(l * D, D), :])).then_inc(loaded, 16)
                sp.dma_start(em[:, :, :], weights(a["eemb"][ds(l * D, D), :])).then_inc(loaded, 16)
                sp.dma_start(te[3:4, :], a["bo"][ds(l, 1), :]).then_inc(loaded, 16)
                sp.dma_start(gain[:, :], a["ln_g"][ds(l, 1), :].to_broadcast([P, D])).then_inc(loaded, 16)
                sp.dma_start(shift[:, :], a["ln_b"][ds(l, 1), :].to_broadcast([P, D])).then_inc(loaded, 16)
                with sp.Fori(0, PAIRS) as i:
                    hold(sp, m["turned"], i + 1, passed)
                    for k in range(NTAB):
                        sp.dma_start(tb[:, k, :, :], rows(g.tabs1[k], i)).then_inc(ld, 16)

            @block.tensor
            def _(pe):
                pe.wait_ge(loaded, 80)
                for k in range(KD):
                    mm = pe.matmul(pe_[:, :], em[:, k, :], wo[:, k, :], start=(k == 0), stop=(k == KD - 1))
                mm.then_inc(embedded, 1)
                pe.wait_ge(te_ready, 1)
                with pe.Fori(0, PAIRS) as i:
                    pe.wait_ge(m["added"], i + 2)
                    pe.wait_ge(m["st_ready"], i + 1)
                    for t in range(2):
                        pe.transpose(pc[:, t * P:(t + 1) * P], tb[:, 0, t, D:ROW1], g.ident[:, :])
                        for k in range(KD):
                            mm = pe.transpose(pt[:, k, t * P:(t + 1) * P], tb[:, 0, t, k * P:(k + 1) * P], g.ident[:, :])
                    mm.then_inc(m["turned"], 1)
                    pe.wait_ge(m["st_ready"], i + 2)
                    pe.wait_ge(m["kept"], i + 1)
                    for t in range(2):
                        for k in range(KD):
                            pe.matmul(po[:, t, :], st[:, k, t * P:(t + 1) * P], wo[:, k, :], start=(k == 0), stop=False)
                        mm = pe.matmul(po[:, t, :], ct[:, t * P:(t + 1) * P], te[:, :], start=False, stop=True)
                    mm.then_inc(m["projected"], 1)

            @block.scalar
            def _(act):
                act.wait_ge(embedded, 1)
                act.activation(te[0:3, :], pe_[:, :], ACT.Copy).then_inc(te_ready, 1)
                with act.Fori(0, PAIRS) as i:
                    act.wait_ge(m["turned"], i + 2)
                    act.wait_ge(m["projected"], i + 1)
                    act.activation(st[:, :, :], pt[:, :, :], ACT.Copy)
                    act.activation(ct[:, :], pc[:, :], ACT.Copy).then_inc(m["st_ready"], 1)
                    act.wait_ge(m["var_ready"], i + 2)
                    act.activation(stat[:, 2, :], stat[:, 1, :], ACT.Sqrt).then_inc(m["std_ready"], 1)

            @block.vector
            def _(dve):
                dve.wait_ge(loaded, 80)
                with dve.Fori(0, PAIRS) as i:
                    link = Chain(dve, chain, i + 1)
                    dve.wait_ge(ld, i * (16 * NTAB) + 16 * NTAB)
                    link(dve.tensor_tensor(tb[:, 0:2, :, :], tb[:, 0:2, :, :], tb[:, 2:4, :, :], ALU.add))
                    dve.tensor_tensor(tb[:, 0, :, :], tb[:, 0, :, :], tb[:, 1, :, :], ALU.add).then_inc(m["added"], 1)
                    dve.wait_ge(m["projected"], i + 2)
                    link(dve.tensor_tensor(z[:, :, :], po[:, :, :], g.hid[:, ds(i * 2, 2), :], ALU.add))
                    ln_pair(dve, link, z[:, :, :], stat, junk, lambda ins: ins.then_inc(m["var_ready"], 1),
                            lambda: dve.wait_ge(m["std_ready"], i + 2))
                    link(dve.tensor_tensor(z[:, :, :], z[:, :, :], over(gain[:, :], 1, [P, 2, D]), ALU.mult))
                    link(dve.tensor_tensor(z[:, :, :], z[:, :, :], over(shift[:, :], 1, [P, 2, D]), ALU.add))
                    dve.tensor_scalar(g.hid[:, ds(i * 2, 2), :], z[:, :, :], 0.0, None, ALU.max).then_inc(m["kept"], 1)


def adjust1(nc, g, a):
    with Room(nc, "ad") as r:
        w1, w2 = (r.sbuf(f"w{j}", [P, KD, D]) for j in (1, 2))
        b1 = r.sbuf("b1", [P, KD])
        b2 = r.sbuf("b2", [P, D])
        un = r.sbuf("un", [P, 2, D])
        xt = r.sbuf("xt", [P, KD, PW])
        h = r.sbuf("h", [P, KD, PW])
        o = r.sbuf("o", [P, 2, D])
        pt = r.psum("pt", [P, KD, PW])
        ph = r.psum("ph", [P, KD, PW])
        po = r.psum("po", [P, 2, D])
        loaded = r.sem("loaded")
        m = {n: r.sem(n) for n in ("copied", "turned", "xt_ready", "hidden", "h_ready", "projected", "kept")}
        chain = r.sems("step", 4)
        credit(nc, list(m.values()))
        with nc.Block() as block:

            @block.sync
            def _(sp):
                for dst, src in ((w1[:, :, :], weights(a["w1T"])), (w2[:, :, :], weights(a["w2T"])), (b1[:, :], a["b1"]), (b2[:, :], to_all(a["b2"], D))):
                    sp.dma_start(dst, src).then_inc(loaded, 16)
                sp.wait_ge(loaded, 64)

            @block.scalar
            def _(act):
                act.wait_ge(loaded, 64)
                with act.Fori(0, PAIRS) as i:
                    act.wait_ge(m["turned"], i + 1)
                    act.activation(un[:, :, :], g.hid[:, ds(i * 2, 2), :], ACT.Copy).then_inc(m["copied"], 1)
                    act.wait_ge(m["hidden"], i + 2)
                    act.wait_ge(m["projected"], i + 1)
                    for c in range(KD):
                        ins = act.activation(h[:, c, :], ph[:, c, :], ACT.Relu, bias=b1[:, c:c + 1])
                    ins.then_inc(m["h_ready"], 1)

            @block.tensor
            def _(pe):
                pe.wait_ge(loaded, 64)
                with pe.Fori(0, PAIRS) as i:
                    pe.wait_ge(m["copied"], i + 2)
                    pe.wait_ge(m["xt_ready"], i + 1)
                    turn_pair(pe, g, pt, un).then_inc(m["turned"], 1)
                    pe.wait_ge(m["xt_ready"], i + 2)
                    pe.wait_ge(m["h_ready"], i + 1)
                    for c in range(KD):
                        for k in range(KD):
                            mm = pe.matmul(ph[:, c, :], w1[:, k, c * P:(c + 1) * P], xt[:, k, :], start=(k == 0), stop=(k == KD - 1))
                    mm.then_inc(m["hidden"], 1)
                    pe.wait_ge(m["h_ready"], i + 2)
                    pe.wait_ge(m["kept"], i + 1)
                    for t in range(2):
                        for k in range(KD):
                            mm = pe.matmul(po[:, t, :], h[:, k, t * P:(t + 1) * P], w2[:, k, :], start=(k == 0), stop=(k == KD - 1))
                    mm.then_inc(m["projected"], 1)

            @block.vector
            def _(dve):
                dve.wait_ge(loaded, 64)
                with dve.Fori(0, PAIRS) as i:
                    link = Chain(dve, chain, i + 1)
                    dve.wait_ge(m["turned"], i + 2)
                    dve.wait_ge(m["hidden"], i + 1)
                    dve.tensor_copy(xt[:, :, :], pt[:, :, :]).then_inc(m["xt_ready"], 1)
                    dve.wait_ge(m["projected"], i + 2)
                    link(dve.tensor_tensor(o[:, :, :], po[:, :, :], over(b2[:, :], 1, [P, 2, D]), ALU.add))
                    link(dve.tensor_tensor(o[:, :, :], o[:, :, :], g.u[:, ds(i * 2, 2), :], ALU.add))
                    dve.tensor_tensor(g.x[:, ds(i * 2, 2), :], g.x[:, ds(i * 2, 2), :], o[:, :, :], ALU.add).then_inc(m["kept"], 1)


def mix1_keys(nc, g, a):
    with Room(nc, "mk") as r:
        w = r.sbuf("w", [P, KD, 3 * D])
        bias = r.sbuf("bias", [P, 3 * D])
        un = r.sbuf("un", [P, 2, D])
        xt = r.sbuf("xt", [P, KD, PW])
        qk = r.sbuf("qk", [P, 2, 2, D])
        v = r.sbuf("v", [P, 2, D])
        k2 = r.sbuf("k2", [P, 2, D])
        junk = r.sbuf("junk", [P, 2, D])
        st = r.sbuf("st", [P, 4, 2, 2])
        qn = r.sbuf("qn", [P, 2, 2])
        colsq = r.sbuf("colsq", [P, KD])
        pt = r.psum("pt", [P, KD, PW])
        pqk = [r.psum(f"pqk{t}", [P, 2, D]) for t in range(2)]
        pv = r.psum("pv", [P, 2, D])
        pkv = r.psum("pkv", [P, KD, D])
        pcs = r.psum("pcs", [P, KD])
        loaded, zeroed, step, rooted, asked = (r.sem(n) for n in ("loaded", "zeroed", "step", "rooted", "asked"))
        m = {n: r.sem(n) for n in ("copied", "turned", "xt_ready", "projected", "v_ready", "k_ready", "k2_ready", "multiplied",
                                   "q_squared", "q_rooted", "kept", "kv_added", "scaled")}
        chain = r.sems("step", 16)
        credit(nc, list(m.values()))
        with nc.Block() as block:

            @block.sync
            def _(sp):
                sp.dma_start(w[:, :, :], weights(a["mqkv"])).then_inc(loaded, 16)
                sp.dma_start(bias[:, :], to_all(a["mb"], 3 * D)).then_inc(loaded, 16)
                sp.wait_ge(loaded, 32)

            @block.scalar
            def _(act):
                act.wait_ge(loaded, 32)
                with act.Fori(0, PAIRS) as i:
                    before, now = i + 1, i + 2
                    act.wait_ge(m["turned"], before)
                    act.activation(un[:, :, :], g.u[:, ds(i * 2, 2), :], ACT.Copy).then_inc(m["copied"], 1)
                    act.wait_ge(m["k_ready"], now)
                    act.wait_ge(m["multiplied"], before)
                    act.activation(k2[:, :, :], qk[:, :, 1, :], ACT.Square).then_inc(m["k2_ready"], 1)
                    for t in range(2):
                        ins = act.activation(junk[:, t, :], qk[:, t, 0, :], ACT.Square, accum_out=qn[:, 0, t:t + 1])
                    ins.then_inc(m["q_squared"], 1)
                    act.wait_ge(m["q_squared"], now)
                    act.activation(qn[:, 1, :], qn[:, 0, :], ACT.Sqrt).then_inc(m["q_rooted"], 1)
                    act.wait_ge(m["v_ready"], now)
                    act.activation(g.v[:, ds(i * 2, 2), :], v[:, :, :], ACT.Copy).then_inc(m["kept"], 1)
                act.wait_ge(asked, 1)
                act.activation(colsq[:, :], colsq[:, :], ACT.Sqrt).then_inc(rooted, 1)

            @block.tensor
            def _(pe):
                pe.wait_ge(loaded, 32)
                with pe.Fori(0, PAIRS) as i:
                    before, now = i + 1, i + 2
                    pe.wait_ge(m["copied"], now)
                    pe.wait_ge(m["xt_ready"], before)
                    turn_pair(pe, g, pt, un).then_inc(m["turned"], 1)
                    pe.wait_ge(m["xt_ready"], now)
                    pe.wait_ge(m["v_ready"], before)
                    for t in range(2):
                        for dst, c in ((pqk[t][:, :, :], slice(0, 2 * D)), (pv[:, t, :], slice(2 * D, 3 * D))):
                            for k in range(KD):
                                mm = pe.matmul(dst, xt[:, k, t * P:(t + 1) * P], w[:, k, c], start=(k == 0), stop=(k == KD - 1))
                    mm.then_inc(m["projected"], 1)
                    pe.wait_ge(m["k_ready"], now)
                    pe.wait_ge(m["k2_ready"], now)
                    pe.wait_ge(m["v_ready"], now)
                    pe.wait_ge(m["kv_added"], before)
                    for c in range(KD):
                        for t in range(2):
                            pe.matmul(pkv[:, c, :], qk[:, t, 1, c * P:(c + 1) * P], v[:, t, :], start=(t == 0), stop=(t == 1))
                        for t in range(2):
                            mm = pe.matmul(pcs[:, c:c + 1], k2[:, t, c * P:(c + 1) * P], g.ones[:, 0:1], start=(t == 0), stop=(t == 1))
                    mm.then_inc(m["multiplied"], 1)

            @block.vector
            def _(dve):
                dve.memset(g.kvm[:, :, :], 0.0)
                dve.memset(colsq[:, :], 0.0)
                dve.wait_ge(loaded, 32)
                with dve.Fori(0, PAIRS) as i:
                    before, now = i + 1, i + 2
                    link = Chain(dve, chain, i + 1)
                    dve.wait_ge(m["turned"], now)
                    dve.wait_ge(m["projected"], before)
                    dve.tensor_copy(xt[:, :, :], pt[:, :, :]).then_inc(m["xt_ready"], 1)
                    dve.wait_ge(m["projected"], now)
                    dve.wait_ge(m["multiplied"], before)
                    dve.wait_ge(m["kept"], before)
                    for t in range(2):
                        dve.tensor_tensor(qk[:, t, :, :], pqk[t][:, :, :], bias[:, 0:2 * D].rearrange("p (a b) -> p a b", a=2), ALU.add)
                    link(dve.tensor_tensor(v[:, :, :], pv[:, :, :], over(bias[:, 2 * D:3 * D], 1, [P, 2, D]), ALU.add))
                    dve.sem_inc(m["v_ready"])
                    s, rs, cent = st[:, 0, :, :], st[:, 1, :, :], st[:, 2, :, :]
                    full = [P, 2, 2, D]
                    link(dve.tensor_reduce(s, qk[:, :, :, :], AX, ALU.add))
                    link(dve.tensor_scalar(cent, s, -1.0 / D, None, ALU.mult))
                    link(dve.tensor_tensor(qk[:, :, :, :], qk[:, :, :, :], over(cent, 3, full), ALU.add))
                    link(dve.tensor_tensor(qk[:, :, :, :], qk[:, :, :, :], qk[:, :, :, :], ALU.mult))
                    link(dve.tensor_reduce(s, qk[:, :, :, :], AX, ALU.add))
                    link(dve.tensor_scalar(s, s, 1e-7, None, ALU.add))
                    link(dve.reciprocal(rs, s))
                    link(dve.tensor_tensor(rs[:, :, 1], rs[:, :, 1], g.valid[:, ds(i * 2, 2)], ALU.mult))
                    link(dve.tensor_tensor(qk[:, :, :, :], qk[:, :, :, :], over(rs, 3, full), ALU.mult))
                    dve.sem_inc(m["k_ready"])
                    dve.wait_ge(m["q_rooted"], now)
                    link(dve.tensor_scalar(qn[:, 1, :], qn[:, 1, :], 1e-12, None, ALU.max))
                    link(dve.reciprocal(qn[:, 1, :], qn[:, 1, :]))
                    dve.tensor_tensor(g.q[:, ds(i * 2, 2), :], qk[:, :, 0, :], over(qn[:, 1, :], 2, [P, 2, D]), ALU.mult)
                    dve.wait_ge(m["multiplied"], now)
                    dve.tensor_tensor(g.kvm[:, :, :], g.kvm[:, :, :], pkv[:, :, :], ALU.add)
                    dve.tensor_tensor(colsq[:, :], colsq[:, :], pcs[:, :], ALU.add).then_inc(m["kv_added"], 1)
                dve.wait_ge(m["kv_added"], PAIRS + 1)
                dve.sem_inc(asked)
                dve.wait_ge(rooted, 1)
                dve.tensor_scalar(colsq[:, :], colsq[:, :], 1e-12, None, ALU.max).then_inc(step, 1)
                dve.wait_ge(step, 1)
                dve.reciprocal(colsq[:, :], colsq[:, :]).then_inc(step, 1)
                dve.wait_ge(step, 2)
                dve.tensor_scalar(colsq[:, :], colsq[:, :], NODES ** -0.5, None, ALU.mult).then_inc(step, 1)
                dve.wait_ge(step, 3)
                dve.tensor_tensor(g.kvm[:, :, :], g.kvm[:, :, :], over(colsq[:, :], 2, [P, KD, D]), ALU.mult).then_inc(step, 1)


def mix1_out(nc, g, a):
    with Room(nc, "mo") as r:
        w = r.sbuf("w", [P, KD, D])
        bias = r.sbuf("bias", [P, D])
        un = r.sbuf("un", [P, 2, D])
        qt = r.sbuf("qt", [P, KD, PW])
        at = r.sbuf("at", [P, KD, PW])
        att = r.sbuf("att", [P, 2, D])
        o = r.sbuf("o", [P, 2, D])
        pt, pt2 = r.psum("pt", [P, KD, PW]), r.psum("pt2", [P, KD, PW])
        pa, po = r.psum("pa", [P, 2, D]), r.psum("po", [P, 2, D])
        loaded = r.sem("loaded")
        m = {n: r.sem(n) for n in ("copied", "turned", "qt_ready", "attended", "att_ready", "att_turned", "at_ready", "projected", "kept")}
        chain = r.sems("step", 2)
        credit(nc, list(m.values()))
        with nc.Block() as block:

            @block.sync
            def _(sp):
                sp.dma_start(w[:, :, :], weights(a["mout"])).then_inc(loaded, 16)
                sp.dma_start(bias[:, :], to_all(a["mbo"], D)).then_inc(loaded, 16)
                sp.wait_ge(loaded, 32)

            @block.scalar
            def _(act):
                with act.Fori(0, PAIRS) as i:
                    act.wait_ge(m["turned"], i + 1)
                    act.activation(un[:, :, :], g.q[:, ds(i * 2, 2), :], ACT.Copy).then_inc(m["copied"], 1)
                    act.wait_ge(m["att_turned"], i + 2)
                    act.wait_ge(m["projected"], i + 1)
                    act.activation(at[:, :, :], pt2[:, :, :], ACT.Copy).then_inc(m["at_ready"], 1)

            @block.tensor
            def _(pe):
                pe.wait_ge(loaded, 32)
                with pe.Fori(0, PAIRS) as i:
                    before, now = i + 1, i + 2
                    pe.wait_ge(m["copied"], now)
                    pe.wait_ge(m["qt_ready"], before)
                    turn_pair(pe, g, pt, un).then_inc(m["turned"], 1)
                    pe.wait_ge(m["qt_ready"], now)
                    pe.wait_ge(m["att_ready"], before)
                    for t in range(2):
                        for k in range(KD):
                            mm = pe.matmul(pa[:, t, :], qt[:, k, t * P:(t + 1) * P], g.kvm[:, k, :], start=(k == 0), stop=(k == KD - 1))
                    mm.then_inc(m["attended"], 1)
                    pe.wait_ge(m["att_ready"], now)
                    pe.wait_ge(m["at_ready"], before)
                    turn_pair(pe, g, pt2, att).then_inc(m["att_turned"], 1)
                    pe.wait_ge(m["at_ready"], now)
                    pe.wait_ge(m["kept"], before)
                    for t in range(2):
                        for k in range(KD):
                            mm = pe.matmul(po[:, t, :], at[:, k, t * P:(t + 1) * P], w[:, k, :], start=(k == 0), stop=(k == KD - 1))
                    mm.then_inc(m["projected"], 1)

            @block.vector
            def _(dve):
                dve.wait_ge(loaded, 32)
                with dve.Fori(0, PAIRS) as i:
                    before, now = i + 1, i + 2
                    link = Chain(dve, chain, i + 1)
                    dve.wait_ge(m["turned"], now)
                    dve.wait_ge(m["attended"], before)
                    dve.tensor_copy(qt[:, :, :], pt[:, :, :]).then_inc(m["qt_ready"], 1)
                    dve.wait_ge(m["attended"], now)
                    dve.wait_ge(m["att_turned"], before)
                    dve.tensor_tensor(att[:, :, :], pa[:, :, :], g.v[:, ds(i * 2, 2), :], ALU.add).then_inc(m["att_ready"], 1)
                    dve.wait_ge(m["projected"], now)
                    link(dve.tensor_tensor(o[:, :, :], po[:, :, :], over(bias[:, :], 1, [P, 2, D]), ALU.add))
                    dve.tensor_tensor(g.x[:, ds(i * 2, 2), :], g.x[:, ds(i * 2, 2), :], o[:, :, :], ALU.add).then_inc(m["kept"], 1)


def route1(nc, g, a):
    E = EXPERTS1
    CAP = float(math.ceil(NODES * 1.25 / E))
    with Room(nc, "ro") as r:
        part = r.sbuf("part", [P, 2, D])
        xm = r.sbuf("xm", [P, KD, P])
        wr = r.sbuf("wr", [P, KD, E])
        br = r.sbuf("br", [P, E])
        lg = r.sbuf("lg", [P, 3, 1, E])
        st = r.sbuf("st", [P, 4])
        hot = r.sbuf("hot", [P, 2])
        offs = r.sbuf("offs", [P, 8])
        offi = r.sbuf("offi", [P, 8], I32)
        rowf = r.sbuf("rowf", [P, 2, 8])
        rowi = r.sbuf("rowi", [P, 2, 8], I32)
        picks = Picks(r, E, 1)
        px = [r.psum(f"px{k}", [P, P]) for k in range(KD)]
        pl = r.psum("pl", [P, E])
        b2 = r.sbuf("b2", [P, 2, D])
        (loaded, made, parted, summed, xm_ready, logits, asked, exped, gapped, gap_exped, rows_ready, gathered, biased) = (
            r.sem(n) for n in ("loaded", "made", "parted", "summed", "xm_ready", "logits", "asked", "exped", "gapped", "gap_exped",
                               "rows_ready", "gathered", "biased"))
        step = r.sem("step")
        with nc.Block() as block:

            @block.sync
            def _(sp):
                sp.dma_start(wr[:, :, :], weights(a["wr"])).then_inc(loaded, 16)
                sp.dma_start(br[:, :], to_all(a["br"], E)).then_inc(loaded, 16)

            @block.gpsimd
            def _(pool):
                for k in range(4):
                    ins = pool.iota(offi[:, k:k + 1], pattern=[[0, 1]], base=k * P, channel_multiplier=1)
                ins = pool.memset(offi[:, 4:8], 0)
                ins.then_inc(made, 1)
                pool.wait_ge(rows_ready, 1)
                at = lambda j, k: bass.IndirectOffsetOnAxis(ap=rowi[:, j, k:k + 1], axis=0)
                for j in range(2):
                    for k in range(KD):
                        pool.indirect_dma_start(out=g.fw1[:, j, k, :], out_offset=None, in_=a["fw1"], in_offset=at(j, k)).then_inc(gathered, 16)
                    for k in range(KF):
                        pool.indirect_dma_start(out=g.fw2[:, j, k, :], out_offset=None, in_=a["fw2"], in_offset=at(j, 2 + k)).then_inc(gathered, 16)
                    pool.indirect_dma_start(out=g.fb1[:, j, :], out_offset=None, in_=a["fb1"], in_offset=at(j, 6)).then_inc(gathered, 16)
                    pool.indirect_dma_start(out=b2[:, j, :], out_offset=None, in_=a["fb2"], in_offset=at(j, 7)).then_inc(gathered, 16)
                pool.wait_ge(gathered, 16 * 2 * (KD + KF + 2))

            @block.tensor
            def _(pe):
                pe.wait_ge(parted, 1)
                for k in range(KD):
                    mm = pe.matmul(px[k][:, :], part[:, 1, k * P:(k + 1) * P], g.ones[:, :], start=True, stop=True)
                mm.then_inc(summed, 1)
                pe.wait_ge(xm_ready, 1)
                pe.wait_ge(loaded, 32)
                for k in range(KD):
                    mm = pe.matmul(pl[:, :], xm[:, k, :], wr[:, k, :], start=(k == 0), stop=(k == KD - 1))
                mm.then_inc(logits, 1)

            @block.scalar
            def _(act):
                for n in range(2):
                    act.wait_ge(asked, n + 1)
                    act.activation(lg[:, 1, 0, :], lg[:, 0, 0, :], ACT.Exp).then_inc(exped, 1)
                act.wait_ge(gapped, 1)
                act.activation(picks.small[:, 7, :], picks.small[:, 4, :], ACT.Exp).then_inc(gap_exped, 1)

            @block.vector
            def _(dve):
                count = [0]

                def link(ins):
                    count[0] += 1
                    ins.then_inc(step, 1)
                    dve.wait_ge(step, count[0])

                link(picks.order_of(dve))
                link(dve.tensor_reduce(part[:, 0, :], g.u[:, 0:FULL, :].rearrange("p t d -> p d t"), AX, ALU.add))
                dve.scalar_tensor_tensor(out=part[:, 1, :], in0=g.u[:, FULL, :], scalar=g.valid[:, FULL:FULL + 1], in1=part[:, 0, :],
                                         op0=ALU.mult, op1=ALU.add).then_inc(parted, 1)
                dve.wait_ge(summed, 1)
                for k in range(KD):
                    ins = dve.tensor_scalar(xm[:, k, :], px[k][:, :], 1.0 / NODES, None, ALU.mult)
                ins.then_inc(xm_ready, 1)
                dve.wait_ge(logits, 1)
                link(dve.tensor_tensor(lg[:, 0, 0, :], pl[:, :], br[:, :], ALU.add))
                link(dve.tensor_reduce(st[:, 0:1], lg[:, 0, 0, :], AX, ALU.max))
                for n in range(2):
                    dve.tensor_scalar(lg[:, 0, 0, :], lg[:, 0, 0, :], st[:, 0:1], None, ALU.subtract).then_inc(asked, 1)
                    dve.wait_ge(exped, n + 1)
                    link(dve.tensor_reduce(st[:, 1:2], lg[:, 1, 0, :], AX, ALU.add))
                    link(dve.reciprocal(st[:, 1:2], st[:, 1:2]))
                    link(dve.tensor_scalar(lg[:, 1, 0, :], lg[:, 1, 0, :], st[:, 1:2], None, ALU.mult))
                    if n == 0:
                        link(dve.tensor_scalar(lg[:, 2, 0, :], lg[:, 1, 0, :], float(NODES), None, ALU.mult))
                        link(dve.reciprocal(lg[:, 2, 0, :], lg[:, 2, 0, :]))
                        link(dve.tensor_scalar(lg[:, 2, 0, :], lg[:, 2, 0, :], CAP, 1.0, ALU.mult, ALU.min))
                        link(dve.tensor_tensor(lg[:, 0, 0, :], lg[:, 1, 0, :], lg[:, 2, 0, :], ALU.mult))
                        link(dve.tensor_reduce(st[:, 0:1], lg[:, 0, 0, :], AX, ALU.max))

                def wait_exp(ins):
                    ins.then_inc(gapped, 1)
                    dve.wait_ge(gap_exped, 1)

                link(pick_two(dve, link, lg[:, 1, :, :], picks, E, 1, wait_exp))
                link(dve.tensor_copy(g.fw[:, :], picks.small[:, 5:7, 0]))
                dve.wait_ge(made, 1)
                link(dve.tensor_copy(offs[:, :], offi[:, :]))
                for j in range(2):
                    e = picks.small[:, 2 + j, :]
                    for at, n, size in ((0, KD, D), (2, KF, F1), (6, 1, P), (7, 1, 1)):
                        base = offs[:, 0:n] if at != 7 else offs[:, 4:5]
                        link(dve.scalar_tensor_tensor(out=rowf[:, j, at:at + n], in0=e.to_broadcast([P, n]), scalar=float(size), in1=base,
                                                      op0=ALU.mult, op1=ALU.add))
                dve.tensor_copy(rowi[:, :, :], rowf[:, :, :]).then_inc(rows_ready, 1)
                dve.wait_ge(gathered, 16 * 2 * (KD + KF + 2))
                link(dve.tensor_scalar(b2[:, 0, :], b2[:, 0, :], g.fw[:, 0:1], None, ALU.mult))
                link(dve.scalar_tensor_tensor(out=g.fb2[:, :], in0=b2[:, 1, :], scalar=g.fw[:, 1:2], in1=b2[:, 0, :], op0=ALU.mult, op1=ALU.add))


def experts1(nc, g, a, out):
    with Room(nc, "fe") as r:
        gamma, beta = r.sbuf("gamma", [P, D]), r.sbuf("beta", [P, D])
        un = r.sbuf("un", [P, 2, D])
        xt = r.sbuf("xt", [P, KD, PW])
        h = r.sbuf("h", [P, 2, KF, PW])
        z = r.sbuf("z", [P, 2, D])
        junk = r.sbuf("junk", [P, 2, D])
        stat = r.sbuf("stat", [P, 3, 2])
        pt = r.psum("pt", [P, KD, PW])
        ph = [[r.psum(f"ph{j}{c}", [P, 2, PW]) for c in range(2)] for j in range(2)]
        po = [r.psum(f"po{j}", [P, 2, D]) for j in range(2)]
        loaded, stored, passed = r.sem("loaded"), r.sem("stored"), r.sem("passed")
        m = {n: r.sem(n) for n in ("copied", "turned", "xt_ready", "hidden0", "hidden1", "h0_ready", "h1_ready", "projected",
                                   "var_ready", "std_ready", "mixed", "res_ready")}
        chain = r.sems("step", 16)
        credit(nc, list(m.values()))
        with nc.Block() as block:

            @block.sync
            def _(sp):
                sp.dma_start(gamma[:, :], to_all(a["fg"], D)).then_inc(loaded, 16)
                sp.dma_start(beta[:, :], to_all(a["fb"], D)).then_inc(loaded, 16)
                sp.wait_ge(loaded, 32)
                sp.wait_ge(m["res_ready"], PAIRS + 1)
                sp.dma_start(out[0:FULL * P, :].rearrange("(t p) c -> p t c", p=P), g.x[:, 0:FULL, :]).then_inc(stored, 16)
                sp.dma_start(out[FULL * P:NODES, :], g.x[0:REST, FULL, :]).then_inc(stored, 16)
                sp.wait_ge(stored, 32)

            @block.scalar
            def _(act):
                with act.Fori(0, PAIRS) as i:
                    before, now = i + 1, i + 2
                    act.wait_ge(m["turned"], before)
                    act.wait_ge(m["mixed"], before)
                    act.activation(un[:, :, :], g.u[:, ds(i * 2, 2), :], ACT.Copy).then_inc(m["copied"], 1)
                    act.wait_ge(m["projected"], before)
                    for j in range(2):
                        act.wait_ge(m[f"hidden{j}"], now)
                        for c in range(KF):
                            ins = act.activation(h[:, j, c, :], ph[j][c // 2][:, c % 2, :], ACT.Gelu, bias=g.fb1[:, j, c:c + 1])
                        ins.then_inc(m[f"h{j}_ready"], 1)
                    act.wait_ge(m["var_ready"], now)
                    act.activation(stat[:, 2, :], stat[:, 1, :], ACT.Sqrt).then_inc(m["std_ready"], 1)

            @block.tensor
            def _(pe):
                with pe.Fori(0, PAIRS) as i:
                    before, now = i + 1, i + 2
                    pe.wait_ge(m["copied"], now)
                    pe.wait_ge(m["xt_ready"], before)
                    turn_pair(pe, g, pt, un).then_inc(m["turned"], 1)
                    pe.wait_ge(m["xt_ready"], now)
                    pe.wait_ge(m["h1_ready"], before)
                    for j in range(2):
                        for c in range(KF):
                            for k in range(KD):
                                mm = pe.matmul(ph[j][c // 2][:, c % 2, :], g.fw1[:, j, k, c * P:(c + 1) * P], xt[:, k, :],
                                               start=(k == 0), stop=(k == KD - 1))
                        mm.then_inc(m[f"hidden{j}"], 1)
                    pe.wait_ge(m["mixed"], before)
                    for j in range(2):
                        pe.wait_ge(m[f"h{j}_ready"], now)
                        for t in range(2):
                            for k in range(KF):
                                mm = pe.matmul(po[j][:, t, :], h[:, j, k, t * P:(t + 1) * P], g.fw2[:, j, k, :], start=(k == 0), stop=(k == KF - 1))
                    mm.then_inc(m["projected"], 1)

            @block.vector
            def _(dve):
                dve.wait_ge(loaded, 32)
                with dve.Fori(0, PAIRS) as i:
                    before, now = i + 1, i + 2
                    link = Chain(dve, chain, i + 1)
                    dve.wait_ge(m["turned"], now)
                    dve.wait_ge(m["hidden1"], before)
                    dve.tensor_copy(xt[:, :, :], pt[:, :, :]).then_inc(m["xt_ready"], 1)
                    dve.wait_ge(m["copied"], now)
                    dve.wait_ge(m["res_ready"], before)
                    link(dve.tensor_tensor(z[:, :, :], un[:, :, :], over(g.fb2[:, :], 1, [P, 2, D]), ALU.add))
                    dve.wait_ge(m["projected"], now)
                    for j in range(2):
                        ins = dve.scalar_tensor_tensor(out=z[:, :, :], in0=po[j][:, :, :], scalar=g.fw[:, j:j + 1], in1=z[:, :, :],
                                                       op0=ALU.mult, op1=ALU.add)
                        if j == 0:
                            link(ins)
                    ins.then_inc(m["mixed"], 1)
                    dve.wait_ge(m["mixed"], now)
                    ln_pair(dve, link, z[:, :, :], stat, junk, lambda ins: ins.then_inc(m["var_ready"], 1),
                            lambda: dve.wait_ge(m["std_ready"], now))
                    link(dve.tensor_tensor(z[:, :, :], z[:, :, :], over(gamma[:, :], 1, [P, 2, D]), ALU.mult))
                    link(dve.tensor_tensor(z[:, :, :], z[:, :, :], over(beta[:, :], 1, [P, 2, D]), ALU.add))
                    dve.tensor_tensor(g.x[:, ds(i * 2, 2), :], g.x[:, ds(i * 2, 2), :], z[:, :, :], ALU.add).then_inc(m["res_ready"], 1)


class Shared:
    pass


def gps_kernel(nc, a, out, scratch):
    with Room(nc, "g") as room:
        g = Shared()
        g.x = room.sbuf("x", [P, NT, D])
        g.u = room.sbuf("u", [P, NT, D])
        g.ut = room.sbuf("ut", [P, KD, NPAD])
        g.idx = room.sbuf("idx", [P, ET, 4], I32)
        g.kinds = room.sbuf("kinds", [P, ET, 4])
        g.ident = room.sbuf("ident", [P, P])
        g.identb = room.sbuf("identb", [P, P], BF16)
        g.ones = room.sbuf("ones", [P, P])
        g.lower = room.sbuf("lower", [P, P])
        g.picks = room.sbuf("picks", [P, H0, P])
        g.spill = room.sbuf("spill", [P, 1])
        g.valid = room.sbuf("valid", [P, NT])
        g.g0 = room.sbuf("g0", [P, NT])
        g.usum = room.sbuf("usum", [P, KD])
        g.bn_scale = room.sbuf("bn_scale", [P, QKV])
        g.bn_beta = room.sbuf("bn_beta", [P, QKV])
        g.rowf = room.sbuf("rowf", [P, ET, 2])
        g.tabs0 = [scratch(f"tabs0_{k}", (TROWS, H0 * (D0 + 1) + H0), F32) for k in range(NTAB)]
        g.hid = g.ut[:, :, :].rearrange("p k n -> p (k n)").rearrange("p (t d) -> p t d", d=D)
        g.qrows = scratch("qrows", (NPAD, D), F32)
        g.kvrows = scratch("kvrows", (NPAD, 2 * D), F32)
        g.tabs1 = [scratch(f"tabs1_{k}", (TROWS, ROW1), F32) for k in range(NTAB)]
        g.hc = scratch("hc", (NPAD, QKV), F32)
        g.table0 = scratch("table0", (NPAD, ROW0), F32)
        load_inputs(nc, g, a)
        normalize(nc, g, "norm0", g.g0[:, :])
        log_scale(nc, g)
        node_rows(nc, g, a)
        mix_stats(nc, g, a)
        mix(nc, g, a)
        spill_duplicates(nc, g)
        attend0(nc, g, a)
        merge0(nc, g, a)
        normalize(nc, g, "norm1")
        experts0(nc, g, a)
        normalize(nc, g, "norm2")
        enter1(nc, g, a)
        with nc.Fori(0, LAYERS) as l:
            project1(nc, g, a, l)
            attend1(nc, g)
            update1(nc, g, a, l)
        adjust1(nc, g, a)
        with Room(nc, "m1") as r:
            g.q = g.hid
            g.v = r.sbuf("v", [P, NT, D])
            g.kvm = r.sbuf("kvm", [P, KD, D])
            mix1_keys(nc, g, a)
            mix1_out(nc, g, a)
        normalize(nc, g, "norm3")
        with Room(nc, "f1") as r:
            g.fw1 = r.sbuf("fw1", [P, 2, KD, F1])
            g.fw2 = r.sbuf("fw2", [P, 2, KF, D])
            g.fb1 = r.sbuf("fb1", [P, 2, KF])
            g.fb2 = r.sbuf("fb2", [P, D])
            g.fw = r.sbuf("fw", [P, 2])
            route1(nc, g, a)
            experts1(nc, g, a, out)


def _layout(v):
    import numpy as _np

    n = {k: _np.asarray(t) for k, t in v.items()}
    f = _np.float32
    ea = _np.zeros((P * ET, 3), f)
    ea[:EDGES] = n["edge_attr_3"]
    ablk = _np.zeros((D, 2 * H0), f)
    for h in range(H0):
        ablk[h * D0:(h + 1) * D0, h] = n["L0_gnn_a_src"][h]
        ablk[h * D0:(h + 1) * D0, H0 + h] = n["L0_gnn_a_dst"][h]
    pw = _np.zeros((QKV, P), f)
    for grp in range(QKV // GD):
        c = (grp * GD) % P
        pw[grp * GD:(grp + 1) * GD, c:c + GD] = n["L0_mix_w_pw"][grp * GD:(grp + 1) * GD, :, 0].T
    t = lambda w: _np.swapaxes(w, -1, -2)
    flat = lambda w: w.reshape(-1, w.shape[-1])
    return dict(
        x=n["x"], src=n["src"], dst=n["dst"], kind=n["edge_type_3"],
        ea=ea.reshape(P, ET, 3).transpose(2, 1, 0),
        gW=n["L0_gnn_W"], gWT=t(n["L0_gnn_W"]), ablk=ablk, eWT=t(n["L0_gnn_edge_W"]),
        eb=n["L0_gnn_edge_b"], gbias=n["L0_gnn_bias"],
        wqkv=t(n["L0_mix_w_qkv"][:, :, 2]), gamma=n["L0_mix_bn_gamma"], beta=n["L0_mix_bn_beta"],
        wdw=n["L0_mix_w_dw"][:, 0, 2].reshape(-1, P).T, pw=pw, wres=t(n["L0_mix_w_res"][:, :, 0]), bres=n["L0_mix_b_res"],
        rw1=n["L0_ffn_router_w1"], rb1=n["L0_ffn_router_b1"].reshape(P, 1), rw2=n["L0_ffn_router_w2"], rb2=n["L0_ffn_router_b2"],
        ew1=flat(n["L0_ffn_expert_w1"]), eb1=n["L0_ffn_expert_b1"].reshape(-1, P).T, ew2=flat(n["L0_ffn_expert_w2"]), eb2=n["L0_ffn_expert_b2"].reshape(-1, P).T,
        ew3=flat(n["L0_ffn_expert_w3"]), eb3=n["L0_ffn_expert_b3"],
        winT=t(n["L1_gnn_Win"]), b_in=n["L1_gnn_b_in"],
        wqT=flat(t(n["L1_gnn_Wq"])), bq=n["L1_gnn_bq"], wkT=flat(t(n["L1_gnn_Wk"])), bk=n["L1_gnn_bk"],
        wvT=flat(t(n["L1_gnn_Wv"])), bv=n["L1_gnn_bv"], eemb=flat(t(n["L1_gnn_Eemb"])),
        woT=flat(t(n["L1_gnn_Wo"])), bo=n["L1_gnn_bo"], ln_g=n["L1_gnn_ln_g"], ln_b=n["L1_gnn_ln_b"],
        w1T=t(n["L1_gnn_W1"]), b1=n["L1_gnn_b1"].reshape(-1, P).T, w2T=t(n["L1_gnn_W2"]), b2=n["L1_gnn_b2"],
        mqkv=n["L1_mix_W_qkv"], mb=n["L1_mix_b_qkv"], mout=n["L1_mix_W_out"], mbo=n["L1_mix_b_out"],
        wr=n["L1_ffn_Wr"], br=n["L1_ffn_br"], fw1=flat(n["L1_ffn_W1"]), fb1=n["L1_ffn_b1"].reshape(EXPERTS1, KF, P).transpose(0, 2, 1).reshape(-1, KF),
        fw2=flat(n["L1_ffn_W2"]), fb2=n["L1_ffn_b2"], fg=n["L1_ffn_gamma"], fb=n["L1_ffn_beta"],
    )


def kernel(**inputs):
    import numpy as _np
    import concourse.bacc as _bacc
    from concourse import mybir as _mybir
    from concourse.bass_utils import run_bass_kernel_spmd as _run

    nc = _bacc.Bacc("TRN2", target_bir_lowering=False, num_devices=1)
    arrays, drams = {}, {}
    for name, v in _layout(inputs).items():
        v = _np.ascontiguousarray(v)
        arrays[f"in_{name}_dram"] = v
        drams[name] = nc.dram_tensor(f"in_{name}_dram", v.shape, _mybir.dt.from_np(v.dtype), kind="ExternalInput").ap()
    out = nc.dram_tensor("out_0_dram", (NODES, D), F32, kind="ExternalOutput").ap()

    def scratch(name, shape, dt):
        return nc.dram_tensor(name, shape, dt, kind=SCRATCH).ap()

    gps_kernel(nc, drams, out, scratch)
    r = _run(nc, [arrays], core_ids=[0])
    return r.results[0]["out_0_dram"]


SCRATCH = "Internal"
```

```python
import math
from contextlib import ExitStack

import numpy as np

import concourse.bass as bass
from concourse import mybir

F32 = mybir.dt.float32
BF16 = mybir.dt.bfloat16
I32 = mybir.dt.int32
ALU = mybir.AluOpType
ACT = mybir.ActivationFunctionType
AX = mybir.AxisListType.X
ds = bass.ds

P = 128
NODES = 3125
D = 256
KD = D // P
NT = 26
NPAD = NT * P
PAIRS = NT // 2
PW = 2 * P
FULL = NODES // P
REST = NODES - FULL * P
EDGES = 50000
ET = 392
U = 4
TURNS = ET // U
LASTP = EDGES // ET
LASTN = EDGES - LASTP * ET
H0, D0 = 8, 32
ROW0 = D + 2 * H0
ACC0 = H0 * (D0 + 1)
HG, DG = 4, 64
ROW1 = D + 4
TROWS = NPAD + P
NTAB = 4
LAYERS = 3
QKV = 3 * D
GRP, GD = 16, 32
EXPERTS0 = 6
EXPERTS1, F1, KF = 8, 512, 4
LOWEST = -3.0e38
EPS = 1e-5
BALL = float(np.float32(1.0 - 1e-5))
ATANH_BALL = 0.5 * math.log((1.0 + BALL) / (1.0 - BALL))
MIN_NORM = 1e-15
ATT_EPS = 1e-15


class Room:

    def __init__(self, nc, name):
        self.nc, self.name, self.ctx, self.taken = nc, name, ExitStack(), []

    def __enter__(self):
        return self

    def __exit__(self, *a):
        self.nc.clear_and_free_semaphores(self.taken)
        self.nc.all_engine_barrier()
        return self.ctx.__exit__(*a)

    def sbuf(self, name, shape, dt=F32):
        return self.ctx.enter_context(self.nc.sbuf_tensor(f"{self.name}_{name}", shape, dt))

    def psum(self, name, shape, dt=F32):
        return self.ctx.enter_context(self.nc.psum_tensor(f"{self.name}_{name}", shape, dt))

    def sem(self, name):
        self.taken.append(self.nc.alloc_semaphore(f"{self.name}_{name}"))
        return self.taken[-1]

    def sems(self, name, n):
        return [self.sem(f"{name}{i}") for i in range(n)]


class Chain:

    def __init__(self, eng, sems, turn):
        self.eng, self.sems, self.turn, self.n = eng, sems, turn, 0

    def __call__(self, ins):
        ins.then_inc(self.sems[self.n], 1)
        self.eng.wait_ge(self.sems[self.n], self.turn)
        self.n += 1


def credit(nc, sems, n=1):
    with nc.Block() as block:

        @block.sync
        def _(sp):
            for s in sems:
                sp.sem_inc(s, n)


def hold(eng, sem, value, passed):
    eng.wait_ge(sem, value)
    eng.sem_inc(passed)


def over(ap, axis, shape):
    return ap.unsqueeze(axis).to_broadcast(shape)


def weights(w):
    return w.rearrange("(k p) n -> p k n", p=P)


def to_all(v, n):
    return v.rearrange("(a n) -> a n", a=1).to_broadcast([P, n])


def rows(t, i, width=PW):
    return t[ds(i * width, width), :].rearrange("(t p) c -> p t c", p=P)


def load_inputs(nc, g, a):
    with Room(nc, "load") as r:
        idx1 = [r.sbuf(f"idx{i}", [P, ET], I32) for i in range(3)]
        tf = r.sbuf("typef", [P, ET])
        pi = r.sbuf("pidx", [P, 1], I32)
        pads, loaded = r.sem("pads_ready"), r.sem("loaded")
        steps, made, pool = r.sem("steps"), r.sem("made"), r.sem("pool")
        with nc.Block() as block:

            @block.vector
            def _(dve):
                dve.memset(g.x[:, FULL:NT, :], 0.0).then_inc(pads, 1)
                for i in range(2):
                    dve.memset(idx1[i][96:P, :], NPAD - 1).then_inc(pads, 1)
                dve.memset(idx1[2][96:P, :], 0).then_inc(pads, 1)
                dve.memset(g.ones[:, :], 1.0)
                dve.memset(g.valid[:, 0:FULL], 1.0)
                dve.memset(g.valid[:, FULL:NT], 0.0).then_inc(steps, 1)
                dve.wait_ge(steps, 1)
                dve.memset(g.valid[0:REST, FULL:FULL + 1], 1.0).then_inc(steps, 1)
                dve.wait_ge(loaded, 16 * 10)
                for i in range(2):
                    dve.tensor_copy(g.idx[:, :, i], idx1[i][:, :])
                dve.tensor_copy(tf[:, :], idx1[2][:, :]).then_inc(steps, 1)
                dve.wait_ge(steps, 3)
                for j in range(3):
                    dve.tensor_scalar(g.kinds[:, :, j], tf[:, :], float(j), None, ALU.is_equal)
                dve.memset(g.kinds[:, :, 3], 1.0).then_inc(steps, 1)
                dve.wait_ge(made, 4)
                dve.tensor_copy(g.identb[:, :], g.ident[:, :])
                dve.tensor_copy(g.spill[:, :], pi[:, :])
                dve.wait_ge(steps, 4)

            @block.gpsimd
            def _(pool_):
                pool_.memset(g.ident[:, :], 0.0).then_inc(pool, 1)
                pool_.memset(g.lower[:, :], 1.0).then_inc(pool, 1)
                pool_.wait_ge(pool, 2)
                pool_.affine_select(out=g.ident[:, :], in_=g.ident[:, :], compare_op=ALU.not_equal, fill=1.0,
                                    base=0, pattern=[[-1, P]], channel_multiplier=1).then_inc(made, 1)
                pool_.affine_select(out=g.lower[:, :], in_=g.lower[:, :], compare_op=ALU.is_gt, fill=0.0,
                                    base=0, pattern=[[-1, P]], channel_multiplier=1).then_inc(made, 1)
                pool_.iota(pi[:, :], pattern=[[0, 1]], base=NPAD, channel_multiplier=1).then_inc(made, 1)
                pool_.memset(g.picks[:, :, :], 0.0).then_inc(pool, 1)
                pool_.wait_ge(pool, 3)
                pool_.affine_select(out=g.picks[:, :, :], in_=g.picks[:, :, :], compare_op=ALU.not_equal, fill=1.0,
                                    base=0, pattern=[[-1, H0], [0, P]], channel_multiplier=1).then_inc(made, 1)

            @block.sync
            def _(sp):
                sp.dma_start(g.bn_scale[:, :], to_all(a["gamma"], QKV)).then_inc(loaded, 16)
                sp.dma_start(g.bn_beta[:, :], to_all(a["beta"], QKV)).then_inc(loaded, 16)
                sp.wait_ge(pads, 4)
                sp.dma_start(g.x[:, 0:FULL, :], a["x"][0:FULL * P, :].rearrange("(t p) c -> p t c", p=P)).then_inc(loaded, 16)
                for i, v in enumerate((a["src"], a["dst"], a["kind"])):
                    sp.dma_start(idx1[i][0:LASTP, :], v[0:LASTP * ET].rearrange("(p j) -> p j", j=ET)).then_inc(loaded, 16)
                    sp.dma_start(idx1[i][LASTP:P, 0:LASTN], v[LASTP * ET:EDGES].rearrange("(p j) -> p j", p=1)).then_inc(loaded, 16)
                sp.dma_start(g.x[0:REST, FULL, :], a["x"][FULL * P:NODES, :]).then_inc(loaded, 16)
                sp.wait_ge(loaded, 16 * 10)


def normalize(nc, g, name, squares=None):
    with Room(nc, name) as r:
        sq = r.sbuf("sq", [P, NT, D])
        st = r.sbuf("st", [P, 4, NT])
        step = r.sem("step")
        centred, squared, var, std = r.sem("centred"), r.sem("squared"), r.sem("var_ready"), r.sem("std_ready")
        with nc.Block() as block:

            @block.vector
            def _(dve):
                dve.tensor_reduce(st[:, 0, :], g.x[:, :, :], AX, ALU.add).then_inc(step, 1)
                dve.wait_ge(step, 1)
                dve.tensor_scalar(st[:, 1, :], st[:, 0, :], -1.0 / D, None, ALU.mult).then_inc(step, 1)
                dve.wait_ge(step, 2)
                dve.tensor_tensor(g.u[:, :, :], g.x[:, :, :], over(st[:, 1, :], 2, [P, NT, D]), ALU.add).then_inc(centred, 1)
                dve.wait_ge(squared, 1)
                dve.tensor_reduce(st[:, 0, :], sq[:, :, :], AX, ALU.add).then_inc(step, 1)
                dve.wait_ge(step, 3)
                dve.tensor_scalar(st[:, 2, :], st[:, 0, :], 1.0 / D, EPS, ALU.mult, ALU.add).then_inc(var, 1)
                dve.wait_ge(var, 1)
                dve.wait_ge(std, 1)
                dve.reciprocal(st[:, 2, :], st[:, 3, :]).then_inc(step, 1)
                dve.wait_ge(step, 4)
                dve.tensor_tensor(g.u[:, :, :], g.u[:, :, :], over(st[:, 2, :], 2, [P, NT, D]), ALU.mult).then_inc(step, 1)
                if squares is not None:
                    dve.tensor_tensor(st[:, 3, :], st[:, 2, :], st[:, 2, :], ALU.mult).then_inc(step, 1)
                    dve.wait_ge(step, 6)
                    dve.tensor_tensor(squares, st[:, 3, :], st[:, 0, :], ALU.mult).then_inc(step, 1)

            @block.scalar
            def _(act):
                act.wait_ge(centred, 1)
                act.activation(sq[:, :, :], g.u[:, :, :], ACT.Square).then_inc(squared, 1)
                act.wait_ge(var, 1)
                act.activation(st[:, 3, :], st[:, 2, :], ACT.Sqrt).then_inc(std, 1)


def log_scale(nc, g):
    SMALL = 0.25
    with Room(nc, "logs") as r:
        w = r.sbuf("w", [P, 10, NT])
        n, nn, z, poly, one_m, q, ln, rn, mask, tmp = (w[:, i, :] for i in range(10))
        step, rooted, ratio, logged, asked = r.sem("step"), r.sem("norm_ready"), r.sem("ratio_ready"), r.sem("log_ready"), r.sem("asked")
        with nc.Block() as block:

            @block.vector
            def _(dve):
                count = [0]

                def link(ins):
                    count[0] += 1
                    ins.then_inc(step, 1)
                    dve.wait_ge(step, count[0])

                dve.wait_ge(rooted, 1)
                link(dve.tensor_scalar(n, n, MIN_NORM, None, ALU.max))
                link(dve.tensor_scalar(nn, n, BALL, None, ALU.min))
                link(dve.tensor_scalar(one_m, nn, -1.0, 1.0, ALU.mult, ALU.add))
                link(dve.reciprocal(q, one_m))
                link(dve.tensor_scalar(tmp, nn, 1.0, None, ALU.add))
                dve.tensor_tensor(q, tmp, q, ALU.mult).then_inc(ratio, 1)
                link(dve.tensor_tensor(z, nn, nn, ALU.mult))
                link(dve.tensor_scalar(poly, z, 1.0 / 13, 1.0 / 11, ALU.mult, ALU.add))
                for c in (9, 7, 5, 3, 1):
                    link(dve.tensor_tensor(poly, poly, z, ALU.mult))
                    link(dve.tensor_scalar(poly, poly, 1.0 / c, None, ALU.add))
                link(dve.reciprocal(rn, n))
                dve.wait_ge(logged, 1)
                link(dve.scalar_tensor_tensor(out=ln, in0=ln, scalar=0.5, in1=rn, op0=ALU.mult, op1=ALU.mult))
                link(dve.tensor_scalar(mask, n, SMALL, None, ALU.is_lt))
                link(dve.tensor_tensor(tmp, poly, ln, ALU.subtract))
                link(dve.tensor_tensor(tmp, tmp, mask, ALU.mult))
                link(dve.tensor_tensor(g.g0[:, :], tmp, ln, ALU.add))

            @block.scalar
            def _(act):
                act.activation(n, g.g0[:, :], ACT.Sqrt).then_inc(rooted, 1)
                act.wait_ge(ratio, 1)
                act.activation(ln, q, ACT.Ln).then_inc(logged, 1)


def node_rows(nc, g, a):
    with Room(nc, "rows") as r:
        wnat = r.sbuf("wnat", [P, KD, D])
        ablk = r.sbuf("ablk", [P, KD, 2 * H0])
        wall = r.sbuf("wall", [P, KD, ROW0])
        un = r.sbuf("un", [P, 2, D])
        uts = r.sbuf("uts", [P, KD, PW])
        gs = r.sbuf("gs", [P, 2])
        ho = r.sbuf("ho", [P, 2, ROW0])
        pt = r.psum("pt", [P, KD, PW])
        ph = [r.psum(f"ph{i}", [P, 512]) for i in range(2)]
        pu = r.psum("pu", [P, 512])
        pa = r.psum("pa", [P, 512])
        loaded, folded, wready = r.sem("loaded"), r.sem("folded"), r.sem("wall_ready")
        copied, turned, ut_kept, uts_ready = r.sem("pair_copied"), r.sem("pair_turned"), r.sem("ut_kept"), r.sem("uts_ready")
        summed, added, projected = r.sem("summed"), r.sem("sum_added"), r.sem("projected")
        ho_ready, stored, ho_sent, passed = r.sem("ho_ready"), r.sem("stored"), r.sem("ho_sent"), r.sem("passed")
        credit(nc, [copied, turned, ut_kept, uts_ready, summed, added, projected, ho_ready, ho_sent])
        with nc.Block() as block:

            @block.sync
            def _(sp):
                sp.dma_start(wnat[:, :, :], weights(a["gW"])).then_inc(loaded, 16)
                sp.dma_start(ablk[:, :, :], weights(a["ablk"])).then_inc(loaded, 16)
                sp.dma_start(wall[:, :, 0:D], weights(a["gWT"])).then_inc(loaded, 16)
                with sp.Fori(0, PAIRS) as i:
                    hold(sp, ho_ready, i + 2, passed)
                    sp.dma_start(rows(g.table0, i), ho[:, :, :]).then_inc(stored, 16)
                    hold(sp, stored, i * 16 + 16, ho_sent)

            @block.tensor
            def _(pe):
                pe.wait_ge(loaded, 48)
                for c in range(KD):
                    for k in range(KD):
                        mm = pe.matmul(pa[:, c * 16:c * 16 + 16], wnat[:, k, c * P:(c + 1) * P], ablk[:, k, :],
                                       start=(k == 0), stop=(k == KD - 1))
                mm.then_inc(folded, 1)
                pe.wait_ge(wready, 1)
                with pe.Fori(0, PAIRS) as i:
                    before, now = i + 1, i + 2
                    pe.wait_ge(copied, now)
                    pe.wait_ge(uts_ready, before)
                    for t in range(2):
                        for k in range(KD):
                            mm = pe.transpose(pt[:, k, t * P:(t + 1) * P], un[:, t, k * P:(k + 1) * P], g.ident[:, :])
                    mm.then_inc(turned, 1)
                    pe.wait_ge(added, before)
                    for k in range(KD):
                        for t in range(2):
                            mm = pe.matmul(pu[:, k:k + 1], un[:, t, k * P:(k + 1) * P], gs[:, t:t + 1],
                                           start=(t == 0), stop=(t == 1))
                    mm.then_inc(summed, 1)
                    pe.wait_ge(uts_ready, now)
                    pe.wait_ge(ho_ready, before)
                    for t in range(2):
                        for k in range(KD):
                            mm = pe.matmul(ph[t][:, 0:ROW0], uts[:, k, t * P:(t + 1) * P], wall[:, k, :],
                                           start=(k == 0), stop=(k == KD - 1))
                    mm.then_inc(projected, 1)

            @block.scalar
            def _(act):
                with act.Fori(0, PAIRS) as i:
                    before, now = i + 1, i + 2
                    act.wait_ge(summed, before)
                    act.activation(un[:, :, :], g.u[:, ds(i * 2, 2), :], ACT.Copy)
                    act.activation(gs[:, :], g.g0[:, ds(i * 2, 2)], ACT.Copy).then_inc(copied, 1)
                    act.wait_ge(uts_ready, now)
                    act.activation(g.ut[:, :, ds(i * PW, PW)], uts[:, :, :], ACT.Copy).then_inc(ut_kept, 1)

            @block.vector
            def _(dve):
                dve.memset(g.usum[:, :], 0.0)
                dve.wait_ge(folded, 1)
                dve.tensor_copy(wall[:, :, D:ROW0], pa[:, 0:KD * 16].rearrange("p (k n) -> p k n", k=KD)).then_inc(wready, 1)
                dve.wait_ge(wready, 1)
                with dve.Fori(0, PAIRS) as i:
                    before, now = i + 1, i + 2
                    dve.wait_ge(turned, now)
                    dve.wait_ge(projected, before)
                    dve.wait_ge(ut_kept, before)
                    dve.tensor_copy(uts[:, :, :], pt[:, :, :]).then_inc(uts_ready, 1)
                    dve.wait_ge(summed, now)
                    dve.tensor_tensor(g.usum[:, :], g.usum[:, :], pu[:, 0:KD], ALU.add).then_inc(added, 1)
                    dve.wait_ge(projected, now)
                    dve.wait_ge(ho_sent, before)
                    dve.tensor_copy(ho[:, 0, :], ph[0][:, 0:ROW0])
                    dve.tensor_copy(ho[:, 1, :], ph[1][:, 0:ROW0]).then_inc(ho_ready, 1)


HALF = QKV // 2
KQ = QKV // P


def mix_stats(nc, g, a):
    with Room(nc, "ms") as r:
        w = r.sbuf("w", [P, KD, QKV])
        umean = r.sbuf("umean", [P, KD, P])
        mean = r.sbuf("mean", [P, QKV])
        uts = r.sbuf("uts", [P, KD, PW])
        hc = r.sbuf("hc", [P, 2, QKV])
        sq = r.sbuf("sq", [P, 2, QKV])
        ssum = r.sbuf("ssum", [P, QKV])
        ph = [r.psum(f"ph{i}", [P, 512]) for i in range(4)]
        ps = [r.psum(f"ps{i}", [P, 512]) for i in range(2)]
        loaded, step, msent, mready = r.sem("loaded"), r.sem("step"), r.sem("mean_sent"), r.sem("mean_ready")
        um, std, var = r.sem("umean_ready"), r.sem("std_ready"), r.sem("var_ready")
        copied, projected, hc_ready, squared = r.sem("copied"), r.sem("projected"), r.sem("hc_ready"), r.sem("squared")
        summed, added, stored, hc_sent, passed = r.sem("summed"), r.sem("added"), r.sem("stored"), r.sem("hc_sent"), r.sem("passed")
        credit(nc, [copied, projected, hc_ready, squared, summed, added, hc_sent])
        with nc.Block() as block:

            @block.sync
            def _(sp):
                sp.dma_start(w[:, :, :], weights(a["wqkv"])).then_inc(loaded, 16)
                with sp.Fori(0, PAIRS) as i:
                    hold(sp, hc_ready, i + 2, passed)
                    sp.dma_start(rows(g.hc, i), hc[:, :, :]).then_inc(stored, 16)
                    hold(sp, stored, i * 16 + 16, hc_sent)

            @block.scalar
            def _(act):
                with act.Fori(0, PAIRS) as i:
                    before, now = i + 1, i + 2
                    act.wait_ge(projected, before)
                    act.activation(uts[:, :, :], g.ut[:, :, ds(i * PW, PW)], ACT.Copy).then_inc(copied, 1)
                    act.wait_ge(hc_ready, now)
                    act.wait_ge(summed, before)
                    act.activation(sq[:, 0, :], hc[:, 0, :], ACT.Square, scale=g.valid[:, ds(i * 2, 1)])
                    act.activation(sq[:, 1, :], hc[:, 1, :], ACT.Square, scale=g.valid[:, ds(i * 2 + 1, 1)]).then_inc(squared, 1)
                act.wait_ge(var, 1)
                act.activation(ssum[:, :], ssum[:, :], ACT.Sqrt).then_inc(std, 1)

            @block.tensor
            def _(pe):
                pe.wait_ge(loaded, 16)
                pe.wait_ge(um, 1)
                for h in range(2):
                    for k in range(KD):
                        mm = pe.matmul(ps[h][:, 0:HALF], umean[:, k, :], w[:, k, h * HALF:(h + 1) * HALF],
                                       start=(k == 0), stop=(k == KD - 1))
                mm.then_inc(msent, 1)
                pe.wait_ge(mready, 1)
                with pe.Fori(0, PAIRS) as i:
                    before, now = i + 1, i + 2
                    pe.wait_ge(copied, now)
                    pe.wait_ge(hc_ready, before)
                    for t in range(2):
                        for h in range(2):
                            for k in range(KD):
                                mm = pe.matmul(ph[2 * t + h][:, 0:HALF], uts[:, k, t * P:(t + 1) * P],
                                               w[:, k, h * HALF:(h + 1) * HALF], start=(k == 0), stop=(k == KD - 1))
                    mm.then_inc(projected, 1)
                    pe.wait_ge(squared, now)
                    pe.wait_ge(added, before)
                    for h in range(2):
                        for t in range(2):
                            mm = pe.matmul(ps[h][:, 0:HALF], g.ones[:, :], sq[:, t, h * HALF:(h + 1) * HALF],
                                           start=(t == 0), stop=(t == 1))
                    mm.then_inc(summed, 1)

            @block.vector
            def _(dve):
                dve.tensor_scalar(umean[:, :, :], over(g.usum[:, :], 2, [P, KD, P]), 1.0 / NODES, None, ALU.mult).then_inc(um, 1)
                dve.memset(ssum[:, :], 0.0)
                dve.wait_ge(msent, 1)
                for h in range(2):
                    ins = dve.tensor_copy(mean[:, h * HALF:(h + 1) * HALF], ps[h][:, 0:HALF])
                ins.then_inc(mready, 1)
                dve.wait_ge(mready, 1)
                with dve.Fori(0, PAIRS) as i:
                    before, now = i + 1, i + 2
                    dve.wait_ge(projected, now)
                    dve.wait_ge(hc_sent, before)
                    dve.wait_ge(squared, before)
                    for t in range(2):
                        for h in range(2):
                            c = slice(h * HALF, (h + 1) * HALF)
                            ins = dve.scalar_tensor_tensor(out=hc[:, t, c], in0=ph[2 * t + h][:, 0:HALF],
                                                           scalar=g.g0[:, ds(i * 2 + t, 1)], in1=mean[:, c],
                                                           op0=ALU.mult, op1=ALU.subtract)
                    ins.then_inc(hc_ready, 1)
                    dve.wait_ge(summed, now)
                    for h in range(2):
                        c = slice(h * HALF, (h + 1) * HALF)
                        ins = dve.tensor_tensor(ssum[:, c], ssum[:, c], ps[h][:, 0:HALF], ALU.add)
                    ins.then_inc(added, 1)
                hold(dve, added, PAIRS + 1, passed)
                dve.tensor_scalar(ssum[:, :], ssum[:, :], 1.0 / NODES, EPS, ALU.mult, ALU.add).then_inc(var, 1)
                dve.wait_ge(std, 1)
                dve.reciprocal(ssum[:, :], ssum[:, :]).then_inc(step, 1)
                dve.wait_ge(step, 1)
                dve.tensor_tensor(g.bn_scale[:, :], g.bn_scale[:, :], ssum[:, :], ALU.mult).then_inc(step, 1)


def mix(nc, g, a):
    with Room(nc, "mx") as r:
        bd = r.sbuf("bd", [P, KQ, P])
        wdw = r.sbuf("wdw", [P, KQ])
        wres = r.sbuf("wres", [P, 4, D])
        bres = r.sbuf("bres", [P, D])
        raw = r.sbuf("raw", [P, 2, QKV])
        rr = r.sbuf("r", [P, 2, 2, QKV])
        rt = r.sbuf("rt", [P, KQ, PW])
        s = r.sbuf("s", [P, 2, 2, QKV])
        junk = r.sbuf("junk", [P, 2, 2, QKV])
        junk_o = r.sbuf("junk_o", [P, 2, 512])
        junk_f = r.sbuf("junk_f", [P, 2, D])
        sm = r.sbuf("sm", [P, 11, 2])
        norms = r.sbuf("norms", [P, 2, 5, 2])
        ks = r.sbuf("ks", [P, 2, GRP])
        v = r.sbuf("v", [P, 2, GRP, GD])
        ve = r.sbuf("ve", [P, 2, GRP, GD])
        o = r.sbuf("o", [P, 2, GRP, GD])
        ot = r.sbuf("ot", [P, 4, PW])
        ft = r.sbuf("ft", [P, 2, D])
        prt = [r.psum(f"prt{i}", [P, 2, PW]) for i in range(3)]
        pss = [[r.psum(f"ps{t}{h}", [P, 512]) for h in range(2)] for t in range(2)]
        pf = r.psum("pf", [P, 2, D])
        c1, nc_, kap, tmp_b, c2, tmp_c, nf, th, tmp_d, scale_d = (sm[:, j, :] for j in range(10))
        nr, ns, ncat, no, root = ([norms[:, slot, j, :] for slot in range(2)] for j in range(5))
        loaded, scaled, ld, passed = (r.sem(n) for n in ("loaded", "scaled", "ld", "passed"))
        m = {n: r.sem(n) for n in ("bn_scaled", "bn_ready", "r_ready", "turned", "rt_ready", "mixed", "s_ready", "squared", "rooted", "s_relu", "o_ready", "o_squared",
                                   "o_rooted", "o_turned", "ot_ready", "final", "ft_ready", "f_squared", "f_rooted", "tanh_ready", "xdone")}
        chain_b, chain_c, chain_d = (r.sems(f"step_{n}", k) for n, k in (("b", 16), ("c", 3), ("d", 3)))
        credit(nc, list(m.values()), 2)

        def done(eng, name, n, lag=0):
            eng.wait_ge(m[name], n + (3 - lag))

        with nc.Block() as block:

            @block.sync
            def _(sp):
                sp.dma_start(bd[:, :, :], weights(a["pw"])).then_inc(loaded, 16)
                sp.dma_start(wdw[:, :], a["wdw"]).then_inc(loaded, 16)
                sp.dma_start(wres[:, :, :], weights(a["wres"])).then_inc(loaded, 16)
                sp.dma_start(bres[:, :], to_all(a["bres"], D)).then_inc(loaded, 16)
                with sp.Fori(0, PAIRS) as i:
                    hold(sp, m["bn_scaled"], i + 2, passed)
                    sp.dma_start(raw[:, :, :], rows(g.hc, i)).then_inc(ld, 16)

            def steps(eng, body):
                for n in (-1, 0, 1):
                    body(n, n % 2)
                with eng.Fori(0, (PAIRS - 3) // 2) as i:
                    for slot in range(2):
                        body(i * 2 + (2 + slot), slot)
                for n in range(PAIRS - 1, PAIRS + 2):
                    body(n, n % 2)

            @block.tensor
            def _(pe):
                def step(n, slot):
                    nxt, other = n + 1, 1 - slot
                    if exists(n, 1, PAIRS):
                        done(pe, "r_ready", nxt)
                        done(pe, "ot_ready", nxt, 2)
                        for k in range(KQ):
                            for t in range(2):
                                mm = pe.transpose(prt[k // 2][:, k % 2, t * P:(t + 1) * P], rr[:, other, t, k * P:(k + 1) * P], g.ident[:, :])
                        mm.then_inc(m["turned"], 1)
                        done(pe, "rt_ready", nxt)
                        done(pe, "s_ready", nxt, 1)
                        for t in range(2):
                            for k in range(KQ):
                                mm = pe.matmul(pss[t][k // 4][:, (k % 4) * P:(k % 4 + 1) * P], rt[:, k, t * P:(t + 1) * P], bd[:, k, :],
                                               start=True, stop=True)
                        mm.then_inc(m["mixed"], 1)
                    if exists(n, 0, PAIRS):
                        done(pe, "o_ready", n)
                        for k in range(4):
                            for t in range(2):
                                mm = pe.transpose(prt[k // 2][:, k % 2, t * P:(t + 1) * P],
                                                  o[:, t, 4 * k:4 * k + 4, :].rearrange("p a b -> p (a b)"), g.ident[:, :])
                        mm.then_inc(m["o_turned"], 1)
                        done(pe, "ot_ready", n)
                        done(pe, "ft_ready", n, 1)
                        for t in range(2):
                            for k in range(4):
                                mm = pe.matmul(pf[:, t, :], ot[:, k, t * P:(t + 1) * P], wres[:, k, :], start=(k == 0), stop=(k == 3))
                        mm.then_inc(m["final"], 1)

                pe.wait_ge(scaled, 1)
                steps(pe, step)

            @block.scalar
            def _(act):
                def step(n, slot):
                    nxt, other = n + 1, 1 - slot
                    if exists(n, 1, PAIRS):
                        done(act, "bn_ready", nxt)
                        for t in range(2):
                            ins = act.activation(rr[:, other, t, :], rr[:, other, t, :], ACT.Relu)
                        ins.then_inc(m["r_ready"], 1)
                        done(act, "r_ready", nxt)
                        done(act, "rooted", nxt, 2)
                        for t in range(2):
                            act.activation(junk[:, other, t, :], rr[:, other, t, :], ACT.Square, accum_out=nr[other][:, t:t + 1])
                        done(act, "turned", nxt)
                        for j in range(3):
                            ins = act.activation(rt[:, 2 * j:2 * j + 2, :], prt[j][:, :, :], ACT.Copy)
                        ins.then_inc(m["rt_ready"], 1)
                        done(act, "mixed", nxt)
                        done(act, "o_ready", nxt, 2)
                        for t in range(2):
                            act.activation(s[:, other, t, 0:512], pss[t][0][:, :], ACT.Copy)
                            ins = act.activation(s[:, other, t, 512:QKV], pss[t][1][:, 0:QKV - 512], ACT.Copy)
                        ins.then_inc(m["s_ready"], 1)
                        done(act, "s_ready", nxt)
                        for t in range(2):
                            ins = act.activation(junk[:, other, t, :], s[:, other, t, :], ACT.Square, accum_out=ns[other][:, t:t + 1])
                        ins.then_inc(m["squared"], 1)
                        done(act, "squared", nxt)
                        for t in range(2):
                            part = s[:, other, t, :].rearrange("p (a b) -> p a b", b=3 * GD)[:, :, 0:2 * GD]
                            ins = act.activation(part, part, ACT.Relu)
                        ins.then_inc(m["s_relu"], 1)
                        for t in range(2):
                            act.activation(ncat[other][:, t:t + 1], ns[other][:, t:t + 1], ACT.Sqrt, bias=nr[other][:, t:t + 1])
                        act.activation(root[other], nr[other], ACT.Sqrt).then_inc(m["rooted"], 1)
                    if exists(n, 0, PAIRS):
                        done(act, "o_ready", n)
                        done(act, "o_rooted", n, 1)
                        for t in range(2):
                            ins = act.activation(junk_o[:, t, :], o[:, t, :, :].rearrange("p a b -> p (a b)"), ACT.Square,
                                                 accum_out=no[slot][:, t:t + 1])
                        ins.then_inc(m["o_squared"], 1)
                        done(act, "o_squared", n)
                        act.activation(no[slot], no[slot], ACT.Sqrt).then_inc(m["o_rooted"], 1)
                        done(act, "o_turned", n)
                        done(act, "final", n, 1)
                        for j in range(2):
                            ins = act.activation(ot[:, 2 * j:2 * j + 2, :], prt[j][:, :, :], ACT.Copy)
                        ins.then_inc(m["ot_ready"], 1)
                    if exists(n, -1, PAIRS):
                        done(act, "ft_ready", n, 1)
                        done(act, "xdone", n, 2)
                        for t in range(2):
                            ins = act.activation(junk_f[:, t, :], ft[:, t, :], ACT.Square, accum_out=nf[:, t:t + 1])
                        ins.then_inc(m["f_squared"], 1)
                        done(act, "f_squared", n, 1)
                        act.activation(nf, nf, ACT.Sqrt).then_inc(m["f_rooted"], 1)
                        done(act, "f_rooted", n, 1)
                        act.activation(th, nf, ACT.Tanh).then_inc(m["tanh_ready"], 1)

                steps(act, step)

            @block.vector
            def _(dve):
                def normal(n, slot):
                    dve.wait_ge(ld, n * 16 + 16)
                    done(dve, "turned", n, 2)
                    done(dve, "rooted", n, 2)
                    done(dve, "o_ready", n, 2)
                    dve.tensor_tensor(rr[:, slot, :, :], raw[:, :, :], over(g.bn_scale[:, :], 1, [P, 2, QKV]), ALU.mult).then_inc(m["bn_scaled"], 1)
                    done(dve, "bn_scaled", n)
                    dve.tensor_tensor(rr[:, slot, :, :], rr[:, slot, :, :], over(g.bn_beta[:, :], 1, [P, 2, QKV]), ALU.add).then_inc(m["bn_ready"], 1)

                def finish(n):
                    link = Chain(dve, chain_d, n + 1)
                    done(dve, "tanh_ready", n)
                    done(dve, "xdone", n, 1)
                    link(dve.tensor_scalar(tmp_d, nf, MIN_NORM, None, ALU.max))
                    link(dve.reciprocal(tmp_d, tmp_d))
                    link(dve.scalar_tensor_tensor(out=scale_d, in0=th, scalar=BALL, in1=tmp_d, op0=ALU.min, op1=ALU.mult))
                    for t in range(2):
                        x = tile_of(g.x, n * 2 + t)
                        ins = dve.scalar_tensor_tensor(out=x, in0=ft[:, t, :], scalar=scale_d[:, t:t + 1], in1=x, op0=ALU.mult, op1=ALU.add)
                    ins.then_inc(m["xdone"], 1)

                def attend(n, slot):
                    link = Chain(dve, chain_b, n + 1)
                    nrt, cat = root[slot], ncat[slot]
                    done(dve, "rooted", n)
                    link(dve.tensor_scalar(tmp_b, nrt, MIN_NORM, None, ALU.max))
                    parts = []
                    for t in range(2):
                        parts.append((t, 0, rr[:, slot, t, :].rearrange("p (a b) -> p a b", b=3 * GD)))
                        parts.append((t, GRP // 2, s[:, slot, t, :].rearrange("p (a b) -> p a b", b=3 * GD)))
                    dve.reciprocal(tmp_b, tmp_b).then_inc(chain_b[15], 1)
                    for t, at, part in parts:
                        dve.tensor_reduce(ks[:, t, at:at + 8], part[:, :, GD:2 * GD], AX, ALU.add)
                    dve.wait_ge(chain_b[15], n + 1)
                    link(dve.scalar_tensor_tensor(out=c1, in0=nrt, scalar=ATANH_BALL, in1=tmp_b, op0=ALU.min, op1=ALU.mult))
                    link(dve.tensor_tensor(nc_, c1, cat, ALU.mult))
                    link(dve.tensor_scalar(tmp_b, nc_, MIN_NORM, None, ALU.max))
                    link(dve.reciprocal(tmp_b, tmp_b))
                    link(dve.scalar_tensor_tensor(out=tmp_b, in0=nc_, scalar=ATANH_BALL, in1=tmp_b, op0=ALU.min, op1=ALU.mult))
                    link(dve.tensor_tensor(kap, tmp_b, c1, ALU.mult))
                    for t, at, part in parts:
                        ins = dve.tensor_scalar(v[:, t, at:at + 8, :], part[:, :, 2 * GD:3 * GD], kap[:, t:t + 1], None, ALU.mult)
                    link(ins)
                    link(dve.tensor_scalar(ve[:, :, :, :], v[:, :, :, :], ATT_EPS, None, ALU.add))
                    link(dve.reciprocal(ve[:, :, :, :], ve[:, :, :, :]))
                    link(dve.tensor_tensor(v[:, :, :, :], v[:, :, :, :], ve[:, :, :, :], ALU.mult))
                    done(dve, "o_turned", n, 1)
                    done(dve, "o_squared", n, 1)
                    for t, at, part in parts:
                        ins = dve.tensor_tensor(o[:, t, at:at + 8, :], part[:, :, 0:GD], over(ks[:, t, at:at + 8], 2, [P, 8, GD]), ALU.mult)
                    link(ins)
                    for t in range(2):
                        ins = dve.scalar_tensor_tensor(out=o[:, t, :, :], in0=v[:, t, :, :], scalar=kap[:, t:t + 1], in1=o[:, t, :, :],
                                                       op0=ALU.mult, op1=ALU.mult)
                    link(ins)
                    for t in range(2):
                        ins = dve.tensor_scalar(o[:, t, :, :], o[:, t, :, :], kap[:, t:t + 1], None, ALU.mult)
                    ins.then_inc(m["o_ready"], 1)

                def close(n, slot):
                    link = Chain(dve, chain_c, n + 1)
                    done(dve, "o_rooted", n)
                    link(dve.tensor_scalar(tmp_c, no[slot], MIN_NORM, None, ALU.max))
                    link(dve.reciprocal(tmp_c, tmp_c))
                    link(dve.scalar_tensor_tensor(out=c2, in0=no[slot], scalar=ATANH_BALL, in1=tmp_c, op0=ALU.min, op1=ALU.mult))
                    done(dve, "final", n)
                    done(dve, "xdone", n, 1)
                    for t in range(2):
                        ins = dve.scalar_tensor_tensor(out=ft[:, t, :], in0=pf[:, t, :], scalar=c2[:, t:t + 1], in1=bres[:, :],
                                                       op0=ALU.mult, op1=ALU.add)
                    ins.then_inc(m["ft_ready"], 1)

                def step(n, slot):
                    if exists(n, 1, PAIRS):
                        normal(n + 1, 1 - slot)
                    if exists(n, -2, PAIRS):
                        finish(n - 2)
                    if exists(n, 0, PAIRS):
                        attend(n, slot)
                    if exists(n, -1, PAIRS):
                        close(n - 1, 1 - slot)

                dve.wait_ge(loaded, 64)
                dve.tensor_tensor(bd[:, :, :], bd[:, :, :], over(wdw[:, :], 2, [P, KQ, P]), ALU.mult).then_inc(scaled, 1)
                steps(dve, step)
def spill_duplicates(nc, g):
    with Room(nc, "dup") as r:
        key = r.sbuf("key", [P, 2, U, 2])
        junk = r.sbuf("junk", [P, U, 2, P])
        rank = r.sbuf("rank", [P, 2, U, 2])
        ranks = r.sbuf("ranks", [P, ET, 2])
        keys = r.sbuf("keys", [P, ET, 2])
        pk = [r.psum(f"pk{j}", [P, U, P]) for j in range(4)]
        keyed, spread, counted, kept, step = (r.sem(n) for n in ("keyed", "spread", "counted", "kept", "step"))
        credit(nc, [keyed, spread, counted, kept], 2)
        with nc.Block() as block:

            @block.tensor
            def _(pe):
                with pe.Fori(0, TURNS // 2) as i:
                    for s in range(2):
                        n = i * 2 + s
                        pe.wait_ge(keyed, n + 3)
                        pe.wait_ge(counted, n + 1)
                        for j in range(2):
                            for b in range(U):
                                mm = pe.transpose(pk[2 * s + j][:, b, :], key[:, s, b, j:j + 1].to_broadcast([P, P]), g.ident[:, :])
                        mm.then_inc(spread, 1)

            @block.vector
            def _(dve):
                def make_key(n, s):
                    dve.tensor_copy(key[:, s, :, :], g.idx[:, n * U:(n + 1) * U, 0:2] if isinstance(n, int) else g.idx[:, ds(n * U, U), 0:2]).then_inc(keyed, 1)

                def group(n, s, more=True):
                    dve.wait_ge(spread, n + 3)
                    dve.wait_ge(kept, n + 1)
                    if not isinstance(n, int) or n >= 1:
                        dve.wait_ge(counted, n + 2)
                    for j in range(2):
                        for b in range(U):
                            ins = dve.scalar_tensor_tensor(out=junk[:, b, j, :], in0=pk[2 * s + j][:, b, :], scalar=key[:, s, b, j:j + 1], in1=g.lower[:, :],
                                                           op0=ALU.is_equal, op1=ALU.mult, accum_out=rank[:, s, b, j:j + 1])
                    ins.then_inc(counted, 1)
                    dve.wait_ge(counted, n + 3)
                    if more:
                        make_key(n + 2, s)
                    dve.tensor_copy(ranks[:, n * U:(n + 1) * U, :] if isinstance(n, int) else ranks[:, ds(n * U, U), :], rank[:, s, :, :]).then_inc(kept, 1)

                for s in range(2):
                    make_key(s, s)
                with dve.Fori(0, TURNS // 2 - 1) as i:
                    for s in range(2):
                        group(i * 2 + s, s)
                for s in range(2):
                    group(TURNS - 2 + s, s, False)
                dve.tensor_copy(keys[:, :, :], g.idx[:, :, 0:2]).then_inc(step, 1)
                dve.wait_ge(kept, TURNS + 2)
                dve.tensor_scalar(ranks[:, :, :], ranks[:, :, :], 1.0, None, ALU.min).then_inc(step, 1)
                dve.wait_ge(step, 2)

                dve.tensor_scalar(g.rowf[:, :, :], keys[:, :, :], -1.0, g.spill[:, :], ALU.mult, ALU.add).then_inc(step, 1)
                dve.wait_ge(step, 3)
                dve.tensor_tensor(g.rowf[:, :, :], g.rowf[:, :, :], ranks[:, :, :], ALU.mult).then_inc(step, 1)
                dve.wait_ge(step, 4)
                dve.tensor_tensor(g.rowf[:, :, :], g.rowf[:, :, :], keys[:, :, :], ALU.add).then_inc(step, 1)
                dve.wait_ge(step, 5)
                dve.tensor_copy(g.idx[:, :, 2:4], g.rowf[:, :, :]).then_inc(step, 1)


class Edge:

    def __init__(self, r, marks, dmas, n=U):
        self.marks = {m: r.sem(m) for m in marks}
        self.dmas = {d: r.sems(d, n) for d in dmas}
        self.n = n

    def credit(self, nc):
        credit(nc, list(self.marks.values()), self.n)

    def done(self, eng, name, t, lag=0, passed=None):
        eng.wait_ge(self.marks[name], t + (1 + self.n - lag))
        if passed is not None:
            eng.sem_inc(passed)


def steps_of(eng, body, tiles, first, last, slots=U):
    lead = -(-first // slots) * slots
    for t in range(-first, lead):
        body(t, t // slots, t % slots)
    end = (tiles - lead) // slots * slots
    tail = -(-max(first, last) // slots) * slots
    with eng.Fori(lead // slots, (tiles - tail) // slots) as i:
        for b in range(slots):
            body(i * slots + b, i, b)
    for t in range(tiles - tail, tiles + last):
        body(t, t // slots, t % slots)


def exists(t, k, tiles=ET):
    return not isinstance(t, int) or 0 <= t + k < tiles


def attend0(nc, g, a):
    A = H0 * (D0 + 1)
    with Room(nc, "ga") as r:
        ixa = r.sbuf("ixa", [P, U, 4], I32)
        ixb = r.sbuf("ixb", [P, U, 4], I32)
        attr = r.sbuf("attr", [4, U, P])
        ew = r.sbuf("ew", [4, D])
        srow = r.sbuf("srow", [P, U, ROW0])
        drow = r.sbuf("drow", [P, U, ROW0])
        old = r.sbuf("old", [P, U, A + H0])
        new = r.sbuf("new", [P, U, A + H0])
        key = r.sbuf("key", [P, U, 1])
        same = r.sbuf("same", [P, U, P])
        pen = r.sbuf("pen", [P, U, P], BF16)
        we = r.sbuf("we", [P, U, D])
        z = r.sbuf("z", [P, U, H0])
        alpha = r.sbuf("alpha", [P, U, H0])
        at = r.sbuf("at", [P, U, P])
        mloc = r.sbuf("mloc", [P, U, H0])
        diff = r.sbuf("diff", [P, U, 2, H0])
        prod = r.sbuf("prod", [P, U, H0, D0 + 1])
        fade = r.sbuf("fade", [P, U, H0])
        blank = r.sbuf("blank", [P, A + H0])
        pkey = [r.psum(f"pkey{j}", [P, P]) for j in range(2)]
        penc = [r.psum(f"penc{j}", [P, D]) for j in range(2)]
        pat = r.psum("pat", [H0, P])
        pm = [r.psum(f"pm{j}", [P, 4, P]) for j in range(2)]
        psum = r.psum("psum", [P, A])
        e = Edge(r, ["keyed", "spread", "matched", "encoded", "weighed", "z1", "z2", "z3", "scored", "penned", "turned", "at_ready",
                     "masked0", "masked1", "mloc0", "mloc1", "mnew", "differed", "exped", "faded", "multiplied", "summed", "old_faded", "new_ready"],
                 ["ixa", "ixb", "attr", "srow", "drow", "old", "new"])
        ready, blanked, inited, loaded, ones_set = r.sem("ready"), r.sem("blanked"), r.sem("inited"), r.sem("loaded"), r.sem("ones_set")
        passed, passed_sp = r.sem("passed"), r.sem("passed_sp")
        e.credit(nc)
        with nc.Block() as block:

            @block.vector
            def _(dve):
                dve.memset(blank[:, 0:A], 0.0)
                dve.memset(blank[:, A:A + H0], LOWEST).then_inc(blanked, 1)
                dve.memset(attr[:, :, :], 1.0)
                dve.memset(at[:, :, :], 0.0).then_inc(ones_set, 1)

            @block.sync
            def _(sp):
                sp.dma_start(ew[0:3, :], a["eWT"]).then_inc(loaded, 16)
                sp.dma_start(ew[3:4, :], a["eb"].rearrange("(a n) -> a n", a=1)).then_inc(loaded, 16)
                sp.wait_ge(blanked, 1)
                for t in g.tabs0:
                    sp.dma_start(t.rearrange("(t p) c -> p t c", p=P), over(blank[:, 0:A + H0], 1, [P, TROWS // P, A + H0])).then_inc(inited, 16)
                sp.wait_ge(inited, 16 * NTAB)
                sp.wait_ge(loaded, 32)
        with nc.Block() as block:

            @block.sync
            def _(sp):
                def step(t, i, b):
                    if exists(t, 3):
                        c = (b + 3) % U
                        if not (isinstance(t, int) and t < 1):
                            j = i if b == 0 else i + 1
                            hold(sp, e.dmas["old"][c], j * 16, passed_sp)
                            e.done(sp, "keyed", t, 1, passed_sp)
                            e.done(sp, "encoded", t, 1, passed_sp)
                        sp.dma_start(ixa[:, c, :], g.idx[:, t + 3, :] if isinstance(t, int) else g.idx[:, ds(t + 3, 1), :].rearrange("p a b -> p (a b)")).then_inc(e.dmas["ixa"][c], 16)
                        sp.dma_start(attr[0:3, c, :], a["ea"][:, t + 3, :] if isinstance(t, int) else a["ea"][:, ds(t + 3, 1), :].rearrange("p a b -> p (a b)")).then_inc(e.dmas["attr"][c], 16)
                    if exists(t, 0):
                        if not (isinstance(t, int) and t < U):
                            hold(sp, e.dmas["new"][b], i * 16, passed_sp)
                        sp.dma_start(ixb[:, b, :], g.idx[:, t, :] if isinstance(t, int) else g.idx[:, ds(t, 1), :].rearrange("p a b -> p (a b)")).then_inc(e.dmas["ixb"][b], 16)

                steps_of(sp, step, ET, 3, 0)

            @block.gpsimd
            def _(pool):
                def step(t, i, b):
                    if exists(t, 2):
                        c = (b + 2) % U
                        j = i + 2 if b >= 2 else i + 1
                        pool.wait_ge(e.dmas["ixa"][c], j * 16)
                        if not (isinstance(t, int) and t + 2 < U):
                            e.done(pool, "multiplied", t + 2, U)
                            e.done(pool, "z2", t + 2, U)
                        pool.sem_inc(passed)
                        pool.indirect_dma_start(out=drow[:, c, :], out_offset=None, in_=g.table0[:, :],
                                                in_offset=bass.IndirectOffsetOnAxis(ap=ixa[:, c, 1:2], axis=0)).then_inc(e.dmas["drow"][c], 16)
                        pool.indirect_dma_start(out=srow[:, c, :], out_offset=None, in_=g.table0[:, :],
                                                in_offset=bass.IndirectOffsetOnAxis(ap=ixa[:, c, 0:1], axis=0)).then_inc(e.dmas["srow"][c], 16)
                    if exists(t, 1):
                        c = (b + 1) % U
                        j = i + 1 if b == U - 1 else i
                        if not (isinstance(t, int) and t + 1 < U):
                            pool.wait_ge(e.dmas["new"][c], j * 16)
                            e.done(pool, "old_faded", t + 1, U)
                        pool.wait_ge(e.dmas["ixa"][c], (j + 1) * 16)
                        pool.sem_inc(passed)
                        pool.indirect_dma_start(out=old[:, c, :], out_offset=None, in_=g.tabs0[c][:, :],
                                                in_offset=bass.IndirectOffsetOnAxis(ap=ixa[:, c, 1:2], axis=0)).then_inc(e.dmas["old"][c], 16)
                    if exists(t, -2):
                        c = (b - 2) % U
                        j = i + 1 if b >= 2 else i
                        pool.wait_ge(e.dmas["ixb"][c], j * 16)
                        e.done(pool, "new_ready", t, 2)
                        pool.sem_inc(passed)
                        pool.indirect_dma_start(out=g.tabs0[c][:, :], out_offset=bass.IndirectOffsetOnAxis(ap=ixb[:, c, 3:4], axis=0),
                                                in_=new[:, c, :], in_offset=None).then_inc(e.dmas["new"][c], 16)

                steps_of(pool, step, ET, 2, 2)
                for c in range(U):
                    hold(pool, e.dmas["new"][c], 16 * TURNS, passed)

            @block.tensor
            def _(pe):
                def turn_alpha(t, b):
                    e.done(pe, "scored", t)
                    e.done(pe, "at_ready", t, 1)
                    pe.transpose(pat[:, :], alpha[:, b, :], g.ident[:, :]).then_inc(e.marks["turned"], 1)

                def encode(t, i, b):
                    e.done(pe, "keyed", t)
                    e.done(pe, "matched", t, 2)
                    pe.transpose(pkey[b % 2][:, :], key[:, b, :].to_broadcast([P, P]), g.ident[:, :]).then_inc(e.marks["spread"], 1)
                    pe.wait_ge(e.dmas["attr"][b], i * 16 + 16)
                    e.done(pe, "weighed", t, 2)
                    pe.matmul(penc[b % 2][:, :], attr[:, b, :], ew[:, :], start=True, stop=True).then_inc(e.marks["encoded"], 1)

                def mask(t, b):
                    e.done(pe, "at_ready", t)
                    e.done(pe, "penned", t)
                    for j in range(2):
                        e.done(pe, f"mloc{j}", t, 1)
                        for h in range(4):
                            pe.matmul(pm[j][:, h, :], g.picks[:, 4 * j + h, :], at[:, b, :], start=(h == 0), stop=False)
                        pe.matmul(pm[j][:, :, :], g.identb[:, :], over(pen[:, b, :], 1, [P, 4, P]), start=False, stop=True).then_inc(e.marks[f"masked{j}"], 1)

                def total(t, b):
                    e.done(pe, "multiplied", t)
                    e.done(pe, "new_ready", t, 1)
                    pe.matmul(psum[:, :], same[:, b, :], prod[:, b, :, :].rearrange("p a b -> p (a b)"), start=True, stop=True).then_inc(e.marks["summed"], 1)

                def step(t, i, b):
                    if exists(t, 1):
                        turn_alpha(t + 1, (b + 1) % U)
                    if exists(t, 2):
                        encode(t + 2, i + 1 if b >= 2 else i, (b + 2) % U)
                    if exists(t, 1):
                        mask(t + 1, (b + 1) % U)
                    if exists(t, 0):
                        total(t, b)

                encode(0, 0, 0)
                steps_of(pe, lambda t, i, b: step(t, i, b) if not (isinstance(t, int) and t < -1) else None, ET, 1, 0)

            @block.scalar
            def _(act):
                def step(t, i, b):
                    c = (b + 1) % U
                    if exists(t, 1):
                        e.done(act, "matched", t + 1)
                        act.activation(pen[:, c, :], same[:, c, :], ACT.Copy, scale=-LOWEST, bias=LOWEST).then_inc(e.marks["penned"], 1)
                    if exists(t, 1):
                        e.done(act, "turned", t + 1)
                        act.activation(at[0:H0, c, :], pat[:, :], ACT.Copy).then_inc(e.marks["at_ready"], 1)
                    if exists(t, 0):
                        e.done(act, "differed", t)
                        e.done(act, "summed", t, U)
                        act.activation(prod[:, b, :, D0], diff[:, b, 0, :], ACT.Exp).then_inc(e.marks["exped"], 1)
                        act.activation(fade[:, b, :], diff[:, b, 1, :], ACT.Exp).then_inc(e.marks["faded"], 1)
                        e.done(act, "faded", t)
                        for h in range(H0):
                            o = old[:, b, h * (D0 + 1):(h + 1) * (D0 + 1)]
                            ins = act.activation(o, o, ACT.Copy, scale=fade[:, b, h:h + 1])
                        ins.then_inc(e.marks["old_faded"], 1)

                steps_of(act, step, ET, 1, 0)

            @block.vector
            def _(dve):
                m = e.marks

                def make_key(t, i, b):
                    dve.wait_ge(e.dmas["ixa"][b], i * 16 + 16)
                    e.done(dve, "spread", t, U)
                    dve.tensor_copy(key[:, b, :], ixa[:, b, 1:2]).then_inc(m["keyed"], 1)

                def step(t, i, b):
                    now, new_, c, n = exists(t, 0), exists(t, 1), (b + 1) % U, t + 1
                    if exists(t, 2):
                        make_key(t + 2, i + 1 if b >= 2 else i, (b + 2) % U)
                    if new_:
                        j = i + 1 if b == U - 1 else i
                        e.done(dve, "encoded", n)
                        dve.wait_ge(e.dmas["drow"][c], j * 16 + 16)
                        dve.scalar_tensor_tensor(out=we[:, c, :], in0=penc[c % 2][:, :], scalar=0.0, in1=drow[:, c, 0:D], op0=ALU.max,
                                                 op1=ALU.mult).then_inc(m["weighed"], 1)
                        e.done(dve, "spread", n)
                        e.done(dve, "summed", n, U)
                        dve.tensor_scalar(same[:, c, :], pkey[c % 2][:, :], key[:, c, :], None, ALU.is_equal).then_inc(m["matched"], 1)
                        e.done(dve, "weighed", n)
                        dve.tensor_reduce(z[:, c, :], we[:, c, :].rearrange("p (h d) -> p h d", h=H0), AX, ALU.add).then_inc(m["z1"], 1)
                        e.done(dve, "z1", n)
                        dve.tensor_tensor(z[:, c, :], z[:, c, :], drow[:, c, D + H0:ROW0], ALU.add).then_inc(m["z2"], 1)
                        e.done(dve, "z2", n)
                        dve.wait_ge(e.dmas["srow"][c], j * 16 + 16)
                        dve.tensor_tensor(z[:, c, :], z[:, c, :], srow[:, c, D:D + H0], ALU.add).then_inc(m["z3"], 1)
                        e.done(dve, "z3", n)
                        dve.scalar_tensor_tensor(out=alpha[:, c, :], in0=z[:, c, :], scalar=0.2, in1=z[:, c, :], op0=ALU.mult,
                                                 op1=ALU.max).then_inc(m["scored"], 1)
                    if now:
                        for j in range(2):
                            e.done(dve, f"masked{j}", t)
                            dve.tensor_reduce(mloc[:, b, 4 * j:4 * j + 4], pm[j][:, :, :], AX, ALU.max).then_inc(m[f"mloc{j}"], 1)
                        e.done(dve, "mloc1", t)
                        dve.wait_ge(e.dmas["old"][b], i * 16 + 16)
                        if not (isinstance(t, int) and t < U):
                            dve.wait_ge(e.dmas["new"][b], i * 16)
                        dve.tensor_tensor(new[:, b, A:A + H0], mloc[:, b, :], old[:, b, A:A + H0], ALU.max).then_inc(m["mnew"], 1)
                        e.done(dve, "mnew", t)
                        dve.tensor_tensor(diff[:, b, 0, :], alpha[:, b, :], new[:, b, A:A + H0], ALU.subtract)
                        dve.tensor_tensor(diff[:, b, 1, :], old[:, b, A:A + H0], new[:, b, A:A + H0], ALU.subtract).then_inc(m["differed"], 1)
                    if exists(t, -1):
                        k = (b - 1) % U
                        e.done(dve, "old_faded", t, 1)
                        e.done(dve, "summed", t, 1)
                        dve.tensor_tensor(new[:, k, 0:A], old[:, k, 0:A], psum[:, :], ALU.add).then_inc(m["new_ready"], 1)
                    if now:
                        e.done(dve, "exped", t)
                        dve.tensor_tensor(prod[:, b, :, 0:D0], srow[:, b, 0:D].rearrange("p (h d) -> p h d", h=H0),
                                          prod[:, b, :, D0:D0 + 1].to_broadcast([P, H0, D0]), ALU.mult).then_inc(m["multiplied"], 1)

                steps_of(dve, step, ET, 2, 1)


def merge0(nc, g, a):
    A = H0 * (D0 + 1)
    with Room(nc, "m0") as r:
        tb = r.sbuf("tb", [P, NTAB, 2, A + H0])
        mx = r.sbuf("mx", [P, 2, 2, H0])
        top = r.sbuf("top", [P, 2, H0])
        diff = r.sbuf("diff", [P, NTAB, 2, H0])
        fade = r.sbuf("fade", [P, NTAB, 2, H0])
        rden = r.sbuf("rden", [P, 2, H0])
        res = r.sbuf("res", [P, 2, D])
        bias = r.sbuf("bias", [P, D])
        loaded, ld, differed, exped, xdone, passed = (r.sem(n) for n in ("loaded", "ld", "differed", "exped", "x_done", "passed"))
        chain = r.sems("step", 16)
        credit(nc, [differed, exped, xdone])
        with nc.Block() as block:

            @block.sync
            def _(sp):
                sp.dma_start(bias[:, :], to_all(a["gbias"], D)).then_inc(loaded, 16)
                with sp.Fori(0, PAIRS) as i:
                    hold(sp, xdone, i + 1, passed)
                    for k in range(NTAB):
                        sp.dma_start(tb[:, k, :, :], rows(g.tabs0[k], i)).then_inc(ld, 16)

            @block.scalar
            def _(act):
                with act.Fori(0, PAIRS) as i:
                    act.wait_ge(differed, i + 2)
                    act.activation(fade[:, :, :, :], diff[:, :, :, :], ACT.Exp).then_inc(exped, 1)

            @block.vector
            def _(dve):
                dve.wait_ge(loaded, 16)
                with dve.Fori(0, PAIRS) as i:
                    now = i + 2
                    link = Chain(dve, chain, i + 1)
                    dve.wait_ge(ld, i * (16 * NTAB) + 16 * NTAB)
                    link(dve.tensor_tensor(mx[:, :, :, :], tb[:, 0:2, :, A:A + H0], tb[:, 2:4, :, A:A + H0], ALU.max))
                    link(dve.tensor_tensor(top[:, :, :], mx[:, 0, :, :], mx[:, 1, :, :], ALU.max))
                    dve.tensor_tensor(diff[:, :, :, :], tb[:, :, :, A:A + H0], over(top[:, :, :], 1, [P, NTAB, 2, H0]), ALU.subtract).then_inc(differed, 1)
                    dve.wait_ge(exped, now)
                    for k in range(NTAB):
                        v = tb[:, k, :, 0:A].rearrange("p t (h d) -> p t h d", h=H0)
                        ins = dve.tensor_tensor(v, v, over(fade[:, k, :, :], 3, [P, 2, H0, D0 + 1]), ALU.mult)
                    link(ins)
                    link(dve.tensor_tensor(tb[:, 0:2, :, 0:A], tb[:, 0:2, :, 0:A], tb[:, 2:4, :, 0:A], ALU.add))
                    link(dve.tensor_tensor(tb[:, 0, :, 0:A], tb[:, 0, :, 0:A], tb[:, 1, :, 0:A], ALU.add))
                    v = tb[:, 0, :, 0:A].rearrange("p t (h d) -> p t h d", h=H0)
                    link(dve.tensor_scalar(rden[:, :, :], v[:, :, :, D0], 1e-10, None, ALU.max))
                    link(dve.reciprocal(rden[:, :, :], rden[:, :, :]))
                    link(dve.tensor_tensor(res[:, :, :].rearrange("p t (h d) -> p t h d", h=H0), v[:, :, :, 0:D0],
                                           over(rden[:, :, :], 3, [P, 2, H0, D0]), ALU.mult))
                    link(dve.tensor_tensor(res[:, :, :], res[:, :, :], over(bias[:, :], 1, [P, 2, D]), ALU.add))
                    dve.tensor_tensor(g.x[:, ds(i * 2, 2), :], g.x[:, ds(i * 2, 2), :], res[:, :, :], ALU.add).then_inc(xdone, 1)


def turn_pair(pe, g, pt, un):
    for t in range(2):
        for k in range(KD):
            mm = pe.transpose(pt[:, k, t * P:(t + 1) * P], un[:, t, k * P:(k + 1) * P], g.ident[:, :])
    return mm


def pick_two(dve, link, p, w, n, m, wait_exp):
    s = w.scratch
    shape = [P, m, n]
    m1, m2, i1, i2, gap = (s.small[:, j, :] for j in range(5))
    link(dve.tensor_reduce(m1, p, AX, ALU.max))
    link(dve.tensor_tensor(s.eq, p, over(m1, 2, shape), ALU.is_equal))
    link(dve.scalar_tensor_tensor(out=s.cand, in0=s.eq, scalar=-float(n), in1=s.order_n, op0=ALU.mult, op1=ALU.add))
    link(dve.tensor_reduce(i1, s.cand, AX, ALU.min))
    link(dve.tensor_tensor(s.sel1, s.order, over(i1, 2, shape), ALU.is_equal))
    link(dve.scalar_tensor_tensor(out=s.rest, in0=s.sel1, scalar=-4.0, in1=p, op0=ALU.mult, op1=ALU.add))
    link(dve.tensor_reduce(m2, s.rest, AX, ALU.max))
    link(dve.tensor_tensor(s.eq, s.rest, over(m2, 2, shape), ALU.is_equal))
    link(dve.scalar_tensor_tensor(out=s.cand, in0=s.eq, scalar=-float(n), in1=s.order_n, op0=ALU.mult, op1=ALU.add))
    link(dve.tensor_reduce(i2, s.cand, AX, ALU.min))
    link(dve.tensor_tensor(s.sel2, s.order, over(i2, 2, shape), ALU.is_equal))
    wait_exp(dve.tensor_tensor(gap, m2, m1, ALU.subtract))
    w1, w2 = s.small[:, 5, :], s.small[:, 6, :]
    link(dve.tensor_scalar(w1, s.small[:, 7, :], 1.0, None, ALU.add))
    link(dve.reciprocal(w1, w1))
    link(dve.tensor_tensor(w2, s.small[:, 7, :], w1, ALU.mult))
    link(dve.tensor_tensor(s.eq, s.sel1, over(w1, 2, shape), ALU.mult))
    link(dve.tensor_tensor(s.cand, s.sel2, over(w2, 2, shape), ALU.mult))
    return dve.tensor_tensor(w.w, s.eq, s.cand, ALU.add)


class Picks:

    def __init__(self, r, n, m):
        self.w = r.sbuf("pick_w", [P, m, n])[:, :, :]
        self.scratch = self
        self.eq, self.cand, self.sel1, self.sel2, self.rest, self.order, self.order_n = (
            r.sbuf(f"pick_{name}", [P, m, n])[:, :, :] for name in ("eq", "cand", "sel1", "sel2", "rest", "order", "order_n"))
        self.small = r.sbuf("pick_small", [P, 8, m])
        self.n, self.m = n, m

    def order_of(self, dve):
        for j in range(self.n):
            dve.memset(self.order[:, :, j], float(j))
            ins = dve.memset(self.order_n[:, :, j], float(j + self.n))
        return ins


def experts0(nc, g, a):
    E = EXPERTS0
    with Room(nc, "ex") as r:
        rw1 = r.sbuf("rw1", [P, KD, P])
        rw2 = r.sbuf("rw2", [P, E])
        rb1 = r.sbuf("rb1", [P, 1])
        rb2 = r.sbuf("rb2", [P, E])
        w1, w2, w3 = (r.sbuf(f"w{j}", [P, E * KD, D]) for j in (1, 2, 3))
        b1, b2 = (r.sbuf(f"b{j}", [P, E * KD]) for j in (1, 2))
        b3 = r.sbuf("b3", [E, D])
        un = r.sbuf("un", [P, 2, D])
        xt = r.sbuf("xt", [P, KD, PW])
        rh = r.sbuf("rh", [P, PW])
        lg = r.sbuf("lg", [P, 2, E])
        ex = r.sbuf("exl", [P, 2, E])
        tot = r.sbuf("tot", [P, 2, 2])
        wt = r.sbuf("wt", [E, PW])
        h1 = r.sbuf("h1", [P, 2, KD, PW])
        h2 = r.sbuf("h2", [P, 2, KD, PW])
        acc = r.sbuf("acc", [P, 2, D])
        picks = Picks(r, E, 2)
        pt = r.psum("pt", [P, KD, PW])
        pr = r.psum("pr", [P, 512])
        p1, p2, p3 = ([r.psum(f"p{j}{s}", [P, KD, PW]) for s in range(2)] for j in (1, 2, 3))
        loaded, passed = r.sem("loaded"), r.sem("passed")
        m = {n: r.sem(n) for n in ("copied", "turned", "xt_ready", "routed1", "rh_ready", "logits", "centred", "exped", "gapped",
                                   "gap_exped", "picked", "w_turned", "wt_ready", "biased", "acc_ready", "xdone")}
        x = {n: r.sem(n) for n in ("l1", "h1_ready", "l2", "h2_ready", "l3", "combined")}
        chain = r.sems("step", 32)
        credit(nc, list(m.values()))
        credit(nc, list(x.values()), 2)
        with nc.Block() as block:

            @block.sync
            def _(sp):
                for dst, src in ((rw1[:, :, :], weights(a["rw1"])), (rw2[:, :], a["rw2"]), (rb1[:, :], a["rb1"]), (rb2[:, :], to_all(a["rb2"], E)),
                                 (w1[:, :, :], weights(a["ew1"])), (w2[:, :, :], weights(a["ew2"])), (w3[:, :, :], weights(a["ew3"])),
                                 (b1[:, :], a["eb1"]), (b2[:, :], a["eb2"]), (b3[:, :], a["eb3"])):
                    sp.dma_start(dst, src).then_inc(loaded, 16)
                sp.wait_ge(loaded, 160)

            @block.tensor
            def _(pe):
                pe.wait_ge(loaded, 160)
                with pe.Fori(0, PAIRS) as i:
                    before, now = i + 1, i + 2

                    def layer(s, e, p, w, src, need, out, free):
                        n = i * E + e
                        if need is not None:
                            pe.wait_ge(x[need], n + 3)
                        pe.wait_ge(x[free], n + 1)
                        for c in range(KD):
                            for k in range(KD):
                                mm = pe.matmul(p[:, c, :], w[:, e * KD + k, c * P:(c + 1) * P], src[:, k, :], start=(k == 0), stop=(k == KD - 1))
                        mm.then_inc(x[out], 1)

                    def last(e):
                        n = i * E + e
                        pe.wait_ge(x["h2_ready"], n + 3)
                        pe.wait_ge(x["combined"], n + 1)
                        for t in range(2):
                            for k in range(KD):
                                mm = pe.matmul(p3[e % 2][:, t, :], h2[:, e % 2, k, t * P:(t + 1) * P], w3[:, e * KD + k, :],
                                               start=(k == 0), stop=(k == KD - 1))
                        mm.then_inc(x["l3"], 1)

                    pe.wait_ge(m["copied"], now)
                    pe.wait_ge(m["wt_ready"], before)
                    turn_pair(pe, g, pt, un).then_inc(m["turned"], 1)
                    pe.wait_ge(m["xt_ready"], now)
                    pe.wait_ge(m["acc_ready"], before)
                    for k in range(KD):
                        mm = pe.matmul(pr[:, 0:PW], rw1[:, k, :], xt[:, k, :], start=(k == 0), stop=(k == KD - 1))
                    mm.then_inc(m["routed1"], 1)
                    for s in range(E + 2):
                        if s < E:
                            layer(s, s, p1[s % 2], w1, xt, None, "l1", "h1_ready")
                        if s == 0:
                            pe.wait_ge(m["rh_ready"], now)
                            for t in range(2):
                                mm = pe.matmul(pr[:, t * E:(t + 1) * E], rh[:, t * P:(t + 1) * P], rw2[:, :], start=True, stop=True)
                            mm.then_inc(m["logits"], 1)
                        if 0 <= s - 1 < E:
                            layer(s, s - 1, p2[(s - 1) % 2], w2, h1[:, (s - 1) % 2, :, :], "h1_ready", "l2", "h2_ready")
                        if s == 2:
                            pe.wait_ge(m["picked"], now)
                            for t in range(2):
                                mm = pe.transpose(pt[0:E, 0, t * P:(t + 1) * P], picks.w[:, t, :], g.ident[:, :])
                            mm.then_inc(m["w_turned"], 1)
                            pe.wait_ge(m["wt_ready"], now)
                            for t in range(2):
                                mm = pe.matmul(pr[:, t * D:(t + 1) * D], wt[:, t * P:(t + 1) * P], b3[:, :], start=True, stop=True)
                            mm.then_inc(m["biased"], 1)
                        if 0 <= s - 2 < E:
                            last(s - 2)

            @block.scalar
            def _(act):
                act.wait_ge(loaded, 160)
                with act.Fori(0, PAIRS) as i:
                    before, now = i + 1, i + 2

                    def relu(e, h, p, b, need, out, free, lag):
                        n = i * E + e
                        act.wait_ge(x[need], n + 3)
                        act.wait_ge(x[free], n + lag)
                        for c in range(KD):
                            ins = act.activation(h[:, e % 2, c, :], p[e % 2][:, c, :], ACT.Relu, bias=b[:, e * KD + c:e * KD + c + 1])
                        ins.then_inc(x[out], 1)

                    act.wait_ge(m["turned"], before)
                    act.activation(un[:, :, :], g.u[:, ds(i * 2, 2), :], ACT.Copy).then_inc(m["copied"], 1)
                    act.wait_ge(m["routed1"], now)
                    act.activation(rh[:, :], pr[:, 0:PW], ACT.Relu, bias=rb1[:, :]).then_inc(m["rh_ready"], 1)
                    for s in range(E + 1):
                        if s < E:
                            relu(s, h1, p1, b1, "l1", "h1_ready", "l2", 1)
                        if s == 0:
                            act.wait_ge(m["centred"], now)
                            act.activation(ex[:, :, :], lg[:, :, :], ACT.Exp).then_inc(m["exped"], 1)
                        if 0 <= s - 1 < E:
                            relu(s - 1, h2, p2, b2, "l2", "h2_ready", "l3", 1)
                        if s == 1:
                            act.wait_ge(m["gapped"], now)
                            act.activation(picks.small[:, 7, :], picks.small[:, 4, :], ACT.Exp).then_inc(m["gap_exped"], 1)
                            act.wait_ge(m["w_turned"], now)
                            act.activation(wt[:, :], pt[0:E, 0, :], ACT.Copy).then_inc(m["wt_ready"], 1)

            @block.vector
            def _(dve):
                dve.wait_ge(loaded, 160)
                picks.order_of(dve)
                with dve.Fori(0, PAIRS) as i:
                    before, now = i + 1, i + 2
                    link = Chain(dve, chain, i + 1)
                    dve.wait_ge(m["turned"], now)
                    dve.wait_ge(x["l1"], i * E + 2)
                    dve.tensor_copy(xt[:, :, :], pt[:, :, :]).then_inc(m["xt_ready"], 1)
                    dve.wait_ge(m["logits"], now)
                    link(dve.tensor_tensor(lg[:, :, :], pr[:, 0:2 * E].rearrange("p (t e) -> p t e", t=2), over(rb2[:, :], 1, [P, 2, E]), ALU.add))
                    link(dve.tensor_reduce(tot[:, 0, :], lg[:, :, :], AX, ALU.max))
                    dve.tensor_tensor(lg[:, :, :], lg[:, :, :], over(tot[:, 0, :], 2, [P, 2, E]), ALU.subtract).then_inc(m["centred"], 1)
                    dve.wait_ge(m["exped"], now)
                    link(dve.tensor_reduce(tot[:, 1, :], ex[:, :, :], AX, ALU.add))
                    link(dve.reciprocal(tot[:, 1, :], tot[:, 1, :]))
                    link(dve.tensor_tensor(ex[:, :, :], ex[:, :, :], over(tot[:, 1, :], 2, [P, 2, E]), ALU.mult))

                    def wait_exp(ins):
                        ins.then_inc(m["gapped"], 1)
                        dve.wait_ge(m["gap_exped"], now)

                    pick_two(dve, link, ex[:, :, :], picks, E, 2, wait_exp).then_inc(m["picked"], 1)
                    dve.wait_ge(m["biased"], now)
                    dve.tensor_tensor(acc[:, :, :], g.x[:, ds(i * 2, 2), :], pr[:, :].rearrange("p (t d) -> p t d", t=2), ALU.add).then_inc(m["acc_ready"], 1)
                    dve.wait_ge(m["acc_ready"], now)
                    for e in range(E):
                        n = i * E + e
                        dve.wait_ge(x["l3"], n + 3)
                        for t in range(2):
                            dst = acc[:, t, :] if e < E - 1 else g.x[:, ds(i * 2 + t, 1), :].rearrange("p a b -> p (a b)")
                            ins = dve.scalar_tensor_tensor(out=dst, in0=p3[e % 2][:, t, :], scalar=picks.w[:, t, e:e + 1], in1=acc[:, t, :],
                                                           op0=ALU.mult, op1=ALU.add)
                        ins.then_inc(x["combined"], 1)
                        dve.wait_ge(x["combined"], n + 3)


def enter1(nc, g, a):
    with Room(nc, "en") as r:
        w = r.sbuf("w", [P, KD, D])
        bias = r.sbuf("bias", [P, D])
        un = r.sbuf("un", [P, 2, D])
        xt = r.sbuf("xt", [P, KD, PW])
        pt = r.psum("pt", [P, KD, PW])
        po = r.psum("po", [P, 2, D])
        loaded = r.sem("loaded")
        m = {n: r.sem(n) for n in ("copied", "turned", "xt_ready", "projected", "kept")}
        credit(nc, list(m.values()))
        with nc.Block() as block:

            @block.sync
            def _(sp):
                sp.dma_start(w[:, :, :], weights(a["winT"])).then_inc(loaded, 16)
                sp.dma_start(bias[:, :], to_all(a["b_in"], D)).then_inc(loaded, 16)
                sp.wait_ge(loaded, 32)

            @block.scalar
            def _(act):
                with act.Fori(0, PAIRS) as i:
                    act.wait_ge(m["turned"], i + 1)
                    act.activation(un[:, :, :], g.u[:, ds(i * 2, 2), :], ACT.Copy).then_inc(m["copied"], 1)

            @block.tensor
            def _(pe):
                pe.wait_ge(loaded, 32)
                with pe.Fori(0, PAIRS) as i:
                    pe.wait_ge(m["copied"], i + 2)
                    pe.wait_ge(m["xt_ready"], i + 1)
                    turn_pair(pe, g, pt, un).then_inc(m["turned"], 1)
                    pe.wait_ge(m["xt_ready"], i + 2)
                    pe.wait_ge(m["kept"], i + 1)
                    for t in range(2):
                        for k in range(KD):
                            mm = pe.matmul(po[:, t, :], xt[:, k, t * P:(t + 1) * P], w[:, k, :], start=(k == 0), stop=(k == KD - 1))
                    mm.then_inc(m["projected"], 1)

            @block.vector
            def _(dve):
                dve.wait_ge(loaded, 32)
                with dve.Fori(0, PAIRS) as i:
                    dve.wait_ge(m["turned"], i + 2)
                    dve.wait_ge(m["projected"], i + 1)
                    dve.tensor_copy(xt[:, :, :], pt[:, :, :]).then_inc(m["xt_ready"], 1)
                    dve.wait_ge(m["projected"], i + 2)
                    dve.tensor_tensor(g.hid[:, ds(i * 2, 2), :], po[:, :, :], over(bias[:, :], 1, [P, 2, D]), ALU.add).then_inc(m["kept"], 1)


def project1(nc, g, a, l):
    with Room(nc, "pj") as r:
        wq, wk, wv = (r.sbuf(f"w{n}", [P, KD, D]) for n in "qkv")
        bias = r.sbuf("bias", [P, 3, D])
        un = r.sbuf("un", [P, 2, D])
        xt = r.sbuf("xt", [P, KD, PW])
        qo = r.sbuf("qo", [P, 2, D])
        kvo = r.sbuf("kvo", [P, 2, 2 * D])
        blank = r.sbuf("blank", [P, ROW1])
        pt = r.psum("pt", [P, KD, PW])
        pq = r.psum("pq", [P, 2, D])
        pkv = [r.psum(f"pkv{t}", [P, 2 * D]) for t in range(2)]
        loaded, blanked, inited, stored, passed = (r.sem(n) for n in ("loaded", "blanked", "inited", "stored", "passed"))
        m = {n: r.sem(n) for n in ("copied", "turned", "xt_ready", "projected", "rows_ready", "sent")}
        credit(nc, list(m.values()))
        with nc.Block() as block:

            @block.sync
            def _(sp):
                for dst, w in ((wq, a["wqT"]), (wk, a["wkT"]), (wv, a["wvT"])):
                    sp.dma_start(dst[:, :, :], weights(w[ds(l * D, D), :])).then_inc(loaded, 16)
                for j, b in enumerate((a["bq"], a["bk"], a["bv"])):
                    sp.dma_start(bias[:, j, :], b[ds(l, 1), :].to_broadcast([P, D])).then_inc(loaded, 16)
                sp.wait_ge(blanked, 1)
                for t in g.tabs1:
                    sp.dma_start(t.rearrange("(t p) c -> p t c", p=P), over(blank[:, :], 1, [P, TROWS // P, ROW1])).then_inc(inited, 16)
                with sp.Fori(0, PAIRS) as i:
                    hold(sp, m["rows_ready"], i + 2, passed)
                    sp.dma_start(rows(g.qrows, i), qo[:, :, :]).then_inc(stored, 16)
                    sp.dma_start(rows(g.kvrows, i), kvo[:, :, :]).then_inc(stored, 16)
                    hold(sp, stored, i * 32 + 32, m["sent"])
                sp.wait_ge(inited, 16 * NTAB)

            @block.scalar
            def _(act):
                with act.Fori(0, PAIRS) as i:
                    act.wait_ge(m["turned"], i + 1)
                    act.activation(un[:, :, :], g.hid[:, ds(i * 2, 2), :], ACT.Copy).then_inc(m["copied"], 1)

            @block.tensor
            def _(pe):
                pe.wait_ge(loaded, 96)
                with pe.Fori(0, PAIRS) as i:
                    pe.wait_ge(m["copied"], i + 2)
                    pe.wait_ge(m["xt_ready"], i + 1)
                    turn_pair(pe, g, pt, un).then_inc(m["turned"], 1)
                    pe.wait_ge(m["xt_ready"], i + 2)
                    pe.wait_ge(m["rows_ready"], i + 1)
                    for dst, w in (([pq[:, t, :] for t in range(2)], wq), ([pkv[t][:, 0:D] for t in range(2)], wk),
                                   ([pkv[t][:, D:2 * D] for t in range(2)], wv)):
                        for t in range(2):
                            for k in range(KD):
                                mm = pe.matmul(dst[t], xt[:, k, t * P:(t + 1) * P], w[:, k, :], start=(k == 0), stop=(k == KD - 1))
                    mm.then_inc(m["projected"], 1)

            @block.vector
            def _(dve):
                dve.memset(blank[:, :], 0.0).then_inc(blanked, 1)
                dve.wait_ge(loaded, 96)
                with dve.Fori(0, PAIRS) as i:
                    dve.wait_ge(m["turned"], i + 2)
                    dve.wait_ge(m["projected"], i + 1)
                    dve.tensor_copy(xt[:, :, :], pt[:, :, :]).then_inc(m["xt_ready"], 1)
                    dve.wait_ge(m["projected"], i + 2)
                    dve.wait_ge(m["sent"], i + 1)
                    dve.tensor_tensor(qo[:, :, :], pq[:, :, :], over(bias[:, 0, :], 1, [P, 2, D]), ALU.add)
                    for t in range(2):
                        ins = dve.tensor_tensor(kvo[:, t, :], pkv[t][:, :], bias[:, 1:3, :].rearrange("p a b -> p (a b)"), ALU.add)
                    ins.then_inc(m["rows_ready"], 1)


DVE_HEADS = 1


def attend1(nc, g):
    AH = HG - DVE_HEADS
    S = 2 * U
    ASK = 4
    with Room(nc, "at") as r:
        ixa = r.sbuf("ixa", [P, S, 4], I32)
        ixb = r.sbuf("ixb", [P, S, 4], I32)
        q = r.sbuf("q", [P, S, D])
        kv = r.sbuf("kv", [P, S, 2 * D])
        key = r.sbuf("key", [P, S, 1])
        same = r.sbuf("same", [P, S, P])
        qk = r.sbuf("qk", [P, 2, HG, HG, DG])
        sc = r.sbuf("sc", [P, S, HG, HG])
        mx = r.sbuf("mx", [P, S, HG])
        ex = r.sbuf("exl", [P, S, HG, HG])
        den = r.sbuf("den", [P, S, HG])
        att = r.sbuf("att", [P, S, HG, HG])
        wv = r.sbuf("wv", [P, S, HG, D])
        new = r.sbuf("new", [P, S, ROW1])
        pkey = [r.psum(f"pkey{j}", [P, P]) for j in range(2)]
        pm = [r.psum(f"pm{j}", [P, ROW1]) for j in range(2)]
        e = Edge(r, ["keyed", "spread", "matched", "paired", "scored", "topped", "centred", "exped", "summed", "inverted", "attended",
                     "weighted_a", "weighted_v", "totalled", "new_ready"], ["ixa", "ixb", "q", "kv", "new"], S)
        passed, passed_sp = r.sem("passed"), r.sem("passed_sp")
        e.credit(nc)
        with nc.Block() as block:

            @block.sync
            def _(sp):
                def step(t, i, b):
                    if exists(t, ASK + 2):
                        c = (b + ASK + 2) % S
                        if not (isinstance(t, int) and t + ASK + 2 < S):
                            j = i if b < S - ASK - 2 else i + 1
                            hold(sp, e.dmas["q"][c], j * 16, passed_sp)
                            hold(sp, e.dmas["kv"][c], j * 16, passed_sp)
                            e.done(sp, "keyed", t + ASK + 2, S, passed_sp)
                        sp.dma_start(ixa[:, c, :], tile_of(g.idx, t + ASK + 2)).then_inc(e.dmas["ixa"][c], 16)
                    if exists(t, 0):
                        if not (isinstance(t, int) and t < S):
                            hold(sp, e.dmas["new"][b], i * 16, passed_sp)
                        sp.dma_start(ixb[:, b, :], tile_of(g.idx, t)).then_inc(e.dmas["ixb"][b], 16)

                steps_of(sp, step, ET, ASK + 2, 0, S)

            @block.gpsimd
            def _(pool):
                def step(t, i, b):
                    if exists(t, ASK):
                        c = (b + ASK) % S
                        j = i + 2 if b >= S - ASK else i + 1
                        pool.wait_ge(e.dmas["ixa"][c], j * 16)
                        if not (isinstance(t, int) and t + ASK < S):
                            e.done(pool, "weighted_a", t + ASK, S)
                            e.done(pool, "weighted_v", t + ASK, S)
                            e.done(pool, "paired", t + ASK, S)
                        pool.sem_inc(passed)
                        pool.indirect_dma_start(out=q[:, c, :], out_offset=None, in_=g.qrows[:, :],
                                                in_offset=bass.IndirectOffsetOnAxis(ap=ixa[:, c, 0:1], axis=0)).then_inc(e.dmas["q"][c], 16)
                        pool.indirect_dma_start(out=kv[:, c, :], out_offset=None, in_=g.kvrows[:, :],
                                                in_offset=bass.IndirectOffsetOnAxis(ap=ixa[:, c, 1:2], axis=0)).then_inc(e.dmas["kv"][c], 16)
                    if exists(t, -3):
                        c = (b - 3) % S
                        j = i + 1 if b >= 3 else i
                        pool.wait_ge(e.dmas["ixb"][c], j * 16)
                        if not (isinstance(t, int) and t - 3 < NTAB):
                            pool.wait_ge(e.dmas["new"][(c - NTAB) % S], (j if c >= NTAB else j - 1) * 16)
                        e.done(pool, "new_ready", t, 3)
                        pool.sem_inc(passed)
                        pool.indirect_dma_start(out=g.tabs1[c % NTAB][:, :], out_offset=bass.IndirectOffsetOnAxis(ap=ixb[:, c, 2:3], axis=0),
                                                in_=new[:, c, :], in_offset=None, compute_op=ALU.add).then_inc(e.dmas["new"][c], 16)

                steps_of(pool, step, ET, ASK, 3, S)
                for c in range(S):
                    hold(pool, e.dmas["new"][c], 16 * (ET // S), passed)

            @block.tensor
            def _(pe):
                def spread(t, b):
                    e.done(pe, "keyed", t)
                    e.done(pe, "matched", t, 2)
                    pe.transpose(pkey[b % 2][:, :], key[:, b, :].to_broadcast([P, P]), g.ident[:, :]).then_inc(e.marks["spread"], 1)

                def total(t, b):
                    e.done(pe, "weighted_a", t)
                    e.done(pe, "weighted_v", t)
                    e.done(pe, "new_ready", t, 2)
                    p = pm[b % 2]
                    e.done(pe, "matched", t)
                    pe.matmul(p[:, D:ROW1], same[:, b, :], tile_of(g.kinds, t), start=True, stop=True)
                    for h in range(HG):
                        mm = pe.matmul(p[:, 0:D], same[:, b, :], wv[:, b, h, :], start=(h == 0), stop=(h == HG - 1))
                    mm.then_inc(e.marks["totalled"], 1)

                def step(t, i, b):
                    if exists(t, 2):
                        spread(t + 2, (b + 2) % S)
                    if exists(t, -1):
                        total(t + -1, (b - 1) % S)

                steps_of(pe, step, ET, 2, 1, S)

            @block.scalar
            def _(act):
                def step(t, i, b):
                    if exists(t, -1):
                        c = (b - 1) % S
                        e.done(act, "attended", t, 1)
                        e.done(act, "totalled", t - 1, S)
                        for h in range(AH):
                            for s in range(HG):
                                ins = act.activation(wv[:, c, h, s * DG:(s + 1) * DG], kv[:, c, D + h * DG:D + (h + 1) * DG], ACT.Copy,
                                                     scale=att[:, c, s, h:h + 1])
                        ins.then_inc(e.marks["weighted_a"], 1)
                    if exists(t, -2):
                        c = (b - 2) % S
                        e.done(act, "totalled", t, 2)
                        if not (isinstance(t, int) and t - 2 < S):
                            act.wait_ge(e.dmas["new"][c], (i if b >= 2 else i - 1) * 16)
                        act.activation(new[:, c, :], pm[b % 2][:, :], ACT.Copy).then_inc(e.marks["new_ready"], 1)
                    if exists(t, 1):
                        c = (b + 1) % S
                        e.done(act, "centred", t + 1)
                        act.activation(ex[:, c, :, :], sc[:, c, :, :], ACT.Exp, scale=DG ** -0.5).then_inc(e.marks["exped"], 1)

                steps_of(act, step, ET, 1, 2, S)

            @block.vector
            def _(dve):
                m = e.marks

                def make_key(t, i, b):
                    dve.wait_ge(e.dmas["ixa"][b], i * 16 + 16)
                    e.done(dve, "spread", t, S)
                    dve.tensor_copy(key[:, b, :], ixa[:, b, 0:1]).then_inc(m["keyed"], 1)

                def step(t, i, b):
                    now, new_, c = exists(t, 0), exists(t, 1), (b + 1) % S
                    if new_:
                        n = i + 1 if b == S - 1 else i
                        dve.wait_ge(e.dmas["q"][c], n * 16 + 16)
                        dve.wait_ge(e.dmas["kv"][c], n * 16 + 16)
                        e.done(dve, "scored", t, 1)
                        qs = q[:, c, :].rearrange("p (h d) -> p h d", h=HG)
                        ks = kv[:, c, 0:D].rearrange("p (h d) -> p h d", h=HG)
                        dve.tensor_tensor(qk[:, c % 2, :, :, :], over(qs, 2, [P, HG, HG, DG]), over(ks, 1, [P, HG, HG, DG]), ALU.mult).then_inc(m["paired"], 1)
                    if now:
                        e.done(dve, "exped", t)
                        dve.tensor_reduce(den[:, b, :], ex[:, b, :, :], AX, ALU.add).then_inc(m["summed"], 1)
                    if new_:
                        e.done(dve, "paired", t + 1)
                        dve.tensor_reduce(sc[:, c, :, :], qk[:, c % 2, :, :, :], AX, ALU.add).then_inc(m["scored"], 1)
                    if now:
                        e.done(dve, "summed", t)
                        dve.reciprocal(den[:, b, :], den[:, b, :]).then_inc(m["inverted"], 1)
                    if new_:
                        e.done(dve, "spread", t + 1)
                        e.done(dve, "totalled", t + 1, S)
                        dve.tensor_scalar(same[:, c, :], pkey[c % 2][:, :], key[:, c, :], None, ALU.is_equal).then_inc(m["matched"], 1)
                        e.done(dve, "scored", t + 1)
                        dve.tensor_reduce(mx[:, c, :], sc[:, c, :, :], AX, ALU.max).then_inc(m["topped"], 1)
                    if now:
                        e.done(dve, "inverted", t)
                        dve.tensor_tensor(att[:, b, :, :], ex[:, b, :, :], over(den[:, b, :], 2, [P, HG, HG]), ALU.mult).then_inc(m["attended"], 1)
                    if exists(t, 2):
                        make_key(t + 2, i + 1 if b >= S - 2 else i, (b + 2) % S)
                    if new_:
                        e.done(dve, "topped", t + 1)
                        dve.tensor_tensor(sc[:, c, :, :], sc[:, c, :, :], over(mx[:, c, :], 2, [P, HG, HG]), ALU.subtract).then_inc(m["centred"], 1)
                    if now:
                        e.done(dve, "attended", t)
                        e.done(dve, "totalled", t, S)
                        for h in range(AH, HG):
                            ins = dve.tensor_tensor(wv[:, b, h, :].rearrange("p (s d) -> p s d", s=HG),
                                                    over(kv[:, b, D + h * DG:D + (h + 1) * DG], 1, [P, HG, DG]),
                                                    att[:, b, :, h:h + 1].to_broadcast([P, HG, DG]), ALU.mult)
                        ins.then_inc(m["weighted_v"], 1)

                steps_of(dve, step, ET, 2, 0, S)


def tile_of(buf, t):
    return buf[:, t, :] if isinstance(t, int) else buf[:, ds(t, 1), :].rearrange("p a b -> p (a b)")


def ln_pair(dve, link, z, stat, junk, ask, got):
    s, v = stat[:, 0, :], stat[:, 1, :]
    link(dve.tensor_reduce(s, z, AX, ALU.add))
    link(dve.tensor_scalar(s, s, -1.0 / D, None, ALU.mult))
    link(dve.tensor_tensor(z, z, over(s, 2, [P, 2, D]), ALU.add))
    for t in range(2):
        ins = dve.tensor_tensor_reduce(junk[:, t, :], z[:, t, :], z[:, t, :], 1.0, 0.0, ALU.mult, ALU.add, stat[:, 1, t:t + 1])
    link(ins)
    ask(dve.tensor_scalar(v, v, 1.0 / D, EPS, ALU.mult, ALU.add))
    got()
    link(dve.reciprocal(s, stat[:, 2, :]))
    link(dve.tensor_tensor(z, z, over(s, 2, [P, 2, D]), ALU.mult))


def update1(nc, g, a, l):
    with Room(nc, "up") as r:
        wo = r.sbuf("wo", [P, KD, D])
        em = r.sbuf("em", [P, KD, 3])
        te = r.sbuf("te", [4, D])
        gain, shift = r.sbuf("gain", [P, D]), r.sbuf("shift", [P, D])
        tb = r.sbuf("tb", [P, NTAB, 2, ROW1])
        st = r.sbuf("st", [P, KD, PW])
        ct = r.sbuf("ct", [4, PW])
        z = r.sbuf("z", [P, 2, D])
        junk = r.sbuf("junk", [P, 2, D])
        stat = r.sbuf("stat", [P, 3, 2])
        pt = r.psum("pt", [P, KD, PW])
        pc = r.psum("pc", [4, PW])
        po = r.psum("po", [P, 2, D])
        pe_ = r.psum("pe", [3, D])
        loaded, embedded, te_ready, ld, passed = (r.sem(n) for n in ("loaded", "embedded", "te_ready", "ld", "passed"))
        m = {n: r.sem(n) for n in ("added", "turned", "st_ready", "projected", "var_ready", "std_ready", "kept")}
        chain = r.sems("step", 16)
        credit(nc, list(m.values()))
        with nc.Block() as block:

            @block.sync
            def _(sp):
                sp.dma_start(wo[:, :, :], weights(a["woT"][ds(l * D, D), :])).then_inc(loaded, 16)
                sp.dma_start(em[:, :, :], weights(a["eemb"][ds(l * D, D), :])).then_inc(loaded, 16)
                sp.dma_start(te[3:4, :], a["bo"][ds(l, 1), :]).then_inc(loaded, 16)
                sp.dma_start(gain[:, :], a["ln_g"][ds(l, 1), :].to_broadcast([P, D])).then_inc(loaded, 16)
                sp.dma_start(shift[:, :], a["ln_b"][ds(l, 1), :].to_broadcast([P, D])).then_inc(loaded, 16)
                with sp.Fori(0, PAIRS) as i:
                    hold(sp, m["turned"], i + 1, passed)
                    for k in range(NTAB):
                        sp.dma_start(tb[:, k, :, :], rows(g.tabs1[k], i)).then_inc(ld, 16)

            @block.tensor
            def _(pe):
                pe.wait_ge(loaded, 80)
                for k in range(KD):
                    mm = pe.matmul(pe_[:, :], em[:, k, :], wo[:, k, :], start=(k == 0), stop=(k == KD - 1))
                mm.then_inc(embedded, 1)
                pe.wait_ge(te_ready, 1)
                with pe.Fori(0, PAIRS) as i:
                    pe.wait_ge(m["added"], i + 2)
                    pe.wait_ge(m["st_ready"], i + 1)
                    for t in range(2):
                        pe.transpose(pc[:, t * P:(t + 1) * P], tb[:, 0, t, D:ROW1], g.ident[:, :])
                        for k in range(KD):
                            mm = pe.transpose(pt[:, k, t * P:(t + 1) * P], tb[:, 0, t, k * P:(k + 1) * P], g.ident[:, :])
                    mm.then_inc(m["turned"], 1)
                    pe.wait_ge(m["st_ready"], i + 2)
                    pe.wait_ge(m["kept"], i + 1)
                    for t in range(2):
                        for k in range(KD):
                            pe.matmul(po[:, t, :], st[:, k, t * P:(t + 1) * P], wo[:, k, :], start=(k == 0), stop=False)
                        mm = pe.matmul(po[:, t, :], ct[:, t * P:(t + 1) * P], te[:, :], start=False, stop=True)
                    mm.then_inc(m["projected"], 1)

            @block.scalar
            def _(act):
                act.wait_ge(embedded, 1)
                act.activation(te[0:3, :], pe_[:, :], ACT.Copy).then_inc(te_ready, 1)
                with act.Fori(0, PAIRS) as i:
                    act.wait_ge(m["turned"], i + 2)
                    act.wait_ge(m["projected"], i + 1)
                    act.activation(st[:, :, :], pt[:, :, :], ACT.Copy)
                    act.activation(ct[:, :], pc[:, :], ACT.Copy).then_inc(m["st_ready"], 1)
                    act.wait_ge(m["var_ready"], i + 2)
                    act.activation(stat[:, 2, :], stat[:, 1, :], ACT.Sqrt).then_inc(m["std_ready"], 1)

            @block.vector
            def _(dve):
                dve.wait_ge(loaded, 80)
                with dve.Fori(0, PAIRS) as i:
                    link = Chain(dve, chain, i + 1)
                    dve.wait_ge(ld, i * (16 * NTAB) + 16 * NTAB)
                    link(dve.tensor_tensor(tb[:, 0:2, :, :], tb[:, 0:2, :, :], tb[:, 2:4, :, :], ALU.add))
                    dve.tensor_tensor(tb[:, 0, :, :], tb[:, 0, :, :], tb[:, 1, :, :], ALU.add).then_inc(m["added"], 1)
                    dve.wait_ge(m["projected"], i + 2)
                    link(dve.tensor_tensor(z[:, :, :], po[:, :, :], g.hid[:, ds(i * 2, 2), :], ALU.add))
                    ln_pair(dve, link, z[:, :, :], stat, junk, lambda ins: ins.then_inc(m["var_ready"], 1),
                            lambda: dve.wait_ge(m["std_ready"], i + 2))
                    link(dve.tensor_tensor(z[:, :, :], z[:, :, :], over(gain[:, :], 1, [P, 2, D]), ALU.mult))
                    link(dve.tensor_tensor(z[:, :, :], z[:, :, :], over(shift[:, :], 1, [P, 2, D]), ALU.add))
                    dve.tensor_scalar(g.hid[:, ds(i * 2, 2), :], z[:, :, :], 0.0, None, ALU.max).then_inc(m["kept"], 1)


def adjust1(nc, g, a):
    with Room(nc, "ad") as r:
        w1, w2 = (r.sbuf(f"w{j}", [P, KD, D]) for j in (1, 2))
        b1 = r.sbuf("b1", [P, KD])
        b2 = r.sbuf("b2", [P, D])
        un = r.sbuf("un", [P, 2, D])
        xt = r.sbuf("xt", [P, KD, PW])
        h = r.sbuf("h", [P, KD, PW])
        o = r.sbuf("o", [P, 2, D])
        pt = r.psum("pt", [P, KD, PW])
        ph = r.psum("ph", [P, KD, PW])
        po = r.psum("po", [P, 2, D])
        loaded = r.sem("loaded")
        m = {n: r.sem(n) for n in ("copied", "turned", "xt_ready", "hidden", "h_ready", "projected", "kept")}
        chain = r.sems("step", 4)
        credit(nc, list(m.values()))
        with nc.Block() as block:

            @block.sync
            def _(sp):
                for dst, src in ((w1[:, :, :], weights(a["w1T"])), (w2[:, :, :], weights(a["w2T"])), (b1[:, :], a["b1"]), (b2[:, :], to_all(a["b2"], D))):
                    sp.dma_start(dst, src).then_inc(loaded, 16)
                sp.wait_ge(loaded, 64)

            @block.scalar
            def _(act):
                act.wait_ge(loaded, 64)
                with act.Fori(0, PAIRS) as i:
                    act.wait_ge(m["turned"], i + 1)
                    act.activation(un[:, :, :], g.hid[:, ds(i * 2, 2), :], ACT.Copy).then_inc(m["copied"], 1)
                    act.wait_ge(m["hidden"], i + 2)
                    act.wait_ge(m["projected"], i + 1)
                    for c in range(KD):
                        ins = act.activation(h[:, c, :], ph[:, c, :], ACT.Relu, bias=b1[:, c:c + 1])
                    ins.then_inc(m["h_ready"], 1)

            @block.tensor
            def _(pe):
                pe.wait_ge(loaded, 64)
                with pe.Fori(0, PAIRS) as i:
                    pe.wait_ge(m["copied"], i + 2)
                    pe.wait_ge(m["xt_ready"], i + 1)
                    turn_pair(pe, g, pt, un).then_inc(m["turned"], 1)
                    pe.wait_ge(m["xt_ready"], i + 2)
                    pe.wait_ge(m["h_ready"], i + 1)
                    for c in range(KD):
                        for k in range(KD):
                            mm = pe.matmul(ph[:, c, :], w1[:, k, c * P:(c + 1) * P], xt[:, k, :], start=(k == 0), stop=(k == KD - 1))
                    mm.then_inc(m["hidden"], 1)
                    pe.wait_ge(m["h_ready"], i + 2)
                    pe.wait_ge(m["kept"], i + 1)
                    for t in range(2):
                        for k in range(KD):
                            mm = pe.matmul(po[:, t, :], h[:, k, t * P:(t + 1) * P], w2[:, k, :], start=(k == 0), stop=(k == KD - 1))
                    mm.then_inc(m["projected"], 1)

            @block.vector
            def _(dve):
                dve.wait_ge(loaded, 64)
                with dve.Fori(0, PAIRS) as i:
                    link = Chain(dve, chain, i + 1)
                    dve.wait_ge(m["turned"], i + 2)
                    dve.wait_ge(m["hidden"], i + 1)
                    dve.tensor_copy(xt[:, :, :], pt[:, :, :]).then_inc(m["xt_ready"], 1)
                    dve.wait_ge(m["projected"], i + 2)
                    link(dve.tensor_tensor(o[:, :, :], po[:, :, :], over(b2[:, :], 1, [P, 2, D]), ALU.add))
                    link(dve.tensor_tensor(o[:, :, :], o[:, :, :], g.u[:, ds(i * 2, 2), :], ALU.add))
                    dve.tensor_tensor(g.x[:, ds(i * 2, 2), :], g.x[:, ds(i * 2, 2), :], o[:, :, :], ALU.add).then_inc(m["kept"], 1)


def mix1_keys(nc, g, a):
    with Room(nc, "mk") as r:
        w = r.sbuf("w", [P, KD, 3 * D])
        bias = r.sbuf("bias", [P, 3 * D])
        un = r.sbuf("un", [P, 2, D])
        xt = r.sbuf("xt", [P, KD, PW])
        qk = r.sbuf("qk", [P, 2, 2, D])
        v = r.sbuf("v", [P, 2, D])
        k2 = r.sbuf("k2", [P, 2, D])
        junk = r.sbuf("junk", [P, 2, D])
        st = r.sbuf("st", [P, 4, 2, 2])
        qn = r.sbuf("qn", [P, 2, 2])
        colsq = r.sbuf("colsq", [P, KD])
        pt = r.psum("pt", [P, KD, PW])
        pqk = [r.psum(f"pqk{t}", [P, 2, D]) for t in range(2)]
        pv = r.psum("pv", [P, 2, D])
        pkv = r.psum("pkv", [P, KD, D])
        pcs = r.psum("pcs", [P, KD])
        loaded, zeroed, step, rooted, asked = (r.sem(n) for n in ("loaded", "zeroed", "step", "rooted", "asked"))
        m = {n: r.sem(n) for n in ("copied", "turned", "xt_ready", "projected", "v_ready", "k_ready", "k2_ready", "multiplied",
                                   "q_squared", "q_rooted", "kept", "kv_added", "scaled")}
        chain = r.sems("step", 16)
        credit(nc, list(m.values()))
        with nc.Block() as block:

            @block.sync
            def _(sp):
                sp.dma_start(w[:, :, :], weights(a["mqkv"])).then_inc(loaded, 16)
                sp.dma_start(bias[:, :], to_all(a["mb"], 3 * D)).then_inc(loaded, 16)
                sp.wait_ge(loaded, 32)

            @block.scalar
            def _(act):
                act.wait_ge(loaded, 32)
                with act.Fori(0, PAIRS) as i:
                    before, now = i + 1, i + 2
                    act.wait_ge(m["turned"], before)
                    act.activation(un[:, :, :], g.u[:, ds(i * 2, 2), :], ACT.Copy).then_inc(m["copied"], 1)
                    act.wait_ge(m["k_ready"], now)
                    act.wait_ge(m["multiplied"], before)
                    act.activation(k2[:, :, :], qk[:, :, 1, :], ACT.Square).then_inc(m["k2_ready"], 1)
                    for t in range(2):
                        ins = act.activation(junk[:, t, :], qk[:, t, 0, :], ACT.Square, accum_out=qn[:, 0, t:t + 1])
                    ins.then_inc(m["q_squared"], 1)
                    act.wait_ge(m["q_squared"], now)
                    act.activation(qn[:, 1, :], qn[:, 0, :], ACT.Sqrt).then_inc(m["q_rooted"], 1)
                    act.wait_ge(m["v_ready"], now)
                    act.activation(g.v[:, ds(i * 2, 2), :], v[:, :, :], ACT.Copy).then_inc(m["kept"], 1)
                act.wait_ge(asked, 1)
                act.activation(colsq[:, :], colsq[:, :], ACT.Sqrt).then_inc(rooted, 1)

            @block.tensor
            def _(pe):
                pe.wait_ge(loaded, 32)
                with pe.Fori(0, PAIRS) as i:
                    before, now = i + 1, i + 2
                    pe.wait_ge(m["copied"], now)
                    pe.wait_ge(m["xt_ready"], before)
                    turn_pair(pe, g, pt, un).then_inc(m["turned"], 1)
                    pe.wait_ge(m["xt_ready"], now)
                    pe.wait_ge(m["v_ready"], before)
                    for t in range(2):
                        for dst, c in ((pqk[t][:, :, :], slice(0, 2 * D)), (pv[:, t, :], slice(2 * D, 3 * D))):
                            for k in range(KD):
                                mm = pe.matmul(dst, xt[:, k, t * P:(t + 1) * P], w[:, k, c], start=(k == 0), stop=(k == KD - 1))
                    mm.then_inc(m["projected"], 1)
                    pe.wait_ge(m["k_ready"], now)
                    pe.wait_ge(m["k2_ready"], now)
                    pe.wait_ge(m["v_ready"], now)
                    pe.wait_ge(m["kv_added"], before)
                    for c in range(KD):
                        for t in range(2):
                            pe.matmul(pkv[:, c, :], qk[:, t, 1, c * P:(c + 1) * P], v[:, t, :], start=(t == 0), stop=(t == 1))
                        for t in range(2):
                            mm = pe.matmul(pcs[:, c:c + 1], k2[:, t, c * P:(c + 1) * P], g.ones[:, 0:1], start=(t == 0), stop=(t == 1))
                    mm.then_inc(m["multiplied"], 1)

            @block.vector
            def _(dve):
                dve.memset(g.kvm[:, :, :], 0.0)
                dve.memset(colsq[:, :], 0.0)
                dve.wait_ge(loaded, 32)
                with dve.Fori(0, PAIRS) as i:
                    before, now = i + 1, i + 2
                    link = Chain(dve, chain, i + 1)
                    dve.wait_ge(m["turned"], now)
                    dve.wait_ge(m["projected"], before)
                    dve.tensor_copy(xt[:, :, :], pt[:, :, :]).then_inc(m["xt_ready"], 1)
                    dve.wait_ge(m["projected"], now)
                    dve.wait_ge(m["multiplied"], before)
                    dve.wait_ge(m["kept"], before)
                    for t in range(2):
                        dve.tensor_tensor(qk[:, t, :, :], pqk[t][:, :, :], bias[:, 0:2 * D].rearrange("p (a b) -> p a b", a=2), ALU.add)
                    link(dve.tensor_tensor(v[:, :, :], pv[:, :, :], over(bias[:, 2 * D:3 * D], 1, [P, 2, D]), ALU.add))
                    dve.sem_inc(m["v_ready"])
                    s, rs, cent = st[:, 0, :, :], st[:, 1, :, :], st[:, 2, :, :]
                    full = [P, 2, 2, D]
                    link(dve.tensor_reduce(s, qk[:, :, :, :], AX, ALU.add))
                    link(dve.tensor_scalar(cent, s, -1.0 / D, None, ALU.mult))
                    link(dve.tensor_tensor(qk[:, :, :, :], qk[:, :, :, :], over(cent, 3, full), ALU.add))
                    link(dve.tensor_tensor(qk[:, :, :, :], qk[:, :, :, :], qk[:, :, :, :], ALU.mult))
                    link(dve.tensor_reduce(s, qk[:, :, :, :], AX, ALU.add))
                    link(dve.tensor_scalar(s, s, 1e-7, None, ALU.add))
                    link(dve.reciprocal(rs, s))
                    link(dve.tensor_tensor(rs[:, :, 1], rs[:, :, 1], g.valid[:, ds(i * 2, 2)], ALU.mult))
                    link(dve.tensor_tensor(qk[:, :, :, :], qk[:, :, :, :], over(rs, 3, full), ALU.mult))
                    dve.sem_inc(m["k_ready"])
                    dve.wait_ge(m["q_rooted"], now)
                    link(dve.tensor_scalar(qn[:, 1, :], qn[:, 1, :], 1e-12, None, ALU.max))
                    link(dve.reciprocal(qn[:, 1, :], qn[:, 1, :]))
                    dve.tensor_tensor(g.q[:, ds(i * 2, 2), :], qk[:, :, 0, :], over(qn[:, 1, :], 2, [P, 2, D]), ALU.mult)
                    dve.wait_ge(m["multiplied"], now)
                    dve.tensor_tensor(g.kvm[:, :, :], g.kvm[:, :, :], pkv[:, :, :], ALU.add)
                    dve.tensor_tensor(colsq[:, :], colsq[:, :], pcs[:, :], ALU.add).then_inc(m["kv_added"], 1)
                dve.wait_ge(m["kv_added"], PAIRS + 1)
                dve.sem_inc(asked)
                dve.wait_ge(rooted, 1)
                dve.tensor_scalar(colsq[:, :], colsq[:, :], 1e-12, None, ALU.max).then_inc(step, 1)
                dve.wait_ge(step, 1)
                dve.reciprocal(colsq[:, :], colsq[:, :]).then_inc(step, 1)
                dve.wait_ge(step, 2)
                dve.tensor_scalar(colsq[:, :], colsq[:, :], NODES ** -0.5, None, ALU.mult).then_inc(step, 1)
                dve.wait_ge(step, 3)
                dve.tensor_tensor(g.kvm[:, :, :], g.kvm[:, :, :], over(colsq[:, :], 2, [P, KD, D]), ALU.mult).then_inc(step, 1)


def mix1_out(nc, g, a):
    with Room(nc, "mo") as r:
        w = r.sbuf("w", [P, KD, D])
        bias = r.sbuf("bias", [P, D])
        un = r.sbuf("un", [P, 2, D])
        qt = r.sbuf("qt", [P, KD, PW])
        at = r.sbuf("at", [P, KD, PW])
        att = r.sbuf("att", [P, 2, D])
        o = r.sbuf("o", [P, 2, D])
        pt, pt2 = r.psum("pt", [P, KD, PW]), r.psum("pt2", [P, KD, PW])
        pa, po = r.psum("pa", [P, 2, D]), r.psum("po", [P, 2, D])
        loaded = r.sem("loaded")
        m = {n: r.sem(n) for n in ("copied", "turned", "qt_ready", "attended", "att_ready", "att_turned", "at_ready", "projected", "kept")}
        chain = r.sems("step", 2)
        credit(nc, list(m.values()))
        with nc.Block() as block:

            @block.sync
            def _(sp):
                sp.dma_start(w[:, :, :], weights(a["mout"])).then_inc(loaded, 16)
                sp.dma_start(bias[:, :], to_all(a["mbo"], D)).then_inc(loaded, 16)
                sp.wait_ge(loaded, 32)

            @block.scalar
            def _(act):
                with act.Fori(0, PAIRS) as i:
                    act.wait_ge(m["turned"], i + 1)
                    act.activation(un[:, :, :], g.q[:, ds(i * 2, 2), :], ACT.Copy).then_inc(m["copied"], 1)
                    act.wait_ge(m["att_turned"], i + 2)
                    act.wait_ge(m["projected"], i + 1)
                    act.activation(at[:, :, :], pt2[:, :, :], ACT.Copy).then_inc(m["at_ready"], 1)

            @block.tensor
            def _(pe):
                pe.wait_ge(loaded, 32)
                with pe.Fori(0, PAIRS) as i:
                    before, now = i + 1, i + 2
                    pe.wait_ge(m["copied"], now)
                    pe.wait_ge(m["qt_ready"], before)
                    turn_pair(pe, g, pt, un).then_inc(m["turned"], 1)
                    pe.wait_ge(m["qt_ready"], now)
                    pe.wait_ge(m["att_ready"], before)
                    for t in range(2):
                        for k in range(KD):
                            mm = pe.matmul(pa[:, t, :], qt[:, k, t * P:(t + 1) * P], g.kvm[:, k, :], start=(k == 0), stop=(k == KD - 1))
                    mm.then_inc(m["attended"], 1)
                    pe.wait_ge(m["att_ready"], now)
                    pe.wait_ge(m["at_ready"], before)
                    turn_pair(pe, g, pt2, att).then_inc(m["att_turned"], 1)
                    pe.wait_ge(m["at_ready"], now)
                    pe.wait_ge(m["kept"], before)
                    for t in range(2):
                        for k in range(KD):
                            mm = pe.matmul(po[:, t, :], at[:, k, t * P:(t + 1) * P], w[:, k, :], start=(k == 0), stop=(k == KD - 1))
                    mm.then_inc(m["projected"], 1)

            @block.vector
            def _(dve):
                dve.wait_ge(loaded, 32)
                with dve.Fori(0, PAIRS) as i:
                    before, now = i + 1, i + 2
                    link = Chain(dve, chain, i + 1)
                    dve.wait_ge(m["turned"], now)
                    dve.wait_ge(m["attended"], before)
                    dve.tensor_copy(qt[:, :, :], pt[:, :, :]).then_inc(m["qt_ready"], 1)
                    dve.wait_ge(m["attended"], now)
                    dve.wait_ge(m["att_turned"], before)
                    dve.tensor_tensor(att[:, :, :], pa[:, :, :], g.v[:, ds(i * 2, 2), :], ALU.add).then_inc(m["att_ready"], 1)
                    dve.wait_ge(m["projected"], now)
                    link(dve.tensor_tensor(o[:, :, :], po[:, :, :], over(bias[:, :], 1, [P, 2, D]), ALU.add))
                    dve.tensor_tensor(g.x[:, ds(i * 2, 2), :], g.x[:, ds(i * 2, 2), :], o[:, :, :], ALU.add).then_inc(m["kept"], 1)


def route1(nc, g, a):
    E = EXPERTS1
    CAP = float(math.ceil(NODES * 1.25 / E))
    with Room(nc, "ro") as r:
        part = r.sbuf("part", [P, 2, D])
        xm = r.sbuf("xm", [P, KD, P])
        wr = r.sbuf("wr", [P, KD, E])
        br = r.sbuf("br", [P, E])
        lg = r.sbuf("lg", [P, 3, 1, E])
        st = r.sbuf("st", [P, 4])
        hot = r.sbuf("hot", [P, 2])
        offs = r.sbuf("offs", [P, 8])
        offi = r.sbuf("offi", [P, 8], I32)
        rowf = r.sbuf("rowf", [P, 2, 8])
        rowi = r.sbuf("rowi", [P, 2, 8], I32)
        picks = Picks(r, E, 1)
        px = [r.psum(f"px{k}", [P, P]) for k in range(KD)]
        pl = r.psum("pl", [P, E])
        b2 = r.sbuf("b2", [P, 2, D])
        (loaded, made, parted, summed, xm_ready, logits, asked, exped, gapped, gap_exped, rows_ready, gathered, biased) = (
            r.sem(n) for n in ("loaded", "made", "parted", "summed", "xm_ready", "logits", "asked", "exped", "gapped", "gap_exped",
                               "rows_ready", "gathered", "biased"))
        step = r.sem("step")
        with nc.Block() as block:

            @block.sync
            def _(sp):
                sp.dma_start(wr[:, :, :], weights(a["wr"])).then_inc(loaded, 16)
                sp.dma_start(br[:, :], to_all(a["br"], E)).then_inc(loaded, 16)

            @block.gpsimd
            def _(pool):
                for k in range(4):
                    ins = pool.iota(offi[:, k:k + 1], pattern=[[0, 1]], base=k * P, channel_multiplier=1)
                ins = pool.memset(offi[:, 4:8], 0)
                ins.then_inc(made, 1)
                pool.wait_ge(rows_ready, 1)
                at = lambda j, k: bass.IndirectOffsetOnAxis(ap=rowi[:, j, k:k + 1], axis=0)
                for j in range(2):
                    for k in range(KD):
                        pool.indirect_dma_start(out=g.fw1[:, j, k, :], out_offset=None, in_=a["fw1"], in_offset=at(j, k)).then_inc(gathered, 16)
                    for k in range(KF):
                        pool.indirect_dma_start(out=g.fw2[:, j, k, :], out_offset=None, in_=a["fw2"], in_offset=at(j, 2 + k)).then_inc(gathered, 16)
                    pool.indirect_dma_start(out=g.fb1[:, j, :], out_offset=None, in_=a["fb1"], in_offset=at(j, 6)).then_inc(gathered, 16)
                    pool.indirect_dma_start(out=b2[:, j, :], out_offset=None, in_=a["fb2"], in_offset=at(j, 7)).then_inc(gathered, 16)
                pool.wait_ge(gathered, 16 * 2 * (KD + KF + 2))

            @block.tensor
            def _(pe):
                pe.wait_ge(parted, 1)
                for k in range(KD):
                    mm = pe.matmul(px[k][:, :], part[:, 1, k * P:(k + 1) * P], g.ones[:, :], start=True, stop=True)
                mm.then_inc(summed, 1)
                pe.wait_ge(xm_ready, 1)
                pe.wait_ge(loaded, 32)
                for k in range(KD):
                    mm = pe.matmul(pl[:, :], xm[:, k, :], wr[:, k, :], start=(k == 0), stop=(k == KD - 1))
                mm.then_inc(logits, 1)

            @block.scalar
            def _(act):
                for n in range(2):
                    act.wait_ge(asked, n + 1)
                    act.activation(lg[:, 1, 0, :], lg[:, 0, 0, :], ACT.Exp).then_inc(exped, 1)
                act.wait_ge(gapped, 1)
                act.activation(picks.small[:, 7, :], picks.small[:, 4, :], ACT.Exp).then_inc(gap_exped, 1)

            @block.vector
            def _(dve):
                count = [0]

                def link(ins):
                    count[0] += 1
                    ins.then_inc(step, 1)
                    dve.wait_ge(step, count[0])

                link(picks.order_of(dve))
                link(dve.tensor_reduce(part[:, 0, :], g.u[:, 0:FULL, :].rearrange("p t d -> p d t"), AX, ALU.add))
                dve.scalar_tensor_tensor(out=part[:, 1, :], in0=g.u[:, FULL, :], scalar=g.valid[:, FULL:FULL + 1], in1=part[:, 0, :],
                                         op0=ALU.mult, op1=ALU.add).then_inc(parted, 1)
                dve.wait_ge(summed, 1)
                for k in range(KD):
                    ins = dve.tensor_scalar(xm[:, k, :], px[k][:, :], 1.0 / NODES, None, ALU.mult)
                ins.then_inc(xm_ready, 1)
                dve.wait_ge(logits, 1)
                link(dve.tensor_tensor(lg[:, 0, 0, :], pl[:, :], br[:, :], ALU.add))
                link(dve.tensor_reduce(st[:, 0:1], lg[:, 0, 0, :], AX, ALU.max))
                for n in range(2):
                    dve.tensor_scalar(lg[:, 0, 0, :], lg[:, 0, 0, :], st[:, 0:1], None, ALU.subtract).then_inc(asked, 1)
                    dve.wait_ge(exped, n + 1)
                    link(dve.tensor_reduce(st[:, 1:2], lg[:, 1, 0, :], AX, ALU.add))
                    link(dve.reciprocal(st[:, 1:2], st[:, 1:2]))
                    link(dve.tensor_scalar(lg[:, 1, 0, :], lg[:, 1, 0, :], st[:, 1:2], None, ALU.mult))
                    if n == 0:
                        link(dve.tensor_scalar(lg[:, 2, 0, :], lg[:, 1, 0, :], float(NODES), None, ALU.mult))
                        link(dve.reciprocal(lg[:, 2, 0, :], lg[:, 2, 0, :]))
                        link(dve.tensor_scalar(lg[:, 2, 0, :], lg[:, 2, 0, :], CAP, 1.0, ALU.mult, ALU.min))
                        link(dve.tensor_tensor(lg[:, 0, 0, :], lg[:, 1, 0, :], lg[:, 2, 0, :], ALU.mult))
                        link(dve.tensor_reduce(st[:, 0:1], lg[:, 0, 0, :], AX, ALU.max))

                def wait_exp(ins):
                    ins.then_inc(gapped, 1)
                    dve.wait_ge(gap_exped, 1)

                link(pick_two(dve, link, lg[:, 1, :, :], picks, E, 1, wait_exp))
                link(dve.tensor_copy(g.fw[:, :], picks.small[:, 5:7, 0]))
                dve.wait_ge(made, 1)
                link(dve.tensor_copy(offs[:, :], offi[:, :]))
                for j in range(2):
                    e = picks.small[:, 2 + j, :]
                    for at, n, size in ((0, KD, D), (2, KF, F1), (6, 1, P), (7, 1, 1)):
                        base = offs[:, 0:n] if at != 7 else offs[:, 4:5]
                        link(dve.scalar_tensor_tensor(out=rowf[:, j, at:at + n], in0=e.to_broadcast([P, n]), scalar=float(size), in1=base,
                                                      op0=ALU.mult, op1=ALU.add))
                dve.tensor_copy(rowi[:, :, :], rowf[:, :, :]).then_inc(rows_ready, 1)
                dve.wait_ge(gathered, 16 * 2 * (KD + KF + 2))
                link(dve.tensor_scalar(b2[:, 0, :], b2[:, 0, :], g.fw[:, 0:1], None, ALU.mult))
                link(dve.scalar_tensor_tensor(out=g.fb2[:, :], in0=b2[:, 1, :], scalar=g.fw[:, 1:2], in1=b2[:, 0, :], op0=ALU.mult, op1=ALU.add))


def experts1(nc, g, a, out):
    with Room(nc, "fe") as r:
        gamma, beta = r.sbuf("gamma", [P, D]), r.sbuf("beta", [P, D])
        un = r.sbuf("un", [P, 2, D])
        xt = r.sbuf("xt", [P, KD, PW])
        h = r.sbuf("h", [P, 2, KF, PW])
        z = r.sbuf("z", [P, 2, D])
        junk = r.sbuf("junk", [P, 2, D])
        stat = r.sbuf("stat", [P, 3, 2])
        pt = r.psum("pt", [P, KD, PW])
        ph = [[r.psum(f"ph{j}{c}", [P, 2, PW]) for c in range(2)] for j in range(2)]
        po = [r.psum(f"po{j}", [P, 2, D]) for j in range(2)]
        loaded, stored, passed = r.sem("loaded"), r.sem("stored"), r.sem("passed")
        m = {n: r.sem(n) for n in ("copied", "turned", "xt_ready", "hidden0", "hidden1", "h0_ready", "h1_ready", "projected",
                                   "var_ready", "std_ready", "mixed", "res_ready")}
        chain = r.sems("step", 16)
        credit(nc, list(m.values()))
        with nc.Block() as block:

            @block.sync
            def _(sp):
                sp.dma_start(gamma[:, :], to_all(a["fg"], D)).then_inc(loaded, 16)
                sp.dma_start(beta[:, :], to_all(a["fb"], D)).then_inc(loaded, 16)
                sp.wait_ge(loaded, 32)
                sp.wait_ge(m["res_ready"], PAIRS + 1)
                sp.dma_start(out[0:FULL * P, :].rearrange("(t p) c -> p t c", p=P), g.x[:, 0:FULL, :]).then_inc(stored, 16)
                sp.dma_start(out[FULL * P:NODES, :], g.x[0:REST, FULL, :]).then_inc(stored, 16)
                sp.wait_ge(stored, 32)

            @block.scalar
            def _(act):
                with act.Fori(0, PAIRS) as i:
                    before, now = i + 1, i + 2
                    act.wait_ge(m["turned"], before)
                    act.wait_ge(m["mixed"], before)
                    act.activation(un[:, :, :], g.u[:, ds(i * 2, 2), :], ACT.Copy).then_inc(m["copied"], 1)
                    act.wait_ge(m["projected"], before)
                    for j in range(2):
                        act.wait_ge(m[f"hidden{j}"], now)
                        for c in range(KF):
                            ins = act.activation(h[:, j, c, :], ph[j][c // 2][:, c % 2, :], ACT.Gelu, bias=g.fb1[:, j, c:c + 1])
                        ins.then_inc(m[f"h{j}_ready"], 1)
                    act.wait_ge(m["var_ready"], now)
                    act.activation(stat[:, 2, :], stat[:, 1, :], ACT.Sqrt).then_inc(m["std_ready"], 1)

            @block.tensor
            def _(pe):
                with pe.Fori(0, PAIRS) as i:
                    before, now = i + 1, i + 2
                    pe.wait_ge(m["copied"], now)
                    pe.wait_ge(m["xt_ready"], before)
                    turn_pair(pe, g, pt, un).then_inc(m["turned"], 1)
                    pe.wait_ge(m["xt_ready"], now)
                    pe.wait_ge(m["h1_ready"], before)
                    for j in range(2):
                        for c in range(KF):
                            for k in range(KD):
                                mm = pe.matmul(ph[j][c // 2][:, c % 2, :], g.fw1[:, j, k, c * P:(c + 1) * P], xt[:, k, :],
                                               start=(k == 0), stop=(k == KD - 1))
                        mm.then_inc(m[f"hidden{j}"], 1)
                    pe.wait_ge(m["mixed"], before)
                    for j in range(2):
                        pe.wait_ge(m[f"h{j}_ready"], now)
                        for t in range(2):
                            for k in range(KF):
                                mm = pe.matmul(po[j][:, t, :], h[:, j, k, t * P:(t + 1) * P], g.fw2[:, j, k, :], start=(k == 0), stop=(k == KF - 1))
                    mm.then_inc(m["projected"], 1)

            @block.vector
            def _(dve):
                dve.wait_ge(loaded, 32)
                with dve.Fori(0, PAIRS) as i:
                    before, now = i + 1, i + 2
                    link = Chain(dve, chain, i + 1)
                    dve.wait_ge(m["turned"], now)
                    dve.wait_ge(m["hidden1"], before)
                    dve.tensor_copy(xt[:, :, :], pt[:, :, :]).then_inc(m["xt_ready"], 1)
                    dve.wait_ge(m["copied"], now)
                    dve.wait_ge(m["res_ready"], before)
                    link(dve.tensor_tensor(z[:, :, :], un[:, :, :], over(g.fb2[:, :], 1, [P, 2, D]), ALU.add))
                    dve.wait_ge(m["projected"], now)
                    for j in range(2):
                        ins = dve.scalar_tensor_tensor(out=z[:, :, :], in0=po[j][:, :, :], scalar=g.fw[:, j:j + 1], in1=z[:, :, :],
                                                       op0=ALU.mult, op1=ALU.add)
                        if j == 0:
                            link(ins)
                    ins.then_inc(m["mixed"], 1)
                    dve.wait_ge(m["mixed"], now)
                    ln_pair(dve, link, z[:, :, :], stat, junk, lambda ins: ins.then_inc(m["var_ready"], 1),
                            lambda: dve.wait_ge(m["std_ready"], now))
                    link(dve.tensor_tensor(z[:, :, :], z[:, :, :], over(gamma[:, :], 1, [P, 2, D]), ALU.mult))
                    link(dve.tensor_tensor(z[:, :, :], z[:, :, :], over(beta[:, :], 1, [P, 2, D]), ALU.add))
                    dve.tensor_tensor(g.x[:, ds(i * 2, 2), :], g.x[:, ds(i * 2, 2), :], z[:, :, :], ALU.add).then_inc(m["res_ready"], 1)


class Shared:
    pass


def gps_kernel(nc, a, out, scratch):
    with Room(nc, "g") as room:
        g = Shared()
        g.x = room.sbuf("x", [P, NT, D])
        g.u = room.sbuf("u", [P, NT, D])
        g.ut = room.sbuf("ut", [P, KD, NPAD])
        g.idx = room.sbuf("idx", [P, ET, 4], I32)
        g.kinds = room.sbuf("kinds", [P, ET, 4])
        g.ident = room.sbuf("ident", [P, P])
        g.identb = room.sbuf("identb", [P, P], BF16)
        g.ones = room.sbuf("ones", [P, P])
        g.lower = room.sbuf("lower", [P, P])
        g.picks = room.sbuf("picks", [P, H0, P])
        g.spill = room.sbuf("spill", [P, 1])
        g.valid = room.sbuf("valid", [P, NT])
        g.g0 = room.sbuf("g0", [P, NT])
        g.usum = room.sbuf("usum", [P, KD])
        g.bn_scale = room.sbuf("bn_scale", [P, QKV])
        g.bn_beta = room.sbuf("bn_beta", [P, QKV])
        g.rowf = room.sbuf("rowf", [P, ET, 2])
        g.tabs0 = [scratch(f"tabs0_{k}", (TROWS, H0 * (D0 + 1) + H0), F32) for k in range(NTAB)]
        g.hid = g.ut[:, :, :].rearrange("p k n -> p (k n)").rearrange("p (t d) -> p t d", d=D)
        g.qrows = scratch("qrows", (NPAD, D), F32)
        g.kvrows = scratch("kvrows", (NPAD, 2 * D), F32)
        g.tabs1 = [scratch(f"tabs1_{k}", (TROWS, ROW1), F32) for k in range(NTAB)]
        g.hc = scratch("hc", (NPAD, QKV), F32)
        g.table0 = scratch("table0", (NPAD, ROW0), F32)
        load_inputs(nc, g, a)
        normalize(nc, g, "norm0", g.g0[:, :])
        log_scale(nc, g)
        node_rows(nc, g, a)
        mix_stats(nc, g, a)
        mix(nc, g, a)
        spill_duplicates(nc, g)
        attend0(nc, g, a)
        merge0(nc, g, a)
        normalize(nc, g, "norm1")
        experts0(nc, g, a)
        normalize(nc, g, "norm2")
        enter1(nc, g, a)
        with nc.Fori(0, LAYERS) as l:
            project1(nc, g, a, l)
            attend1(nc, g)
            update1(nc, g, a, l)
        adjust1(nc, g, a)
        with Room(nc, "m1") as r:
            g.q = g.hid
            g.v = r.sbuf("v", [P, NT, D])
            g.kvm = r.sbuf("kvm", [P, KD, D])
            mix1_keys(nc, g, a)
            mix1_out(nc, g, a)
        normalize(nc, g, "norm3")
        with Room(nc, "f1") as r:
            g.fw1 = r.sbuf("fw1", [P, 2, KD, F1])
            g.fw2 = r.sbuf("fw2", [P, 2, KF, D])
            g.fb1 = r.sbuf("fb1", [P, 2, KF])
            g.fb2 = r.sbuf("fb2", [P, D])
            g.fw = r.sbuf("fw", [P, 2])
            route1(nc, g, a)
            experts1(nc, g, a, out)


def _layout(v):
    import numpy as _np

    n = {k: _np.asarray(t) for k, t in v.items()}
    f = _np.float32
    ea = _np.zeros((P * ET, 3), f)
    ea[:EDGES] = n["edge_attr_3"]
    ablk = _np.zeros((D, 2 * H0), f)
    for h in range(H0):
        ablk[h * D0:(h + 1) * D0, h] = n["L0_gnn_a_src"][h]
        ablk[h * D0:(h + 1) * D0, H0 + h] = n["L0_gnn_a_dst"][h]
    pw = _np.zeros((QKV, P), f)
    for grp in range(QKV // GD):
        c = (grp * GD) % P
        pw[grp * GD:(grp + 1) * GD, c:c + GD] = n["L0_mix_w_pw"][grp * GD:(grp + 1) * GD, :, 0].T
    t = lambda w: _np.swapaxes(w, -1, -2)
    flat = lambda w: w.reshape(-1, w.shape[-1])
    return dict(
        x=n["x"], src=n["src"], dst=n["dst"], kind=n["edge_type_3"],
        ea=ea.reshape(P, ET, 3).transpose(2, 1, 0),
        gW=n["L0_gnn_W"], gWT=t(n["L0_gnn_W"]), ablk=ablk, eWT=t(n["L0_gnn_edge_W"]),
        eb=n["L0_gnn_edge_b"], gbias=n["L0_gnn_bias"],
        wqkv=t(n["L0_mix_w_qkv"][:, :, 2]), gamma=n["L0_mix_bn_gamma"], beta=n["L0_mix_bn_beta"],
        wdw=n["L0_mix_w_dw"][:, 0, 2].reshape(-1, P).T, pw=pw, wres=t(n["L0_mix_w_res"][:, :, 0]), bres=n["L0_mix_b_res"],
        rw1=n["L0_ffn_router_w1"], rb1=n["L0_ffn_router_b1"].reshape(P, 1), rw2=n["L0_ffn_router_w2"], rb2=n["L0_ffn_router_b2"],
        ew1=flat(n["L0_ffn_expert_w1"]), eb1=n["L0_ffn_expert_b1"].reshape(-1, P).T, ew2=flat(n["L0_ffn_expert_w2"]), eb2=n["L0_ffn_expert_b2"].reshape(-1, P).T,
        ew3=flat(n["L0_ffn_expert_w3"]), eb3=n["L0_ffn_expert_b3"],
        winT=t(n["L1_gnn_Win"]), b_in=n["L1_gnn_b_in"],
        wqT=flat(t(n["L1_gnn_Wq"])), bq=n["L1_gnn_bq"], wkT=flat(t(n["L1_gnn_Wk"])), bk=n["L1_gnn_bk"],
        wvT=flat(t(n["L1_gnn_Wv"])), bv=n["L1_gnn_bv"], eemb=flat(t(n["L1_gnn_Eemb"])),
        woT=flat(t(n["L1_gnn_Wo"])), bo=n["L1_gnn_bo"], ln_g=n["L1_gnn_ln_g"], ln_b=n["L1_gnn_ln_b"],
        w1T=t(n["L1_gnn_W1"]), b1=n["L1_gnn_b1"].reshape(-1, P).T, w2T=t(n["L1_gnn_W2"]), b2=n["L1_gnn_b2"],
        mqkv=n["L1_mix_W_qkv"], mb=n["L1_mix_b_qkv"], mout=n["L1_mix_W_out"], mbo=n["L1_mix_b_out"],
        wr=n["L1_ffn_Wr"], br=n["L1_ffn_br"], fw1=flat(n["L1_ffn_W1"]), fb1=n["L1_ffn_b1"].reshape(EXPERTS1, KF, P).transpose(0, 2, 1).reshape(-1, KF),
        fw2=flat(n["L1_ffn_W2"]), fb2=n["L1_ffn_b2"], fg=n["L1_ffn_gamma"], fb=n["L1_ffn_beta"],
    )


def kernel(**inputs):
    import numpy as _np
    import concourse.bacc as _bacc
    from concourse import mybir as _mybir
    from concourse.bass_utils import run_bass_kernel_spmd as _run

    nc = _bacc.Bacc("TRN2", target_bir_lowering=False, num_devices=1)
    arrays, drams = {}, {}
    for name, v in _layout(inputs).items():
        v = _np.ascontiguousarray(v)
        arrays[f"in_{name}_dram"] = v
        drams[name] = nc.dram_tensor(f"in_{name}_dram", v.shape, _mybir.dt.from_np(v.dtype), kind="ExternalInput").ap()
    out = nc.dram_tensor("out_0_dram", (NODES, D), F32, kind="ExternalOutput").ap()

    def scratch(name, shape, dt):
        return nc.dram_tensor(name, shape, dt, kind=SCRATCH).ap()

    gps_kernel(nc, drams, out, scratch)
    r = _run(nc, [arrays], core_ids=[0])
    return r.results[0]["out_0_dram"]


SCRATCH = "Internal"
```

```python
import math
from contextlib import ExitStack

import numpy as np

import concourse.bass as bass
from concourse import mybir

F32 = mybir.dt.float32
BF16 = mybir.dt.bfloat16
I32 = mybir.dt.int32
ALU = mybir.AluOpType
ACT = mybir.ActivationFunctionType
AX = mybir.AxisListType.X
ds = bass.ds

P = 128
NODES = 3125
D = 256
KD = D // P
NT = 26
NPAD = NT * P
PAIRS = NT // 2
PW = 2 * P
FULL = NODES // P
REST = NODES - FULL * P
EDGES = 50000
ET = 392
U = 4
TURNS = ET // U
LASTP = EDGES // ET
LASTN = EDGES - LASTP * ET
H0, D0 = 8, 32
ROW0 = D + 2 * H0
ACC0 = H0 * (D0 + 1)
HG, DG = 4, 64
ROW1 = D + 4
TROWS = NPAD + P
NTAB = 4
LAYERS = 3
QKV = 3 * D
GRP, GD = 16, 32
EXPERTS0 = 6
EXPERTS1, F1, KF = 8, 512, 4
LOWEST = -3.0e38
EPS = 1e-5
BALL = float(np.float32(1.0 - 1e-5))
ATANH_BALL = 0.5 * math.log((1.0 + BALL) / (1.0 - BALL))
MIN_NORM = 1e-15
ATT_EPS = 1e-15


class Room:

    def __init__(self, nc, name):
        self.nc, self.name, self.ctx, self.taken = nc, name, ExitStack(), []

    def __enter__(self):
        return self

    def __exit__(self, *a):
        self.nc.clear_and_free_semaphores(self.taken)
        self.nc.all_engine_barrier()
        return self.ctx.__exit__(*a)

    def sbuf(self, name, shape, dt=F32):
        return self.ctx.enter_context(self.nc.sbuf_tensor(f"{self.name}_{name}", shape, dt))

    def psum(self, name, shape, dt=F32):
        return self.ctx.enter_context(self.nc.psum_tensor(f"{self.name}_{name}", shape, dt))

    def sem(self, name):
        self.taken.append(self.nc.alloc_semaphore(f"{self.name}_{name}"))
        return self.taken[-1]

    def sems(self, name, n):
        return [self.sem(f"{name}{i}") for i in range(n)]


class Chain:

    def __init__(self, eng, sems, turn):
        self.eng, self.sems, self.turn, self.n = eng, sems, turn, 0

    def __call__(self, ins):
        ins.then_inc(self.sems[self.n], 1)
        self.eng.wait_ge(self.sems[self.n], self.turn)
        self.n += 1


def credit(nc, sems, n=1):
    with nc.Block() as block:

        @block.sync
        def _(sp):
            for s in sems:
                sp.sem_inc(s, n)


def rows_of(buf, n):
    return buf[:, 2 * n:2 * n + 2, :] if isinstance(n, int) else buf[:, ds(n * 2, 2), :]


def pair_steps(eng, body, first, last):
    lead = last + last % 2
    turns = (PAIRS - first - lead) // 2
    for n in range(-first, lead):
        body(n, n % 2)
    with eng.Fori(0, turns) as i:
        for slot in range(2):
            body(i * 2 + (lead + slot), slot)
    for n in range(lead + 2 * turns, PAIRS + last):
        body(n, n % 2)


class Marks:

    def __init__(self, nc, r, names):
        self.sems = {n: r.sem(n) for n in names}
        credit(nc, list(self.sems.values()), 2)

    def __getitem__(self, name):
        return self.sems[name]

    def done(self, eng, name, n, lag=0):
        eng.wait_ge(self.sems[name], n + (3 - lag))


def hold(eng, sem, value, passed):
    eng.wait_ge(sem, value)
    eng.sem_inc(passed)


def over(ap, axis, shape):
    return ap.unsqueeze(axis).to_broadcast(shape)


def weights(w):
    return w.rearrange("(k p) n -> p k n", p=P)


def to_all(v, n):
    return v.rearrange("(a n) -> a n", a=1).to_broadcast([P, n])


def rows(t, i, width=PW):
    return t[ds(i * width, width), :].rearrange("(t p) c -> p t c", p=P)


def load_inputs(nc, g, a):
    with Room(nc, "load") as r:
        idx1 = [r.sbuf(f"idx{i}", [P, ET], I32) for i in range(3)]
        tf = r.sbuf("typef", [P, ET])
        pi = r.sbuf("pidx", [P, 1], I32)
        pads, loaded = r.sem("pads_ready"), r.sem("loaded")
        steps, made, pool = r.sem("steps"), r.sem("made"), r.sem("pool")
        with nc.Block() as block:

            @block.vector
            def _(dve):
                dve.memset(g.x[:, FULL:NT, :], 0.0).then_inc(pads, 1)
                for i in range(2):
                    dve.memset(idx1[i][96:P, :], NPAD - 1).then_inc(pads, 1)
                dve.memset(idx1[2][96:P, :], 0).then_inc(pads, 1)
                dve.memset(g.ones[:, :], 1.0)
                dve.memset(g.valid[:, 0:FULL], 1.0)
                dve.memset(g.valid[:, FULL:NT], 0.0).then_inc(steps, 1)
                dve.wait_ge(steps, 1)
                dve.memset(g.valid[0:REST, FULL:FULL + 1], 1.0).then_inc(steps, 1)
                dve.wait_ge(loaded, 16 * 10)
                for i in range(2):
                    dve.tensor_copy(g.idx[:, :, i], idx1[i][:, :])
                dve.tensor_copy(tf[:, :], idx1[2][:, :]).then_inc(steps, 1)
                dve.wait_ge(steps, 3)
                for j in range(3):
                    dve.tensor_scalar(g.kinds[:, :, j], tf[:, :], float(j), None, ALU.is_equal)
                dve.memset(g.kinds[:, :, 3], 1.0).then_inc(steps, 1)
                dve.wait_ge(made, 4)
                dve.tensor_copy(g.identb[:, :], g.ident[:, :])
                dve.tensor_copy(g.spill[:, :], pi[:, :])
                dve.wait_ge(steps, 4)

            @block.gpsimd
            def _(pool_):
                pool_.memset(g.ident[:, :], 0.0).then_inc(pool, 1)
                pool_.memset(g.lower[:, :], 1.0).then_inc(pool, 1)
                pool_.wait_ge(pool, 2)
                pool_.affine_select(out=g.ident[:, :], in_=g.ident[:, :], compare_op=ALU.not_equal, fill=1.0,
                                    base=0, pattern=[[-1, P]], channel_multiplier=1).then_inc(made, 1)
                pool_.affine_select(out=g.lower[:, :], in_=g.lower[:, :], compare_op=ALU.is_gt, fill=0.0,
                                    base=0, pattern=[[-1, P]], channel_multiplier=1).then_inc(made, 1)
                pool_.iota(pi[:, :], pattern=[[0, 1]], base=NPAD, channel_multiplier=1).then_inc(made, 1)
                pool_.memset(g.picks[:, :, :], 0.0).then_inc(pool, 1)
                pool_.wait_ge(pool, 3)
                pool_.affine_select(out=g.picks[:, :, :], in_=g.picks[:, :, :], compare_op=ALU.not_equal, fill=1.0,
                                    base=0, pattern=[[-1, H0], [0, P]], channel_multiplier=1).then_inc(made, 1)

            @block.sync
            def _(sp):
                sp.dma_start(g.bn_scale[:, :], to_all(a["gamma"], QKV)).then_inc(loaded, 16)
                sp.dma_start(g.bn_beta[:, :], to_all(a["beta"], QKV)).then_inc(loaded, 16)
                sp.wait_ge(pads, 4)
                sp.dma_start(g.x[:, 0:FULL, :], a["x"][0:FULL * P, :].rearrange("(t p) c -> p t c", p=P)).then_inc(loaded, 16)
                for i, v in enumerate((a["src"], a["dst"], a["kind"])):
                    sp.dma_start(idx1[i][0:LASTP, :], v[0:LASTP * ET].rearrange("(p j) -> p j", j=ET)).then_inc(loaded, 16)
                    sp.dma_start(idx1[i][LASTP:P, 0:LASTN], v[LASTP * ET:EDGES].rearrange("(p j) -> p j", p=1)).then_inc(loaded, 16)
                sp.dma_start(g.x[0:REST, FULL, :], a["x"][FULL * P:NODES, :]).then_inc(loaded, 16)
                sp.wait_ge(loaded, 16 * 10)


def normalize(nc, g, name, squares=None):
    with Room(nc, name) as r:
        sq = r.sbuf("sq", [P, NT, D])
        st = r.sbuf("st", [P, 4, NT])
        step = r.sem("step")
        centred, squared, var, std = r.sem("centred"), r.sem("squared"), r.sem("var_ready"), r.sem("std_ready")
        with nc.Block() as block:

            @block.vector
            def _(dve):
                dve.tensor_reduce(st[:, 0, :], g.x[:, :, :], AX, ALU.add).then_inc(step, 1)
                dve.wait_ge(step, 1)
                dve.tensor_scalar(st[:, 1, :], st[:, 0, :], -1.0 / D, None, ALU.mult).then_inc(step, 1)
                dve.wait_ge(step, 2)
                dve.tensor_tensor(g.u[:, :, :], g.x[:, :, :], over(st[:, 1, :], 2, [P, NT, D]), ALU.add).then_inc(centred, 1)
                dve.wait_ge(squared, 1)
                dve.tensor_reduce(st[:, 0, :], sq[:, :, :], AX, ALU.add).then_inc(step, 1)
                dve.wait_ge(step, 3)
                dve.tensor_scalar(st[:, 2, :], st[:, 0, :], 1.0 / D, EPS, ALU.mult, ALU.add).then_inc(var, 1)
                dve.wait_ge(var, 1)
                dve.wait_ge(std, 1)
                dve.reciprocal(st[:, 2, :], st[:, 3, :]).then_inc(step, 1)
                dve.wait_ge(step, 4)
                dve.tensor_tensor(g.u[:, :, :], g.u[:, :, :], over(st[:, 2, :], 2, [P, NT, D]), ALU.mult).then_inc(step, 1)
                if squares is not None:
                    dve.tensor_tensor(st[:, 3, :], st[:, 2, :], st[:, 2, :], ALU.mult).then_inc(step, 1)
                    dve.wait_ge(step, 6)
                    dve.tensor_tensor(squares, st[:, 3, :], st[:, 0, :], ALU.mult).then_inc(step, 1)

            @block.scalar
            def _(act):
                act.wait_ge(centred, 1)
                act.activation(sq[:, :, :], g.u[:, :, :], ACT.Square).then_inc(squared, 1)
                act.wait_ge(var, 1)
                act.activation(st[:, 3, :], st[:, 2, :], ACT.Sqrt).then_inc(std, 1)


def log_scale(nc, g):
    SMALL = 0.25
    with Room(nc, "logs") as r:
        w = r.sbuf("w", [P, 10, NT])
        n, nn, z, poly, one_m, q, ln, rn, mask, tmp = (w[:, i, :] for i in range(10))
        step, rooted, ratio, logged, asked = r.sem("step"), r.sem("norm_ready"), r.sem("ratio_ready"), r.sem("log_ready"), r.sem("asked")
        with nc.Block() as block:

            @block.vector
            def _(dve):
                count = [0]

                def link(ins):
                    count[0] += 1
                    ins.then_inc(step, 1)
                    dve.wait_ge(step, count[0])

                dve.wait_ge(rooted, 1)
                link(dve.tensor_scalar(n, n, MIN_NORM, None, ALU.max))
                link(dve.tensor_scalar(nn, n, BALL, None, ALU.min))
                link(dve.tensor_scalar(one_m, nn, -1.0, 1.0, ALU.mult, ALU.add))
                link(dve.reciprocal(q, one_m))
                link(dve.tensor_scalar(tmp, nn, 1.0, None, ALU.add))
                dve.tensor_tensor(q, tmp, q, ALU.mult).then_inc(ratio, 1)
                link(dve.tensor_tensor(z, nn, nn, ALU.mult))
                link(dve.tensor_scalar(poly, z, 1.0 / 13, 1.0 / 11, ALU.mult, ALU.add))
                for c in (9, 7, 5, 3, 1):
                    link(dve.tensor_tensor(poly, poly, z, ALU.mult))
                    link(dve.tensor_scalar(poly, poly, 1.0 / c, None, ALU.add))
                link(dve.reciprocal(rn, n))
                dve.wait_ge(logged, 1)
                link(dve.scalar_tensor_tensor(out=ln, in0=ln, scalar=0.5, in1=rn, op0=ALU.mult, op1=ALU.mult))
                link(dve.tensor_scalar(mask, n, SMALL, None, ALU.is_lt))
                link(dve.tensor_tensor(tmp, poly, ln, ALU.subtract))
                link(dve.tensor_tensor(tmp, tmp, mask, ALU.mult))
                link(dve.tensor_tensor(g.g0[:, :], tmp, ln, ALU.add))

            @block.scalar
            def _(act):
                act.activation(n, g.g0[:, :], ACT.Sqrt).then_inc(rooted, 1)
                act.wait_ge(ratio, 1)
                act.activation(ln, q, ACT.Ln).then_inc(logged, 1)


def node_rows(nc, g, a):
    with Room(nc, "rows") as r:
        wnat = r.sbuf("wnat", [P, KD, D])
        ablk = r.sbuf("ablk", [P, KD, 2 * H0])
        wall = r.sbuf("wall", [P, KD, ROW0])
        un = r.sbuf("un", [P, 2, D])
        uts = r.sbuf("uts", [P, KD, PW])
        gs = r.sbuf("gs", [P, 2])
        ho = r.sbuf("ho", [P, 2, ROW0])
        pt = r.psum("pt", [P, KD, PW])
        ph = [r.psum(f"ph{i}", [P, 512]) for i in range(2)]
        pu = r.psum("pu", [P, 512])
        pa = r.psum("pa", [P, 512])
        loaded, folded, wready = r.sem("loaded"), r.sem("folded"), r.sem("wall_ready")
        copied, turned, ut_kept, uts_ready = r.sem("pair_copied"), r.sem("pair_turned"), r.sem("ut_kept"), r.sem("uts_ready")
        summed, added, projected = r.sem("summed"), r.sem("sum_added"), r.sem("projected")
        ho_ready, stored, ho_sent, passed = r.sem("ho_ready"), r.sem("stored"), r.sem("ho_sent"), r.sem("passed")
        credit(nc, [copied, turned, ut_kept, uts_ready, summed, added, projected, ho_ready, ho_sent])
        with nc.Block() as block:

            @block.sync
            def _(sp):
                sp.dma_start(wnat[:, :, :], weights(a["gW"])).then_inc(loaded, 16)
                sp.dma_start(ablk[:, :, :], weights(a["ablk"])).then_inc(loaded, 16)
                sp.dma_start(wall[:, :, 0:D], weights(a["gWT"])).then_inc(loaded, 16)
                with sp.Fori(0, PAIRS) as i:
                    hold(sp, ho_ready, i + 2, passed)
                    sp.dma_start(rows(g.table0, i), ho[:, :, :]).then_inc(stored, 16)
                    hold(sp, stored, i * 16 + 16, ho_sent)

            @block.tensor
            def _(pe):
                pe.wait_ge(loaded, 48)
                for c in range(KD):
                    for k in range(KD):
                        mm = pe.matmul(pa[:, c * 16:c * 16 + 16], wnat[:, k, c * P:(c + 1) * P], ablk[:, k, :],
                                       start=(k == 0), stop=(k == KD - 1))
                mm.then_inc(folded, 1)
                pe.wait_ge(wready, 1)
                with pe.Fori(0, PAIRS) as i:
                    before, now = i + 1, i + 2
                    pe.wait_ge(copied, now)
                    pe.wait_ge(uts_ready, before)
                    for t in range(2):
                        for k in range(KD):
                            mm = pe.transpose(pt[:, k, t * P:(t + 1) * P], un[:, t, k * P:(k + 1) * P], g.ident[:, :])
                    mm.then_inc(turned, 1)
                    pe.wait_ge(added, before)
                    for k in range(KD):
                        for t in range(2):
                            mm = pe.matmul(pu[:, k:k + 1], un[:, t, k * P:(k + 1) * P], gs[:, t:t + 1],
                                           start=(t == 0), stop=(t == 1))
                    mm.then_inc(summed, 1)
                    pe.wait_ge(uts_ready, now)
                    pe.wait_ge(ho_ready, before)
                    for t in range(2):
                        for k in range(KD):
                            mm = pe.matmul(ph[t][:, 0:ROW0], uts[:, k, t * P:(t + 1) * P], wall[:, k, :],
                                           start=(k == 0), stop=(k == KD - 1))
                    mm.then_inc(projected, 1)

            @block.scalar
            def _(act):
                with act.Fori(0, PAIRS) as i:
                    before, now = i + 1, i + 2
                    act.wait_ge(summed, before)
                    act.activation(un[:, :, :], g.u[:, ds(i * 2, 2), :], ACT.Copy)
                    act.activation(gs[:, :], g.g0[:, ds(i * 2, 2)], ACT.Copy).then_inc(copied, 1)
                    act.wait_ge(uts_ready, now)
                    act.activation(g.ut[:, :, ds(i * PW, PW)], uts[:, :, :], ACT.Copy).then_inc(ut_kept, 1)

            @block.vector
            def _(dve):
                dve.memset(g.usum[:, :], 0.0)
                dve.wait_ge(folded, 1)
                dve.tensor_copy(wall[:, :, D:ROW0], pa[:, 0:KD * 16].rearrange("p (k n) -> p k n", k=KD)).then_inc(wready, 1)
                dve.wait_ge(wready, 1)
                with dve.Fori(0, PAIRS) as i:
                    before, now = i + 1, i + 2
                    dve.wait_ge(turned, now)
                    dve.wait_ge(projected, before)
                    dve.wait_ge(ut_kept, before)
                    dve.tensor_copy(uts[:, :, :], pt[:, :, :]).then_inc(uts_ready, 1)
                    dve.wait_ge(summed, now)
                    dve.tensor_tensor(g.usum[:, :], g.usum[:, :], pu[:, 0:KD], ALU.add).then_inc(added, 1)
                    dve.wait_ge(projected, now)
                    dve.wait_ge(ho_sent, before)
                    dve.tensor_copy(ho[:, 0, :], ph[0][:, 0:ROW0])
                    dve.tensor_copy(ho[:, 1, :], ph[1][:, 0:ROW0]).then_inc(ho_ready, 1)


HALF = QKV // 2
KQ = QKV // P


def mix_stats(nc, g, a):
    with Room(nc, "ms") as r:
        w = r.sbuf("w", [P, KD, QKV])
        umean = r.sbuf("umean", [P, KD, P])
        mean = r.sbuf("mean", [P, QKV])
        uts = r.sbuf("uts", [P, 2, KD, PW])
        hc = r.sbuf("hc", [P, 2, 2, QKV])
        sq = r.sbuf("sq", [P, 2, QKV])
        ssum = r.sbuf("ssum", [P, QKV])
        ph = [r.psum(f"ph{i}", [P, 512]) for i in range(4)]
        ps = [r.psum(f"ps{i}", [P, 512]) for i in range(2)]
        loaded, last, msent, mready = r.sem("loaded"), r.sem("last"), r.sem("mean_sent"), r.sem("mean_ready")
        um, std, var = r.sem("umean_ready"), r.sem("std_ready"), r.sem("var_ready")
        stored, passed = r.sems("stored", 2), r.sem("passed")
        m = Marks(nc, r, ("copied", "projected", "hc_ready", "squared", "summed", "added", "hc_sent"))
        with nc.Block() as block:

            @block.sync
            def _(sp):
                sp.dma_start(w[:, :, :], weights(a["wqkv"])).then_inc(loaded, 16)

                def store(n, slot):
                    hold(sp, m["hc_ready"], n + 3, passed)
                    sp.dma_start(rows(g.hc, n), hc[:, slot, :, :]).then_inc(stored[slot], 16)

                store(0, 0)
                with sp.Fori(0, PAIRS // 2) as i:
                    store(i * 2 + 1, 1)
                    hold(sp, stored[0], i * 16 + 16, m["hc_sent"])
                    store(i * 2 + 2, 0)
                    hold(sp, stored[1], i * 16 + 16, m["hc_sent"])
                hold(sp, stored[0], (PAIRS // 2 + 1) * 16, m["hc_sent"])

            @block.scalar
            def _(act):
                def step(n, slot):
                    if exists(n, 2, PAIRS):
                        m.done(act, "projected", n)
                        at = g.ut[:, :, (n + 2) * PW:(n + 3) * PW] if isinstance(n, int) else g.ut[:, :, ds((n + 2) * PW, PW)]
                        act.activation(uts[:, slot, :, :], at, ACT.Copy).then_inc(m["copied"], 1)
                    if exists(n, 0, PAIRS):
                        m.done(act, "hc_ready", n)
                        m.done(act, "summed", n, 1)
                        for t in range(2):
                            valid = g.valid[:, 2 * n + t:2 * n + t + 1] if isinstance(n, int) else g.valid[:, ds(n * 2 + t, 1)]
                            ins = act.activation(sq[:, t, :], hc[:, slot, t, :], ACT.Square, scale=valid)
                        ins.then_inc(m["squared"], 1)

                pair_steps(act, step, 2, 0)
                act.wait_ge(var, 1)
                act.activation(ssum[:, :], ssum[:, :], ACT.Sqrt).then_inc(std, 1)

            @block.tensor
            def _(pe):
                pe.wait_ge(loaded, 16)
                pe.wait_ge(um, 1)
                for h in range(2):
                    for k in range(KD):
                        mm = pe.matmul(ps[h][:, 0:HALF], umean[:, k, :], w[:, k, h * HALF:(h + 1) * HALF],
                                       start=(k == 0), stop=(k == KD - 1))
                mm.then_inc(msent, 1)
                pe.wait_ge(mready, 1)

                def step(n, slot):
                    if exists(n, 0, PAIRS):
                        m.done(pe, "copied", n)
                        m.done(pe, "hc_ready", n, 1)
                        for t in range(2):
                            for h in range(2):
                                for k in range(KD):
                                    mm = pe.matmul(ph[2 * t + h][:, 0:HALF], uts[:, slot, k, t * P:(t + 1) * P],
                                                   w[:, k, h * HALF:(h + 1) * HALF], start=(k == 0), stop=(k == KD - 1))
                        mm.then_inc(m["projected"], 1)
                    if exists(n, -1, PAIRS):
                        m.done(pe, "squared", n, 1)
                        m.done(pe, "added", n, 2)
                        for h in range(2):
                            for t in range(2):
                                mm = pe.matmul(ps[h][:, 0:HALF], g.ones[:, :], sq[:, t, h * HALF:(h + 1) * HALF],
                                               start=(t == 0), stop=(t == 1))
                        mm.then_inc(m["summed"], 1)

                pair_steps(pe, step, 0, 1)

            @block.vector
            def _(dve):
                dve.tensor_scalar(umean[:, :, :], over(g.usum[:, :], 2, [P, KD, P]), 1.0 / NODES, None, ALU.mult).then_inc(um, 1)
                dve.memset(ssum[:, :], 0.0)
                dve.wait_ge(msent, 1)
                for h in range(2):
                    ins = dve.tensor_copy(mean[:, h * HALF:(h + 1) * HALF], ps[h][:, 0:HALF])
                ins.then_inc(mready, 1)
                dve.wait_ge(mready, 1)

                def step(n, slot):
                    if exists(n, 0, PAIRS):
                        m.done(dve, "projected", n)
                        m.done(dve, "hc_sent", n, 2)
                        m.done(dve, "squared", n, 2)
                        for t in range(2):
                            scale = g.g0[:, 2 * n + t:2 * n + t + 1] if isinstance(n, int) else g.g0[:, ds(n * 2 + t, 1)]
                            for h in range(2):
                                c = slice(h * HALF, (h + 1) * HALF)
                                ins = dve.scalar_tensor_tensor(out=hc[:, slot, t, c], in0=ph[2 * t + h][:, 0:HALF], scalar=scale, in1=mean[:, c],
                                                               op0=ALU.mult, op1=ALU.subtract)
                        ins.then_inc(m["hc_ready"], 1)
                    if exists(n, -1, PAIRS):
                        m.done(dve, "summed", n, 1)
                        m.done(dve, "added", n, 2)
                        for h in range(2):
                            c = slice(h * HALF, (h + 1) * HALF)
                            ins = dve.tensor_tensor(ssum[:, c], ssum[:, c], ps[h][:, 0:HALF], ALU.add)
                        ins.then_inc(m["added"], 1)

                pair_steps(dve, step, 0, 1)
                m.done(dve, "added", PAIRS - 1)
                dve.sem_inc(passed)
                dve.tensor_scalar(ssum[:, :], ssum[:, :], 1.0 / NODES, EPS, ALU.mult, ALU.add).then_inc(var, 1)
                dve.wait_ge(std, 1)
                dve.reciprocal(ssum[:, :], ssum[:, :]).then_inc(last, 1)
                dve.wait_ge(last, 1)
                dve.tensor_tensor(g.bn_scale[:, :], g.bn_scale[:, :], ssum[:, :], ALU.mult).then_inc(last, 1)


def mix(nc, g, a):
    with Room(nc, "mx") as r:
        bd = r.sbuf("bd", [P, KQ, P])
        wdw = r.sbuf("wdw", [P, KQ])
        wres = r.sbuf("wres", [P, 4, D])
        bres = r.sbuf("bres", [P, D])
        raw = r.sbuf("raw", [P, 2, QKV])
        rr = r.sbuf("r", [P, 2, 2, QKV])
        rt = r.sbuf("rt", [P, KQ, PW])
        s = r.sbuf("s", [P, 2, 2, QKV])
        junk = r.sbuf("junk", [P, 2, 2, QKV])
        junk_o = r.sbuf("junk_o", [P, 2, 512])
        junk_f = r.sbuf("junk_f", [P, 2, D])
        sm = r.sbuf("sm", [P, 11, 2])
        norms = r.sbuf("norms", [P, 2, 5, 2])
        ks = r.sbuf("ks", [P, 2, GRP])
        v = r.sbuf("v", [P, 2, GRP, GD])
        ve = r.sbuf("ve", [P, 2, GRP, GD])
        o = r.sbuf("o", [P, 2, GRP, GD])
        ot = r.sbuf("ot", [P, 4, PW])
        ft = r.sbuf("ft", [P, 2, D])
        prt = [r.psum(f"prt{i}", [P, 2, PW]) for i in range(3)]
        pss = [[r.psum(f"ps{t}{h}", [P, 512]) for h in range(2)] for t in range(2)]
        pf = r.psum("pf", [P, 2, D])
        c1, nc_, kap, tmp_b, c2, tmp_c, nf, th, tmp_d, scale_d = (sm[:, j, :] for j in range(10))
        nr, ns, ncat, no, root = ([norms[:, slot, j, :] for slot in range(2)] for j in range(5))
        loaded, scaled, ld, passed = (r.sem(n) for n in ("loaded", "scaled", "ld", "passed"))
        m = Marks(nc, r, ("bn_scaled", "bn_ready", "r_ready", "turned", "rt_ready", "mixed", "s_ready", "squared", "rooted", "s_relu", "o_ready", "o_squared",
                                   "o_rooted", "o_turned", "ot_ready", "final", "ft_ready", "f_squared", "f_rooted", "tanh_ready", "xdone"))
        done = m.done
        chain_b, chain_c, chain_d = (r.sems(f"step_{n}", k) for n, k in (("b", 16), ("c", 3), ("d", 3)))
        with nc.Block() as block:

            @block.sync
            def _(sp):
                sp.dma_start(bd[:, :, :], weights(a["pw"])).then_inc(loaded, 16)
                sp.dma_start(wdw[:, :], a["wdw"]).then_inc(loaded, 16)
                sp.dma_start(wres[:, :, :], weights(a["wres"])).then_inc(loaded, 16)
                sp.dma_start(bres[:, :], to_all(a["bres"], D)).then_inc(loaded, 16)
                with sp.Fori(0, PAIRS) as i:
                    hold(sp, m["bn_scaled"], i + 2, passed)
                    sp.dma_start(raw[:, :, :], rows(g.hc, i)).then_inc(ld, 16)

            @block.tensor
            def _(pe):
                def step(n, slot):
                    nxt, other = n + 1, 1 - slot
                    if exists(n, 1, PAIRS):
                        done(pe, "r_ready", nxt)
                        done(pe, "ot_ready", nxt, 2)
                        for k in range(KQ):
                            for t in range(2):
                                mm = pe.transpose(prt[k // 2][:, k % 2, t * P:(t + 1) * P], rr[:, other, t, k * P:(k + 1) * P], g.ident[:, :])
                        mm.then_inc(m["turned"], 1)
                        done(pe, "rt_ready", nxt)
                        done(pe, "s_ready", nxt, 1)
                        for t in range(2):
                            for k in range(KQ):
                                mm = pe.matmul(pss[t][k // 4][:, (k % 4) * P:(k % 4 + 1) * P], rt[:, k, t * P:(t + 1) * P], bd[:, k, :],
                                               start=True, stop=True)
                        mm.then_inc(m["mixed"], 1)
                    if exists(n, 0, PAIRS):
                        done(pe, "o_ready", n)
                        for k in range(4):
                            for t in range(2):
                                mm = pe.transpose(prt[k // 2][:, k % 2, t * P:(t + 1) * P],
                                                  o[:, t, 4 * k:4 * k + 4, :].rearrange("p a b -> p (a b)"), g.ident[:, :])
                        mm.then_inc(m["o_turned"], 1)
                        done(pe, "ot_ready", n)
                        done(pe, "ft_ready", n, 1)
                        for t in range(2):
                            for k in range(4):
                                mm = pe.matmul(pf[:, t, :], ot[:, k, t * P:(t + 1) * P], wres[:, k, :], start=(k == 0), stop=(k == 3))
                        mm.then_inc(m["final"], 1)

                pe.wait_ge(scaled, 1)
                pair_steps(pe, step, 1, 2)

            @block.scalar
            def _(act):
                def step(n, slot):
                    nxt, other = n + 1, 1 - slot
                    if exists(n, 1, PAIRS):
                        done(act, "bn_ready", nxt)
                        for t in range(2):
                            ins = act.activation(rr[:, other, t, :], rr[:, other, t, :], ACT.Relu)
                        ins.then_inc(m["r_ready"], 1)
                        done(act, "r_ready", nxt)
                        done(act, "rooted", nxt, 2)
                        for t in range(2):
                            act.activation(junk[:, other, t, :], rr[:, other, t, :], ACT.Square, accum_out=nr[other][:, t:t + 1])
                        done(act, "turned", nxt)
                        for j in range(3):
                            ins = act.activation(rt[:, 2 * j:2 * j + 2, :], prt[j][:, :, :], ACT.Copy)
                        ins.then_inc(m["rt_ready"], 1)
                        done(act, "mixed", nxt)
                        done(act, "o_ready", nxt, 2)
                        for t in range(2):
                            act.activation(s[:, other, t, 0:512], pss[t][0][:, :], ACT.Copy)
                            ins = act.activation(s[:, other, t, 512:QKV], pss[t][1][:, 0:QKV - 512], ACT.Copy)
                        ins.then_inc(m["s_ready"], 1)
                        done(act, "s_ready", nxt)
                        for t in range(2):
                            ins = act.activation(junk[:, other, t, :], s[:, other, t, :], ACT.Square, accum_out=ns[other][:, t:t + 1])
                        ins.then_inc(m["squared"], 1)
                        done(act, "squared", nxt)
                        for t in range(2):
                            part = s[:, other, t, :].rearrange("p (a b) -> p a b", b=3 * GD)[:, :, 0:2 * GD]
                            ins = act.activation(part, part, ACT.Relu)
                        ins.then_inc(m["s_relu"], 1)
                        for t in range(2):
                            act.activation(ncat[other][:, t:t + 1], ns[other][:, t:t + 1], ACT.Sqrt, bias=nr[other][:, t:t + 1])
                        act.activation(root[other], nr[other], ACT.Sqrt).then_inc(m["rooted"], 1)
                    if exists(n, 0, PAIRS):
                        done(act, "o_ready", n)
                        done(act, "o_rooted", n, 1)
                        for t in range(2):
                            ins = act.activation(junk_o[:, t, :], o[:, t, :, :].rearrange("p a b -> p (a b)"), ACT.Square,
                                                 accum_out=no[slot][:, t:t + 1])
                        ins.then_inc(m["o_squared"], 1)
                        done(act, "o_squared", n)
                        act.activation(no[slot], no[slot], ACT.Sqrt).then_inc(m["o_rooted"], 1)
                        done(act, "o_turned", n)
                        done(act, "final", n, 1)
                        for j in range(2):
                            ins = act.activation(ot[:, 2 * j:2 * j + 2, :], prt[j][:, :, :], ACT.Copy)
                        ins.then_inc(m["ot_ready"], 1)
                    if exists(n, -1, PAIRS):
                        done(act, "ft_ready", n, 1)
                        done(act, "xdone", n, 2)
                        for t in range(2):
                            ins = act.activation(junk_f[:, t, :], ft[:, t, :], ACT.Square, accum_out=nf[:, t:t + 1])
                        ins.then_inc(m["f_squared"], 1)
                        done(act, "f_squared", n, 1)
                        act.activation(nf, nf, ACT.Sqrt).then_inc(m["f_rooted"], 1)
                        done(act, "f_rooted", n, 1)
                        act.activation(th, nf, ACT.Tanh).then_inc(m["tanh_ready"], 1)

                pair_steps(act, step, 1, 2)

            @block.vector
            def _(dve):
                def normal(n, slot):
                    dve.wait_ge(ld, n * 16 + 16)
                    done(dve, "turned", n, 2)
                    done(dve, "rooted", n, 2)
                    done(dve, "o_ready", n, 2)
                    dve.tensor_tensor(rr[:, slot, :, :], raw[:, :, :], over(g.bn_scale[:, :], 1, [P, 2, QKV]), ALU.mult).then_inc(m["bn_scaled"], 1)
                    done(dve, "bn_scaled", n)
                    dve.tensor_tensor(rr[:, slot, :, :], rr[:, slot, :, :], over(g.bn_beta[:, :], 1, [P, 2, QKV]), ALU.add).then_inc(m["bn_ready"], 1)

                def finish(n):
                    link = Chain(dve, chain_d, n + 1)
                    done(dve, "tanh_ready", n)
                    done(dve, "xdone", n, 1)
                    link(dve.tensor_scalar(tmp_d, nf, MIN_NORM, None, ALU.max))
                    link(dve.reciprocal(tmp_d, tmp_d))
                    link(dve.scalar_tensor_tensor(out=scale_d, in0=th, scalar=BALL, in1=tmp_d, op0=ALU.min, op1=ALU.mult))
                    for t in range(2):
                        x = tile_of(g.x, n * 2 + t)
                        ins = dve.scalar_tensor_tensor(out=x, in0=ft[:, t, :], scalar=scale_d[:, t:t + 1], in1=x, op0=ALU.mult, op1=ALU.add)
                    ins.then_inc(m["xdone"], 1)

                def attend(n, slot):
                    link = Chain(dve, chain_b, n + 1)
                    nrt, cat = root[slot], ncat[slot]
                    done(dve, "rooted", n)
                    link(dve.tensor_scalar(tmp_b, nrt, MIN_NORM, None, ALU.max))
                    parts = []
                    for t in range(2):
                        parts.append((t, 0, rr[:, slot, t, :].rearrange("p (a b) -> p a b", b=3 * GD)))
                        parts.append((t, GRP // 2, s[:, slot, t, :].rearrange("p (a b) -> p a b", b=3 * GD)))
                    dve.reciprocal(tmp_b, tmp_b).then_inc(chain_b[15], 1)
                    for t, at, part in parts:
                        dve.tensor_reduce(ks[:, t, at:at + 8], part[:, :, GD:2 * GD], AX, ALU.add)
                    dve.wait_ge(chain_b[15], n + 1)
                    link(dve.scalar_tensor_tensor(out=c1, in0=nrt, scalar=ATANH_BALL, in1=tmp_b, op0=ALU.min, op1=ALU.mult))
                    link(dve.tensor_tensor(nc_, c1, cat, ALU.mult))
                    link(dve.tensor_scalar(tmp_b, nc_, MIN_NORM, None, ALU.max))
                    link(dve.reciprocal(tmp_b, tmp_b))
                    link(dve.scalar_tensor_tensor(out=tmp_b, in0=nc_, scalar=ATANH_BALL, in1=tmp_b, op0=ALU.min, op1=ALU.mult))
                    link(dve.tensor_tensor(kap, tmp_b, c1, ALU.mult))
                    for t, at, part in parts:
                        ins = dve.tensor_scalar(v[:, t, at:at + 8, :], part[:, :, 2 * GD:3 * GD], kap[:, t:t + 1], None, ALU.mult)
                    link(ins)
                    link(dve.tensor_scalar(ve[:, :, :, :], v[:, :, :, :], ATT_EPS, None, ALU.add))
                    link(dve.reciprocal(ve[:, :, :, :], ve[:, :, :, :]))
                    link(dve.tensor_tensor(v[:, :, :, :], v[:, :, :, :], ve[:, :, :, :], ALU.mult))
                    done(dve, "o_turned", n, 1)
                    done(dve, "o_squared", n, 1)
                    for t, at, part in parts:
                        ins = dve.tensor_tensor(o[:, t, at:at + 8, :], part[:, :, 0:GD], over(ks[:, t, at:at + 8], 2, [P, 8, GD]), ALU.mult)
                    link(ins)
                    for t in range(2):
                        ins = dve.scalar_tensor_tensor(out=o[:, t, :, :], in0=v[:, t, :, :], scalar=kap[:, t:t + 1], in1=o[:, t, :, :],
                                                       op0=ALU.mult, op1=ALU.mult)
                    link(ins)
                    for t in range(2):
                        ins = dve.tensor_scalar(o[:, t, :, :], o[:, t, :, :], kap[:, t:t + 1], None, ALU.mult)
                    ins.then_inc(m["o_ready"], 1)

                def close(n, slot):
                    link = Chain(dve, chain_c, n + 1)
                    done(dve, "o_rooted", n)
                    link(dve.tensor_scalar(tmp_c, no[slot], MIN_NORM, None, ALU.max))
                    link(dve.reciprocal(tmp_c, tmp_c))
                    link(dve.scalar_tensor_tensor(out=c2, in0=no[slot], scalar=ATANH_BALL, in1=tmp_c, op0=ALU.min, op1=ALU.mult))
                    done(dve, "final", n)
                    done(dve, "xdone", n, 1)
                    for t in range(2):
                        ins = dve.scalar_tensor_tensor(out=ft[:, t, :], in0=pf[:, t, :], scalar=c2[:, t:t + 1], in1=bres[:, :],
                                                       op0=ALU.mult, op1=ALU.add)
                    ins.then_inc(m["ft_ready"], 1)

                def step(n, slot):
                    if exists(n, 1, PAIRS):
                        normal(n + 1, 1 - slot)
                    if exists(n, -2, PAIRS):
                        finish(n - 2)
                    if exists(n, 0, PAIRS):
                        attend(n, slot)
                    if exists(n, -1, PAIRS):
                        close(n - 1, 1 - slot)

                dve.wait_ge(loaded, 64)
                dve.tensor_tensor(bd[:, :, :], bd[:, :, :], over(wdw[:, :], 2, [P, KQ, P]), ALU.mult).then_inc(scaled, 1)
                pair_steps(dve, step, 1, 2)


def spill_duplicates(nc, g):
    A = H0 * (D0 + 1)
    with Room(nc, "dup") as r:
        blank = r.sbuf("blank", [P, A + H0])
        blanked, inited = r.sem("blanked"), r.sem("inited")
        key = r.sbuf("key", [P, 2, U, 2])
        junk = r.sbuf("junk", [P, U, 2, P])
        rank = r.sbuf("rank", [P, 2, U, 2])
        ranks = r.sbuf("ranks", [P, ET, 2])
        keys = r.sbuf("keys", [P, ET, 2])
        pk = [r.psum(f"pk{j}", [P, U, P]) for j in range(4)]
        keyed, spread, counted, kept, step = (r.sem(n) for n in ("keyed", "spread", "counted", "kept", "step"))
        credit(nc, [keyed, spread, counted, kept], 2)
        with nc.Block() as block:

            @block.gpsimd
            def _(pool):
                pool.memset(blank[:, 0:A], 0.0)
                pool.memset(blank[:, A:A + H0], LOWEST).then_inc(blanked, 1)

            @block.sync
            def _(sp):
                sp.wait_ge(blanked, 1)
                for t in g.tabs0:
                    sp.dma_start(t.rearrange("(t p) c -> p t c", p=P), over(blank[:, 0:A + H0], 1, [P, TROWS // P, A + H0])).then_inc(inited, 16)
                sp.wait_ge(inited, 16 * NTAB)

            @block.tensor
            def _(pe):
                with pe.Fori(0, TURNS // 2) as i:
                    for s in range(2):
                        n = i * 2 + s
                        pe.wait_ge(keyed, n + 3)
                        pe.wait_ge(counted, n + 1)
                        for j in range(2):
                            for b in range(U):
                                mm = pe.transpose(pk[2 * s + j][:, b, :], key[:, s, b, j:j + 1].to_broadcast([P, P]), g.ident[:, :])
                        mm.then_inc(spread, 1)

            @block.vector
            def _(dve):
                def make_key(n, s):
                    dve.tensor_copy(key[:, s, :, :], g.idx[:, n * U:(n + 1) * U, 0:2] if isinstance(n, int) else g.idx[:, ds(n * U, U), 0:2]).then_inc(keyed, 1)

                def group(n, s, more=True):
                    dve.wait_ge(spread, n + 3)
                    dve.wait_ge(kept, n + 1)
                    if not isinstance(n, int) or n >= 1:
                        dve.wait_ge(counted, n + 2)
                    for j in range(2):
                        for b in range(U):
                            ins = dve.scalar_tensor_tensor(out=junk[:, b, j, :], in0=pk[2 * s + j][:, b, :], scalar=key[:, s, b, j:j + 1], in1=g.lower[:, :],
                                                           op0=ALU.is_equal, op1=ALU.mult, accum_out=rank[:, s, b, j:j + 1])
                    ins.then_inc(counted, 1)
                    dve.wait_ge(counted, n + 3)
                    if more:
                        make_key(n + 2, s)
                    dve.tensor_copy(ranks[:, n * U:(n + 1) * U, :] if isinstance(n, int) else ranks[:, ds(n * U, U), :], rank[:, s, :, :]).then_inc(kept, 1)

                for s in range(2):
                    make_key(s, s)
                with dve.Fori(0, TURNS // 2 - 1) as i:
                    for s in range(2):
                        group(i * 2 + s, s)
                for s in range(2):
                    group(TURNS - 2 + s, s, False)
                dve.tensor_copy(keys[:, :, :], g.idx[:, :, 0:2]).then_inc(step, 1)
                dve.wait_ge(kept, TURNS + 2)
                dve.tensor_scalar(ranks[:, :, :], ranks[:, :, :], 1.0, None, ALU.min).then_inc(step, 1)
                dve.wait_ge(step, 2)

                dve.tensor_scalar(g.rowf[:, :, :], keys[:, :, :], -1.0, g.spill[:, :], ALU.mult, ALU.add).then_inc(step, 1)
                dve.wait_ge(step, 3)
                dve.tensor_tensor(g.rowf[:, :, :], g.rowf[:, :, :], ranks[:, :, :], ALU.mult).then_inc(step, 1)
                dve.wait_ge(step, 4)
                dve.tensor_tensor(g.rowf[:, :, :], g.rowf[:, :, :], keys[:, :, :], ALU.add).then_inc(step, 1)
                dve.wait_ge(step, 5)
                dve.tensor_copy(g.idx[:, :, 2:4], g.rowf[:, :, :]).then_inc(step, 1)


class Edge:

    def __init__(self, r, marks, dmas, n=U):
        self.marks = {m: r.sem(m) for m in marks}
        self.dmas = {d: r.sems(d, n) for d in dmas}
        self.n = n

    def credit(self, nc):
        credit(nc, list(self.marks.values()), self.n)

    def done(self, eng, name, t, lag=0, passed=None):
        eng.wait_ge(self.marks[name], t + (1 + self.n - lag))
        if passed is not None:
            eng.sem_inc(passed)


def steps_of(eng, body, tiles, first, last, slots=U):
    lead = -(-first // slots) * slots
    for t in range(-first, lead):
        body(t, t // slots, t % slots)
    end = (tiles - lead) // slots * slots
    tail = -(-max(first, last) // slots) * slots
    with eng.Fori(lead // slots, (tiles - tail) // slots) as i:
        for b in range(slots):
            body(i * slots + b, i, b)
    for t in range(tiles - tail, tiles + last):
        body(t, t // slots, t % slots)


def exists(t, k, tiles=ET):
    return not isinstance(t, int) or 0 <= t + k < tiles


def attend0(nc, g, a):
    A = H0 * (D0 + 1)
    with Room(nc, "ga") as r:
        ixa = r.sbuf("ixa", [P, U, 4], I32)
        ixb = r.sbuf("ixb", [P, U, 4], I32)
        attr = r.sbuf("attr", [4, U, P])
        ew = r.sbuf("ew", [4, D])
        srow = r.sbuf("srow", [P, U, ROW0])
        drow = r.sbuf("drow", [P, U, ROW0])
        old = r.sbuf("old", [P, U, A + H0])
        new = r.sbuf("new", [P, U, A + H0])
        key = r.sbuf("key", [P, U, 1])
        same = r.sbuf("same", [P, U, P])
        pen = r.sbuf("pen", [P, U, P], BF16)
        we = r.sbuf("we", [P, U, D])
        z = r.sbuf("z", [P, U, H0])
        alpha = r.sbuf("alpha", [P, U, H0])
        at = r.sbuf("at", [P, U, P])
        mloc = r.sbuf("mloc", [P, U, H0])
        diff = r.sbuf("diff", [P, U, 2, H0])
        prod = r.sbuf("prod", [P, U, H0, D0 + 1])
        fade = r.sbuf("fade", [P, U, H0])
        pkey = [r.psum(f"pkey{j}", [P, P]) for j in range(2)]
        penc = [r.psum(f"penc{j}", [P, D]) for j in range(2)]
        pat = r.psum("pat", [H0, P])
        pm = [r.psum(f"pm{j}", [P, 4, P]) for j in range(2)]
        psum = r.psum("psum", [P, A])
        e = Edge(r, ["keyed", "spread", "matched", "encoded", "weighed", "z1", "z2", "z3", "scored", "penned", "turned", "at_ready",
                     "masked0", "masked1", "mloc0", "mloc1", "mnew", "differed", "exped", "faded", "multiplied", "summed", "old_faded", "new_ready"],
                 ["ixa", "ixb", "attr", "srow", "drow", "old", "new"])
        loaded, ones_set = r.sem("loaded"), r.sem("ones_set")
        passed, passed_sp = r.sem("passed"), r.sem("passed_sp")
        e.credit(nc)
        with nc.Block() as block:

            @block.vector
            def _(dve):
                dve.memset(attr[:, :, :], 1.0)
                dve.memset(at[:, :, :], 0.0).then_inc(ones_set, 1)

            @block.sync
            def _(sp):
                sp.dma_start(ew[0:3, :], a["eWT"]).then_inc(loaded, 16)
                sp.dma_start(ew[3:4, :], a["eb"].rearrange("(a n) -> a n", a=1)).then_inc(loaded, 16)
                sp.wait_ge(loaded, 32)
        with nc.Block() as block:

            @block.sync
            def _(sp):
                def step(t, i, b):
                    if exists(t, 3):
                        c = (b + 3) % U
                        if not (isinstance(t, int) and t < 1):
                            j = i if b == 0 else i + 1
                            hold(sp, e.dmas["old"][c], j * 16, passed_sp)
                            e.done(sp, "keyed", t, 1, passed_sp)
                            e.done(sp, "encoded", t, 1, passed_sp)
                        sp.dma_start(ixa[:, c, :], g.idx[:, t + 3, :] if isinstance(t, int) else g.idx[:, ds(t + 3, 1), :].rearrange("p a b -> p (a b)")).then_inc(e.dmas["ixa"][c], 16)
                        sp.dma_start(attr[0:3, c, :], a["ea"][:, t + 3, :] if isinstance(t, int) else a["ea"][:, ds(t + 3, 1), :].rearrange("p a b -> p (a b)")).then_inc(e.dmas["attr"][c], 16)
                    if exists(t, 0):
                        if not (isinstance(t, int) and t < U):
                            hold(sp, e.dmas["new"][b], i * 16, passed_sp)
                        sp.dma_start(ixb[:, b, :], g.idx[:, t, :] if isinstance(t, int) else g.idx[:, ds(t, 1), :].rearrange("p a b -> p (a b)")).then_inc(e.dmas["ixb"][b], 16)

                steps_of(sp, step, ET, 3, 0)

            @block.gpsimd
            def _(pool):
                def step(t, i, b):
                    if exists(t, 2):
                        c = (b + 2) % U
                        j = i + 2 if b >= 2 else i + 1
                        pool.wait_ge(e.dmas["ixa"][c], j * 16)
                        if not (isinstance(t, int) and t + 2 < U):
                            e.done(pool, "multiplied", t + 2, U)
                            e.done(pool, "z2", t + 2, U)
                        pool.sem_inc(passed)
                        pool.indirect_dma_start(out=drow[:, c, :], out_offset=None, in_=g.table0[:, :],
                                                in_offset=bass.IndirectOffsetOnAxis(ap=ixa[:, c, 1:2], axis=0)).then_inc(e.dmas["drow"][c], 16)
                        pool.indirect_dma_start(out=srow[:, c, :], out_offset=None, in_=g.table0[:, :],
                                                in_offset=bass.IndirectOffsetOnAxis(ap=ixa[:, c, 0:1], axis=0)).then_inc(e.dmas["srow"][c], 16)
                    if exists(t, 1):
                        c = (b + 1) % U
                        j = i + 1 if b == U - 1 else i
                        if not (isinstance(t, int) and t + 1 < U):
                            pool.wait_ge(e.dmas["new"][c], j * 16)
                            e.done(pool, "old_faded", t + 1, U)
                        pool.wait_ge(e.dmas["ixa"][c], (j + 1) * 16)
                        pool.sem_inc(passed)
                        pool.indirect_dma_start(out=old[:, c, :], out_offset=None, in_=g.tabs0[c][:, :],
                                                in_offset=bass.IndirectOffsetOnAxis(ap=ixa[:, c, 1:2], axis=0)).then_inc(e.dmas["old"][c], 16)
                    if exists(t, -2):
                        c = (b - 2) % U
                        j = i + 1 if b >= 2 else i
                        pool.wait_ge(e.dmas["ixb"][c], j * 16)
                        e.done(pool, "new_ready", t, 2)
                        pool.sem_inc(passed)
                        pool.indirect_dma_start(out=g.tabs0[c][:, :], out_offset=bass.IndirectOffsetOnAxis(ap=ixb[:, c, 3:4], axis=0),
                                                in_=new[:, c, :], in_offset=None).then_inc(e.dmas["new"][c], 16)

                steps_of(pool, step, ET, 2, 2)
                for c in range(U):
                    hold(pool, e.dmas["new"][c], 16 * TURNS, passed)

            @block.tensor
            def _(pe):
                def turn_alpha(t, b):
                    e.done(pe, "scored", t)
                    e.done(pe, "at_ready", t, 1)
                    pe.transpose(pat[:, :], alpha[:, b, :], g.ident[:, :]).then_inc(e.marks["turned"], 1)

                def encode(t, i, b):
                    e.done(pe, "keyed", t)
                    e.done(pe, "matched", t, 2)
                    pe.transpose(pkey[b % 2][:, :], key[:, b, :].to_broadcast([P, P]), g.ident[:, :]).then_inc(e.marks["spread"], 1)
                    pe.wait_ge(e.dmas["attr"][b], i * 16 + 16)
                    e.done(pe, "weighed", t, 2)
                    pe.matmul(penc[b % 2][:, :], attr[:, b, :], ew[:, :], start=True, stop=True).then_inc(e.marks["encoded"], 1)

                def mask(t, b):
                    e.done(pe, "at_ready", t)
                    e.done(pe, "penned", t)
                    for j in range(2):
                        e.done(pe, f"mloc{j}", t, 1)
                        for h in range(4):
                            pe.matmul(pm[j][:, h, :], g.picks[:, 4 * j + h, :], at[:, b, :], start=(h == 0), stop=False)
                        pe.matmul(pm[j][:, :, :], g.identb[:, :], over(pen[:, b, :], 1, [P, 4, P]), start=False, stop=True).then_inc(e.marks[f"masked{j}"], 1)

                def total(t, b):
                    e.done(pe, "multiplied", t)
                    e.done(pe, "new_ready", t, 1)
                    pe.matmul(psum[:, :], same[:, b, :], prod[:, b, :, :].rearrange("p a b -> p (a b)"), start=True, stop=True).then_inc(e.marks["summed"], 1)

                def step(t, i, b):
                    if exists(t, 1):
                        turn_alpha(t + 1, (b + 1) % U)
                    if exists(t, 2):
                        encode(t + 2, i + 1 if b >= 2 else i, (b + 2) % U)
                    if exists(t, 1):
                        mask(t + 1, (b + 1) % U)
                    if exists(t, 0):
                        total(t, b)

                encode(0, 0, 0)
                steps_of(pe, lambda t, i, b: step(t, i, b) if not (isinstance(t, int) and t < -1) else None, ET, 1, 0)

            @block.scalar
            def _(act):
                def step(t, i, b):
                    c = (b + 1) % U
                    if exists(t, 1):
                        e.done(act, "matched", t + 1)
                        act.activation(pen[:, c, :], same[:, c, :], ACT.Copy, scale=-LOWEST, bias=LOWEST).then_inc(e.marks["penned"], 1)
                    if exists(t, 1):
                        e.done(act, "turned", t + 1)
                        act.activation(at[0:H0, c, :], pat[:, :], ACT.Copy).then_inc(e.marks["at_ready"], 1)
                    if exists(t, 0):
                        e.done(act, "differed", t)
                        e.done(act, "summed", t, U)
                        act.activation(prod[:, b, :, D0], diff[:, b, 0, :], ACT.Exp).then_inc(e.marks["exped"], 1)
                        act.activation(fade[:, b, :], diff[:, b, 1, :], ACT.Exp).then_inc(e.marks["faded"], 1)
                        e.done(act, "faded", t)
                        for h in range(H0):
                            o = old[:, b, h * (D0 + 1):(h + 1) * (D0 + 1)]
                            ins = act.activation(o, o, ACT.Copy, scale=fade[:, b, h:h + 1])
                        ins.then_inc(e.marks["old_faded"], 1)

                steps_of(act, step, ET, 1, 0)

            @block.vector
            def _(dve):
                m = e.marks

                def make_key(t, i, b):
                    dve.wait_ge(e.dmas["ixa"][b], i * 16 + 16)
                    e.done(dve, "spread", t, U)
                    dve.tensor_copy(key[:, b, :], ixa[:, b, 1:2]).then_inc(m["keyed"], 1)

                def step(t, i, b):
                    now, new_, c, n = exists(t, 0), exists(t, 1), (b + 1) % U, t + 1
                    if exists(t, 2):
                        make_key(t + 2, i + 1 if b >= 2 else i, (b + 2) % U)
                    if new_:
                        j = i + 1 if b == U - 1 else i
                        e.done(dve, "encoded", n)
                        dve.wait_ge(e.dmas["drow"][c], j * 16 + 16)
                        dve.scalar_tensor_tensor(out=we[:, c, :], in0=penc[c % 2][:, :], scalar=0.0, in1=drow[:, c, 0:D], op0=ALU.max,
                                                 op1=ALU.mult).then_inc(m["weighed"], 1)
                        e.done(dve, "spread", n)
                        e.done(dve, "summed", n, U)
                        dve.tensor_scalar(same[:, c, :], pkey[c % 2][:, :], key[:, c, :], None, ALU.is_equal).then_inc(m["matched"], 1)
                        e.done(dve, "weighed", n)
                        dve.tensor_reduce(z[:, c, :], we[:, c, :].rearrange("p (h d) -> p h d", h=H0), AX, ALU.add).then_inc(m["z1"], 1)
                        e.done(dve, "z1", n)
                        dve.tensor_tensor(z[:, c, :], z[:, c, :], drow[:, c, D + H0:ROW0], ALU.add).then_inc(m["z2"], 1)
                        e.done(dve, "z2", n)
                        dve.wait_ge(e.dmas["srow"][c], j * 16 + 16)
                        dve.tensor_tensor(z[:, c, :], z[:, c, :], srow[:, c, D:D + H0], ALU.add).then_inc(m["z3"], 1)
                        e.done(dve, "z3", n)
                        dve.scalar_tensor_tensor(out=alpha[:, c, :], in0=z[:, c, :], scalar=0.2, in1=z[:, c, :], op0=ALU.mult,
                                                 op1=ALU.max).then_inc(m["scored"], 1)
                    if now:
                        for j in range(2):
                            e.done(dve, f"masked{j}", t)
                            dve.tensor_reduce(mloc[:, b, 4 * j:4 * j + 4], pm[j][:, :, :], AX, ALU.max).then_inc(m[f"mloc{j}"], 1)
                        e.done(dve, "mloc1", t)
                        dve.wait_ge(e.dmas["old"][b], i * 16 + 16)
                        if not (isinstance(t, int) and t < U):
                            dve.wait_ge(e.dmas["new"][b], i * 16)
                        dve.tensor_tensor(new[:, b, A:A + H0], mloc[:, b, :], old[:, b, A:A + H0], ALU.max).then_inc(m["mnew"], 1)
                        e.done(dve, "mnew", t)
                        dve.tensor_tensor(diff[:, b, 0, :], alpha[:, b, :], new[:, b, A:A + H0], ALU.subtract)
                        dve.tensor_tensor(diff[:, b, 1, :], old[:, b, A:A + H0], new[:, b, A:A + H0], ALU.subtract).then_inc(m["differed"], 1)
                    if exists(t, -1):
                        k = (b - 1) % U
                        e.done(dve, "old_faded", t, 1)
                        e.done(dve, "summed", t, 1)
                        dve.tensor_tensor(new[:, k, 0:A], old[:, k, 0:A], psum[:, :], ALU.add).then_inc(m["new_ready"], 1)
                    if now:
                        e.done(dve, "exped", t)
                        dve.tensor_tensor(prod[:, b, :, 0:D0], srow[:, b, 0:D].rearrange("p (h d) -> p h d", h=H0),
                                          prod[:, b, :, D0:D0 + 1].to_broadcast([P, H0, D0]), ALU.mult).then_inc(m["multiplied"], 1)

                steps_of(dve, step, ET, 2, 1)


def merge0(nc, g, a):
    A = H0 * (D0 + 1)
    with Room(nc, "m0") as r:
        tb = r.sbuf("tb", [P, 2, NTAB, 2, A + H0])
        mx = r.sbuf("mx", [P, 2, 2, H0])
        top = r.sbuf("top", [P, 2, H0])
        diff = r.sbuf("diff", [P, 2, NTAB, 2, H0])
        fade = r.sbuf("fade", [P, 2, NTAB, 2, H0])
        rden = r.sbuf("rden", [P, 2, H0])
        res = r.sbuf("res", [P, 2, D])
        bias = r.sbuf("bias", [P, D])
        loaded, ld, passed = (r.sem(n) for n in ("loaded", "ld", "passed"))
        chain = r.sems("step", 16)
        m = Marks(nc, r, ("differed", "exped", "merged", "xdone"))
        with nc.Block() as block:

            @block.sync
            def _(sp):
                def load(n, slot):
                    hold(sp, m["merged"], n + 1, passed)
                    for k in range(NTAB):
                        sp.dma_start(tb[:, slot, k, :, :], rows(g.tabs0[k], n)).then_inc(ld, 16)

                sp.dma_start(bias[:, :], to_all(a["gbias"], D)).then_inc(loaded, 16)
                load(0, 0)
                with sp.Fori(0, PAIRS // 2) as i:
                    for slot in range(2):
                        n = i * 2 + (slot + 1)
                        hold(sp, ld, n * (16 * NTAB), passed)
                        load(n, 1 - slot)

            @block.scalar
            def _(act):
                def step(n, slot):
                    m.done(act, "differed", n)
                    m.done(act, "merged", n, 2)
                    act.activation(fade[:, slot, :, :, :], diff[:, slot, :, :, :], ACT.Exp).then_inc(m["exped"], 1)

                pair_steps(act, step, 0, 0)

            @block.vector
            def _(dve):
                def head(n, slot):
                    link = Chain(dve, chain[0:2], n + 1)
                    dve.wait_ge(ld, n * (16 * NTAB) + 16 * NTAB)
                    link(dve.tensor_tensor(mx[:, :, :, :], tb[:, slot, 0:2, :, A:A + H0], tb[:, slot, 2:4, :, A:A + H0], ALU.max))
                    link(dve.tensor_tensor(top[:, :, :], mx[:, 0, :, :], mx[:, 1, :, :], ALU.max))
                    m.done(dve, "exped", n, 2)
                    m.done(dve, "differed", n, 1)
                    dve.tensor_tensor(diff[:, slot, :, :, :], tb[:, slot, :, :, A:A + H0], over(top[:, :, :], 1, [P, NTAB, 2, H0]),
                                      ALU.subtract).then_inc(m["differed"], 1)

                def merge(n, slot):
                    link = Chain(dve, chain[2:], n + 1)
                    m.done(dve, "exped", n)
                    for k in range(NTAB):
                        v = tb[:, slot, k, :, 0:A].rearrange("p t (h d) -> p t h d", h=H0)
                        ins = dve.tensor_tensor(v, v, over(fade[:, slot, k, :, :], 3, [P, 2, H0, D0 + 1]), ALU.mult)
                    link(ins)
                    link(dve.tensor_tensor(tb[:, slot, 0:2, :, 0:A], tb[:, slot, 0:2, :, 0:A], tb[:, slot, 2:4, :, 0:A], ALU.add))
                    link(dve.tensor_tensor(tb[:, slot, 0, :, 0:A], tb[:, slot, 0, :, 0:A], tb[:, slot, 1, :, 0:A], ALU.add))
                    v = tb[:, slot, 0, :, 0:A].rearrange("p t (h d) -> p t h d", h=H0)
                    link(dve.tensor_scalar(rden[:, :, :], v[:, :, :, D0], 1e-10, None, ALU.max))
                    link(dve.reciprocal(rden[:, :, :], rden[:, :, :]))
                    m.done(dve, "xdone", n, 1)
                    dve.tensor_tensor(res[:, :, :].rearrange("p t (h d) -> p t h d", h=H0), v[:, :, :, 0:D0],
                                      over(rden[:, :, :], 3, [P, 2, H0, D0]), ALU.mult).then_inc(m["merged"], 1)
                    m.done(dve, "merged", n)
                    link(dve.tensor_tensor(res[:, :, :], res[:, :, :], over(bias[:, :], 1, [P, 2, D]), ALU.add))
                    dve.tensor_tensor(rows_of(g.x, n), rows_of(g.x, n), res[:, :, :], ALU.add).then_inc(m["xdone"], 1)

                def step(n, slot):
                    if exists(n, 1, PAIRS):
                        head(n + 1, 1 - slot)
                    if exists(n, 0, PAIRS):
                        merge(n, slot)

                dve.wait_ge(loaded, 16)
                pair_steps(dve, step, 1, 0)


def turn_pair(pe, g, pt, un):
    for t in range(2):
        for k in range(KD):
            mm = pe.transpose(pt[:, k, t * P:(t + 1) * P], un[:, t, k * P:(k + 1) * P], g.ident[:, :])
    return mm


def pick_two(dve, link, p, w, n, m, wait_exp):
    s = w.scratch
    shape = [P, m, n]
    m1, m2, i1, i2, gap = (s.small[:, j, :] for j in range(5))
    link(dve.tensor_reduce(m1, p, AX, ALU.max))
    link(dve.tensor_tensor(s.eq, p, over(m1, 2, shape), ALU.is_equal))
    link(dve.scalar_tensor_tensor(out=s.cand, in0=s.eq, scalar=-float(n), in1=s.order_n, op0=ALU.mult, op1=ALU.add))
    link(dve.tensor_reduce(i1, s.cand, AX, ALU.min))
    link(dve.tensor_tensor(s.sel1, s.order, over(i1, 2, shape), ALU.is_equal))
    link(dve.scalar_tensor_tensor(out=s.rest, in0=s.sel1, scalar=-4.0, in1=p, op0=ALU.mult, op1=ALU.add))
    link(dve.tensor_reduce(m2, s.rest, AX, ALU.max))
    link(dve.tensor_tensor(s.eq, s.rest, over(m2, 2, shape), ALU.is_equal))
    link(dve.scalar_tensor_tensor(out=s.cand, in0=s.eq, scalar=-float(n), in1=s.order_n, op0=ALU.mult, op1=ALU.add))
    link(dve.tensor_reduce(i2, s.cand, AX, ALU.min))
    link(dve.tensor_tensor(s.sel2, s.order, over(i2, 2, shape), ALU.is_equal))
    wait_exp(dve.tensor_tensor(gap, m2, m1, ALU.subtract))
    w1, w2 = s.small[:, 5, :], s.small[:, 6, :]
    link(dve.tensor_scalar(w1, s.small[:, 7, :], 1.0, None, ALU.add))
    link(dve.reciprocal(w1, w1))
    link(dve.tensor_tensor(w2, s.small[:, 7, :], w1, ALU.mult))
    link(dve.tensor_tensor(s.eq, s.sel1, over(w1, 2, shape), ALU.mult))
    link(dve.tensor_tensor(s.cand, s.sel2, over(w2, 2, shape), ALU.mult))
    return dve.tensor_tensor(w.w, s.eq, s.cand, ALU.add)


class Picks:

    def __init__(self, r, n, m):
        self.w = r.sbuf("pick_w", [P, m, n])[:, :, :]
        self.scratch = self
        self.eq, self.cand, self.sel1, self.sel2, self.rest, self.order, self.order_n = (
            r.sbuf(f"pick_{name}", [P, m, n])[:, :, :] for name in ("eq", "cand", "sel1", "sel2", "rest", "order", "order_n"))
        self.small = r.sbuf("pick_small", [P, 8, m])
        self.n, self.m = n, m

    def order_of(self, dve):
        for j in range(self.n):
            dve.memset(self.order[:, :, j], float(j))
            ins = dve.memset(self.order_n[:, :, j], float(j + self.n))
        return ins


def experts0(nc, g, a):
    E = EXPERTS0
    with Room(nc, "ex") as r:
        rw1 = r.sbuf("rw1", [P, KD, P])
        rw2 = r.sbuf("rw2", [P, E])
        rb1 = r.sbuf("rb1", [P, 1])
        rb2 = r.sbuf("rb2", [P, E])
        w1, w2, w3 = (r.sbuf(f"w{j}", [P, E * KD, D]) for j in (1, 2, 3))
        b1, b2 = (r.sbuf(f"b{j}", [P, E * KD]) for j in (1, 2))
        b3 = r.sbuf("b3", [E, D])
        un = r.sbuf("un", [P, 2, D])
        xt = r.sbuf("xt", [P, 2, KD, PW])
        rh = r.sbuf("rh", [P, PW])
        lg = r.sbuf("lg", [P, 2, E])
        ex = r.sbuf("exl", [P, 2, E])
        tot = r.sbuf("tot", [P, 2, 2])
        wt = r.sbuf("wt", [E, PW])
        h1 = r.sbuf("h1", [P, 2, KD, PW])
        h2 = r.sbuf("h2", [P, 2, KD, PW])
        acc = r.sbuf("acc", [P, 2, D])
        picks = Picks(r, E, 2)
        pt = r.psum("pt", [P, KD, PW])
        pr = r.psum("pr", [P, 512])
        p1, p2, p3 = ([r.psum(f"p{j}{s}", [P, KD, PW]) for s in range(2)] for j in (1, 2, 3))
        loaded, passed = r.sem("loaded"), r.sem("passed")
        m = {n: r.sem(n) for n in ("copied", "turned", "xt_ready", "routed1", "rh_ready", "logits", "centred", "exped", "gapped",
                                   "gap_exped", "picked", "w_turned", "wt_ready", "biased", "acc_ready", "xdone")}
        x = {n: r.sem(n) for n in ("l1", "h1_ready", "l2", "h2_ready", "l3", "combined")}
        chain = r.sems("step", 32)
        credit(nc, list(m.values()))
        credit(nc, list(x.values()), 2)
        with nc.Block() as block:

            @block.sync
            def _(sp):
                for dst, src in ((rw1[:, :, :], weights(a["rw1"])), (rw2[:, :], a["rw2"]), (rb1[:, :], a["rb1"]), (rb2[:, :], to_all(a["rb2"], E)),
                                 (w1[:, :, :], weights(a["ew1"])), (w2[:, :, :], weights(a["ew2"])), (w3[:, :, :], weights(a["ew3"])),
                                 (b1[:, :], a["eb1"]), (b2[:, :], a["eb2"]), (b3[:, :], a["eb3"])):
                    sp.dma_start(dst, src).then_inc(loaded, 16)
                sp.wait_ge(loaded, 160)

            @block.tensor
            def _(pe):
                pe.wait_ge(loaded, 160)
                def step(i, slot):
                    before, now = i + 1, i + 2

                    def turn_next():
                        if exists(i, 1, PAIRS):
                            pe.wait_ge(m["copied"], i + 3)
                            pe.wait_ge(m["wt_ready"], now)
                            turn_pair(pe, g, pt, un).then_inc(m["turned"], 1)

                    def layer(s, e, p, w, src, need, out, free):
                        n = i * E + e
                        if need is not None:
                            pe.wait_ge(x[need], n + 3)
                        pe.wait_ge(x[free], n + 1)
                        for c in range(KD):
                            for k in range(KD):
                                mm = pe.matmul(p[:, c, :], w[:, e * KD + k, c * P:(c + 1) * P], src[:, k, :], start=(k == 0), stop=(k == KD - 1))
                        mm.then_inc(x[out], 1)

                    def last(e):
                        n = i * E + e
                        pe.wait_ge(x["h2_ready"], n + 3)
                        pe.wait_ge(x["combined"], n + 1)
                        for t in range(2):
                            for k in range(KD):
                                mm = pe.matmul(p3[e % 2][:, t, :], h2[:, e % 2, k, t * P:(t + 1) * P], w3[:, e * KD + k, :],
                                               start=(k == 0), stop=(k == KD - 1))
                        mm.then_inc(x["l3"], 1)

                    if not exists(i, 0, PAIRS):
                        turn_next()
                        return
                    pe.wait_ge(m["xt_ready"], now)
                    pe.wait_ge(m["acc_ready"], before)
                    for k in range(KD):
                        mm = pe.matmul(pr[:, 0:PW], rw1[:, k, :], xt[:, slot, k, :], start=(k == 0), stop=(k == KD - 1))
                    mm.then_inc(m["routed1"], 1)
                    for s in range(E + 2):
                        if s < E:
                            layer(s, s, p1[s % 2], w1, xt[:, slot, :, :], None, "l1", "h1_ready")
                        if s == 0:
                            pe.wait_ge(m["rh_ready"], now)
                            for t in range(2):
                                mm = pe.matmul(pr[:, t * E:(t + 1) * E], rh[:, t * P:(t + 1) * P], rw2[:, :], start=True, stop=True)
                            mm.then_inc(m["logits"], 1)
                        if 0 <= s - 1 < E:
                            layer(s, s - 1, p2[(s - 1) % 2], w2, h1[:, (s - 1) % 2, :, :], "h1_ready", "l2", "h2_ready")
                        if s == 2:
                            pe.wait_ge(m["picked"], now)
                            for t in range(2):
                                mm = pe.transpose(pt[0:E, 0, t * P:(t + 1) * P], picks.w[:, t, :], g.ident[:, :])
                            mm.then_inc(m["w_turned"], 1)
                            pe.wait_ge(m["wt_ready"], now)
                            for t in range(2):
                                mm = pe.matmul(pr[:, t * D:(t + 1) * D], wt[:, t * P:(t + 1) * P], b3[:, :], start=True, stop=True)
                            mm.then_inc(m["biased"], 1)
                        if s == 4:
                            turn_next()
                        if 0 <= s - 2 < E:
                            last(s - 2)

                pair_steps(pe, step, 1, 0)

            @block.scalar
            def _(act):
                act.wait_ge(loaded, 160)
                def step(i, slot):
                    before, now = i + 1, i + 2

                    def copy_next():
                        if exists(i, 1, PAIRS):
                            act.wait_ge(m["turned"], now)
                            act.activation(un[:, :, :], rows_of(g.u, i + 1), ACT.Copy).then_inc(m["copied"], 1)

                    def relu(e, h, p, b, need, out, free, lag):
                        n = i * E + e
                        act.wait_ge(x[need], n + 3)
                        act.wait_ge(x[free], n + lag)
                        for c in range(KD):
                            ins = act.activation(h[:, e % 2, c, :], p[e % 2][:, c, :], ACT.Relu, bias=b[:, e * KD + c:e * KD + c + 1])
                        ins.then_inc(x[out], 1)

                    if not exists(i, 0, PAIRS):
                        copy_next()
                        return
                    act.wait_ge(m["routed1"], now)
                    act.activation(rh[:, :], pr[:, 0:PW], ACT.Relu, bias=rb1[:, :]).then_inc(m["rh_ready"], 1)
                    for s in range(E + 1):
                        if s < E:
                            relu(s, h1, p1, b1, "l1", "h1_ready", "l2", 1)
                        if s == 0:
                            act.wait_ge(m["centred"], now)
                            act.activation(ex[:, :, :], lg[:, :, :], ACT.Exp).then_inc(m["exped"], 1)
                        if 0 <= s - 1 < E:
                            relu(s - 1, h2, p2, b2, "l2", "h2_ready", "l3", 1)
                        if s == 2:
                            copy_next()
                        if s == 1:
                            act.wait_ge(m["gapped"], now)
                            act.activation(picks.small[:, 7, :], picks.small[:, 4, :], ACT.Exp).then_inc(m["gap_exped"], 1)
                            act.wait_ge(m["w_turned"], now)
                            act.activation(wt[:, :], pt[0:E, 0, :], ACT.Copy).then_inc(m["wt_ready"], 1)

                pair_steps(act, step, 1, 0)

            @block.vector
            def _(dve):
                dve.wait_ge(loaded, 160)
                picks.order_of(dve)
                def step(i, slot):
                    before, now = i + 1, i + 2
                    link = Chain(dve, chain, i + 1)

                    def take_next():
                        if exists(i, 1, PAIRS):
                            dve.wait_ge(m["turned"], i + 3)
                            if not isinstance(i, int) or i >= 0:
                                dve.wait_ge(x["l1"], i * E + 2)
                            dve.tensor_copy(xt[:, 1 - slot, :, :], pt[:, :, :]).then_inc(m["xt_ready"], 1)

                    if not exists(i, 0, PAIRS):
                        take_next()
                        return
                    dve.wait_ge(m["logits"], now)
                    link(dve.tensor_tensor(lg[:, :, :], pr[:, 0:2 * E].rearrange("p (t e) -> p t e", t=2), over(rb2[:, :], 1, [P, 2, E]), ALU.add))
                    link(dve.tensor_reduce(tot[:, 0, :], lg[:, :, :], AX, ALU.max))
                    dve.tensor_tensor(lg[:, :, :], lg[:, :, :], over(tot[:, 0, :], 2, [P, 2, E]), ALU.subtract).then_inc(m["centred"], 1)
                    dve.wait_ge(m["exped"], now)
                    link(dve.tensor_reduce(tot[:, 1, :], ex[:, :, :], AX, ALU.add))
                    link(dve.reciprocal(tot[:, 1, :], tot[:, 1, :]))
                    link(dve.tensor_tensor(ex[:, :, :], ex[:, :, :], over(tot[:, 1, :], 2, [P, 2, E]), ALU.mult))

                    def wait_exp(ins):
                        ins.then_inc(m["gapped"], 1)
                        dve.wait_ge(m["gap_exped"], now)

                    pick_two(dve, link, ex[:, :, :], picks, E, 2, wait_exp).then_inc(m["picked"], 1)
                    dve.wait_ge(m["biased"], now)
                    dve.tensor_tensor(acc[:, :, :], rows_of(g.x, i), pr[:, :].rearrange("p (t d) -> p t d", t=2), ALU.add).then_inc(m["acc_ready"], 1)
                    dve.wait_ge(m["acc_ready"], now)
                    for e in range(E):
                        n = i * E + e
                        if e == 2:
                            take_next()
                        dve.wait_ge(x["l3"], n + 3)
                        for t in range(2):
                            dst = acc[:, t, :] if e < E - 1 else tile_of(g.x, i * 2 + t)
                            ins = dve.scalar_tensor_tensor(out=dst, in0=p3[e % 2][:, t, :], scalar=picks.w[:, t, e:e + 1], in1=acc[:, t, :],
                                                           op0=ALU.mult, op1=ALU.add)
                        ins.then_inc(x["combined"], 1)
                        dve.wait_ge(x["combined"], n + 3)

                pair_steps(dve, step, 1, 0)


def enter1(nc, g, a):
    with Room(nc, "en") as r:
        w = r.sbuf("w", [P, KD, D])
        bias = r.sbuf("bias", [P, D])
        un = r.sbuf("un", [P, 2, D])
        xt = r.sbuf("xt", [P, KD, PW])
        pt = r.psum("pt", [P, KD, PW])
        po = r.psum("po", [P, 2, D])
        loaded = r.sem("loaded")
        m = {n: r.sem(n) for n in ("copied", "turned", "xt_ready", "projected", "kept")}
        credit(nc, list(m.values()))
        with nc.Block() as block:

            @block.sync
            def _(sp):
                sp.dma_start(w[:, :, :], weights(a["winT"])).then_inc(loaded, 16)
                sp.dma_start(bias[:, :], to_all(a["b_in"], D)).then_inc(loaded, 16)
                sp.wait_ge(loaded, 32)

            @block.scalar
            def _(act):
                with act.Fori(0, PAIRS) as i:
                    act.wait_ge(m["turned"], i + 1)
                    act.activation(un[:, :, :], g.u[:, ds(i * 2, 2), :], ACT.Copy).then_inc(m["copied"], 1)

            @block.tensor
            def _(pe):
                pe.wait_ge(loaded, 32)
                with pe.Fori(0, PAIRS) as i:
                    pe.wait_ge(m["copied"], i + 2)
                    pe.wait_ge(m["xt_ready"], i + 1)
                    turn_pair(pe, g, pt, un).then_inc(m["turned"], 1)
                    pe.wait_ge(m["xt_ready"], i + 2)
                    pe.wait_ge(m["kept"], i + 1)
                    for t in range(2):
                        for k in range(KD):
                            mm = pe.matmul(po[:, t, :], xt[:, k, t * P:(t + 1) * P], w[:, k, :], start=(k == 0), stop=(k == KD - 1))
                    mm.then_inc(m["projected"], 1)

            @block.vector
            def _(dve):
                dve.wait_ge(loaded, 32)
                with dve.Fori(0, PAIRS) as i:
                    dve.wait_ge(m["turned"], i + 2)
                    dve.wait_ge(m["projected"], i + 1)
                    dve.tensor_copy(xt[:, :, :], pt[:, :, :]).then_inc(m["xt_ready"], 1)
                    dve.wait_ge(m["projected"], i + 2)
                    dve.tensor_tensor(g.hid[:, ds(i * 2, 2), :], po[:, :, :], over(bias[:, :], 1, [P, 2, D]), ALU.add).then_inc(m["kept"], 1)


def project1(nc, g, a, l):
    with Room(nc, "pj") as r:
        wq, wk, wv = (r.sbuf(f"w{n}", [P, KD, D]) for n in "qkv")
        bias = r.sbuf("bias", [P, 3, D])
        un = r.sbuf("un", [P, 2, D])
        xt = r.sbuf("xt", [P, 2, KD, PW])
        qo = r.sbuf("qo", [P, 2, 2, D])
        kvo = r.sbuf("kvo", [P, 2, 2, 2 * D])
        blank = r.sbuf("blank", [P, ROW1])
        pt = r.psum("pt", [P, KD, PW])
        pq = [r.psum(f"pq{s}", [P, 2, D]) for s in range(2)]
        pkv = [[r.psum(f"pkv{s}{t}", [P, 2 * D]) for t in range(2)] for s in range(2)]
        loaded, blanked, inited, passed = (r.sem(n) for n in ("loaded", "blanked", "inited", "passed"))
        stored = r.sems("stored", 2)
        m = Marks(nc, r, ("copied", "turned", "xt_ready", "projected", "rows_ready", "sent"))
        with nc.Block() as block:

            @block.sync
            def _(sp):
                for dst, w in ((wq, a["wqT"]), (wk, a["wkT"]), (wv, a["wvT"])):
                    sp.dma_start(dst[:, :, :], weights(w[ds(l * D, D), :])).then_inc(loaded, 16)
                for j, b in enumerate((a["bq"], a["bk"], a["bv"])):
                    sp.dma_start(bias[:, j, :], b[ds(l, 1), :].to_broadcast([P, D])).then_inc(loaded, 16)
                sp.wait_ge(blanked, 1)
                for t in g.tabs1:
                    sp.dma_start(t.rearrange("(t p) c -> p t c", p=P), over(blank[:, :], 1, [P, TROWS // P, ROW1])).then_inc(inited, 16)

                def store(n, slot):
                    hold(sp, m["rows_ready"], n + 3, passed)
                    sp.dma_start(rows(g.qrows, n), qo[:, slot, :, :]).then_inc(stored[slot], 16)
                    sp.dma_start(rows(g.kvrows, n), kvo[:, slot, :, :]).then_inc(stored[slot], 16)

                store(0, 0)
                with sp.Fori(0, PAIRS // 2) as i:
                    store(i * 2 + 1, 1)
                    hold(sp, stored[0], i * 32 + 32, m["sent"])
                    store(i * 2 + 2, 0)
                    hold(sp, stored[1], i * 32 + 32, m["sent"])
                hold(sp, stored[0], (PAIRS // 2 + 1) * 32, m["sent"])
                sp.wait_ge(inited, 16 * NTAB)

            @block.scalar
            def _(act):
                def step(n, slot):
                    if exists(n, 1, PAIRS):
                        m.done(act, "turned", n + 1, 1)
                        act.activation(un[:, :, :], rows_of(g.hid, n + 1), ACT.Copy).then_inc(m["copied"], 1)
                        m.done(act, "turned", n + 1)
                        m.done(act, "projected", n + 1, 2)
                        act.activation(xt[:, 1 - slot, :, :], pt[:, :, :], ACT.Copy).then_inc(m["xt_ready"], 1)

                pair_steps(act, step, 1, 0)

            @block.tensor
            def _(pe):
                def step(n, slot):
                    if exists(n, 1, PAIRS):
                        m.done(pe, "copied", n + 1)
                        m.done(pe, "xt_ready", n + 1, 1)
                        turn_pair(pe, g, pt, un).then_inc(m["turned"], 1)
                    if exists(n, 0, PAIRS):
                        m.done(pe, "xt_ready", n)
                        m.done(pe, "rows_ready", n, 2)
                        for dst, w in (([pq[slot][:, t, :] for t in range(2)], wq), ([pkv[slot][t][:, 0:D] for t in range(2)], wk),
                                       ([pkv[slot][t][:, D:2 * D] for t in range(2)], wv)):
                            for t in range(2):
                                for k in range(KD):
                                    mm = pe.matmul(dst[t], xt[:, slot, k, t * P:(t + 1) * P], w[:, k, :], start=(k == 0), stop=(k == KD - 1))
                        mm.then_inc(m["projected"], 1)

                pe.wait_ge(loaded, 96)
                pair_steps(pe, step, 1, 0)

            @block.vector
            def _(dve):
                def step(n, slot):
                    m.done(dve, "projected", n)
                    m.done(dve, "sent", n, 2)
                    dve.tensor_tensor(qo[:, slot, :, :], pq[slot][:, :, :], over(bias[:, 0, :], 1, [P, 2, D]), ALU.add)
                    for t in range(2):
                        ins = dve.tensor_tensor(kvo[:, slot, t, :], pkv[slot][t][:, :], bias[:, 1:3, :].rearrange("p a b -> p (a b)"), ALU.add)
                    ins.then_inc(m["rows_ready"], 1)

                dve.memset(blank[:, :], 0.0).then_inc(blanked, 1)
                dve.wait_ge(loaded, 96)
                pair_steps(dve, step, 0, 0)


DVE_HEADS = 1


def attend1(nc, g):
    AH = HG - DVE_HEADS
    S = 2 * U
    ASK = 4
    with Room(nc, "at") as r:
        ixa = r.sbuf("ixa", [P, S, 4], I32)
        ixb = r.sbuf("ixb", [P, S, 4], I32)
        q = r.sbuf("q", [P, S, D])
        kv = r.sbuf("kv", [P, S, 2 * D])
        key = r.sbuf("key", [P, S, 1])
        same = r.sbuf("same", [P, S, P])
        qk = r.sbuf("qk", [P, 2, HG, HG, DG])
        sc = r.sbuf("sc", [P, S, HG, HG])
        mx = r.sbuf("mx", [P, S, HG])
        ex = r.sbuf("exl", [P, S, HG, HG])
        den = r.sbuf("den", [P, S, HG])
        att = r.sbuf("att", [P, S, HG, HG])
        wv = r.sbuf("wv", [P, S, HG, D])
        new = r.sbuf("new", [P, S, ROW1])
        pkey = [r.psum(f"pkey{j}", [P, P]) for j in range(2)]
        pm = [r.psum(f"pm{j}", [P, ROW1]) for j in range(2)]
        e = Edge(r, ["keyed", "spread", "matched", "paired", "scored", "topped", "centred", "exped", "summed", "inverted", "attended",
                     "weighted_a", "weighted_v", "totalled", "new_ready"], ["ixa", "ixb", "q", "kv", "new"], S)
        passed, passed_sp = r.sem("passed"), r.sem("passed_sp")
        e.credit(nc)
        with nc.Block() as block:

            @block.sync
            def _(sp):
                def step(t, i, b):
                    if exists(t, ASK + 2):
                        c = (b + ASK + 2) % S
                        if not (isinstance(t, int) and t + ASK + 2 < S):
                            j = i if b < S - ASK - 2 else i + 1
                            hold(sp, e.dmas["q"][c], j * 16, passed_sp)
                            hold(sp, e.dmas["kv"][c], j * 16, passed_sp)
                            e.done(sp, "keyed", t + ASK + 2, S, passed_sp)
                        sp.dma_start(ixa[:, c, :], tile_of(g.idx, t + ASK + 2)).then_inc(e.dmas["ixa"][c], 16)
                    if exists(t, 0):
                        if not (isinstance(t, int) and t < S):
                            hold(sp, e.dmas["new"][b], i * 16, passed_sp)
                        sp.dma_start(ixb[:, b, :], tile_of(g.idx, t)).then_inc(e.dmas["ixb"][b], 16)

                steps_of(sp, step, ET, ASK + 2, 0, S)

            @block.gpsimd
            def _(pool):
                def step(t, i, b):
                    if exists(t, ASK):
                        c = (b + ASK) % S
                        j = i + 2 if b >= S - ASK else i + 1
                        pool.wait_ge(e.dmas["ixa"][c], j * 16)
                        if not (isinstance(t, int) and t + ASK < S):
                            e.done(pool, "weighted_a", t + ASK, S)
                            e.done(pool, "weighted_v", t + ASK, S)
                            e.done(pool, "paired", t + ASK, S)
                        pool.sem_inc(passed)
                        pool.indirect_dma_start(out=q[:, c, :], out_offset=None, in_=g.qrows[:, :],
                                                in_offset=bass.IndirectOffsetOnAxis(ap=ixa[:, c, 0:1], axis=0)).then_inc(e.dmas["q"][c], 16)
                        pool.indirect_dma_start(out=kv[:, c, :], out_offset=None, in_=g.kvrows[:, :],
                                                in_offset=bass.IndirectOffsetOnAxis(ap=ixa[:, c, 1:2], axis=0)).then_inc(e.dmas["kv"][c], 16)
                    if exists(t, -3):
                        c = (b - 3) % S
                        j = i + 1 if b >= 3 else i
                        pool.wait_ge(e.dmas["ixb"][c], j * 16)
                        if not (isinstance(t, int) and t - 3 < NTAB):
                            pool.wait_ge(e.dmas["new"][(c - NTAB) % S], (j if c >= NTAB else j - 1) * 16)
                        e.done(pool, "new_ready", t, 3)
                        pool.sem_inc(passed)
                        pool.indirect_dma_start(out=g.tabs1[c % NTAB][:, :], out_offset=bass.IndirectOffsetOnAxis(ap=ixb[:, c, 2:3], axis=0),
                                                in_=new[:, c, :], in_offset=None, compute_op=ALU.add).then_inc(e.dmas["new"][c], 16)

                steps_of(pool, step, ET, ASK, 3, S)
                for c in range(S):
                    hold(pool, e.dmas["new"][c], 16 * (ET // S), passed)

            @block.tensor
            def _(pe):
                def spread(t, b):
                    e.done(pe, "keyed", t)
                    e.done(pe, "matched", t, 2)
                    pe.transpose(pkey[b % 2][:, :], key[:, b, :].to_broadcast([P, P]), g.ident[:, :]).then_inc(e.marks["spread"], 1)

                def total(t, b):
                    e.done(pe, "weighted_a", t)
                    e.done(pe, "weighted_v", t)
                    e.done(pe, "new_ready", t, 2)
                    p = pm[b % 2]
                    e.done(pe, "matched", t)
                    pe.matmul(p[:, D:ROW1], same[:, b, :], tile_of(g.kinds, t), start=True, stop=True)
                    for h in range(HG):
                        mm = pe.matmul(p[:, 0:D], same[:, b, :], wv[:, b, h, :], start=(h == 0), stop=(h == HG - 1))
                    mm.then_inc(e.marks["totalled"], 1)

                def step(t, i, b):
                    if exists(t, 2):
                        spread(t + 2, (b + 2) % S)
                    if exists(t, -1):
                        total(t + -1, (b - 1) % S)

                steps_of(pe, step, ET, 2, 1, S)

            @block.scalar
            def _(act):
                def step(t, i, b):
                    if exists(t, -1):
                        c = (b - 1) % S
                        e.done(act, "attended", t, 1)
                        e.done(act, "totalled", t - 1, S)
                        for h in range(AH):
                            for s in range(HG):
                                ins = act.activation(wv[:, c, h, s * DG:(s + 1) * DG], kv[:, c, D + h * DG:D + (h + 1) * DG], ACT.Copy,
                                                     scale=att[:, c, s, h:h + 1])
                        ins.then_inc(e.marks["weighted_a"], 1)
                    if exists(t, -2):
                        c = (b - 2) % S
                        e.done(act, "totalled", t, 2)
                        if not (isinstance(t, int) and t - 2 < S):
                            act.wait_ge(e.dmas["new"][c], (i if b >= 2 else i - 1) * 16)
                        act.activation(new[:, c, :], pm[b % 2][:, :], ACT.Copy).then_inc(e.marks["new_ready"], 1)
                    if exists(t, 1):
                        c = (b + 1) % S
                        e.done(act, "centred", t + 1)
                        act.activation(ex[:, c, :, :], sc[:, c, :, :], ACT.Exp, scale=DG ** -0.5).then_inc(e.marks["exped"], 1)

                steps_of(act, step, ET, 1, 2, S)

            @block.vector
            def _(dve):
                m = e.marks

                def make_key(t, i, b):
                    dve.wait_ge(e.dmas["ixa"][b], i * 16 + 16)
                    e.done(dve, "spread", t, S)
                    dve.tensor_copy(key[:, b, :], ixa[:, b, 0:1]).then_inc(m["keyed"], 1)

                def step(t, i, b):
                    now, new_, c = exists(t, 0), exists(t, 1), (b + 1) % S
                    if new_:
                        n = i + 1 if b == S - 1 else i
                        dve.wait_ge(e.dmas["q"][c], n * 16 + 16)
                        dve.wait_ge(e.dmas["kv"][c], n * 16 + 16)
                        e.done(dve, "scored", t, 1)
                        qs = q[:, c, :].rearrange("p (h d) -> p h d", h=HG)
                        ks = kv[:, c, 0:D].rearrange("p (h d) -> p h d", h=HG)
                        dve.tensor_tensor(qk[:, c % 2, :, :, :], over(qs, 2, [P, HG, HG, DG]), over(ks, 1, [P, HG, HG, DG]), ALU.mult).then_inc(m["paired"], 1)
                    if now:
                        e.done(dve, "exped", t)
                        dve.tensor_reduce(den[:, b, :], ex[:, b, :, :], AX, ALU.add).then_inc(m["summed"], 1)
                    if new_:
                        e.done(dve, "paired", t + 1)
                        dve.tensor_reduce(sc[:, c, :, :], qk[:, c % 2, :, :, :], AX, ALU.add).then_inc(m["scored"], 1)
                    if now:
                        e.done(dve, "summed", t)
                        dve.reciprocal(den[:, b, :], den[:, b, :]).then_inc(m["inverted"], 1)
                    if new_:
                        e.done(dve, "spread", t + 1)
                        e.done(dve, "totalled", t + 1, S)
                        dve.tensor_scalar(same[:, c, :], pkey[c % 2][:, :], key[:, c, :], None, ALU.is_equal).then_inc(m["matched"], 1)
                        e.done(dve, "scored", t + 1)
                        dve.tensor_reduce(mx[:, c, :], sc[:, c, :, :], AX, ALU.max).then_inc(m["topped"], 1)
                    if now:
                        e.done(dve, "inverted", t)
                        dve.tensor_tensor(att[:, b, :, :], ex[:, b, :, :], over(den[:, b, :], 2, [P, HG, HG]), ALU.mult).then_inc(m["attended"], 1)
                    if exists(t, 2):
                        make_key(t + 2, i + 1 if b >= S - 2 else i, (b + 2) % S)
                    if new_:
                        e.done(dve, "topped", t + 1)
                        dve.tensor_tensor(sc[:, c, :, :], sc[:, c, :, :], over(mx[:, c, :], 2, [P, HG, HG]), ALU.subtract).then_inc(m["centred"], 1)
                    if now:
                        e.done(dve, "attended", t)
                        e.done(dve, "totalled", t, S)
                        for h in range(AH, HG):
                            ins = dve.tensor_tensor(wv[:, b, h, :].rearrange("p (s d) -> p s d", s=HG),
                                                    over(kv[:, b, D + h * DG:D + (h + 1) * DG], 1, [P, HG, DG]),
                                                    att[:, b, :, h:h + 1].to_broadcast([P, HG, DG]), ALU.mult)
                        ins.then_inc(m["weighted_v"], 1)

                steps_of(dve, step, ET, 2, 0, S)


def tile_of(buf, t):
    return buf[:, t, :] if isinstance(t, int) else buf[:, ds(t, 1), :].rearrange("p a b -> p (a b)")


def ln_pair(dve, link, z, stat, junk, ask, got):
    s, v = stat[:, 0, :], stat[:, 1, :]
    link(dve.tensor_reduce(s, z, AX, ALU.add))
    link(dve.tensor_scalar(s, s, -1.0 / D, None, ALU.mult))
    link(dve.tensor_tensor(z, z, over(s, 2, [P, 2, D]), ALU.add))
    for t in range(2):
        ins = dve.tensor_tensor_reduce(junk[:, t, :], z[:, t, :], z[:, t, :], 1.0, 0.0, ALU.mult, ALU.add, stat[:, 1, t:t + 1])
    link(ins)
    ask(dve.tensor_scalar(v, v, 1.0 / D, EPS, ALU.mult, ALU.add))
    got()
    link(dve.reciprocal(s, stat[:, 2, :]))
    link(dve.tensor_tensor(z, z, over(s, 2, [P, 2, D]), ALU.mult))


def update1(nc, g, a, l):
    with Room(nc, "up") as r:
        wo = r.sbuf("wo", [P, KD, D])
        em = r.sbuf("em", [P, KD, 3])
        te = r.sbuf("te", [4, D])
        gain, shift = r.sbuf("gain", [P, D]), r.sbuf("shift", [P, D])
        tb = r.sbuf("tb", [P, 2, NTAB, 2, ROW1])
        st = r.sbuf("st", [P, KD, PW])
        ct = r.sbuf("ct", [4, PW])
        z = r.sbuf("z", [P, 2, 2, D])
        y = r.sbuf("y", [P, 2, D])
        eps = r.sbuf("eps", [P, 1])
        junk = r.sbuf("junk", [P, 2, D])
        stat = r.sbuf("stat", [P, 2, 5, 2])
        pt = r.psum("pt", [P, KD, PW])
        pc = r.psum("pc", [4, PW])
        po = r.psum("po", [P, 2, D])
        pe_ = r.psum("pe", [3, D])
        loaded, embedded, te_ready, ld, passed = (r.sem(n) for n in ("loaded", "embedded", "te_ready", "ld", "passed"))
        m = Marks(nc, r, ("added", "turned", "st_ready", "projected", "z_ready", "centred", "squared", "rooted", "scaled", "kept"))
        chain = r.sems("step", 4)
        with nc.Block() as block:

            @block.sync
            def _(sp):
                sp.dma_start(wo[:, :, :], weights(a["woT"][ds(l * D, D), :])).then_inc(loaded, 16)
                sp.dma_start(em[:, :, :], weights(a["eemb"][ds(l * D, D), :])).then_inc(loaded, 16)
                sp.dma_start(te[3:4, :], a["bo"][ds(l, 1), :]).then_inc(loaded, 16)
                sp.dma_start(gain[:, :], a["ln_g"][ds(l, 1), :].to_broadcast([P, D])).then_inc(loaded, 16)
                sp.dma_start(shift[:, :], a["ln_b"][ds(l, 1), :].to_broadcast([P, D])).then_inc(loaded, 16)

                def load(n, slot):
                    hold(sp, m["turned"], n + 1, passed)
                    for k in range(NTAB):
                        sp.dma_start(tb[:, slot, k, :, :], rows(g.tabs1[k], n)).then_inc(ld, 16)

                load(0, 0)
                with sp.Fori(0, PAIRS // 2) as i:
                    for slot in range(2):
                        n = i * 2 + (slot + 1)
                        hold(sp, ld, n * (16 * NTAB), passed)
                        load(n, 1 - slot)

            @block.tensor
            def _(pe):
                pe.wait_ge(loaded, 80)
                for k in range(KD):
                    mm = pe.matmul(pe_[:, :], em[:, k, :], wo[:, k, :], start=(k == 0), stop=(k == KD - 1))
                mm.then_inc(embedded, 1)
                pe.wait_ge(te_ready, 1)

                def step(n, slot):
                    if exists(n, 1, PAIRS):
                        s = 1 - slot
                        m.done(pe, "added", n + 1)
                        m.done(pe, "st_ready", n)
                        for t in range(2):
                            pe.transpose(pc[:, t * P:(t + 1) * P], tb[:, s, 0, t, D:ROW1], g.ident[:, :])
                            for k in range(KD):
                                mm = pe.transpose(pt[:, k, t * P:(t + 1) * P], tb[:, s, 0, t, k * P:(k + 1) * P], g.ident[:, :])
                        mm.then_inc(m["turned"], 1)
                        m.done(pe, "st_ready", n + 1)
                        m.done(pe, "z_ready", n)
                        for t in range(2):
                            for k in range(KD):
                                pe.matmul(po[:, t, :], st[:, k, t * P:(t + 1) * P], wo[:, k, :], start=(k == 0), stop=False)
                            mm = pe.matmul(po[:, t, :], ct[:, t * P:(t + 1) * P], te[:, :], start=False, stop=True)
                        mm.then_inc(m["projected"], 1)

                pair_steps(pe, step, 1, 0)

            @block.scalar
            def _(act):
                def step(n, slot):
                    if exists(n, 1, PAIRS):
                        m.done(act, "turned", n + 1)
                        m.done(act, "projected", n)
                        act.activation(st[:, :, :], pt[:, :, :], ACT.Copy)
                        act.activation(ct[:, :], pc[:, :], ACT.Copy).then_inc(m["st_ready"], 1)
                    if exists(n, 0, PAIRS):
                        m.done(act, "centred", n)
                        m.done(act, "squared", n, 1)
                        for t in range(2):
                            ins = act.activation(junk[:, t, :], z[:, slot, t, :], ACT.Square, bias=stat[:, slot, 1, t:t + 1],
                                                 accum_out=stat[:, slot, 2, t:t + 1])
                        ins.then_inc(m["squared"], 1)
                        m.done(act, "squared", n)
                        act.activation(stat[:, slot, 3, :], stat[:, slot, 2, :], ACT.Sqrt, scale=1.0 / D, bias=eps[:, :]).then_inc(m["rooted"], 1)
                    if exists(n, -1, PAIRS):
                        m.done(act, "scaled", n, 1)
                        act.activation(rows_of(g.hid, n - 1), y[:, :, :], ACT.Relu).then_inc(m["kept"], 1)

                act.wait_ge(embedded, 1)
                act.activation(te[0:3, :], pe_[:, :], ACT.Copy).then_inc(te_ready, 1)
                pair_steps(act, step, 1, 1)

            @block.vector
            def _(dve):
                def add(n, slot):
                    dve.wait_ge(ld, n * (16 * NTAB) + 16 * NTAB)
                    link = Chain(dve, chain[0:1], n + 1)
                    link(dve.tensor_tensor(tb[:, slot, 0:2, :, :], tb[:, slot, 0:2, :, :], tb[:, slot, 2:4, :, :], ALU.add))
                    dve.tensor_tensor(tb[:, slot, 0, :, :], tb[:, slot, 0, :, :], tb[:, slot, 1, :, :], ALU.add).then_inc(m["added"], 1)

                def centre(n, slot):
                    link = Chain(dve, chain[1:2], n + 1)
                    m.done(dve, "projected", n)
                    dve.tensor_tensor(z[:, slot, :, :], po[:, :, :], rows_of(g.hid, n), ALU.add).then_inc(m["z_ready"], 1)
                    m.done(dve, "z_ready", n)
                    link(dve.tensor_reduce(stat[:, slot, 0, :], z[:, slot, :, :], AX, ALU.add))
                    dve.tensor_scalar(stat[:, slot, 1, :], stat[:, slot, 0, :], -1.0 / D, None, ALU.mult).then_inc(m["centred"], 1)

                def scale(n, slot):
                    link = Chain(dve, chain[2:4], n + 1)
                    m.done(dve, "rooted", n)
                    m.done(dve, "kept", n, 1)
                    dve.reciprocal(stat[:, slot, 4, :], stat[:, slot, 3, :])
                    for t in range(2):
                        ins = dve.scalar_tensor_tensor(out=y[:, t, :], in0=z[:, slot, t, :], scalar=stat[:, slot, 1, t:t + 1], in1=gain[:, :],
                                                       op0=ALU.add, op1=ALU.mult)
                    link(ins)
                    for t in range(2):
                        ins = dve.scalar_tensor_tensor(out=y[:, t, :], in0=y[:, t, :], scalar=stat[:, slot, 4, t:t + 1], in1=shift[:, :],
                                                       op0=ALU.mult, op1=ALU.add)
                    ins.then_inc(m["scaled"], 1)

                def step(n, slot):
                    if exists(n, 1, PAIRS):
                        add(n + 1, 1 - slot)
                    if exists(n, 0, PAIRS):
                        centre(n, slot)
                    if exists(n, -1, PAIRS):
                        scale(n - 1, 1 - slot)

                dve.memset(eps[:, :], EPS)
                dve.wait_ge(loaded, 80)
                pair_steps(dve, step, 1, 1)


def adjust1(nc, g, a):
    with Room(nc, "ad") as r:
        w1, w2 = (r.sbuf(f"w{j}", [P, KD, D]) for j in (1, 2))
        b1 = r.sbuf("b1", [P, KD])
        b2 = r.sbuf("b2", [P, D])
        un = r.sbuf("un", [P, 2, D])
        xt = r.sbuf("xt", [P, KD, PW])
        h = r.sbuf("h", [P, KD, PW])
        o = r.sbuf("o", [P, 2, D])
        pt = r.psum("pt", [P, KD, PW])
        ph = r.psum("ph", [P, KD, PW])
        po = r.psum("po", [P, 2, D])
        loaded = r.sem("loaded")
        m = {n: r.sem(n) for n in ("copied", "turned", "xt_ready", "hidden", "h_ready", "projected", "kept")}
        chain = r.sems("step", 4)
        credit(nc, list(m.values()))
        with nc.Block() as block:

            @block.sync
            def _(sp):
                for dst, src in ((w1[:, :, :], weights(a["w1T"])), (w2[:, :, :], weights(a["w2T"])), (b1[:, :], a["b1"]), (b2[:, :], to_all(a["b2"], D))):
                    sp.dma_start(dst, src).then_inc(loaded, 16)
                sp.wait_ge(loaded, 64)

            @block.scalar
            def _(act):
                act.wait_ge(loaded, 64)
                with act.Fori(0, PAIRS) as i:
                    act.wait_ge(m["turned"], i + 1)
                    act.activation(un[:, :, :], g.hid[:, ds(i * 2, 2), :], ACT.Copy).then_inc(m["copied"], 1)
                    act.wait_ge(m["hidden"], i + 2)
                    act.wait_ge(m["projected"], i + 1)
                    for c in range(KD):
                        ins = act.activation(h[:, c, :], ph[:, c, :], ACT.Relu, bias=b1[:, c:c + 1])
                    ins.then_inc(m["h_ready"], 1)

            @block.tensor
            def _(pe):
                pe.wait_ge(loaded, 64)
                with pe.Fori(0, PAIRS) as i:
                    pe.wait_ge(m["copied"], i + 2)
                    pe.wait_ge(m["xt_ready"], i + 1)
                    turn_pair(pe, g, pt, un).then_inc(m["turned"], 1)
                    pe.wait_ge(m["xt_ready"], i + 2)
                    pe.wait_ge(m["h_ready"], i + 1)
                    for c in range(KD):
                        for k in range(KD):
                            mm = pe.matmul(ph[:, c, :], w1[:, k, c * P:(c + 1) * P], xt[:, k, :], start=(k == 0), stop=(k == KD - 1))
                    mm.then_inc(m["hidden"], 1)
                    pe.wait_ge(m["h_ready"], i + 2)
                    pe.wait_ge(m["kept"], i + 1)
                    for t in range(2):
                        for k in range(KD):
                            mm = pe.matmul(po[:, t, :], h[:, k, t * P:(t + 1) * P], w2[:, k, :], start=(k == 0), stop=(k == KD - 1))
                    mm.then_inc(m["projected"], 1)

            @block.vector
            def _(dve):
                dve.wait_ge(loaded, 64)
                with dve.Fori(0, PAIRS) as i:
                    link = Chain(dve, chain, i + 1)
                    dve.wait_ge(m["turned"], i + 2)
                    dve.wait_ge(m["hidden"], i + 1)
                    dve.tensor_copy(xt[:, :, :], pt[:, :, :]).then_inc(m["xt_ready"], 1)
                    dve.wait_ge(m["projected"], i + 2)
                    link(dve.tensor_tensor(o[:, :, :], po[:, :, :], over(b2[:, :], 1, [P, 2, D]), ALU.add))
                    link(dve.tensor_tensor(o[:, :, :], o[:, :, :], g.u[:, ds(i * 2, 2), :], ALU.add))
                    dve.tensor_tensor(g.x[:, ds(i * 2, 2), :], g.x[:, ds(i * 2, 2), :], o[:, :, :], ALU.add).then_inc(m["kept"], 1)


def mix1_keys(nc, g, a):
    with Room(nc, "mk") as r:
        w = r.sbuf("w", [P, KD, 3 * D])
        bias = r.sbuf("bias", [P, 3 * D])
        un = r.sbuf("un", [P, 2, D])
        xt = r.sbuf("xt", [P, 2, KD, PW])
        qk = r.sbuf("qk", [P, 2, 2, 2, D])
        v = r.sbuf("v", [P, 2, 2, D])
        k2 = r.sbuf("k2", [P, 2, 2, D])
        junk = r.sbuf("junk", [P, 2, D])
        st = r.sbuf("st", [P, 4, 2, 2])
        qn = r.sbuf("qn", [P, 2, 2, 2])
        colsq = r.sbuf("colsq", [P, KD])
        pt = r.psum("pt", [P, KD, PW])
        pqk = [r.psum(f"pqk{t}", [P, 2, D]) for t in range(2)]
        pv = r.psum("pv", [P, 2, D])
        pkv = r.psum("pkv", [P, KD, D])
        pcs = r.psum("pcs", [P, KD])
        loaded, zeroed, last, rooted, asked = (r.sem(n) for n in ("loaded", "zeroed", "last", "rooted", "asked"))
        m = Marks(nc, r, ("copied", "turned", "xt_ready", "projected", "v_ready", "centred", "squared", "k_ready", "k2_ready", "multiplied",
                          "q_squared", "q_rooted", "kept", "q_kept", "kv_added"))
        chain = r.sems("step", 16)
        with nc.Block() as block:

            @block.sync
            def _(sp):
                sp.dma_start(w[:, :, :], weights(a["mqkv"])).then_inc(loaded, 16)
                sp.dma_start(bias[:, :], to_all(a["mb"], 3 * D)).then_inc(loaded, 16)
                sp.wait_ge(loaded, 32)

            @block.scalar
            def _(act):
                def step(n, slot):
                    if exists(n, 1, PAIRS):
                        m.done(act, "turned", n + 1)
                        m.done(act, "projected", n + 1, 2)
                        act.activation(xt[:, 1 - slot, :, :], pt[:, :, :], ACT.Copy).then_inc(m["xt_ready"], 1)
                    if exists(n, 2, PAIRS):
                        m.done(act, "turned", n + 2, 1)
                        act.activation(un[:, :, :], rows_of(g.u, n + 2), ACT.Copy).then_inc(m["copied"], 1)
                    if exists(n, 0, PAIRS):
                        m.done(act, "centred", n)
                        for t in range(2):
                            for j in range(2):
                                ins = act.activation(qk[:, slot, t, j, :], qk[:, slot, t, j, :], ACT.Square, bias=st[:, 2, t, j:j + 1],
                                                     accum_out=st[:, 3, t, j:j + 1])
                        ins.then_inc(m["squared"], 1)
                        m.done(act, "v_ready", n)
                        act.activation(rows_of(g.v, n), v[:, slot, :, :], ACT.Copy).then_inc(m["kept"], 1)
                        m.done(act, "k_ready", n)
                        m.done(act, "multiplied", n, 2)
                        act.activation(k2[:, slot, :, :], qk[:, slot, :, 1, :], ACT.Square).then_inc(m["k2_ready"], 1)
                        m.done(act, "q_rooted", n, 1)
                        for t in range(2):
                            ins = act.activation(junk[:, t, :], qk[:, slot, t, 0, :], ACT.Square, accum_out=qn[:, slot, 0, t:t + 1])
                        ins.then_inc(m["q_squared"], 1)
                        m.done(act, "q_squared", n)
                        act.activation(qn[:, slot, 1, :], qn[:, slot, 0, :], ACT.Sqrt).then_inc(m["q_rooted"], 1)

                act.wait_ge(loaded, 32)
                pair_steps(act, step, 2, 0)
                act.wait_ge(asked, 1)
                act.activation(colsq[:, :], colsq[:, :], ACT.Sqrt).then_inc(rooted, 1)

            @block.tensor
            def _(pe):
                def step(n, slot):
                    if exists(n, 1, PAIRS):
                        m.done(pe, "copied", n + 1)
                        m.done(pe, "xt_ready", n)
                        turn_pair(pe, g, pt, un).then_inc(m["turned"], 1)
                    if exists(n, 0, PAIRS):
                        m.done(pe, "xt_ready", n)
                        m.done(pe, "v_ready", n, 1)
                        for t in range(2):
                            for dst, c in ((pqk[t][:, :, :], slice(0, 2 * D)), (pv[:, t, :], slice(2 * D, 3 * D))):
                                for k in range(KD):
                                    mm = pe.matmul(dst, xt[:, slot, k, t * P:(t + 1) * P], w[:, k, c], start=(k == 0), stop=(k == KD - 1))
                        mm.then_inc(m["projected"], 1)
                    if exists(n, -1, PAIRS):
                        other = 1 - slot
                        m.done(pe, "k_ready", n, 1)
                        m.done(pe, "k2_ready", n, 1)
                        m.done(pe, "kv_added", n, 2)
                        for c in range(KD):
                            for t in range(2):
                                pe.matmul(pkv[:, c, :], qk[:, other, t, 1, c * P:(c + 1) * P], v[:, other, t, :], start=(t == 0), stop=(t == 1))
                            for t in range(2):
                                mm = pe.matmul(pcs[:, c:c + 1], k2[:, other, t, c * P:(c + 1) * P], g.ones[:, 0:1], start=(t == 0), stop=(t == 1))
                        mm.then_inc(m["multiplied"], 1)

                pe.wait_ge(loaded, 32)
                pair_steps(pe, step, 1, 1)

            @block.vector
            def _(dve):
                full = [P, 2, 2, D]
                s, rs, cent, sq = (st[:, j, :, :] for j in range(4))

                def centre(n, slot):
                    link = Chain(dve, chain[0:2], n + 1)
                    m.done(dve, "projected", n)
                    m.done(dve, "multiplied", n, 2)
                    m.done(dve, "kept", n, 2)
                    m.done(dve, "q_kept", n, 2)
                    for t in range(2):
                        ins = dve.tensor_tensor(qk[:, slot, t, :, :], pqk[t][:, :, :], bias[:, 0:2 * D].rearrange("p (a b) -> p a b", a=2), ALU.add)
                    ins.then_inc(chain[8], 1)
                    dve.tensor_tensor(v[:, slot, :, :], pv[:, :, :], over(bias[:, 2 * D:3 * D], 1, [P, 2, D]), ALU.add).then_inc(m["v_ready"], 1)
                    dve.wait_ge(chain[8], n + 1)
                    link(dve.tensor_reduce(s, qk[:, slot, :, :, :], AX, ALU.add))
                    dve.tensor_scalar(cent, s, -1.0 / D, None, ALU.mult).then_inc(m["centred"], 1)

                def keep(n, slot):
                    link = Chain(dve, chain[2:4], n + 1)
                    m.done(dve, "q_rooted", n)
                    link(dve.tensor_scalar(qn[:, slot, 1, :], qn[:, slot, 1, :], 1e-12, None, ALU.max))
                    link(dve.reciprocal(qn[:, slot, 1, :], qn[:, slot, 1, :]))
                    dve.tensor_tensor(rows_of(g.q, n), qk[:, slot, :, 0, :], over(qn[:, slot, 1, :], 2, [P, 2, D]), ALU.mult).then_inc(m["q_kept"], 1)

                def add(n):
                    m.done(dve, "multiplied", n)
                    m.done(dve, "kv_added", n, 1)
                    dve.tensor_tensor(g.kvm[:, :, :], g.kvm[:, :, :], pkv[:, :, :], ALU.add)
                    dve.tensor_tensor(colsq[:, :], colsq[:, :], pcs[:, :], ALU.add).then_inc(m["kv_added"], 1)

                def scale(n, slot):
                    link = Chain(dve, chain[4:7], n + 1)
                    m.done(dve, "squared", n)
                    link(dve.tensor_scalar(s, sq, 1e-7, None, ALU.add))
                    link(dve.reciprocal(rs, s))
                    valid = g.valid[:, 2 * n:2 * n + 2] if isinstance(n, int) else g.valid[:, ds(n * 2, 2)]
                    link(dve.tensor_tensor(rs[:, :, 1], rs[:, :, 1], valid, ALU.mult))
                    dve.tensor_tensor(qk[:, slot, :, :, :], qk[:, slot, :, :, :], over(rs, 3, full), ALU.mult).then_inc(m["k_ready"], 1)

                def step(n, slot):
                    if exists(n, 0, PAIRS):
                        centre(n, slot)
                    if exists(n, -1, PAIRS):
                        keep(n - 1, 1 - slot)
                    if exists(n, -2, PAIRS):
                        add(n - 2)
                    if exists(n, 0, PAIRS):
                        scale(n, slot)

                dve.memset(g.kvm[:, :, :], 0.0)
                dve.memset(colsq[:, :], 0.0).then_inc(zeroed, 1)
                dve.wait_ge(zeroed, 1)
                dve.wait_ge(loaded, 32)
                pair_steps(dve, step, 0, 2)
                dve.wait_ge(m["kv_added"], PAIRS + 2)
                dve.sem_inc(asked)
                dve.wait_ge(rooted, 1)
                dve.tensor_scalar(colsq[:, :], colsq[:, :], 1e-12, None, ALU.max).then_inc(last, 1)
                dve.wait_ge(last, 1)
                dve.reciprocal(colsq[:, :], colsq[:, :]).then_inc(last, 1)
                dve.wait_ge(last, 2)
                dve.tensor_scalar(colsq[:, :], colsq[:, :], NODES ** -0.5, None, ALU.mult).then_inc(last, 1)
                dve.wait_ge(last, 3)
                dve.tensor_tensor(g.kvm[:, :, :], g.kvm[:, :, :], over(colsq[:, :], 2, [P, KD, D]), ALU.mult).then_inc(last, 1)


def mix1_out(nc, g, a):
    with Room(nc, "mo") as r:
        w = r.sbuf("w", [P, KD, D])
        bias = r.sbuf("bias", [P, D])
        un = r.sbuf("un", [P, 2, D])
        qt = r.sbuf("qt", [P, 2, KD, PW])
        at = r.sbuf("at", [P, 2, KD, PW])
        att = r.sbuf("att", [P, 2, 2, D])
        o = r.sbuf("o", [P, 2, D])
        pt, pt2 = r.psum("pt", [P, KD, PW]), r.psum("pt2", [P, KD, PW])
        pa = [r.psum(f"pa{s}", [P, 2, D]) for s in range(2)]
        po = [r.psum(f"po{s}", [P, 2, D]) for s in range(2)]
        loaded = r.sem("loaded")
        m = Marks(nc, r, ("copied", "turned", "qt_ready", "attended", "att_ready", "att_turned", "at_ready", "projected", "biased", "kept"))
        with nc.Block() as block:

            @block.sync
            def _(sp):
                sp.dma_start(w[:, :, :], weights(a["mout"])).then_inc(loaded, 16)
                sp.dma_start(bias[:, :], to_all(a["mbo"], D)).then_inc(loaded, 16)
                sp.wait_ge(loaded, 32)

            @block.scalar
            def _(act):
                def step(n, slot):
                    if exists(n, 1, PAIRS):
                        m.done(act, "turned", n + 1, 1)
                        act.activation(un[:, :, :], rows_of(g.q, n + 1), ACT.Copy).then_inc(m["copied"], 1)
                    if exists(n, -1, PAIRS):
                        m.done(act, "att_turned", n, 1)
                        m.done(act, "projected", n, 3)
                        act.activation(at[:, 1 - slot, :, :], pt2[:, :, :], ACT.Copy).then_inc(m["at_ready"], 1)

                pair_steps(act, step, 1, 2)

            @block.tensor
            def _(pe):
                def step(n, slot):
                    if exists(n, 1, PAIRS):
                        m.done(pe, "copied", n + 1)
                        m.done(pe, "qt_ready", n)
                        turn_pair(pe, g, pt, un).then_inc(m["turned"], 1)
                    if exists(n, 0, PAIRS):
                        m.done(pe, "qt_ready", n)
                        m.done(pe, "att_ready", n, 2)
                        for t in range(2):
                            for k in range(KD):
                                mm = pe.matmul(pa[slot][:, t, :], qt[:, slot, k, t * P:(t + 1) * P], g.kvm[:, k, :], start=(k == 0), stop=(k == KD - 1))
                        mm.then_inc(m["attended"], 1)
                    if exists(n, -1, PAIRS):
                        m.done(pe, "att_ready", n, 1)
                        m.done(pe, "at_ready", n, 2)
                        for t in range(2):
                            for k in range(KD):
                                mm = pe.transpose(pt2[:, k, t * P:(t + 1) * P], att[:, 1 - slot, t, k * P:(k + 1) * P], g.ident[:, :])
                        mm.then_inc(m["att_turned"], 1)
                    if exists(n, -2, PAIRS):
                        m.done(pe, "at_ready", n, 2)
                        m.done(pe, "biased", n, 4)
                        for t in range(2):
                            for k in range(KD):
                                mm = pe.matmul(po[slot][:, t, :], at[:, slot, k, t * P:(t + 1) * P], w[:, k, :], start=(k == 0), stop=(k == KD - 1))
                        mm.then_inc(m["projected"], 1)

                pe.wait_ge(loaded, 32)
                pair_steps(pe, step, 1, 2)

            @block.vector
            def _(dve):
                def step(n, slot):
                    if exists(n, 1, PAIRS):
                        m.done(dve, "turned", n + 1)
                        m.done(dve, "attended", n, 1)
                        dve.tensor_copy(qt[:, 1 - slot, :, :], pt[:, :, :]).then_inc(m["qt_ready"], 1)
                    if exists(n, 0, PAIRS):
                        m.done(dve, "attended", n)
                        m.done(dve, "att_turned", n, 2)
                        dve.tensor_tensor(att[:, slot, :, :], pa[slot][:, :, :], rows_of(g.v, n), ALU.add).then_inc(m["att_ready"], 1)
                    if exists(n, -2, PAIRS):
                        m.done(dve, "projected", n, 2)
                        m.done(dve, "kept", n, 3)
                        dve.tensor_tensor(o[:, :, :], po[slot][:, :, :], over(bias[:, :], 1, [P, 2, D]), ALU.add).then_inc(m["biased"], 1)
                        m.done(dve, "biased", n, 2)
                        dve.tensor_tensor(rows_of(g.x, n - 2), rows_of(g.x, n - 2), o[:, :, :], ALU.add).then_inc(m["kept"], 1)

                dve.wait_ge(loaded, 32)
                pair_steps(dve, step, 1, 2)


def route1(nc, g, a):
    E = EXPERTS1
    CAP = float(math.ceil(NODES * 1.25 / E))
    with Room(nc, "ro") as r:
        part = r.sbuf("part", [P, 2, D])
        xm = r.sbuf("xm", [P, KD, P])
        wr = r.sbuf("wr", [P, KD, E])
        br = r.sbuf("br", [P, E])
        lg = r.sbuf("lg", [P, 3, 1, E])
        st = r.sbuf("st", [P, 4])
        hot = r.sbuf("hot", [P, 2])
        offs = r.sbuf("offs", [P, 8])
        offi = r.sbuf("offi", [P, 8], I32)
        rowf = r.sbuf("rowf", [P, 2, 8])
        rowi = r.sbuf("rowi", [P, 2, 8], I32)
        picks = Picks(r, E, 1)
        px = [r.psum(f"px{k}", [P, P]) for k in range(KD)]
        pl = r.psum("pl", [P, E])
        b2 = r.sbuf("b2", [P, 2, D])
        (loaded, made, parted, summed, xm_ready, logits, asked, exped, gapped, gap_exped, rows_ready, gathered, biased) = (
            r.sem(n) for n in ("loaded", "made", "parted", "summed", "xm_ready", "logits", "asked", "exped", "gapped", "gap_exped",
                               "rows_ready", "gathered", "biased"))
        step = r.sem("step")
        with nc.Block() as block:

            @block.sync
            def _(sp):
                sp.dma_start(wr[:, :, :], weights(a["wr"])).then_inc(loaded, 16)
                sp.dma_start(br[:, :], to_all(a["br"], E)).then_inc(loaded, 16)

            @block.gpsimd
            def _(pool):
                for k in range(4):
                    ins = pool.iota(offi[:, k:k + 1], pattern=[[0, 1]], base=k * P, channel_multiplier=1)
                ins = pool.memset(offi[:, 4:8], 0)
                ins.then_inc(made, 1)
                pool.wait_ge(rows_ready, 1)
                at = lambda j, k: bass.IndirectOffsetOnAxis(ap=rowi[:, j, k:k + 1], axis=0)
                for j in range(2):
                    for k in range(KD):
                        pool.indirect_dma_start(out=g.fw1[:, j, k, :], out_offset=None, in_=a["fw1"], in_offset=at(j, k)).then_inc(gathered, 16)
                    for k in range(KF):
                        pool.indirect_dma_start(out=g.fw2[:, j, k, :], out_offset=None, in_=a["fw2"], in_offset=at(j, 2 + k)).then_inc(gathered, 16)
                    pool.indirect_dma_start(out=g.fb1[:, j, :], out_offset=None, in_=a["fb1"], in_offset=at(j, 6)).then_inc(gathered, 16)
                    pool.indirect_dma_start(out=b2[:, j, :], out_offset=None, in_=a["fb2"], in_offset=at(j, 7)).then_inc(gathered, 16)
                pool.wait_ge(gathered, 16 * 2 * (KD + KF + 2))

            @block.tensor
            def _(pe):
                pe.wait_ge(parted, 1)
                for k in range(KD):
                    mm = pe.matmul(px[k][:, :], part[:, 1, k * P:(k + 1) * P], g.ones[:, :], start=True, stop=True)
                mm.then_inc(summed, 1)
                pe.wait_ge(xm_ready, 1)
                pe.wait_ge(loaded, 32)
                for k in range(KD):
                    mm = pe.matmul(pl[:, :], xm[:, k, :], wr[:, k, :], start=(k == 0), stop=(k == KD - 1))
                mm.then_inc(logits, 1)

            @block.scalar
            def _(act):
                for n in range(2):
                    act.wait_ge(asked, n + 1)
                    act.activation(lg[:, 1, 0, :], lg[:, 0, 0, :], ACT.Exp).then_inc(exped, 1)
                act.wait_ge(gapped, 1)
                act.activation(picks.small[:, 7, :], picks.small[:, 4, :], ACT.Exp).then_inc(gap_exped, 1)

            @block.vector
            def _(dve):
                count = [0]

                def link(ins):
                    count[0] += 1
                    ins.then_inc(step, 1)
                    dve.wait_ge(step, count[0])

                link(picks.order_of(dve))
                link(dve.tensor_reduce(part[:, 0, :], g.u[:, 0:FULL, :].rearrange("p t d -> p d t"), AX, ALU.add))
                dve.scalar_tensor_tensor(out=part[:, 1, :], in0=g.u[:, FULL, :], scalar=g.valid[:, FULL:FULL + 1], in1=part[:, 0, :],
                                         op0=ALU.mult, op1=ALU.add).then_inc(parted, 1)
                dve.wait_ge(summed, 1)
                for k in range(KD):
                    ins = dve.tensor_scalar(xm[:, k, :], px[k][:, :], 1.0 / NODES, None, ALU.mult)
                ins.then_inc(xm_ready, 1)
                dve.wait_ge(logits, 1)
                link(dve.tensor_tensor(lg[:, 0, 0, :], pl[:, :], br[:, :], ALU.add))
                link(dve.tensor_reduce(st[:, 0:1], lg[:, 0, 0, :], AX, ALU.max))
                for n in range(2):
                    dve.tensor_scalar(lg[:, 0, 0, :], lg[:, 0, 0, :], st[:, 0:1], None, ALU.subtract).then_inc(asked, 1)
                    dve.wait_ge(exped, n + 1)
                    link(dve.tensor_reduce(st[:, 1:2], lg[:, 1, 0, :], AX, ALU.add))
                    link(dve.reciprocal(st[:, 1:2], st[:, 1:2]))
                    link(dve.tensor_scalar(lg[:, 1, 0, :], lg[:, 1, 0, :], st[:, 1:2], None, ALU.mult))
                    if n == 0:
                        link(dve.tensor_scalar(lg[:, 2, 0, :], lg[:, 1, 0, :], float(NODES), None, ALU.mult))
                        link(dve.reciprocal(lg[:, 2, 0, :], lg[:, 2, 0, :]))
                        link(dve.tensor_scalar(lg[:, 2, 0, :], lg[:, 2, 0, :], CAP, 1.0, ALU.mult, ALU.min))
                        link(dve.tensor_tensor(lg[:, 0, 0, :], lg[:, 1, 0, :], lg[:, 2, 0, :], ALU.mult))
                        link(dve.tensor_reduce(st[:, 0:1], lg[:, 0, 0, :], AX, ALU.max))

                def wait_exp(ins):
                    ins.then_inc(gapped, 1)
                    dve.wait_ge(gap_exped, 1)

                link(pick_two(dve, link, lg[:, 1, :, :], picks, E, 1, wait_exp))
                link(dve.tensor_copy(g.fw[:, :], picks.small[:, 5:7, 0]))
                dve.wait_ge(made, 1)
                link(dve.tensor_copy(offs[:, :], offi[:, :]))
                for j in range(2):
                    e = picks.small[:, 2 + j, :]
                    for at, n, size in ((0, KD, D), (2, KF, F1), (6, 1, P), (7, 1, 1)):
                        base = offs[:, 0:n] if at != 7 else offs[:, 4:5]
                        link(dve.scalar_tensor_tensor(out=rowf[:, j, at:at + n], in0=e.to_broadcast([P, n]), scalar=float(size), in1=base,
                                                      op0=ALU.mult, op1=ALU.add))
                dve.tensor_copy(rowi[:, :, :], rowf[:, :, :]).then_inc(rows_ready, 1)
                dve.wait_ge(gathered, 16 * 2 * (KD + KF + 2))
                link(dve.tensor_scalar(b2[:, 0, :], b2[:, 0, :], g.fw[:, 0:1], None, ALU.mult))
                link(dve.scalar_tensor_tensor(out=g.fb2[:, :], in0=b2[:, 1, :], scalar=g.fw[:, 1:2], in1=b2[:, 0, :], op0=ALU.mult, op1=ALU.add))


def experts1(nc, g, a, out):
    with Room(nc, "fe") as r:
        gamma, beta = r.sbuf("gamma", [P, D]), r.sbuf("beta", [P, D])
        un = r.sbuf("un", [P, 2, 2, D])
        xt = r.sbuf("xt", [P, 2, KD, PW])
        h = r.sbuf("h", [P, 2, KF, PW])
        z = r.sbuf("z", [P, 2, D])
        junk = r.sbuf("junk", [P, 2, D])
        stat = r.sbuf("stat", [P, 3, 2])
        pt = r.psum("pt", [P, KD, PW])
        ph = [[r.psum(f"ph{j}{c}", [P, 2, PW]) for c in range(2)] for j in range(2)]
        po = [r.psum(f"po{j}", [P, 2, D]) for j in range(2)]
        loaded, stored, passed = r.sem("loaded"), r.sem("stored"), r.sem("passed")
        m = Marks(nc, r, ("copied", "turned", "xt_ready", "hidden0", "hidden1", "h0_ready", "h1_ready", "projected",
                          "started", "var_ready", "std_ready", "mixed", "res_ready"))
        chain = r.sems("step", 16)
        with nc.Block() as block:

            @block.sync
            def _(sp):
                sp.dma_start(gamma[:, :], to_all(a["fg"], D)).then_inc(loaded, 16)
                sp.dma_start(beta[:, :], to_all(a["fb"], D)).then_inc(loaded, 16)
                sp.wait_ge(loaded, 32)
                m.done(sp, "res_ready", PAIRS - 1)
                sp.sem_inc(passed)
                sp.dma_start(out[0:FULL * P, :].rearrange("(t p) c -> p t c", p=P), g.x[:, 0:FULL, :]).then_inc(stored, 16)
                sp.dma_start(out[FULL * P:NODES, :], g.x[0:REST, FULL, :]).then_inc(stored, 16)
                sp.wait_ge(stored, 32)

            @block.scalar
            def _(act):
                def step(n, slot):
                    if exists(n, 0, PAIRS):
                        m.done(act, "projected", n, 1)
                        for j in range(2):
                            m.done(act, f"hidden{j}", n)
                            for c in range(KF):
                                ins = act.activation(h[:, j, c, :], ph[j][c // 2][:, c % 2, :], ACT.Gelu, bias=g.fb1[:, j, c:c + 1])
                            ins.then_inc(m[f"h{j}_ready"], 1)
                    if exists(n, -1, PAIRS):
                        m.done(act, "var_ready", n, 1)
                        act.activation(stat[:, 2, :], stat[:, 1, :], ACT.Sqrt).then_inc(m["std_ready"], 1)
                    if exists(n, 2, PAIRS):
                        m.done(act, "turned", n)
                        m.done(act, "started", n)
                        act.activation(un[:, slot, :, :], rows_of(g.u, n + 2), ACT.Copy).then_inc(m["copied"], 1)

                pair_steps(act, step, 2, 1)

            @block.tensor
            def _(pe):
                def step(n, slot):
                    if exists(n, 1, PAIRS):
                        m.done(pe, "copied", n + 1)
                        m.done(pe, "xt_ready", n)
                        for t in range(2):
                            for k in range(KD):
                                mm = pe.transpose(pt[:, k, t * P:(t + 1) * P], un[:, 1 - slot, t, k * P:(k + 1) * P], g.ident[:, :])
                        mm.then_inc(m["turned"], 1)
                    if exists(n, 0, PAIRS):
                        m.done(pe, "xt_ready", n)
                        for j in range(2):
                            m.done(pe, f"h{j}_ready", n, 1)
                            for c in range(KF):
                                for k in range(KD):
                                    mm = pe.matmul(ph[j][c // 2][:, c % 2, :], g.fw1[:, j, k, c * P:(c + 1) * P], xt[:, slot, k, :],
                                                   start=(k == 0), stop=(k == KD - 1))
                            mm.then_inc(m[f"hidden{j}"], 1)
                        m.done(pe, "mixed", n, 1)
                        for j in range(2):
                            m.done(pe, f"h{j}_ready", n)
                            for t in range(2):
                                for k in range(KF):
                                    mm = pe.matmul(po[j][:, t, :], h[:, j, k, t * P:(t + 1) * P], g.fw2[:, j, k, :], start=(k == 0), stop=(k == KF - 1))
                        mm.then_inc(m["projected"], 1)

                pair_steps(pe, step, 1, 0)

            @block.vector
            def _(dve):
                def step(n, slot):
                    if exists(n, 1, PAIRS):
                        m.done(dve, "turned", n + 1)
                        m.done(dve, "hidden1", n + 1, 2)
                        dve.tensor_copy(xt[:, 1 - slot, :, :], pt[:, :, :]).then_inc(m["xt_ready"], 1)
                    if exists(n, 0, PAIRS):
                        link = Chain(dve, chain, n + 1)
                        m.done(dve, "res_ready", n, 1)
                        dve.tensor_tensor(z[:, :, :], un[:, slot, :, :], over(g.fb2[:, :], 1, [P, 2, D]), ALU.add).then_inc(m["started"], 1)
                        m.done(dve, "started", n)
                        m.done(dve, "projected", n)
                        for j in range(2):
                            ins = dve.scalar_tensor_tensor(out=z[:, :, :], in0=po[j][:, :, :], scalar=g.fw[:, j:j + 1], in1=z[:, :, :],
                                                           op0=ALU.mult, op1=ALU.add)
                            if j == 0:
                                link(ins)
                        ins.then_inc(m["mixed"], 1)
                        m.done(dve, "mixed", n)
                        ln_pair(dve, link, z[:, :, :], stat, junk, lambda ins: ins.then_inc(m["var_ready"], 1),
                                lambda: m.done(dve, "std_ready", n))
                        link(dve.tensor_tensor(z[:, :, :], z[:, :, :], over(gamma[:, :], 1, [P, 2, D]), ALU.mult))
                        link(dve.tensor_tensor(z[:, :, :], z[:, :, :], over(beta[:, :], 1, [P, 2, D]), ALU.add))
                        dve.tensor_tensor(rows_of(g.x, n), rows_of(g.x, n), z[:, :, :], ALU.add).then_inc(m["res_ready"], 1)

                dve.wait_ge(loaded, 32)
                pair_steps(dve, step, 1, 0)


class Shared:
    pass


def gps_kernel(nc, a, out, scratch):
    with Room(nc, "g") as room:
        g = Shared()
        g.x = room.sbuf("x", [P, NT, D])
        g.u = room.sbuf("u", [P, NT, D])
        g.ut = room.sbuf("ut", [P, KD, NPAD])
        g.idx = room.sbuf("idx", [P, ET, 4], I32)
        g.kinds = room.sbuf("kinds", [P, ET, 4])
        g.ident = room.sbuf("ident", [P, P])
        g.identb = room.sbuf("identb", [P, P], BF16)
        g.ones = room.sbuf("ones", [P, P])
        g.lower = room.sbuf("lower", [P, P])
        g.picks = room.sbuf("picks", [P, H0, P])
        g.spill = room.sbuf("spill", [P, 1])
        g.valid = room.sbuf("valid", [P, NT])
        g.g0 = room.sbuf("g0", [P, NT])
        g.usum = room.sbuf("usum", [P, KD])
        g.bn_scale = room.sbuf("bn_scale", [P, QKV])
        g.bn_beta = room.sbuf("bn_beta", [P, QKV])
        g.rowf = room.sbuf("rowf", [P, ET, 2])
        g.tabs0 = [scratch(f"tabs0_{k}", (TROWS, H0 * (D0 + 1) + H0), F32) for k in range(NTAB)]
        g.hid = g.ut[:, :, :].rearrange("p k n -> p (k n)").rearrange("p (t d) -> p t d", d=D)
        g.qrows = scratch("qrows", (NPAD, D), F32)
        g.kvrows = scratch("kvrows", (NPAD, 2 * D), F32)
        g.tabs1 = [scratch(f"tabs1_{k}", (TROWS, ROW1), F32) for k in range(NTAB)]
        g.hc = scratch("hc", (NPAD, QKV), F32)
        g.table0 = scratch("table0", (NPAD, ROW0), F32)
        load_inputs(nc, g, a)
        normalize(nc, g, "norm0", g.g0[:, :])
        log_scale(nc, g)
        node_rows(nc, g, a)
        mix_stats(nc, g, a)
        mix(nc, g, a)
        spill_duplicates(nc, g)
        attend0(nc, g, a)
        merge0(nc, g, a)
        normalize(nc, g, "norm1")
        experts0(nc, g, a)
        normalize(nc, g, "norm2")
        enter1(nc, g, a)
        with nc.Fori(0, LAYERS) as l:
            project1(nc, g, a, l)
            attend1(nc, g)
            update1(nc, g, a, l)
        adjust1(nc, g, a)
        with Room(nc, "m1") as r:
            g.q = g.hid
            g.v = r.sbuf("v", [P, NT, D])
            g.kvm = r.sbuf("kvm", [P, KD, D])
            mix1_keys(nc, g, a)
            mix1_out(nc, g, a)
        normalize(nc, g, "norm3")
        with Room(nc, "f1") as r:
            g.fw1 = r.sbuf("fw1", [P, 2, KD, F1])
            g.fw2 = r.sbuf("fw2", [P, 2, KF, D])
            g.fb1 = r.sbuf("fb1", [P, 2, KF])
            g.fb2 = r.sbuf("fb2", [P, D])
            g.fw = r.sbuf("fw", [P, 2])
            route1(nc, g, a)
            experts1(nc, g, a, out)


def _layout(v):
    import numpy as _np

    n = {k: _np.asarray(t) for k, t in v.items()}
    f = _np.float32
    ea = _np.zeros((P * ET, 3), f)
    ea[:EDGES] = n["edge_attr_3"]
    ablk = _np.zeros((D, 2 * H0), f)
    for h in range(H0):
        ablk[h * D0:(h + 1) * D0, h] = n["L0_gnn_a_src"][h]
        ablk[h * D0:(h + 1) * D0, H0 + h] = n["L0_gnn_a_dst"][h]
    pw = _np.zeros((QKV, P), f)
    for grp in range(QKV // GD):
        c = (grp * GD) % P
        pw[grp * GD:(grp + 1) * GD, c:c + GD] = n["L0_mix_w_pw"][grp * GD:(grp + 1) * GD, :, 0].T
    t = lambda w: _np.swapaxes(w, -1, -2)
    flat = lambda w: w.reshape(-1, w.shape[-1])
    return dict(
        x=n["x"], src=n["src"], dst=n["dst"], kind=n["edge_type_3"],
        ea=ea.reshape(P, ET, 3).transpose(2, 1, 0),
        gW=n["L0_gnn_W"], gWT=t(n["L0_gnn_W"]), ablk=ablk, eWT=t(n["L0_gnn_edge_W"]),
        eb=n["L0_gnn_edge_b"], gbias=n["L0_gnn_bias"],
        wqkv=t(n["L0_mix_w_qkv"][:, :, 2]), gamma=n["L0_mix_bn_gamma"], beta=n["L0_mix_bn_beta"],
        wdw=n["L0_mix_w_dw"][:, 0, 2].reshape(-1, P).T, pw=pw, wres=t(n["L0_mix_w_res"][:, :, 0]), bres=n["L0_mix_b_res"],
        rw1=n["L0_ffn_router_w1"], rb1=n["L0_ffn_router_b1"].reshape(P, 1), rw2=n["L0_ffn_router_w2"], rb2=n["L0_ffn_router_b2"],
        ew1=flat(n["L0_ffn_expert_w1"]), eb1=n["L0_ffn_expert_b1"].reshape(-1, P).T, ew2=flat(n["L0_ffn_expert_w2"]), eb2=n["L0_ffn_expert_b2"].reshape(-1, P).T,
        ew3=flat(n["L0_ffn_expert_w3"]), eb3=n["L0_ffn_expert_b3"],
        winT=t(n["L1_gnn_Win"]), b_in=n["L1_gnn_b_in"],
        wqT=flat(t(n["L1_gnn_Wq"])), bq=n["L1_gnn_bq"], wkT=flat(t(n["L1_gnn_Wk"])), bk=n["L1_gnn_bk"],
        wvT=flat(t(n["L1_gnn_Wv"])), bv=n["L1_gnn_bv"], eemb=flat(t(n["L1_gnn_Eemb"])),
        woT=flat(t(n["L1_gnn_Wo"])), bo=n["L1_gnn_bo"], ln_g=n["L1_gnn_ln_g"], ln_b=n["L1_gnn_ln_b"],
        w1T=t(n["L1_gnn_W1"]), b1=n["L1_gnn_b1"].reshape(-1, P).T, w2T=t(n["L1_gnn_W2"]), b2=n["L1_gnn_b2"],
        mqkv=n["L1_mix_W_qkv"], mb=n["L1_mix_b_qkv"], mout=n["L1_mix_W_out"], mbo=n["L1_mix_b_out"],
        wr=n["L1_ffn_Wr"], br=n["L1_ffn_br"], fw1=flat(n["L1_ffn_W1"]), fb1=n["L1_ffn_b1"].reshape(EXPERTS1, KF, P).transpose(0, 2, 1).reshape(-1, KF),
        fw2=flat(n["L1_ffn_W2"]), fb2=n["L1_ffn_b2"], fg=n["L1_ffn_gamma"], fb=n["L1_ffn_beta"],
    )


def kernel(**inputs):
    import numpy as _np
    import concourse.bacc as _bacc
    from concourse import mybir as _mybir
    from concourse.bass_utils import run_bass_kernel_spmd as _run

    nc = _bacc.Bacc("TRN2", target_bir_lowering=False, num_devices=1)
    arrays, drams = {}, {}
    for name, v in _layout(inputs).items():
        v = _np.ascontiguousarray(v)
        arrays[f"in_{name}_dram"] = v
        drams[name] = nc.dram_tensor(f"in_{name}_dram", v.shape, _mybir.dt.from_np(v.dtype), kind="ExternalInput").ap()
    out = nc.dram_tensor("out_0_dram", (NODES, D), F32, kind="ExternalOutput").ap()

    def scratch(name, shape, dt):
        return nc.dram_tensor(name, shape, dt, kind=SCRATCH).ap()

    gps_kernel(nc, drams, out, scratch)
    r = _run(nc, [arrays], core_ids=[0])
    return r.results[0]["out_0_dram"]


SCRATCH = "Internal"
```
